# Optimizing a Trainium2 kernel written in Bass

```python
import numpy as np
import jax
import jax.numpy as jnp

def _softmax(x, axis=-1):
    return jax.nn.softmax(x, axis=axis)

def _gelu(x):
    return jax.nn.gelu(x, approximate=True)

def _silu(x):
    return jax.nn.silu(x)

def _sigmoid(x):
    return jax.nn.sigmoid(x)

def _layernorm(x, axis=-1, eps=1e-05):
    m = jnp.mean(x, axis=axis, keepdims=True)
    v = jnp.var(x, axis=axis, keepdims=True)
    return (x - m) / jnp.sqrt(v + eps)

def _scatter_add(tgt, idx, src, axis=0):
    return tgt.at[idx].add(src)

def _segment_sum(src, seg, n):
    return jax.ops.segment_sum(src, seg, n)
kernel_name = 'mk_xattn_ffn_d4_seqx_r4_d3f5b5'

def setup_inputs(seed: int=0):
    np.random.seed(seed)
    _w = jnp.asarray

    def _rec_inputs():
        import jax
        import jax.numpy as jnp
        _rk = jax.random.key(seed)
        x = 7.22e-05 + 1 * jax.random.normal(jax.random.fold_in(_rk, 1), (16, 128, 256), jnp.float32)
        _lenS = 128 - jax.random.randint(jax.random.fold_in(_rk, 7), (16,), 0, max(1, 128 // 4) + 1, jnp.int32)
        _lenS2 = 128 - jax.random.randint(jax.random.fold_in(_rk, 8), (16,), 0, max(1, 128 // 4) + 1, jnp.int32)
        _ctx_1024P = jax.random.normal(jax.random.fold_in(_rk, 11), (16, 16, 256), jnp.float32)
        _ctx_1024c = jax.random.dirichlet(jax.random.fold_in(_rk, 511), 0.3 * jnp.ones((16,), jnp.float32), (16, 128))
        _ctx_1024t = jnp.einsum('bsk,bkd->bsd', _ctx_1024c, _ctx_1024P)
        _ctx_1024t = _ctx_1024t * jax.lax.rsqrt(jnp.mean(jnp.square(_ctx_1024t)) + 1e-12) * 0.953939
        ctx_1024 = 4.13588e-05 + 0.999923 * (_ctx_1024t + 0.3 * jax.random.normal(jax.random.fold_in(_rk, 611), (16, 128, 256), jnp.float32))
        _validS = jnp.arange(128)[None, :] < _lenS[:, None]
        _validS2 = jnp.arange(128)[None, :] < _lenS2[:, None]
        _causal = jnp.tril(jnp.ones((128, 128), dtype=bool))
        mask_BxSxS2_ff0 = jnp.where(jnp.ones((16, 128, 128), dtype=bool), 0.0, -1000000000.0).astype(jnp.float32)
        return (x, ctx_1024, mask_BxSxS2_ff0)
    x, ctx_1024, mask_BxSxS2_ff0 = _rec_inputs()

    def _L0_xattn_setup():
        import jax, jax.numpy as jnp
        import numpy as np
        D_K = 256
        HEADS = 16
        HK = 64
        HV = 64
        key = jax.random.key(seed)
        ks = jax.random.split(key, 12)
        B, S = (4, 512)
        sc_in = 1.0 / np.sqrt(D_K)
        sc_u = 1.0 / np.sqrt(HV * HEADS)
        return {'q': jax.random.normal(ks[0], (B, S, D_K), jnp.float32), 'k': jax.random.normal(ks[1], (B, S, D_K), jnp.float32), 'v': jax.random.normal(ks[2], (B, S, D_K), jnp.float32), 'Wq': jax.random.normal(ks[3], (D_K, HK * HEADS), jnp.float32) * sc_in, 'bq': jax.random.normal(ks[4], (HK * HEADS,), jnp.float32) * sc_in, 'Wk': jax.random.normal(ks[5], (D_K, HK * HEADS), jnp.float32) * sc_in, 'bk': jax.random.normal(ks[6], (HK * HEADS,), jnp.float32) * sc_in, 'Wv': jax.random.normal(ks[7], (D_K, HV * HEADS), jnp.float32) * sc_in, 'bv': jax.random.normal(ks[8], (HV * HEADS,), jnp.float32) * sc_in, 'Wu': jax.random.normal(ks[9], (HV * HEADS, D_K), jnp.float32) * sc_u, 'bu': jax.random.normal(ks[10], (D_K,), jnp.float32) * sc_u}
    _L0_xattn_all = _L0_xattn_setup()
    _L0_xattn_in = {k: v for k, v in _L0_xattn_all.items() if k in ('Wq', 'bq', 'Wk', 'bk', 'Wv', 'bv', 'Wu', 'bu')}
    del _L0_xattn_all

    def _L0_ffn_setup():
        import jax, jax.numpy as jnp
        import numpy as np
        D_MODEL = 256
        HIDDEN = 512
        MOE_DIM = 64
        N_EXPERTS = 8
        TOP_K = 2
        EXP_HIDDEN = HIDDEN // 2
        B, S = (4, 512)
        key = jax.random.key(seed)
        ks = jax.random.split(key, 20)

        def w(k, shape, fan_in):
            return (jax.random.normal(k, shape, dtype=jnp.float32) / np.sqrt(fan_in)).astype(jnp.float32)
        return {'inputs_embeds': jax.random.normal(ks[0], (B, S, D_MODEL), dtype=jnp.float32), 'enc_w': w(ks[1], (D_MODEL, HIDDEN), D_MODEL), 'enc_b': jnp.zeros((HIDDEN,), jnp.float32), 's2c_w': w(ks[2], (HIDDEN, MOE_DIM), HIDDEN), 's2c_b': jnp.zeros((MOE_DIM,), jnp.float32), 'r_w1': w(ks[3], (MOE_DIM, 64), MOE_DIM), 'r_b1': jnp.zeros((64,), jnp.float32), 'r_w2': w(ks[4], (64, N_EXPERTS), 64), 'r_b2': jnp.zeros((N_EXPERTS,), jnp.float32), 'e_w1': w(ks[5], (N_EXPERTS, MOE_DIM, EXP_HIDDEN), MOE_DIM), 'e_b1': jnp.zeros((N_EXPERTS, EXP_HIDDEN), jnp.float32), 'e_w2': w(ks[6], (N_EXPERTS, EXP_HIDDEN, MOE_DIM), EXP_HIDDEN), 'e_b2': jnp.zeros((N_EXPERTS, MOE_DIM), jnp.float32), 'c2s_w': w(ks[7], (MOE_DIM, HIDDEN), MOE_DIM), 'c2s_b': jnp.zeros((HIDDEN,), jnp.float32), 'dec_w': w(ks[8], (HIDDEN, D_MODEL), HIDDEN), 'dec_b': jnp.zeros((D_MODEL,), jnp.float32), 'ln_g': jnp.ones((D_MODEL,), jnp.float32), 'ln_b': jnp.zeros((D_MODEL,), jnp.float32)}
    _L0_ffn_all = _L0_ffn_setup()
    _L0_ffn_in = {k: v for k, v in _L0_ffn_all.items() if k in ('enc_w', 'enc_b', 's2c_w', 's2c_b', 'r_w1', 'r_b1', 'r_w2', 'r_b2', 'e_w1', 'e_b1', 'e_w2', 'e_b2', 'c2s_w', 'c2s_b', 'dec_w', 'dec_b', 'ln_g', 'ln_b')}
    del _L0_ffn_all

    def _L1_xattn_setup():
        import jax, jax.numpy as jnp
        import numpy as np
        from jax import lax
        NUM_HEADS = 16
        DIM = 256
        BATCH = 4
        SEQ = 512
        key = jax.random.key(seed)
        ks = jax.random.split(key, 12)
        f32 = jnp.float32
        q = jax.random.normal(ks[0], (BATCH, SEQ, DIM), dtype=f32)
        k = jax.random.normal(ks[1], (BATCH, SEQ, DIM), dtype=f32)
        v = jax.random.normal(ks[2], (BATCH, SEQ, DIM), dtype=f32)
        lim = 1.0 / np.sqrt(DIM)
        Wi = jax.random.uniform(ks[3], (DIM, DIM), minval=-lim, maxval=lim, dtype=f32)
        bi = jax.random.uniform(ks[4], (DIM,), minval=-lim, maxval=lim, dtype=f32)
        Wg = jax.random.uniform(ks[5], (DIM, DIM), minval=-lim, maxval=lim, dtype=f32)
        bg = jax.random.uniform(ks[6], (DIM,), minval=-lim, maxval=lim, dtype=f32)
        Wo = jax.random.uniform(ks[7], (DIM, DIM), minval=-lim, maxval=lim, dtype=f32)
        bo = jax.random.uniform(ks[8], (DIM,), minval=-lim, maxval=lim, dtype=f32)
        A = jax.random.normal(ks[9], (DIM, DIM), dtype=f32) * 0.1
        Bm = jax.random.normal(ks[10], (DIM, DIM), dtype=f32) * 0.1
        decay = jnp.full((1, NUM_HEADS, 1), 0.9, dtype=f32)
        return dict(q=q, k=k, v=v, Wi=Wi, bi=bi, Wg=Wg, bg=bg, A=A, Bm=Bm, Wo=Wo, bo=bo, decay=decay)
    _L1_xattn_all = _L1_xattn_setup()
    _L1_xattn_in = {k: v for k, v in _L1_xattn_all.items() if k in ('Wi', 'bi', 'Wg', 'bg', 'A', 'Bm', 'Wo', 'bo', 'decay')}
    del _L1_xattn_all

    def _L1_ffn_setup():
        import jax, jax.numpy as jnp
        import numpy as np
        B, S, D = (1, 512, 256)
        E, K, F = (64, 8, 192)
        SF = 192
        C = 128
        ROUTED_SCALE = 1.0

        def _moe_forward(x, router_w, w_gate, w_up, w_down, ws_gate_up, ws_down):
            T = x.shape[0]
            logits = x.astype(jnp.float32) @ router_w.T
            probs = jax.nn.softmax(logits, axis=-1)
            topk_w, topk_ids = jax.lax.top_k(probs, K)
            topk_w = topk_w / jnp.sum(topk_w, axis=-1, keepdims=True)
            topk_w = topk_w.astype(x.dtype)
            N = T * K
            flat_e = topk_ids.reshape(-1)
            flat_w = topk_w.reshape(-1)
            tok = jnp.arange(N) // K
            onehot = flat_e[:, None] == jnp.arange(E)[None, :]
            pos = jnp.cumsum(onehot, axis=0)[jnp.arange(N), flat_e] - 1
            valid = pos < C
            idx = jnp.where(valid, flat_e * C + pos, E * C)
            x_buf = jnp.zeros((E * C + 1, x.shape[1]), x.dtype).at[idx].set(x[tok])
            xb = x_buf[:E * C].reshape(E, C, -1)
            g = jnp.einsum('ecd,edf->ecf', xb, w_gate)
            u = jnp.einsum('ecd,edf->ecf', xb, w_up)
            h = jax.nn.silu(g) * u
            y = jnp.einsum('ecf,efd->ecd', h, w_down).reshape(E * C, -1)
            safe = jnp.where(valid, idx, 0)
            contrib = y[safe] * (flat_w * valid.astype(flat_w.dtype))[:, None]
            routed = jax.ops.segment_sum(contrib, tok, num_segments=T)
            routed = routed * ROUTED_SCALE
            gu = x @ ws_gate_up
            sg, su = (gu[:, :SF], gu[:, SF:])
            shared = jax.nn.silu(sg) * su @ ws_down
            return routed + shared
        key = jax.random.key(seed)
        ks = jax.random.split(key, 7)
        w = 0.02
        return {'hidden_states': jax.random.normal(ks[0], (B, S, D), jnp.float32), 'router_w': jax.random.normal(ks[1], (E, D), jnp.float32) * w, 'w_gate': jax.random.normal(ks[2], (E, D, F), jnp.float32) * w, 'w_up': jax.random.normal(ks[3], (E, D, F), jnp.float32) * w, 'w_down': jax.random.normal(ks[4], (E, F, D), jnp.float32) * w, 'ws_gate_up': jax.random.normal(ks[5], (D, 2 * SF), jnp.float32) * w, 'ws_down': jax.random.normal(ks[6], (SF, D), jnp.float32) * w}
    _L1_ffn_all = _L1_ffn_setup()
    _L1_ffn_in = {k: v for k, v in _L1_ffn_all.items() if k in ('router_w', 'w_gate', 'w_up', 'w_down', 'ws_gate_up', 'ws_down')}
    del _L1_ffn_all

    def _L2_xattn_setup():
        import math
        import jax, jax.numpy as jnp
        import numpy as np
        B, S, H, NH = (2, 512, 256, 4)
        DH = H // NH

        def _mlstm_parallel(qh, kh, vh, ig, fg, eps=1e-06):
            b, nh, s, dh = qh.shape
            log_f = jax.nn.log_sigmoid(fg)
            pcs = jnp.pad(jnp.cumsum(log_f, axis=-1), ((0, 0), (0, 0), (1, 0)))
            mat = pcs[..., :, None] - pcs[..., None, :]
            ltr = jnp.tril(jnp.ones((s, s), dtype=bool))
            log_fg_matrix = jnp.where(ltr, mat[..., 1:, 1:], -jnp.inf)
            log_D = log_fg_matrix + ig[..., None, :]
            max_log_D = jnp.max(log_D, axis=-1, keepdims=True)
            D = jnp.exp(log_D - max_log_D)
            qk = jnp.einsum('bhsd,bhtd->bhst', qh, kh) / math.sqrt(dh)
            C = qk * D
            normalizer = jnp.maximum(jnp.abs(C.sum(axis=-1, keepdims=True)), jnp.exp(-max_log_D))
            Cn = C / (normalizer + eps)
            return jnp.einsum('bhst,bhtd->bhsd', Cn, vh)
        key = jax.random.key(seed)
        ks = jax.random.split(key, 8)
        gate_std = 1.0 / math.sqrt(3 * H)
        return {'q': jax.random.normal(ks[0], (B, S, H), jnp.float32), 'k': jax.random.normal(ks[1], (B, S, H), jnp.float32), 'v': jax.random.normal(ks[2], (B, S, H), jnp.float32), 'w_igate': jax.random.normal(ks[3], (NH, 3 * H), jnp.float32) * gate_std, 'b_igate': jax.random.normal(ks[4], (NH,), jnp.float32) * 0.1, 'w_fgate': jax.random.normal(ks[5], (NH, 3 * H), jnp.float32) * gate_std, 'b_fgate': jnp.linspace(3.4, 6.0, NH, dtype=jnp.float32), 'ln_weight': jnp.zeros((H,), jnp.float32)}
    _L2_xattn_all = _L2_xattn_setup()
    _L2_xattn_in = {k: v for k, v in _L2_xattn_all.items() if k in ('w_igate', 'b_igate', 'w_fgate', 'b_fgate', 'ln_weight')}
    del _L2_xattn_all

    def _L2_ffn_setup():
        import jax, jax.numpy as jnp
        import numpy as np
        HIDDEN = 256
        INNER = 1024

        def _weight_quant(w):
            scale = 1.0 / jnp.clip(jnp.mean(jnp.abs(w)), 1e-05)
            wq = jnp.clip(jnp.round(w * scale), -1.0, 1.0) / scale
            return w + jax.lax.stop_gradient(wq - w)

        def _act_quant(x):
            scale = 127.0 / jnp.clip(jnp.max(jnp.abs(x), axis=-1, keepdims=True), 1e-05)
            xq = jnp.clip(jnp.round(x * scale), -128.0, 127.0) / scale
            return x + jax.lax.stop_gradient(xq - x)

        def _bitlinear(x, w):
            return jnp.einsum('bsi,oi->bso', _act_quant(x), _weight_quant(w))
        key = jax.random.key(seed)
        k0, k1, k2, k3 = jax.random.split(key, 4)
        x = jax.random.normal(k0, (4, 512, HIDDEN), dtype=jnp.float32)
        w_gate = jax.random.normal(k1, (INNER, HIDDEN), dtype=jnp.float32) / np.sqrt(HIDDEN)
        w_up = jax.random.normal(k2, (INNER, HIDDEN), dtype=jnp.float32) / np.sqrt(HIDDEN)
        w_down = jax.random.normal(k3, (HIDDEN, INNER), dtype=jnp.float32) / np.sqrt(INNER)
        return {'x': x, 'w_gate': w_gate, 'w_up': w_up, 'w_down': w_down}
    _L2_ffn_all = _L2_ffn_setup()
    _L2_ffn_in = {k: v for k, v in _L2_ffn_all.items() if k in ('w_gate', 'w_up', 'w_down')}
    del _L2_ffn_all

    def _L3_xattn_setup():
        import jax, jax.numpy as jnp
        import numpy as np
        DIM = 256
        CTX_DIM = 256
        HEADS = 16
        DIM_HEAD = 64
        INNER = HEADS * DIM_HEAD
        FF_INNER = 4 * DIM
        EPS = 1e-05

        def layer_norm(x, g, b):
            mu = jnp.mean(x, axis=-1, keepdims=True)
            var = jnp.var(x, axis=-1, keepdims=True)
            return (x - mu) * jax.lax.rsqrt(var + EPS) * g + b
        key = jax.random.key(seed)
        ks = jax.random.split(key, 10)
        b, n, j = (2, 512, 512)
        x = jax.random.normal(ks[0], (b, n, DIM), dtype=jnp.float32)
        context = jax.random.normal(ks[1], (b, j, CTX_DIM), dtype=jnp.float32)
        mask = jnp.zeros((b, n, j), dtype=jnp.float32)
        s = 0.02
        Wq = jax.random.normal(ks[2], (DIM, INNER), dtype=jnp.float32) * s
        Wkv = jax.random.normal(ks[3], (CTX_DIM, 2 * DIM_HEAD), dtype=jnp.float32) * s
        Wout = jax.random.normal(ks[4], (INNER, DIM), dtype=jnp.float32) * s
        W1 = jax.random.normal(ks[5], (DIM, 2 * FF_INNER), dtype=jnp.float32) * s
        W2 = jax.random.normal(ks[6], (FF_INNER, DIM), dtype=jnp.float32) * s
        ln_g = jnp.ones((DIM,), jnp.float32)
        ln_b = jnp.zeros((DIM,), jnp.float32)
        cln_g = jnp.ones((CTX_DIM,), jnp.float32)
        cln_b = jnp.zeros((CTX_DIM,), jnp.float32)
        return {'x': x, 'context': context, 'mask': mask, 'ln_g': ln_g, 'ln_b': ln_b, 'cln_g': cln_g, 'cln_b': cln_b, 'Wq': Wq, 'Wkv': Wkv, 'Wout': Wout, 'W1': W1, 'W2': W2}
    _L3_xattn_all = _L3_xattn_setup()
    _L3_xattn_in = {k: v for k, v in _L3_xattn_all.items() if k in ('ln_g', 'ln_b', 'cln_g', 'cln_b', 'Wq', 'Wkv', 'Wout', 'W1', 'W2')}
    del _L3_xattn_all

    def _L3_ffn_setup():
        import jax, jax.numpy as jnp
        import numpy as np
        D_MODEL, D_FF, RANK = (256, 1024, 64)
        B, S = (4, 1024)
        key = jax.random.key(seed)
        ks = jax.random.split(key, 7)
        return {'x': jax.random.normal(ks[0], (B, S, D_MODEL), dtype=jnp.float32), 'U1': jax.random.normal(ks[1], (D_MODEL, RANK), dtype=jnp.float32) * 0.02, 'V1': jax.random.normal(ks[2], (RANK, D_FF), dtype=jnp.float32) * 0.02, 'b1': jnp.zeros((D_FF,), dtype=jnp.float32), 'U2': jax.random.normal(ks[3], (D_FF, RANK), dtype=jnp.float32) * 0.02, 'V2': jax.random.normal(ks[4], (RANK, D_MODEL), dtype=jnp.float32) * 0.02, 'b2': jnp.zeros((D_MODEL,), dtype=jnp.float32)}
    _L3_ffn_all = _L3_ffn_setup()
    _L3_ffn_in = {k: v for k, v in _L3_ffn_all.items() if k in ('U1', 'V1', 'b1', 'U2', 'V2', 'b2')}
    del _L3_ffn_all
    return {'x': x, 'ctx_1024': ctx_1024, 'mask_BxSxS2_ff0': mask_BxSxS2_ff0, 'L0_xattn_Wq': _L0_xattn_in['Wq'], 'L0_xattn_bq': _L0_xattn_in['bq'], 'L0_xattn_Wk': _L0_xattn_in['Wk'], 'L0_xattn_bk': _L0_xattn_in['bk'], 'L0_xattn_Wv': _L0_xattn_in['Wv'], 'L0_xattn_bv': _L0_xattn_in['bv'], 'L0_xattn_Wu': _L0_xattn_in['Wu'], 'L0_xattn_bu': _L0_xattn_in['bu'], 'L0_ffn_enc_w': _L0_ffn_in['enc_w'], 'L0_ffn_enc_b': _L0_ffn_in['enc_b'], 'L0_ffn_s2c_w': _L0_ffn_in['s2c_w'], 'L0_ffn_s2c_b': _L0_ffn_in['s2c_b'], 'L0_ffn_r_w1': _L0_ffn_in['r_w1'], 'L0_ffn_r_b1': _L0_ffn_in['r_b1'], 'L0_ffn_r_w2': _L0_ffn_in['r_w2'], 'L0_ffn_r_b2': _L0_ffn_in['r_b2'], 'L0_ffn_e_w1': _L0_ffn_in['e_w1'], 'L0_ffn_e_b1': _L0_ffn_in['e_b1'], 'L0_ffn_e_w2': _L0_ffn_in['e_w2'], 'L0_ffn_e_b2': _L0_ffn_in['e_b2'], 'L0_ffn_c2s_w': _L0_ffn_in['c2s_w'], 'L0_ffn_c2s_b': _L0_ffn_in['c2s_b'], 'L0_ffn_dec_w': _L0_ffn_in['dec_w'], 'L0_ffn_dec_b': _L0_ffn_in['dec_b'], 'L0_ffn_ln_g': _L0_ffn_in['ln_g'], 'L0_ffn_ln_b': _L0_ffn_in['ln_b'], 'L1_xattn_Wi': _L1_xattn_in['Wi'], 'L1_xattn_bi': _L1_xattn_in['bi'], 'L1_xattn_Wg': _L1_xattn_in['Wg'], 'L1_xattn_bg': _L1_xattn_in['bg'], 'L1_xattn_A': _L1_xattn_in['A'], 'L1_xattn_Bm': _L1_xattn_in['Bm'], 'L1_xattn_Wo': _L1_xattn_in['Wo'], 'L1_xattn_bo': _L1_xattn_in['bo'], 'L1_xattn_decay': _L1_xattn_in['decay'], 'L1_ffn_router_w': _L1_ffn_in['router_w'], 'L1_ffn_w_gate': _L1_ffn_in['w_gate'], 'L1_ffn_w_up': _L1_ffn_in['w_up'], 'L1_ffn_w_down': _L1_ffn_in['w_down'], 'L1_ffn_ws_gate_up': _L1_ffn_in['ws_gate_up'], 'L1_ffn_ws_down': _L1_ffn_in['ws_down'], 'L2_xattn_w_igate': _L2_xattn_in['w_igate'], 'L2_xattn_b_igate': _L2_xattn_in['b_igate'], 'L2_xattn_w_fgate': _L2_xattn_in['w_fgate'], 'L2_xattn_b_fgate': _L2_xattn_in['b_fgate'], 'L2_xattn_ln_weight': _L2_xattn_in['ln_weight'], 'L2_ffn_w_gate': _L2_ffn_in['w_gate'], 'L2_ffn_w_up': _L2_ffn_in['w_up'], 'L2_ffn_w_down': _L2_ffn_in['w_down'], 'L3_xattn_ln_g': _L3_xattn_in['ln_g'], 'L3_xattn_ln_b': _L3_xattn_in['ln_b'], 'L3_xattn_cln_g': _L3_xattn_in['cln_g'], 'L3_xattn_cln_b': _L3_xattn_in['cln_b'], 'L3_xattn_Wq': _L3_xattn_in['Wq'], 'L3_xattn_Wkv': _L3_xattn_in['Wkv'], 'L3_xattn_Wout': _L3_xattn_in['Wout'], 'L3_xattn_W1': _L3_xattn_in['W1'], 'L3_xattn_W2': _L3_xattn_in['W2'], 'L3_ffn_U1': _L3_ffn_in['U1'], 'L3_ffn_V1': _L3_ffn_in['V1'], 'L3_ffn_b1': _L3_ffn_in['b1'], 'L3_ffn_U2': _L3_ffn_in['U2'], 'L3_ffn_V2': _L3_ffn_in['V2'], 'L3_ffn_b2': _L3_ffn_in['b2']}

def reference(x, ctx_1024, mask_BxSxS2_ff0, L0_xattn_Wq, L0_xattn_bq, L0_xattn_Wk, L0_xattn_bk, L0_xattn_Wv, L0_xattn_bv, L0_xattn_Wu, L0_xattn_bu, L0_ffn_enc_w, L0_ffn_enc_b, L0_ffn_s2c_w, L0_ffn_s2c_b, L0_ffn_r_w1, L0_ffn_r_b1, L0_ffn_r_w2, L0_ffn_r_b2, L0_ffn_e_w1, L0_ffn_e_b1, L0_ffn_e_w2, L0_ffn_e_b2, L0_ffn_c2s_w, L0_ffn_c2s_b, L0_ffn_dec_w, L0_ffn_dec_b, L0_ffn_ln_g, L0_ffn_ln_b, L1_xattn_Wi, L1_xattn_bi, L1_xattn_Wg, L1_xattn_bg, L1_xattn_A, L1_xattn_Bm, L1_xattn_Wo, L1_xattn_bo, L1_xattn_decay, L1_ffn_router_w, L1_ffn_w_gate, L1_ffn_w_up, L1_ffn_w_down, L1_ffn_ws_gate_up, L1_ffn_ws_down, L2_xattn_w_igate, L2_xattn_b_igate, L2_xattn_w_fgate, L2_xattn_b_fgate, L2_xattn_ln_weight, L2_ffn_w_gate, L2_ffn_w_up, L2_ffn_w_down, L3_xattn_ln_g, L3_xattn_ln_b, L3_xattn_cln_g, L3_xattn_cln_b, L3_xattn_Wq, L3_xattn_Wkv, L3_xattn_Wout, L3_xattn_W1, L3_xattn_W2, L3_ffn_U1, L3_ffn_V1, L3_ffn_b1, L3_ffn_U2, L3_ffn_V2, L3_ffn_b2):
    import jax
    import jax.numpy as jnp

    def _L0_xattn_ref(q, k, v, Wq, bq, Wk, bk, Wv, bv, Wu, bu):
        import jax, jax.numpy as jnp
        import numpy as np
        D_K = 256
        HEADS = 16
        HK = 64
        HV = 64
        B, S, _ = q.shape
        qh = (q @ Wq + bq).reshape(B, S, HEADS, HK).transpose(0, 2, 1, 3)
        kh = (k @ Wk + bk).reshape(B, S, HEADS, HK).transpose(0, 2, 1, 3)
        vh = (v @ Wv + bv).reshape(B, S, HEADS, HV).transpose(0, 2, 1, 3)
        scores = jnp.einsum('bhqd,bhkd->bhqk', qh, kh) / jnp.sqrt(jnp.asarray(HK, qh.dtype))
        attn = jax.nn.softmax(scores, axis=-1)
        out = jnp.einsum('bhqk,bhkd->bhqd', attn, vh)
        merged = out.transpose(0, 2, 1, 3).reshape(B, S, HEADS * HV)
        return merged @ Wu + bu

    def _L0_ffn_ref(inputs_embeds, enc_w, enc_b, s2c_w, s2c_b, r_w1, r_b1, r_w2, r_b2, e_w1, e_b1, e_w2, e_b2, c2s_w, c2s_b, dec_w, dec_b, ln_g, ln_b):
        import jax, jax.numpy as jnp
        import numpy as np
        D_MODEL = 256
        HIDDEN = 512
        MOE_DIM = 64
        N_EXPERTS = 8
        TOP_K = 2
        EXP_HIDDEN = HIDDEN // 2
        B, S = (4, 512)
        b, s, _ = inputs_embeds.shape
        spikes = jax.nn.sigmoid(inputs_embeds @ enc_w + enc_b)
        cont = spikes.reshape(b * s, -1) @ s2c_w + s2c_b
        rh = jax.nn.relu(cont @ r_w1 + r_b1)
        probs = jax.nn.softmax(rh @ r_w2 + r_b2, axis=-1)
        topw, topi = jax.lax.top_k(probs, TOP_K)
        topw = topw / jnp.sum(topw, axis=-1, keepdims=True)
        comb = jnp.sum(jax.nn.one_hot(topi, N_EXPERTS, dtype=cont.dtype) * topw[..., None], axis=1)
        eh = jax.nn.relu(jnp.einsum('nd,edh->neh', cont, e_w1) + e_b1)
        eo = jnp.einsum('neh,ehd->ned', eh, e_w2) + e_b2
        moe_out = jnp.einsum('ned,ne->nd', eo, comb)
        rates = jax.nn.sigmoid(moe_out @ c2s_w + c2s_b)
        x = rates.reshape(b, s, -1)
        dec = jax.nn.sigmoid(x @ dec_w + dec_b)
        mu = jnp.mean(dec, axis=-1, keepdims=True)
        var = jnp.var(dec, axis=-1, keepdims=True)
        return (dec - mu) * jax.lax.rsqrt(var + 1e-05) * ln_g + ln_b

    def _L1_xattn_ref(q, k, v, Wi, bi, Wg, bg, A, Bm, Wo, bo, decay):
        import jax, jax.numpy as jnp
        import numpy as np
        from jax import lax
        NUM_HEADS = 16
        DIM = 256
        BATCH = 4
        SEQ = 512
        B, S, D = q.shape
        H = decay.shape[1]
        hd = D // H
        qh = jnp.moveaxis(q.reshape(B, S, H, hd), 1, 0)
        kh = jnp.moveaxis(k.reshape(B, S, H, hd), 1, 0)
        vh = jnp.moveaxis(v.reshape(B, S, H, hd), 1, 0)

        def step(carry, xs):
            r, state = carry
            qt, kt, vt = xs
            r = decay * r + kt * vt
            retained = (qt * r).reshape(B, D)
            inp = retained @ Wi.T + bi
            gate = jax.nn.sigmoid(inp @ Wg.T + bg)
            blended = gate * state + (1.0 - gate) * inp
            state = jnp.tanh(blended @ A.T + inp @ Bm.T)
            out = state @ Wo.T + bo
            return ((r, state), out)
        r0 = jnp.zeros((B, H, hd), dtype=q.dtype)
        s0 = jnp.zeros((B, D), dtype=q.dtype)
        _, outs = lax.scan(step, (r0, s0), (qh, kh, vh))
        return jnp.moveaxis(outs, 0, 1)

    def _L1_ffn_ref(hidden_states, router_w, w_gate, w_up, w_down, ws_gate_up, ws_down):
        import jax, jax.numpy as jnp
        import numpy as np
        B, S, D = (1, 512, 256)
        E, K, F = (64, 8, 192)
        SF = 192
        C = 128
        ROUTED_SCALE = 1.0

        def _moe_forward(x, router_w, w_gate, w_up, w_down, ws_gate_up, ws_down):
            T = x.shape[0]
            logits = x.astype(jnp.float32) @ router_w.T
            probs = jax.nn.softmax(logits, axis=-1)
            topk_w, topk_ids = jax.lax.top_k(probs, K)
            topk_w = topk_w / jnp.sum(topk_w, axis=-1, keepdims=True)
            topk_w = topk_w.astype(x.dtype)
            N = T * K
            flat_e = topk_ids.reshape(-1)
            flat_w = topk_w.reshape(-1)
            tok = jnp.arange(N) // K
            onehot = flat_e[:, None] == jnp.arange(E)[None, :]
            pos = jnp.cumsum(onehot, axis=0)[jnp.arange(N), flat_e] - 1
            valid = pos < C
            idx = jnp.where(valid, flat_e * C + pos, E * C)
            x_buf = jnp.zeros((E * C + 1, x.shape[1]), x.dtype).at[idx].set(x[tok])
            xb = x_buf[:E * C].reshape(E, C, -1)
            g = jnp.einsum('ecd,edf->ecf', xb, w_gate)
            u = jnp.einsum('ecd,edf->ecf', xb, w_up)
            h = jax.nn.silu(g) * u
            y = jnp.einsum('ecf,efd->ecd', h, w_down).reshape(E * C, -1)
            safe = jnp.where(valid, idx, 0)
            contrib = y[safe] * (flat_w * valid.astype(flat_w.dtype))[:, None]
            routed = jax.ops.segment_sum(contrib, tok, num_segments=T)
            routed = routed * ROUTED_SCALE
            gu = x @ ws_gate_up
            sg, su = (gu[:, :SF], gu[:, SF:])
            shared = jax.nn.silu(sg) * su @ ws_down
            return routed + shared
        b, s, d = hidden_states.shape
        x = hidden_states.reshape(-1, d)
        out = _moe_forward(x, router_w, w_gate, w_up, w_down, ws_gate_up, ws_down)
        return out.reshape(b, s, d)

    def _L2_xattn_ref(q, k, v, w_igate, b_igate, w_fgate, b_fgate, ln_weight):
        import math
        import jax, jax.numpy as jnp
        import numpy as np
        B, S, H, NH = (2, 512, 256, 4)
        DH = H // NH

        def _mlstm_parallel(qh, kh, vh, ig, fg, eps=1e-06):
            b, nh, s, dh = qh.shape
            log_f = jax.nn.log_sigmoid(fg)
            pcs = jnp.pad(jnp.cumsum(log_f, axis=-1), ((0, 0), (0, 0), (1, 0)))
            mat = pcs[..., :, None] - pcs[..., None, :]
            ltr = jnp.tril(jnp.ones((s, s), dtype=bool))
            log_fg_matrix = jnp.where(ltr, mat[..., 1:, 1:], -jnp.inf)
            log_D = log_fg_matrix + ig[..., None, :]
            max_log_D = jnp.max(log_D, axis=-1, keepdims=True)
            D = jnp.exp(log_D - max_log_D)
            qk = jnp.einsum('bhsd,bhtd->bhst', qh, kh) / math.sqrt(dh)
            C = qk * D
            normalizer = jnp.maximum(jnp.abs(C.sum(axis=-1, keepdims=True)), jnp.exp(-max_log_D))
            Cn = C / (normalizer + eps)
            return jnp.einsum('bhst,bhtd->bhsd', Cn, vh)
        b, s, h = q.shape
        nh = b_igate.shape[0]
        dh = h // nh
        gin = jnp.concatenate([q, k, v], axis=-1)
        ig = jnp.einsum('bsd,hd->bhs', gin, w_igate) + b_igate[None, :, None]
        fg = jnp.einsum('bsd,hd->bhs', gin, w_fgate) + b_fgate[None, :, None]
        qh = q.reshape(b, s, nh, dh).transpose(0, 2, 1, 3)
        kh = k.reshape(b, s, nh, dh).transpose(0, 2, 1, 3)
        vh = v.reshape(b, s, nh, dh).transpose(0, 2, 1, 3)
        hst = _mlstm_parallel(qh, kh, vh, ig, fg)
        mean = hst.mean(axis=-1, keepdims=True)
        var = hst.var(axis=-1, keepdims=True)
        hn = (hst - mean) / jnp.sqrt(var + 1e-05)
        scale = (1.0 + ln_weight).reshape(nh, dh)
        hn = hn * scale[None, :, None, :]
        return hn.transpose(0, 2, 1, 3).reshape(b, s, h)

    def _L2_ffn_ref(x, w_gate, w_up, w_down):
        import jax, jax.numpy as jnp
        import numpy as np
        HIDDEN = 256
        INNER = 1024

        def _weight_quant(w):
            scale = 1.0 / jnp.clip(jnp.mean(jnp.abs(w)), 1e-05)
            wq = jnp.clip(jnp.round(w * scale), -1.0, 1.0) / scale
            return w + jax.lax.stop_gradient(wq - w)

        def _act_quant(x):
            scale = 127.0 / jnp.clip(jnp.max(jnp.abs(x), axis=-1, keepdims=True), 1e-05)
            xq = jnp.clip(jnp.round(x * scale), -128.0, 127.0) / scale
            return x + jax.lax.stop_gradient(xq - x)

        def _bitlinear(x, w):
            return jnp.einsum('bsi,oi->bso', _act_quant(x), _weight_quant(w))
        gate = jax.nn.silu(_bitlinear(x, w_gate))
        up = _bitlinear(x, w_up)
        return _bitlinear(gate * up, w_down)

    def _L3_xattn_ref(x, context, mask, ln_g, ln_b, cln_g, cln_b, Wq, Wkv, Wout, W1, W2):
        import jax, jax.numpy as jnp
        import numpy as np
        DIM = 256
        CTX_DIM = 256
        HEADS = 16
        DIM_HEAD = 64
        INNER = HEADS * DIM_HEAD
        FF_INNER = 4 * DIM
        EPS = 1e-05

        def layer_norm(x, g, b):
            mu = jnp.mean(x, axis=-1, keepdims=True)
            var = jnp.var(x, axis=-1, keepdims=True)
            return (x - mu) * jax.lax.rsqrt(var + EPS) * g + b
        scale = DIM_HEAD ** (-0.5)
        xn = layer_norm(x, ln_g, ln_b)
        cn = layer_norm(context, cln_g, cln_b)
        b, n, _ = xn.shape
        q = (xn @ Wq).reshape(b, n, HEADS, DIM_HEAD).transpose(0, 2, 1, 3) * scale
        kv = cn @ Wkv
        k, v = jnp.split(kv, 2, axis=-1)
        sim = jnp.einsum('bhid,bjd->bhij', q, k) + mask[:, None, :, :]
        attn = jax.nn.softmax(sim, axis=-1)
        out = jnp.einsum('bhij,bjd->bhid', attn, v)
        out = out.transpose(0, 2, 1, 3).reshape(b, n, INNER) @ Wout
        h = xn @ W1
        val, gate = jnp.split(h, 2, axis=-1)
        out = out + jax.nn.silu(gate) * val @ W2
        return out

    def _L3_ffn_ref(x, U1, V1, b1, U2, V2, b2):
        import jax, jax.numpy as jnp
        import numpy as np
        D_MODEL, D_FF, RANK = (256, 1024, 64)
        B, S = (4, 1024)
        P = jnp.einsum('bsd,dr->bsr', x, U1)
        H = jax.nn.gelu(jnp.einsum('bsr,rf->bsf', P, V1) + b1)
        Q = jnp.einsum('bsf,fr->bsr', H, U2)
        return jnp.einsum('bsr,rd->bsd', Q, V2) + b2
    x = x + _L0_xattn_ref(_layernorm(x, axis=-1), ctx_1024, ctx_1024, L0_xattn_Wq, L0_xattn_bq, L0_xattn_Wk, L0_xattn_bk, L0_xattn_Wv, L0_xattn_bv, L0_xattn_Wu, L0_xattn_bu)
    x = x + _L0_ffn_ref(_layernorm(x, axis=-1), L0_ffn_enc_w, L0_ffn_enc_b, L0_ffn_s2c_w, L0_ffn_s2c_b, L0_ffn_r_w1, L0_ffn_r_b1, L0_ffn_r_w2, L0_ffn_r_b2, L0_ffn_e_w1, L0_ffn_e_b1, L0_ffn_e_w2, L0_ffn_e_b2, L0_ffn_c2s_w, L0_ffn_c2s_b, L0_ffn_dec_w, L0_ffn_dec_b, L0_ffn_ln_g, L0_ffn_ln_b)
    x = x + _L1_xattn_ref(_layernorm(x, axis=-1), ctx_1024, ctx_1024, L1_xattn_Wi, L1_xattn_bi, L1_xattn_Wg, L1_xattn_bg, L1_xattn_A, L1_xattn_Bm, L1_xattn_Wo, L1_xattn_bo, L1_xattn_decay)
    x = x + _L1_ffn_ref(_layernorm(x, axis=-1), L1_ffn_router_w, L1_ffn_w_gate, L1_ffn_w_up, L1_ffn_w_down, L1_ffn_ws_gate_up, L1_ffn_ws_down)
    x = x + _L2_xattn_ref(_layernorm(x, axis=-1), ctx_1024, ctx_1024, L2_xattn_w_igate, L2_xattn_b_igate, L2_xattn_w_fgate, L2_xattn_b_fgate, L2_xattn_ln_weight)
    x = x + _L2_ffn_ref(_layernorm(x, axis=-1), L2_ffn_w_gate, L2_ffn_w_up, L2_ffn_w_down)
    x = x + _L3_xattn_ref(_layernorm(x, axis=-1), ctx_1024, mask_BxSxS2_ff0, L3_xattn_ln_g, L3_xattn_ln_b, L3_xattn_cln_g, L3_xattn_cln_b, L3_xattn_Wq, L3_xattn_Wkv, L3_xattn_Wout, L3_xattn_W1, L3_xattn_W2)
    x = x + _L3_ffn_ref(_layernorm(x, axis=-1), L3_ffn_U1, L3_ffn_V1, L3_ffn_b1, L3_ffn_U2, L3_ffn_V2, L3_ffn_b2)
    return x

_drawn_inputs = setup_inputs


def setup_inputs(seed=0):
    import zlib

    import numpy as np

    out = dict(_drawn_inputs(seed))
    spreads = {'L0_ffn_enc_b': (0.0, 0.1),
     'L0_ffn_s2c_b': (0.0, 0.1),
     'L0_ffn_r_b1': (0.0, 0.1),
     'L0_ffn_r_b2': (0.0, 0.1),
     'L0_ffn_e_b1': (0.0, 0.1),
     'L0_ffn_e_b2': (0.0, 0.1),
     'L0_ffn_c2s_b': (0.0, 0.1),
     'L0_ffn_dec_b': (0.0, 0.1),
     'L0_ffn_ln_g': (1.0, 0.2),
     'L0_ffn_ln_b': (0.0, 0.1),
     'L1_xattn_decay': (0.8999999761581421, 0.2),
     'L2_xattn_ln_weight': (0.0, 0.314),
     'L3_xattn_ln_g': (1.0, 0.6),
     'L3_xattn_ln_b': (0.0, 0.8),
     'L3_xattn_cln_g': (1.0, 0.6),
     'L3_xattn_cln_b': (0.0, 2.0),
     'L3_ffn_b1': (0.0, 0.8),
     'L3_ffn_b2': (0.0, 0.8)}
    factors = {'L0_xattn_bk': 64.0,
     'L1_xattn_bi': 8.0,
     'L1_xattn_bg': 8.0,
     'L1_ffn_router_w': 8.0,
     'L1_ffn_w_gate': 8.0,
     'L1_ffn_w_up': 8.0,
     'L1_ffn_w_down': 8.0,
     'L1_ffn_ws_gate_up': 5.861,
     'L1_ffn_ws_down': 5.865,
     'L2_xattn_b_igate': 64.0,
     'L3_xattn_Wq': 28.752,
     'L3_xattn_W1': 3.505,
     'L3_xattn_W2': 3.436,
     'L3_ffn_U1': 8.0,
     'L3_ffn_V1': 8.0,
     'L3_ffn_U2': 8.0,
     'L3_ffn_V2': 8.0,
     'L2_xattn_w_fgate': 2.944}
    for name, (base, spread) in spreads.items():
        noise = np.random.default_rng([zlib.crc32(name.encode()), seed]).standard_normal(out[name].shape)
        drawn = base * np.exp(spread * noise) if base else spread * noise
        out[name] = jnp.asarray(drawn.astype(out[name].dtype))
    for name, factor in factors.items():
        out[name] = (out[name] * factor).astype(out[name].dtype)
    return out
```

```python
from contextlib import ExitStack

import concourse.bass as bass
from concourse import mybir

ALU = mybir.AluOpType
ACT = mybir.ActivationFunctionType
AX = mybir.AxisListType
F32 = mybir.dt.float32
BF16 = mybir.dt.bfloat16
I32 = mybir.dt.int32
U32 = mybir.dt.uint32

P = 128
B, S, D = 16, 128, 256
KD = D // P
BC = 2
TOK = BC * S
NCH = B // BC
H, HD = 16, 64
HM = H * HD // P
FAN = 4
NE0, EH0, MD = 8, 256, 64
HID0 = 512
NE, CAP, FE = 64, 128, 192
TOPK = 8
HL, DL = 4, 64
INNER = 1024
EPS = 1e-5
LEAD = 512

LAYOUT = {
    "attn": [("wk", KD * 1024), ("wv", KD * 1024), ("wq", KD * 1024), ("bk", HM), ("bq", HM), ("bv", HM),
             ("wu", HM * D), ("bu", D)],
    "spike": [("enc", KD * HID0), ("enc_b", 4), ("s2c", 4 * P), ("s2c_b", 1), ("rw1", 64), ("rb1", 1),
              ("rw2", NE0), ("rb2", NE0), ("ew1", NE0 * P), ("eb1", NE0 * 2), ("ew2", NE0 * 2 * MD),
              ("eb2", NE0 * MD), ("c2s", HID0), ("c2s_b", 4), ("dec", 4 * D), ("dec_b", D), ("ln_g", D),
              ("ln_b", D)],
    "rec": [("wi", KD * D), ("bi", KD), ("wg", KD * D), ("bg", KD), ("a", KD * D), ("bm", KD * D),
            ("wo", KD * D), ("bo", D), ("decay", KD)],
    "moe": [("router", KD * NE), ("sgu", KD * 2 * FE), ("sdown", 2 * D)],
    "mlstm": [("gq", KD * 2 * HL), ("gk", KD * 2 * HL), ("gv", KD * 2 * HL), ("gb", 2 * HL), ("lnw", D)],
    "bit": [("wg", KD * INNER), ("wu", KD * INNER), ("wd", INNER // P * D)],
    "mqa": [("wq", KD * 1024), ("wk", KD * P), ("wv", KD * P), ("wout", HM * D), ("w1", KD * 2 * INNER),
            ("w2", INNER // P * D), ("ln_g", KD), ("ln_b", KD), ("cln_g", KD), ("cln_b", KD)],
    "low": [("u1", KD * P), ("v1", INNER // 2), ("b1", INNER // P), ("u2", INNER // P * 64), ("v2", D), ("b2", D)],
}
CONSTS = [("tri", P), ("tokens", B), ("slot_base", NE), ("spare", B * TOPK), ("late", P)]
COLS = {stage: sum(n for _, n in parts) for stage, parts in LAYOUT.items()}


class Steps:

    def __init__(self, sem):
        self.sem, self.end, self.table, self.next = sem, LEAD, {}, 0

    def plan(self, stage, names, iterations):
        self.table[stage] = (self.end, {n: k for k, n in enumerate(names)}, len(names))
        assert len(set(names)) == len(names)
        self.end += len(names) * iterations
        self.table[stage, "end"] = self.end

    def at(self, stage, i, name, back=0):
        start, index, n = self.table[stage]
        return i * n + (start + index[name] + 1 - back * n)

    def one(self, stage, name):
        index = self.table[stage][1]
        assert index[name] == self.next % len(index), (stage, name, self.next % len(index))
        self.next = (self.next + 1) % len(index)
        return 1

    def all(self, stage):
        return self.table[stage, "end"]
SPACE = 15360


def build(nc, ins, out):
    ctx = ExitStack()
    with ctx:
        block_program(nc, ins, out, ctx)


def block_program(nc, ins, out, ctx):
    def sb(name, shape, dt=F32):
        return ctx.enter_context(nc.sbuf_tensor(name, shape, dt))

    def sem(name):
        return ctx.enter_context(nc.semaphore(name))

    ctxT_dram = ins["ctxT"].rearrange("(k p) t -> p k t", p=P)
    mask_dram = ins["mask"].rearrange("b q k -> q b k")
    x_dram = ins["x"].rearrange("b s d -> s b d")
    ctx_dram = ins["ctx"].rearrange("b s d -> s b d")
    out_dram = out.rearrange("b s d -> s b d")

    x = sb("x", [P, B, D])
    nmr = sb("nmr", [P, B])
    rstd = sb("rstd", [P, B])
    xn = sb("xn", [P, BC, D])
    xnT = sb("xnT", [P, KD, TOK])
    ctxT = sb("ctxT", [P, KD, TOK])
    ident = sb("ident", [P, P])
    ones = sb("ones", [P, P])
    mhalf = sb("mhalf", [P, BC])
    iota8 = sb("iota8", [P, NE0])
    zrow = sb("zrow", [P, D])
    bnst = sb("bnst", [P, BC, 6])
    mv = sb("mv", [P, BC, 2])
    veps = sb("veps", [P, BC])
    w_place = {0: sb("w_even", [P, max(COLS[s] for s in ("attn", "rec", "mqa"))]),
               1: sb("w_odd", [P, max(COLS[s] for s in ("spike", "moe", "bit"))])}
    WPLACE = {"attn": (0, 0), "spike": (1, 0), "rec": (0, 0), "moe": (0, COLS["rec"]), "mlstm": (0, COLS["rec"] + COLS["moe"]),
              "bit": (1, 0), "mqa": (0, 0), "low": (1, 0)}
    space = sb("space", [P, SPACE])
    shape_consts = sb("shape_consts", [P, sum(n for _, n in CONSTS)])

    def C(name):
        at = sum(n for k, (m, n) in enumerate(CONSTS) if k < [m for m, _ in CONSTS].index(name))
        return shape_consts[:, at:at + dict(CONSTS)[name]]
    bank = [ctx.enter_context(nc.psum_tensor(f"bank{n}", [P, 512], F32)) for n in range(8)]

    def area(name, shape, at, dt=F32):
        n = 1
        for s in shape[1:]:
            n *= s
        words = n if dt == F32 else (n + 1) // 2
        assert at + words <= SPACE, (name, at + words)
        ap = space[0:shape[0], at:at + words]
        if dt != F32:
            ap = ap.bitcast(dt)
        if len(shape) == 3:
            ap = ap.rearrange("p (a b) -> p a b", a=shape[1])
        if len(shape) == 4:
            ap = ap.rearrange("p (a b c) -> p a b c", a=shape[1], b=shape[2])
        return ap

    def weight_reader(stage_name):
        place, first = WPLACE[stage_name]
        offsets, at = {}, first
        for n, c in LAYOUT[stage_name]:
            offsets[n] = (at, c)
            at += c
        return lambda n: w_place[place][:, offsets[n][0]:offsets[n][0] + offsets[n][1]]

    weights = {s: weight_reader(s) for s in LAYOUT}

    pe_s, act_s, dve_s, pool_s = (Steps(sem(n)) for n in ("tensor_steps", "scalar_steps", "vector_steps", "gpsimd_steps"))
    consts = sem("consts_written")
    x_loaded = sem("x_loaded")
    w_loaded = {s: sem(f"weights_{s}_loaded") for s in LAYOUT}
    ctxT_loaded = sem("ctxT_chunk_loaded")
    ctxT2_loaded = sem("ctxT_chunk_loaded_for_rec")
    ctxT3_loaded, ctx_loaded = sem("ctxT_chunk_loaded_for_mlstm"), sem("ctx_chunk_loaded_for_mlstm")
    ctx4_loaded, mask_loaded = sem("ctx_chunk_loaded_for_mqa"), sem("mask_chunk_loaded")
    consts_loaded = sem("shape_constants_loaded")
    zeroed = sem("zero_rows_written")
    gidx_set, sidx_set = sem("gather_rows_set"), sem("scatter_rows_set")
    bit_q = sem("weight_quantiser_steps")
    held = sem("waits_held_apart")
    bq8_ready = sem("bq8_ready")
    out_stored = sem("out_stored")

    def stage(name, iterations, pe, act, dve, pool):
        for s, names in ((pe_s, pe), (act_s, act), (dve_s, dve), (pool_s, pool)):
            s.plan(name, names, iterations)

    def others_done(eng, stage_name):
        for s in (pe_s, act_s, dve_s, pool_s):
            eng.wait_ge(s.sem, s.all(stage_name))

    def load_weights(eng, stage_name):
        place, first = WPLACE[stage_name]
        eng.dma_start(w_place[place][:, first:first + COLS[stage_name]], ins["w_" + stage_name]).then_inc(w_loaded[stage_name], 16)

    def after(st, i):
        return tuple(lambda name, back=0, s=s: (s.sem, s.at(st, i, name, back)) for s in (pe_s, act_s, dve_s, pool_s))

    def signals(steps, st):
        return lambda name: (steps.sem, steps.one(st, name))

    def wide(ap, n):
        return ap.unsqueeze(2).to_broadcast([ap.shape[0], ap.shape[1], n])

    def over(ap, n):
        return ap.unsqueeze(1).to_broadcast([ap.shape[0], n, ap.shape[1]])

    LN_DVE = ["bn0", "bn1", "ag0", "ag1", "veps", "nmr"]
    stage("load", NCH, pe=[], act=[], dve=LN_DVE, pool=["rstd"])

    def stats(name, i):
        nc.vector.sem_inc(held, 1)
        for b in range(BC):
            nc.vector.bn_stats(bnst[:, b, :], x[:, bass.ds(i * BC + b, 1), :]).then_inc(dve_s.sem, dve_s.one(name, f"bn{b}"))
        for b in range(BC):
            nc.vector.wait_ge(dve_s.sem, dve_s.at(name, i, f"bn{b}"))
            nc.vector.sem_inc(held, 1)
            nc.vector.bn_aggr(mv[:, b, :], bnst[:, b, :]).then_inc(dve_s.sem, dve_s.one(name, f"ag{b}"))
        nc.vector.wait_ge(dve_s.sem, dve_s.at(name, i, "ag1"))
        nc.vector.tensor_scalar(veps[:], mv[:, :, 1], EPS, None, ALU.add).then_inc(dve_s.sem, dve_s.one(name, "veps"))
        nc.vector.wait_ge(pool_s.sem, pool_s.at(name, i, "rstd"))
        nc.vector.scalar_tensor_tensor(nmr[:, bass.ds(i * BC, BC)], mv[:, :, 0], -1.0, rstd[:, bass.ds(i * BC, BC)],
                                       ALU.mult, ALU.mult).then_inc(dve_s.sem, dve_s.one(name, "nmr"))

    def stats_root(name, i):
        nc.gpsimd.wait_ge(dve_s.sem, dve_s.at(name, i, "veps"))
        nc.gpsimd.tensor_tensor(rstd[:, bass.ds(i * BC, BC)], veps[:], mhalf[:], ALU.pow).then_inc(
            pool_s.sem, pool_s.one(name, "rstd"))

    def prep(name, i):
        for b in range(BC):
            nc.scalar.activation(xn[:, b, :], x[:, bass.ds(i * BC + b, 1), :], ACT.Identity,
                                 bias=nmr[:, bass.ds(i * BC + b, 1)], scale=rstd[:, bass.ds(i * BC + b, 1)]).then_inc(
                act_s.sem, act_s.one(name, f"prep{b}"))

    def turn_x(name, i):
        nc.tensor.wait_ge(act_s.sem, act_s.at(name, i, "prep1"))
        for k in range(KD):
            for b in range(BC):
                last = nc.tensor.transpose(bank[7][:, (k * BC + b) * P:(k * BC + b + 1) * P], xn[:, b, k * P:(k + 1) * P], ident[:])
        last.then_inc(pe_s.sem, pe_s.one(name, "xT"))

    def load_dve():
        nc.vector.sem_inc(dve_s.sem, LEAD)
        nc.vector.wait_ge(x_loaded, 16)
        with nc.vector.Fori(0, NCH) as i:
            stats("load", i)

    def load_pool():
        nc.gpsimd.sem_inc(pool_s.sem, LEAD)
        nc.gpsimd.memset(ident[:], 0.0).then_inc(consts, 1)
        nc.gpsimd.memset(mhalf[:], -0.5).then_inc(consts, 1)
        nc.gpsimd.memset(ones[:], 1.0).then_inc(consts, 1)
        nc.gpsimd.wait_ge(consts, 3)
        nc.gpsimd.affine_select(out=ident[:], in_=ident[:], compare_op=ALU.not_equal, fill=1.0, base=0,
                                pattern=[[-1, P]], channel_multiplier=1).then_inc(consts, 1)
        with nc.gpsimd.Fori(0, NCH) as i:
            stats_root("load", i)

    GROUPS = ["k0", "k1", "v00", "v01", "k2", "k3", "v10", "v11", "q0", "q1", "q2", "q3"]
    UNITS = 2 * HM // FAN * BC
    AW = weights["attn"]
    wk, wv, wq = (AW(n).rearrange("p (k m) -> p k m", k=KD) for n in ("wk", "wv", "wq"))
    wu = AW("wu").rearrange("p (k n) -> p k n", k=HM)
    qT, kT, mT = (area(n, [P, HM, TOK], at) for n, at in (("qT", 0), ("kT", 2048), ("mT", 4096)))
    v = area("v", [P, BC, H * HD], 6144)
    prob = area("prob", [P, 4, FAN, P], 8192)
    probT = area("probT", [P, 2, FAN, P], 10240)
    sm = area("sm", [P, 3, 4, FAN], 11264)
    bq8 = area("bq8", [P, HM], 11328)
    ORDER = []
    for t in range(UNITS + 3):
        ORDER += [("S", t)] * (t < UNITS) + [("T", t - 2)] * (0 <= t - 2 < UNITS) + [("PV", t - 3)] * (0 <= t - 3 < UNITS)

    def unit(t):
        return t // 4, t % 4 // 2, t % 2

    DORDER = []
    for t in range(UNITS + 3):
        DORDER += [("max", t)] * (t < UNITS) + [("rec", t - 1)] * (0 <= t - 1 < UNITS)
        DORDER += [("copy", t - 2)] * (0 <= t - 2 < UNITS) + [("o", t - 3)] * (0 <= t - 3 < UNITS and t % 2 == 0)
    stage("attn", NCH,
          pe=GROUPS[:8] + ["xT"] + GROUPS[8:] + [f"{a}{t}" for a, t in ORDER] + ["out0", "out1"],
          act=["prep0", "prep1", "v00", "v01", "v10", "v11"] + [f"exp{t}" for t in range(UNITS)],
          dve=["k0", "k1", "k2", "k3", "xT", "q0", "q1", "q2", "q3"] + [f"{a}{t}" for a, t in DORDER] + ["res"] + LN_DVE,
          pool=["bu"] + [f"norm{t}" for t in range(UNITS)] + ["rstd"])

    def attn_sp():
        sp = nc.sync
        with sp.Fori(0, NCH) as i:
            sp.wait_ge(pe_s.sem, pe_s.at("attn", i, "v11", back=1))
            sp.dma_start(ctxT[:], ctxT_dram[:, :, bass.ds(i * TOK, TOK)]).then_inc(ctxT_loaded, 16)

    def attn_pe():
        pe, st = nc.tensor, "attn"
        pe.sem_inc(pe_s.sem, LEAD)
        pe.wait_ge(consts, 4)
        pe.wait_ge(w_loaded["attn"], 16)
        with pe.Fori(0, NCH) as i:
            pe.wait_ge(ctxT_loaded, i * 16 + 16)
            for n, g in enumerate(GROUPS):
                if g == "q0":
                    turn_x(st, i)
                    pe.wait_ge(dve_s.sem, dve_s.at(st, i, "xT"))
                if n >= 6:
                    user = GROUPS[n - 6]
                    who = act_s if user[0] == "v" else dve_s
                    pe.wait_ge(who.sem, who.at(st, i, user))
                dst = bank[n % 6]
                if g[0] == "v":
                    b, half = int(g[1]), int(g[2])
                    for k in range(KD):
                        last = nc.tensor.matmul(dst[:], ctxT[:, k, b * P:(b + 1) * P], wv[:, k, half * 512:(half + 1) * 512],
                                                start=k == 0, stop=k == KD - 1)
                else:
                    w, src = (wk, ctxT) if g[0] == "k" else (wq, xnT)
                    for m in range(2):
                        mm = 2 * int(g[1]) + m
                        for k in range(KD):
                            last = nc.tensor.matmul(dst[:, m * TOK:(m + 1) * TOK], w[:, k, mm * P:(mm + 1) * P], src[:, k, :],
                                                    start=k == 0, stop=k == KD - 1)
                last.then_inc(pe_s.sem, pe_s.one(st, g))
            pe.wait_ge(dve_s.sem, dve_s.at(st, i, "q3"))
            pe.wait_ge(act_s.sem, act_s.at(st, i, "v11"))
            for what, t in ORDER:
                b, u, par = unit(t)
                rows = slice(HD * par, HD * par + HD)
                if what == "S":
                    if t >= 2:
                        pe.wait_ge(act_s.sem, act_s.at(st, i, f"exp{t - 2}"))
                    for j in range(FAN):
                        m = FAN * u + j
                        last = nc.tensor.matmul(bank[t % 2][:, j * P:(j + 1) * P], qT[rows, m, b * P:(b + 1) * P],
                                                kT[rows, m, b * P:(b + 1) * P], start=True, stop=True)
                elif what == "T":
                    pe.wait_ge(pool_s.sem, pool_s.at(st, i, f"norm{t}"))
                    if t >= 2:
                        pe.wait_ge(dve_s.sem, dve_s.at(st, i, f"copy{t - 2}"))
                    for j in range(FAN):
                        last = nc.tensor.transpose(bank[2 + t % 2][:, j * P:(j + 1) * P], prob[:, t % 4, j, :], ident[:])
                else:
                    pe.wait_ge(dve_s.sem, dve_s.at(st, i, f"copy{t}"))
                    if b == 1 and par == 0:
                        pe.wait_ge(dve_s.sem, dve_s.at(st, i, f"o{t - 3}"))
                    for j in range(FAN):
                        h = 2 * (FAN * u + j) + par
                        last = nc.tensor.matmul(bank[4 + u][rows, j * P:(j + 1) * P], v[:, b, h * HD:(h + 1) * HD],
                                                probT[:, t % 2, j, :], start=True, stop=True)
                last.then_inc(pe_s.sem, pe_s.one(st, f"{what}{t}"))
            pe.wait_ge(dve_s.sem, dve_s.at(st, i, "res", back=1))
            for b in range(BC):
                pe.wait_ge(dve_s.sem, dve_s.at(st, i, f"o{4 * b + 3}"))
                for k in range(HM):
                    last = nc.tensor.matmul(bank[6][:, b * D:(b + 1) * D], mT[:, k, b * P:(b + 1) * P], wu[:, k, :],
                                            start=k == 0, stop=k == HM - 1)
                last.then_inc(pe_s.sem, pe_s.one(st, f"out{b}"))

    def attn_act():
        act, st = nc.scalar, "attn"
        act.sem_inc(act_s.sem, LEAD)
        act.wait_ge(dve_s.sem, dve_s.all("load"))
        with act.Fori(0, NCH) as i:
            prep(st, i)
            for b in range(BC):
                for half in range(2):
                    act.wait_ge(pe_s.sem, pe_s.at(st, i, f"v{b}{half}"))
                    nc.scalar.copy(v[:, b, half * 512:(half + 1) * 512], bank[GROUPS.index(f"v{b}{half}") % 6][:]).then_inc(
                        act_s.sem, act_s.one(st, f"v{b}{half}"))
            for t in range(UNITS):
                act.wait_ge(dve_s.sem, dve_s.at(st, i, f"max{t}"))
                if t >= 4:
                    act.wait_ge(pe_s.sem, pe_s.at(st, i, f"T{t - 4}"))
                for j in range(FAN):
                    last = nc.scalar.activation(prob[:, t % 4, j, :], bank[t % 2][:, j * P:(j + 1) * P], ACT.Exp,
                                                bias=sm[:, 0, t % 4, j:j + 1], accum_out=sm[:, 1, t % 4, j:j + 1])
                last.then_inc(act_s.sem, act_s.one(st, f"exp{t}"))

    def attn_pool():
        pool, st = nc.gpsimd, "attn"
        pool.wait_ge(w_loaded["attn"], 16)
        with pool.Fori(0, NCH) as i:
            pool.wait_ge(act_s.sem, act_s.at(st, i, "prep1"))
            nc.gpsimd.tensor_tensor(x[:, bass.ds(i * BC, BC), :], x[:, bass.ds(i * BC, BC), :],
                                    AW("bu").unsqueeze(1).to_broadcast([P, BC, D]), ALU.add).then_inc(pool_s.sem, pool_s.one(st, "bu"))
            for t in range(UNITS):
                pool.wait_ge(dve_s.sem, dve_s.at(st, i, f"rec{t}"))
                nc.gpsimd.tensor_tensor(prob[:, t % 4], prob[:, t % 4], sm[:, 2, t % 4, :].unsqueeze(2).to_broadcast([P, FAN, P]),
                                        ALU.mult).then_inc(pool_s.sem, pool_s.one(st, f"norm{t}"))
            stats_root(st, i)

    def attn_dve():
        dve, st = nc.vector, "attn"
        dve.wait_ge(w_loaded["attn"], 16)
        nc.vector.tensor_scalar(bq8[:], AW("bq"), HD ** -0.5, None, ALU.mult).then_inc(bq8_ready, 1)
        dve.wait_ge(bq8_ready, 1)
        with dve.Fori(0, NCH) as i:
            for n in range(4):
                g = f"k{n}"
                dve.wait_ge(pe_s.sem, pe_s.at(st, i, g))
                nc.vector.tensor_tensor(kT[:, 2 * n:2 * n + 2, :], bank[GROUPS.index(g) % 6][:].rearrange("p (m t) -> p m t", m=2),
                                        AW("bk")[:, 2 * n:2 * n + 2].unsqueeze(2).to_broadcast([P, 2, TOK]), ALU.add).then_inc(
                    dve_s.sem, dve_s.one(st, g))
            dve.wait_ge(pe_s.sem, pe_s.at(st, i, "xT"))
            nc.vector.tensor_copy(xnT[:].rearrange("p k t -> p (k t)"), bank[7][:]).then_inc(dve_s.sem, dve_s.one(st, "xT"))
            for n in range(4):
                g = f"q{n}"
                dve.wait_ge(pe_s.sem, pe_s.at(st, i, g))
                nc.vector.scalar_tensor_tensor(qT[:, 2 * n:2 * n + 2, :], bank[GROUPS.index(g) % 6][:].rearrange("p (m t) -> p m t", m=2),
                                               HD ** -0.5, bq8[:, 2 * n:2 * n + 2].unsqueeze(2).to_broadcast([P, 2, TOK]),
                                               ALU.mult, ALU.add).then_inc(dve_s.sem, dve_s.one(st, g))
            for what, t in DORDER:
                b, u, par = unit(t)
                if what == "max":
                    dve.wait_ge(pe_s.sem, pe_s.at(st, i, f"S{t}"))
                    ins = nc.vector.tensor_reduce(sm[:, 0, t % 4, :], bank[t % 2][:].rearrange("p (j s) -> p j s", j=FAN),
                                                  AX.X, ALU.max, negate=True)
                elif what == "rec":
                    dve.wait_ge(act_s.sem, act_s.at(st, i, f"exp{t}"))
                    ins = nc.vector.reciprocal(sm[:, 2, t % 4, :], sm[:, 1, t % 4, :])
                elif what == "copy":
                    dve.wait_ge(pe_s.sem, pe_s.at(st, i, f"T{t}"))
                    ins = nc.vector.tensor_copy(probT[:, t % 2].rearrange("p j s -> p (j s)"), bank[2 + t % 2][:])
                else:
                    dve.wait_ge(pe_s.sem, pe_s.at(st, i, f"PV{t}"))
                    ins = nc.vector.tensor_tensor(mT[:, FAN * u:FAN * u + FAN, b * P:(b + 1) * P],
                                                  bank[4 + u][:].rearrange("p (j s) -> p j s", j=FAN),
                                                  AW("bv")[:, FAN * u:FAN * u + FAN].unsqueeze(2).to_broadcast([P, FAN, P]), ALU.add)
                ins.then_inc(dve_s.sem, dve_s.one(st, f"{what}{t}"))
            dve.wait_ge(pe_s.sem, pe_s.at(st, i, "out1"))
            dve.wait_ge(pool_s.sem, pool_s.at(st, i, "bu"))
            nc.vector.tensor_tensor(x[:, bass.ds(i * BC, BC), :], bank[6][:].rearrange("p (b d) -> p b d", b=BC),
                                    x[:, bass.ds(i * BC, BC), :], ALU.add).then_inc(dve_s.sem, dve_s.one(st, "res"))
            dve.wait_ge(dve_s.sem, dve_s.at(st, i, "res"))
            stats(st, i)


    SW = weights["spike"]
    enc = SW("enc").rearrange("p (k m) -> p k m", k=KD)
    s2c = SW("s2c").rearrange("p (k m) -> p k m", k=4)
    ew1 = SW("ew1").rearrange("p (e m) -> p e m", e=NE0)
    ew2 = SW("ew2").rearrange("p (e m) -> p e m", e=NE0 * 2)
    dec_w = SW("dec").rearrange("p (k m) -> p k m", k=4)
    spT = area("spT", [P, 4, TOK], 0)
    contT = area("contT", [P, TOK], 1024)
    rhT = area("rhT", [64, TOK], 1280)
    ehT = area("ehT", [P, NE0 * 2, TOK], 1536)
    lg0 = area("lg0", [P, BC, NE0], 5632)
    mx0 = area("mx0", [P, BC, 8], 5648)
    ix0 = area("ix0", [P, BC, 8], 5664)
    ixf0 = area("ixf0", [P, BC, 8], 5680)
    gap0 = area("gap0", [P, BC], 5696)
    w0 = area("w0", [P, 2, BC], 5698)
    pick0 = area("pick0", [P, 2, BC, NE0], 5704)
    comb0 = area("comb0", [P, BC, NE0], 5736)
    eo = area("eo", [P, BC, NE0 * MD], 5760)
    moe0 = area("moe0", [P, BC, MD], 6784)
    moe0T = area("moe0T", [64, TOK], 6912)
    rT = area("rT", [P, 4, TOK], 7168)
    dec = area("dec", [P, BC, D], 8192)
    decn = area("decn", [P, BC, D], 8704)
    dnmr = area("dnmr", [P, BC], 9216)
    dveps = area("dveps", [P, BC], 9218)
    drstd = area("drstd", [P, BC], 9220)
    dbn = area("dbn", [P, BC, 6], 9222)
    dmv = area("dmv", [P, BC, 2], 9234)
    EP = NE0 // 2
    stage("spike", NCH,
          pe=["xT", "e0", "e1", "s2c", "rh", "lg"] + [f"h{n}{h}" for n in range(EP) for h in range(2)]
          + ["eo0", "eo1", "mT", "c0", "c1", "dec"],
          act=["prep0", "prep1", "e0", "e1", "rh", "w"] + [f"h{n}" for n in range(EP)] + ["c0", "c1", "dec"],
          dve=["xT", "s2c", "lg", "mx0", "mx1", "ix0", "ix1", "ixf", "gap", "h0"]
          + ["p00", "p01", "p10", "p11", "comb"] + ["h1", "h2", "h3"]
          + ["a0", "m0", "r0", "a1", "m1", "r1", "mT", "dadd", "dbn0", "dbn1", "dag0", "dag1", "dveps", "dn0", "dn1", "res"] + LN_DVE,
          pool=["drstd", "g", "b", "rstd"])

    def spike_pe():
        pe, st = nc.tensor, "spike"
        others_done(pe, "attn")
        pe.wait_ge(w_loaded[st], 16)
        done = signals(pe_s, st)
        with pe.Fori(0, NCH) as i:
            PE, ACTS, DVE, POOL = after(st, i)
            turn_x(st, i)
            pe.wait_ge(*DVE("xT"))
            for n in range(2):
                for m in range(2):
                    for k in range(KD):
                        last = nc.tensor.matmul(bank[n][:, m * TOK:(m + 1) * TOK], enc[:, k, (2 * n + m) * P:(2 * n + m + 1) * P],
                                                xnT[:, k, :], start=k == 0, stop=k == KD - 1)
                last.then_inc(*done(f"e{n}"))
            pe.wait_ge(*ACTS("e1"))
            for k in range(4):
                last = nc.tensor.matmul(bank[2][:, 0:TOK], s2c[:, k, :], spT[:, k, :], start=k == 0, stop=k == 3)
            last.then_inc(*done("s2c"))
            pe.wait_ge(*DVE("s2c"))
            pe.sem_inc(held, 1)
            nc.tensor.matmul(bank[3][0:64, 0:TOK], SW("rw1")[0:64], contT[0:64], start=True, stop=True).then_inc(*done("rh"))
            pe.wait_ge(*ACTS("rh"))
            for b in range(BC):
                last = nc.tensor.matmul(bank[3][:, b * NE0:(b + 1) * NE0], rhT[:, b * P:(b + 1) * P], SW("rw2")[0:64],
                                        start=True, stop=True)
            last.then_inc(*done("lg"))
            pe.wait_ge(*DVE("xT"))
            for n in range(EP):
                if n >= 2:
                    pe.wait_ge(*ACTS(f"h{n - 2}"))
                    pe.wait_ge(*DVE(f"h{n - 2}"))
                for half in range(2):
                    rows = slice(64 * half, 64 * half + 64)
                    for e in range(2):
                        last = nc.tensor.matmul(bank[4 + 2 * (n % 2) + half][:, e * TOK:(e + 1) * TOK], ew1[rows, 2 * n + e, :],
                                                contT[rows, :], start=True, stop=True)
                    last.then_inc(*done(f"h{n}{half}"))
            pe.wait_ge(*ACTS(f"h{EP - 1}"))
            pe.wait_ge(*DVE(f"h{EP - 1}"))
            for b in range(BC):
                for e in range(NE0):
                    for half in range(2):
                        last = nc.tensor.matmul(bank[b][:, e * MD:(e + 1) * MD], ehT[:, 2 * e + half, b * P:(b + 1) * P],
                                                ew2[:, 2 * e + half, :], start=half == 0, stop=half == 1)
                last.then_inc(*done(f"eo{b}"))
            pe.wait_ge(*DVE("r1"))
            pe.sem_inc(held, 1)
            for b in range(BC):
                last = nc.tensor.transpose(bank[2][0:64, b * P:(b + 1) * P], moe0[:, b, :], ident[:])
            last.then_inc(*done("mT"))
            pe.wait_ge(*DVE("mT"))
            for n in range(2):
                for m in range(2):
                    last = nc.tensor.matmul(bank[3 + n][:, m * TOK:(m + 1) * TOK], SW("c2s")[0:64, (2 * n + m) * P:(2 * n + m + 1) * P],
                                            moe0T[:], start=True, stop=True)
                last.then_inc(*done(f"c{n}"))
            pe.wait_ge(*ACTS("c1"))
            for b in range(BC):
                for k in range(4):
                    last = nc.tensor.matmul(bank[5][:, b * D:(b + 1) * D], rT[:, k, b * P:(b + 1) * P], dec_w[:, k, :],
                                            start=k == 0, stop=k == 3)
            last.then_inc(*done("dec"))

    def spike_act():
        act, st = nc.scalar, "spike"
        others_done(act, "attn")
        act.wait_ge(w_loaded[st], 16)
        done = signals(act_s, st)
        with act.Fori(0, NCH) as i:
            PE, ACTS, DVE, POOL = after(st, i)
            prep(st, i)
            for n in range(2):
                act.wait_ge(*PE(f"e{n}"))
                for m in range(2):
                    last = nc.scalar.activation(spT[:, 2 * n + m, :], bank[n][:, m * TOK:(m + 1) * TOK], ACT.Sigmoid,
                                                bias=SW("enc_b")[:, 2 * n + m:2 * n + m + 1])
                last.then_inc(*done(f"e{n}"))
            act.wait_ge(*PE("rh"))
            nc.scalar.activation(rhT[:], bank[3][0:64, 0:TOK], ACT.Relu, bias=SW("rb1")[0:64]).then_inc(*done("rh"))
            act.wait_ge(*DVE("gap"))
            nc.scalar.activation(w0[:, 0, :], gap0[:], ACT.Sigmoid, scale=-1.0)
            nc.scalar.activation(w0[:, 1, :], gap0[:], ACT.Sigmoid).then_inc(*done("w"))
            for n in range(EP):
                act.wait_ge(*PE(f"h{n}0"))
                for e in range(2):
                    last = nc.scalar.activation(ehT[:, 2 * (2 * n + e), :], bank[4 + 2 * (n % 2)][:, e * TOK:(e + 1) * TOK], ACT.Relu,
                                                bias=SW("eb1")[:, 2 * (2 * n + e):2 * (2 * n + e) + 1])
                last.then_inc(*done(f"h{n}"))
            for n in range(2):
                act.wait_ge(*PE(f"c{n}"))
                for m in range(2):
                    last = nc.scalar.activation(rT[:, 2 * n + m, :], bank[3 + n][:, m * TOK:(m + 1) * TOK], ACT.Sigmoid,
                                                bias=SW("c2s_b")[:, 2 * n + m:2 * n + m + 1])
                last.then_inc(*done(f"c{n}"))
            act.wait_ge(*DVE("dadd"))
            nc.scalar.activation(dec[:], dec[:], ACT.Sigmoid).then_inc(*done("dec"))

    def spike_pool():
        pool, st = nc.gpsimd, "spike"
        others_done(pool, "attn")
        pool.wait_ge(w_loaded[st], 16)
        for e in range(NE0):
            last = nc.gpsimd.memset(iota8[:, e:e + 1], float(e))
        last.then_inc(consts, 1)
        done = signals(pool_s, st)
        with pool.Fori(0, NCH) as i:
            PE, ACTS, DVE, POOL = after(st, i)
            pool.wait_ge(*DVE("dveps"))
            nc.gpsimd.tensor_tensor(drstd[:], dveps[:], mhalf[:], ALU.pow).then_inc(*done("drstd"))
            pool.wait_ge(*DVE("dn1"))
            nc.gpsimd.tensor_tensor(decn[:], decn[:], over(SW("ln_g"), BC), ALU.mult).then_inc(*done("g"))
            pool.wait_ge(*POOL("g"))
            nc.gpsimd.tensor_tensor(decn[:], decn[:], over(SW("ln_b"), BC), ALU.add).then_inc(*done("b"))
            stats_root(st, i)

    def spike_dve():
        dve, st = nc.vector, "spike"
        others_done(dve, "attn")
        dve.wait_ge(w_loaded[st], 16)
        dve.wait_ge(consts, 5)
        done = signals(dve_s, st)
        with dve.Fori(0, NCH) as i:
            PE, ACTS, DVE, POOL = after(st, i)

            def relu(n):
                dve.wait_ge(*PE(f"h{n}1"))
                for e in range(2):
                    c = 2 * (2 * n + e) + 1
                    last = nc.vector.tensor_scalar(ehT[:, c, :], bank[5 + 2 * (n % 2)][:, e * TOK:(e + 1) * TOK],
                                                   SW("eb1")[:, c:c + 1], 0.0, ALU.add, ALU.max)
                last.then_inc(*done(f"h{n}"))

            dve.wait_ge(*PE("xT"))
            nc.vector.tensor_copy(xnT[:].rearrange("p k t -> p (k t)"), bank[7][:]).then_inc(*done("xT"))
            dve.wait_ge(*PE("s2c"))
            nc.vector.tensor_scalar(contT[:], bank[2][:, 0:TOK], SW("s2c_b"), None, ALU.add).then_inc(*done("s2c"))
            dve.wait_ge(*PE("lg"))
            nc.vector.tensor_tensor(lg0[:], bank[3][:, 0:BC * NE0].rearrange("p (b e) -> p b e", b=BC), over(SW("rb2"), BC),
                                    ALU.add).then_inc(*done("lg"))
            dve.wait_ge(*DVE("lg"))
            dve.sem_inc(held, 1)
            for b in range(BC):
                nc.vector.max(mx0[:, b, :], lg0[:, b, :]).then_inc(*done(f"mx{b}"))
            dve.wait_ge(*DVE("mx1"))
            dve.sem_inc(held, 1)
            for b in range(BC):
                nc.vector.max_index(ix0[:, b, :].bitcast(U32), mx0[:, b, :], lg0[:, b, :]).then_inc(*done(f"ix{b}"))
            dve.wait_ge(*DVE("ix1"))
            nc.vector.tensor_copy(ixf0[:], ix0[:].bitcast(U32)).then_inc(*done("ixf"))
            nc.vector.tensor_tensor(gap0[:], mx0[:, :, 1], mx0[:, :, 0], ALU.subtract).then_inc(*done("gap"))
            relu(0)
            dve.wait_ge(*ACTS("w"))
            for b in range(BC):
                for k in range(2):
                    nc.vector.tensor_scalar(pick0[:, k, b, :], iota8[:], ixf0[:, b, k:k + 1], w0[:, k, b:b + 1], ALU.is_equal,
                                            ALU.mult).then_inc(*done(f"p{b}{k}"))
            dve.wait_ge(*DVE("p11"))
            nc.vector.tensor_tensor(comb0[:], pick0[:, 0], pick0[:, 1], ALU.add).then_inc(*done("comb"))
            for n in range(1, EP):
                relu(n)
            for b in range(BC):
                dve.wait_ge(*PE(f"eo{b}"))
                nc.vector.tensor_tensor(eo[:, b, :], bank[b][:], SW("eb2"), ALU.add).then_inc(*done(f"a{b}"))
                dve.wait_ge(*DVE(f"a{b}"))
                nc.vector.tensor_tensor(eo[:, b, :].rearrange("p (e d) -> p e d", e=NE0), eo[:, b, :].rearrange("p (e d) -> p e d", e=NE0),
                                        wide(comb0[:, b, :], MD), ALU.mult).then_inc(*done(f"m{b}"))
                dve.wait_ge(*DVE(f"m{b}"))
                nc.vector.tensor_reduce(moe0[:, b, :], eo[:, b, :].rearrange("p (e d) -> p d e", e=NE0), AX.X,
                                        ALU.add).then_inc(*done(f"r{b}"))
            dve.wait_ge(*PE("mT"))
            nc.vector.tensor_copy(moe0T[:], bank[2][0:64, 0:TOK]).then_inc(*done("mT"))
            dve.wait_ge(*PE("dec"))
            nc.vector.tensor_tensor(dec[:], bank[5][:].rearrange("p (b d) -> p b d", b=BC), over(SW("dec_b"), BC),
                                    ALU.add).then_inc(*done("dadd"))
            dve.wait_ge(*ACTS("dec"))
            for b in range(BC):
                nc.vector.bn_stats(dbn[:, b, :], dec[:, b, :]).then_inc(*done(f"dbn{b}"))
            for b in range(BC):
                dve.wait_ge(*DVE(f"dbn{b}"))
                nc.vector.sem_inc(held, 1)
                nc.vector.bn_aggr(dmv[:, b, :], dbn[:, b, :]).then_inc(*done(f"dag{b}"))
            dve.wait_ge(*DVE("dag1"))
            nc.vector.tensor_scalar(dveps[:], dmv[:, :, 1], EPS, None, ALU.add).then_inc(*done("dveps"))
            dve.wait_ge(*POOL("drstd"))
            for b in range(BC):
                nc.vector.tensor_scalar(decn[:, b, :], dec[:, b, :], dmv[:, b, 0:1], drstd[:, b:b + 1], ALU.subtract,
                                        ALU.mult).then_inc(*done(f"dn{b}"))
            dve.wait_ge(*POOL("b"))
            nc.vector.tensor_tensor(x[:, bass.ds(i * BC, BC), :], decn[:], x[:, bass.ds(i * BC, BC), :], ALU.add).then_inc(*done("res"))
            dve.wait_ge(*DVE("res"))
            stats(st, i)

    RW = weights["rec"]
    wi, wg1, wa, wbm, wo1 = (RW(n).rearrange("p (k m) -> p k m", k=KD) for n in ("wi", "wg", "a", "bm", "wo"))
    gate = area("gate", [P, KD, S, B], 0)
    drive = area("drive", [P, KD, S, B], 4096)
    state = area("state", [P, KD, S, B], 8192)
    c2 = area("c2", [P, KD, TOK], 8192)
    rT1 = area("rT1", [P, KD, TOK], 8704)
    ret = area("ret", [P, KD, TOK], 9216)
    inp = area("inp", [P, KD, TOK], 9728)
    gc = area("gc", [P, KD, TOK], 10240)
    cin = area("cin", [P, KD, TOK], 10752)
    z = area("z", [P, KD, B], 12288)
    sT = area("sT", [P, KD, TOK], 12352)
    CH = [f"{k}{b}" for k in range(KD) for b in range(BC)]
    stage("rec_in", NCH, pe=["xT", "inp", "gate", "drive"],
          act=["prep0", "prep1", "inp", "gate", "drive"],
          dve=["c2"] + [f"r{c}" for c in CH] + ["xT", "ret", "gc", "cin"], pool=[])
    stage("rec_0", 1, pe=["t0"], act=["t0"], dve=["z0"], pool=[])
    stage("rec_loop", (S - 2) // 2, pe=["t0", "t1"], act=["t0", "t1"], dve=["z0", "z1"], pool=[])
    stage("rec_9", 1, pe=["t0"], act=["t0"], dve=["z0"], pool=[])
    stage("rec", NCH, pe=["out"], act=["sT"], dve=["res"] + LN_DVE, pool=["bo", "rstd"])

    def rec_sp():
        sp = nc.sync
        others_done(sp, "attn")
        for name in ("rec", "moe", "mlstm"):
            load_weights(sp, name)
        others_done(sp, "spike")
        with sp.Fori(0, NCH) as i:
            sp.wait_ge(dve_s.sem, dve_s.at("rec_in", i, "c2", back=1))
            sp.dma_start(ctxT[:], ctxT_dram[:, :, bass.ds(i * TOK, TOK)]).then_inc(ctxT2_loaded, 16)

    def rec_pe():
        pe, st = nc.tensor, "rec_in"
        others_done(pe, "spike")
        pe.wait_ge(w_loaded["rec"], 16)
        done = signals(pe_s, st)
        with pe.Fori(0, NCH) as i:
            PE, ACTS, DVE, POOL = after(st, i)
            turn_x(st, i)
            for n, (w, src, what) in enumerate(((wi, ret, "inp"), (wg1, inp, "gate"))):
                pe.wait_ge(*(DVE("ret") if n == 0 else ACTS("inp")))
                for m in range(KD):
                    for k in range(KD):
                        last = nc.tensor.matmul(bank[n][:, m * TOK:(m + 1) * TOK], w[:, k, m * P:(m + 1) * P], src[:, k, :],
                                                start=k == 0, stop=k == KD - 1)
                last.then_inc(*done(what))
            pe.wait_ge(*DVE("cin"))
            for m in range(KD):
                for k in range(KD):
                    nc.tensor.matmul(bank[2][:, m * TOK:(m + 1) * TOK], wbm[:, k, m * P:(m + 1) * P], inp[:, k, :],
                                     start=k == 0, stop=False)
                for k in range(KD):
                    last = nc.tensor.matmul(bank[2][:, m * TOK:(m + 1) * TOK], wa[:, k, m * P:(m + 1) * P], cin[:, k, :],
                                            start=False, stop=k == KD - 1)
            last.then_inc(*done("drive"))

        def drive_part(t, bk):
            nc.tensor.matmul(bk[:, 0:KD * B], ident[:], drive[:, :, t, :], start=True, stop=False, skip_group_check=True)

        def state_part(bk, signal):
            for m in range(KD):
                for k in range(KD):
                    last = nc.tensor.matmul(bk[:, m * B:(m + 1) * B], wa[:, k, m * P:(m + 1) * P], z[:, k, :],
                                            start=False, stop=m == KD - 1 and k == KD - 1, skip_group_check=True)
            last.then_inc(*signal)

        pe.wait_ge(act_s.sem, act_s.all("rec_in"))
        drive_part(0, bank[0])
        pe.wait_ge(dve_s.sem, dve_s.at("rec_0", 0, "z0"))
        state_part(bank[0], signals(pe_s, "rec_0")("t0"))
        done = signals(pe_s, "rec_loop")
        with pe.Fori(0, (S - 2) // 2) as i:
            PE, ACTS, DVE, POOL = after("rec_loop", i)
            for u in range(2):
                drive_part(bass.ds(2 * i + 1 + u, 1), bank[(1 + u) % 2])
                pe.wait_ge(*DVE(f"z{u}"))
                state_part(bank[(1 + u) % 2], done(f"t{u}"))
        drive_part(S - 1, bank[1])
        pe.wait_ge(dve_s.sem, dve_s.at("rec_9", 0, "z0"))
        state_part(bank[1], signals(pe_s, "rec_9")("t0"))

        done = signals(pe_s, "rec")
        with pe.Fori(0, NCH) as i:
            PE, ACTS, DVE, POOL = after("rec", i)
            pe.wait_ge(*ACTS("sT"))
            pe.wait_ge(*DVE("res", back=1))
            for b in range(BC):
                for k in range(KD):
                    last = nc.tensor.matmul(bank[3][:, b * D:(b + 1) * D], sT[:, k, b * P:(b + 1) * P], wo1[:, k, :],
                                            start=k == 0, stop=k == KD - 1)
            last.then_inc(*done("out"))

    def rec_act():
        act, st = nc.scalar, "rec_in"
        others_done(act, "spike")
        act.wait_ge(w_loaded["rec"], 16)
        done = signals(act_s, st)
        with act.Fori(0, NCH) as i:
            PE, ACTS, DVE, POOL = after(st, i)
            prep(st, i)
            act.wait_ge(*PE("inp"))
            for m in range(KD):
                last = nc.scalar.activation(inp[:, m, :], bank[0][:, m * TOK:(m + 1) * TOK], ACT.Identity, bias=RW("bi")[:, m:m + 1])
            last.then_inc(*done("inp"))
            act.wait_ge(*PE("gate"))
            act.sem_inc(held, 1)
            for m in range(KD):
                last = nc.scalar.activation(gate[:, m, :, bass.ds(i * BC, BC)].rearrange("p t b -> p b t"),
                                            bank[1][:, m * TOK:(m + 1) * TOK].rearrange("p (b t) -> p b t", b=BC), ACT.Sigmoid,
                                            bias=RW("bg")[:, m:m + 1])
            last.then_inc(*done("gate"))
            act.wait_ge(*PE("drive"))
            act.sem_inc(held, 1)
            for m in range(KD):
                last = nc.scalar.activation(drive[:, m, :, bass.ds(i * BC, BC)].rearrange("p t b -> p b t"),
                                            bank[2][:, m * TOK:(m + 1) * TOK].rearrange("p (b t) -> p b t", b=BC), ACT.Identity)
            last.then_inc(*done("drive"))

        def step(t, bk, signal):
            act.sem_inc(held, 1)
            nc.scalar.activation(state[:, :, t, :], bk[:, 0:KD * B].rearrange("p (k b) -> p k b", k=KD), ACT.Tanh).then_inc(*signal)

        act.wait_ge(pe_s.sem, pe_s.at("rec_0", 0, "t0"))
        step(0, bank[0], signals(act_s, "rec_0")("t0"))
        done = signals(act_s, "rec_loop")
        with act.Fori(0, (S - 2) // 2) as i:
            PE, ACTS, DVE, POOL = after("rec_loop", i)
            for u in range(2):
                act.wait_ge(*PE(f"t{u}"))
                step(bass.ds(2 * i + 1 + u, 1), bank[(1 + u) % 2], done(f"t{u}"))
        act.wait_ge(pe_s.sem, pe_s.at("rec_9", 0, "t0"))
        step(S - 1, bank[1], signals(act_s, "rec_9")("t0"))

        done = signals(act_s, "rec")
        act.wait_ge(act_s.sem, act_s.all("rec_9"))
        with act.Fori(0, NCH) as i:
            PE, ACTS, DVE, POOL = after("rec", i)
            act.wait_ge(*PE("out", back=1))
            act.sem_inc(held, 1)
            for k in range(KD):
                last = nc.scalar.activation(sT[:, k, :].rearrange("p (b t) -> p b t", b=BC),
                                            state[:, k, :, bass.ds(i * BC, BC)].rearrange("p t b -> p b t"), ACT.Identity)
            last.then_inc(*done("sT"))

    def rec_dve():
        dve, st = nc.vector, "rec_in"
        others_done(dve, "spike")
        dve.wait_ge(w_loaded["rec"], 16)
        done = signals(dve_s, st)
        with dve.Fori(0, NCH) as i:
            PE, ACTS, DVE, POOL = after(st, i)
            dve.wait_ge(ctxT2_loaded, i * 16 + 16)
            nc.vector.tensor_tensor(c2[:], ctxT[:], ctxT[:], ALU.mult).then_inc(*done("c2"))
            dve.wait_ge(*DVE("c2"))
            for k in range(KD):
                for b in range(BC):
                    nc.vector.tensor_tensor_scan(rT1[:, k, b * P:(b + 1) * P], RW("decay")[:, k:k + 1].to_broadcast([P, P]),
                                                 c2[:, k, b * P:(b + 1) * P], 0.0, ALU.mult, ALU.add).then_inc(*done(f"r{k}{b}"))
            dve.wait_ge(*PE("xT"))
            nc.vector.tensor_copy(xnT[:].rearrange("p k t -> p (k t)"), bank[7][:]).then_inc(*done("xT"))
            dve.wait_ge(*DVE("xT"))
            nc.vector.tensor_tensor(ret[:], xnT[:], rT1[:], ALU.mult).then_inc(*done("ret"))
            dve.wait_ge(*ACTS("gate"))
            nc.vector.tensor_tensor(gc[:].rearrange("p k (b t) -> p k b t", b=BC),
                                    gate[:, :, :, bass.ds(i * BC, BC)].rearrange("p k t b -> p k b t"),
                                    inp[:].rearrange("p k (b t) -> p k b t", b=BC), ALU.mult).then_inc(*done("gc"))
            dve.wait_ge(*DVE("gc"))
            nc.vector.tensor_tensor(cin[:], inp[:], gc[:], ALU.subtract).then_inc(*done("cin"))

        nc.vector.memset(z[:], 0.0).then_inc(*signals(dve_s, "rec_0")("z0"))

        def gated(t_gate, t_state, signal):
            nc.vector.tensor_tensor(z[:], gate[:, :, t_gate, :], state[:, :, t_state, :], ALU.mult).then_inc(*signal)

        done = signals(dve_s, "rec_loop")
        with dve.Fori(0, (S - 2) // 2) as i:
            PE, ACTS, DVE, POOL = after("rec_loop", i)
            dve.wait_ge(act_s.sem, act_s.at("rec_loop", i, "t1", back=1))
            gated(bass.ds(2 * i + 1, 1), bass.ds(2 * i, 1), done("z0"))
            dve.wait_ge(*ACTS("t0"))
            gated(bass.ds(2 * i + 2, 1), bass.ds(2 * i + 1, 1), done("z1"))
        dve.wait_ge(act_s.sem, act_s.all("rec_loop"))
        gated(S - 1, S - 2, signals(dve_s, "rec_9")("z0"))
        done = signals(dve_s, "rec")
        with dve.Fori(0, NCH) as i:
            PE, ACTS, DVE, POOL = after("rec", i)
            dve.wait_ge(*PE("out"))
            dve.wait_ge(*POOL("bo"))
            nc.vector.tensor_tensor(x[:, bass.ds(i * BC, BC), :], bank[3][:].rearrange("p (b d) -> p b d", b=BC),
                                    x[:, bass.ds(i * BC, BC), :], ALU.add).then_inc(*done("res"))
            dve.wait_ge(*DVE("res"))
            stats("rec", i)

    def rec_pool():
        pool = nc.gpsimd
        others_done(pool, "spike")
        pool.wait_ge(w_loaded["rec"], 16)
        pool.wait_ge(act_s.sem, act_s.all("rec_in"))
        done = signals(pool_s, "rec")
        with pool.Fori(0, NCH) as i:
            nc.gpsimd.tensor_tensor(x[:, bass.ds(i * BC, BC), :], x[:, bass.ds(i * BC, BC), :], over(RW("bo"), BC),
                                    ALU.add).then_inc(*done("bo"))
            stats_root("rec", i)

    MW = weights["moe"]
    router = MW("router").rearrange("p (k e) -> p k e", k=KD)
    sgu = MW("sgu").rearrange("p (k f) -> p k f", k=KD)
    sdown = MW("sdown").rearrange("p (k d) -> p k d", k=2)
    RING = 8
    GU = KD * 2 * FE
    ring = area("ring", [P, RING, GU + 2 * D], 0)
    M0 = RING * (GU + 2 * D)
    lg1 = area("lg1", [P, BC, NE], M0)
    mr1 = area("mr1", [P, BC, NE], M0 + 128)
    pick = area("pick", [P, BC, NE], M0 + 256)
    gates1 = area("gates1", [P, BC, NE], M0 + 384)
    far = area("far", [P, BC, NE], M0 + 512)
    fits = area("fits", [P, BC, NE], M0 + 640)
    key = area("key", [P, BC, NE], M0 + 768)
    same = area("same", [P, TOPK, NE], M0 + 896)
    pickb = area("pickb", [P, BC, NE], M0 + 1408, BF16)
    seen = area("seen", [P, NE], M0 + 1472, BF16)
    mx1 = area("mx1", [P, BC, TOPK], M0 + 1504)
    nmx1 = area("nmx1", [P, BC], M0 + 1520)
    den1 = area("den1", [P, 2, BC], M0 + 1522)
    mk = area("mk", [P, BC, TOPK], M0 + 1526)
    back = area("back", [P, BC, TOPK], M0 + 1542)
    slot = area("slot", [P, BC, TOPK], M0 + 1558).bitcast(I32)
    rows_w = area("rows_w", [P, BC, TOPK, 2], M0 + 1574)
    tri_b = area("tri_b", [P, P], M0 + 1606, BF16)
    ones_b = area("ones_b", [P, P], M0 + 1670, BF16)
    sg = area("sg", [P, BC, FE], M0 + 1734)
    hs = area("hs", [P, BC, FE], M0 + 2118)
    hsT = area("hsT", [P, 2, TOK], M0 + 2502)
    xg = area("xg", [P, 2, D], M0 + 3014)
    xgT = area("xgT", [P, 2, D], M0 + 3526)
    y = area("y", [P, 2, D], M0 + 4038)
    slot_tok = area("slot_tok", [P, NE, 2], M0 + 4550)
    assert M0 + 4678 <= SPACE
    acc_in = xg
    gidx = sb("gather_rows", [P, 2], I32)
    sidx = sb("scatter_rows", [P, 2], I32)
    idx_all = sb("idx_all", [P, NE + 2], I32)
    NSLOT = NE * CAP
    table = nc.dram_tensor("slot_table", (NSLOT + B * S * TOPK, 2), F32, kind="Internal").ap()
    xn_rows = nc.dram_tensor("normalised_rows", (B * S + P, D), F32, kind="Internal").ap()
    acc = nc.dram_tensor("routed_sum", (B * S + P, D), F32, kind="Internal").ap()
    table_set, rows_set, acc_set = sem("table_initialised"), sem("spare_row_zeroed"), sem("routed_sum_zeroed")
    rows_stored, scattered, table_read = sem("rows_stored"), sem("slots_scattered"), sem("table_read")
    gu_in = [sem(f"expert_weights_loaded_{q}") for q in range(RING // 2)]
    gathered = [sem(f"rows_gathered_{u}") for u in range(2)]
    added, acc_read = [sem(f"routed_rows_added_{u}") for u in range(2)], sem("routed_sum_read")
    slots_free, y_free = sem("chunk_scattered"), [sem(f"expert_rows_added_{u}") for u in range(2)]
    moe_ready = sem("moe_constants_ready")
    stage("moe_in", NCH, pe=["xT", "lg", "sgu0", "sgu1", "pos", "hsT", "sout"],
          act=["prep0", "prep1", "ex", "sg0", "sg1"],
          dve=["xT", "lg", "mx0", "mx1", "nmx", "mr0", "mr1", "pick", "pickb", "hs0", "hs1", "em", "sum", "rec", "gates",
               "far", "fits", "seen", "seen2", "key", "mk0", "mk1", "back", "slot0", "slot", "tok", "hsT", "hsT1"]
          + [f"{a}{b}" for b in range(BC) for a in ("eq", "ew", "wk")] + ["sres"], pool=[])
    QS = range(RING // 2)
    stage("moe_ex", NE // RING, pe=[f"{a}{q}{u}" for q in QS for a in "xghd" for u in range(2)],
          act=[f"{a}{q}{u}" for q in QS for a in "xsy" for u in range(2)],
          dve=[f"{a}{q}{u}" for q in QS for a in "ht" for u in range(2)], pool=[])

    def pair_before(q):
        return (q - 1) % (RING // 2), int(q == 0)
    stage("moe", NCH, pe=[], act=[], dve=["res"] + LN_DVE, pool=["rstd"])
    hT = hsT

    def moe_sp():
        sp = nc.sync
        sp.dma_start(table, ins["table0"]).then_inc(table_set, 16)
        others_done(sp, "rec")
        load_weights(sp, "bit")
        with sp.Fori(0, NCH) as i:
            sp.wait_ge(act_s.sem, act_s.at("moe_in", i, "prep1"))
            sp.dma_start(xn_rows[bass.ds(i * TOK, TOK), :].rearrange("(b p) d -> p b d", p=P), xn[:]).then_inc(rows_stored, 16)
        sp.wait_ge(slots_free, NCH + 1)
        sp.dma_start(slot_tok[:], table[0:NSLOT, :].rearrange("(e p) c -> p e c", p=P)).then_inc(table_read, 16)
        sp.wait_ge(moe_ready, 1)
        with sp.Fori(0, NE // RING) as o:
            for q in QS:
                sp.wait_ge(pe_s.sem, pe_s.at("moe_ex", o, f"d{q}1", back=1))
                e = o * RING + 2 * q
                sp.dma_start(ring[:, 2 * q:2 * q + 2, 0:GU], ins["w_gate_up"][bass.ds(e, 2)].rearrange("e p c -> p e c")).then_inc(gu_in[q], 16)
                sp.dma_start(ring[:, 2 * q:2 * q + 2, GU:GU + D], ins["w_down"][bass.ds(e, 2), 0:P].rearrange("e p c -> p e c")).then_inc(gu_in[q], 16)
                sp.dma_start(ring[0:FE - P, 2 * q:2 * q + 2, GU + D:], ins["w_down"][bass.ds(e, 2), P:FE].rearrange("e p c -> p e c")).then_inc(gu_in[q], 16)
        others_done(sp, "moe_ex")
        for u in range(2):
            sp.wait_ge(y_free[u], NE // 2 + 1)
            sp.wait_ge(gathered[u], 8 * NE + 16)
        with sp.Fori(0, NCH) as i:
            sp.wait_ge(dve_s.sem, dve_s.at("moe", i, "res", back=1))
            sp.dma_start(acc_in[:], acc[bass.ds(i * TOK, TOK), :].rearrange("(b p) d -> p b d", p=P)).then_inc(acc_read, 16)

    def moe_pe():
        pe, st = nc.tensor, "moe_in"
        others_done(pe, "rec")
        pe.wait_ge(w_loaded["moe"], 16)
        pe.wait_ge(moe_ready, 2)
        done = signals(pe_s, st)
        with pe.Fori(0, NCH) as i:
            PE, ACTS, DVE, POOL = after(st, i)
            turn_x(st, i)
            pe.wait_ge(*DVE("xT"))
            for b in range(BC):
                for k in range(KD):
                    last = nc.tensor.matmul(bank[0][:, b * NE:(b + 1) * NE], xnT[:, k, b * P:(b + 1) * P], router[:, k, :],
                                            start=k == 0, stop=k == KD - 1)
            last.then_inc(*done("lg"))
            for b in range(BC):
                for k in range(KD):
                    last = nc.tensor.matmul(bank[1 + b][:, 0:2 * FE], xnT[:, k, b * P:(b + 1) * P], sgu[:, k, :],
                                            start=k == 0, stop=k == KD - 1)
                last.then_inc(*done(f"sgu{b}"))
            pe.wait_ge(*DVE("pickb"))
            for b in range(BC):
                parts = [(tri_b, pickb[:, b, :]), (ones_b, seen[:])] + [(ones_b, pickb[:, 0, :])] * b
                for n, (w, m) in enumerate(parts):
                    last = nc.tensor.matmul(bank[3][:, b * NE:(b + 1) * NE], w[:], m, start=n == 0, stop=n == len(parts) - 1)
            last.then_inc(*done("pos"))
            pe.wait_ge(*DVE("hs1"))
            for b in range(BC):
                nc.tensor.transpose(bank[4][:, b * P:(b + 1) * P], hs[:, b, 0:P], ident[:])
            for b in range(BC):
                last = nc.tensor.transpose(bank[5][0:FE - P, b * P:(b + 1) * P], hs[:, b, P:FE], ident[:])
            last.then_inc(*done("hsT"))
            pe.wait_ge(*DVE("hsT1"))
            pe.wait_ge(*DVE("sres", back=1))
            for b in range(BC):
                for k in range(2):
                    last = nc.tensor.matmul(bank[6][:, b * D:(b + 1) * D], hsT[:, k, b * P:(b + 1) * P], sdown[:, k, :],
                                            start=k == 0, stop=k == 1)
            last.then_inc(*done("sout"))

        done = signals(pe_s, "moe_ex")
        others_done(pe, "moe_in")
        with pe.Fori(0, NE // RING) as o:
            PE, ACTS, DVE, POOL = after("moe_ex", o)
            for q in QS:
                for u in range(2):
                    pe.wait_ge(gathered[u], o * (8 * RING) + 16 * (q + 1))
                    for k in range(KD):
                        last = nc.tensor.transpose(bank[u][:, k * P:(k + 1) * P], xg[:, u, k * P:(k + 1) * P], ident[:])
                    last.then_inc(*done(f"x{q}{u}"))
                pe.wait_ge(gu_in[q], o * 48 + 48)
                for u in range(2):
                    pe.wait_ge(*ACTS(f"x{q}{u}"))
                    for k in range(KD):
                        last = nc.tensor.matmul(bank[2 + u][:, 0:2 * FE], xgT[:, u, k * P:(k + 1) * P],
                                                ring[:, 2 * q + u, k * 2 * FE:(k + 1) * 2 * FE], start=k == 0, stop=k == KD - 1)
                    last.then_inc(*done(f"g{q}{u}"))
                for u in range(2):
                    pe.wait_ge(*DVE(f"h{q}{u}"))
                    pe.sem_inc(held, 1)
                    nc.tensor.transpose(bank[4 + u][:, 0:P], hs[:, u, 0:P], ident[:])
                    nc.tensor.transpose(bank[4 + u][0:FE - P, P:2 * P], hs[:, u, P:FE], ident[:]).then_inc(*done(f"h{q}{u}"))
                before, back = pair_before(q)
                for u in range(2):
                    pe.wait_ge(*DVE(f"t{q}{u}"))
                    pe.wait_ge(*ACTS(f"y{before}{u}", back=back))
                    for k in range(2):
                        last = nc.tensor.matmul(bank[6 + u][:, 0:D], hT[:, k, u * P:(u + 1) * P],
                                                ring[:, 2 * q + u, GU + k * D:GU + (k + 1) * D], start=k == 0, stop=k == 1)
                    last.then_inc(*done(f"d{q}{u}"))

    def moe_act():
        act, st = nc.scalar, "moe_in"
        others_done(act, "rec")
        done = signals(act_s, st)
        with act.Fori(0, NCH) as i:
            PE, ACTS, DVE, POOL = after(st, i)
            act.wait_ge(rows_stored, i * 16 + 16)
            act.sem_inc(held, 1)
            prep(st, i)
            act.wait_ge(*DVE("nmx"))
            for b in range(BC):
                last = nc.scalar.activation(gates1[:, b, :], lg1[:, b, :], ACT.Exp, bias=nmx1[:, b:b + 1])
            last.then_inc(*done("ex"))
            for b in range(BC):
                act.wait_ge(*PE(f"sgu{b}"))
                nc.scalar.activation(sg[:, b, :], bank[1 + b][:, 0:FE], ACT.Silu).then_inc(*done(f"sg{b}"))
        done = signals(act_s, "moe_ex")
        others_done(act, "moe_in")
        act.wait_ge(table_read, 16)
        with act.Fori(0, NE // RING) as o:
            PE, ACTS, DVE, POOL = after("moe_ex", o)
            for q in QS:
                for u in range(2):
                    act.wait_ge(*PE(f"x{q}{u}"))
                    nc.scalar.activation(xgT[:, u, :], bank[u][:, 0:D], ACT.Identity).then_inc(*done(f"x{q}{u}"))
                for u in range(2):
                    act.wait_ge(*PE(f"g{q}{u}"))
                    nc.scalar.activation(sg[:, u, :], bank[2 + u][:, 0:FE], ACT.Silu).then_inc(*done(f"s{q}{u}"))
                for u in range(2):
                    act.wait_ge(*PE(f"d{q}{u}"))
                    act.wait_ge(y_free[u], o * (RING // 2) + q + 1)
                    act.sem_inc(held, 1)
                    nc.scalar.activation(y[:, u, :], bank[6 + u][:, 0:D], ACT.Identity,
                                         scale=slot_tok[:, bass.ds(o * RING + 2 * q + u, 1), 1]).then_inc(*done(f"y{q}{u}"))

    def moe_pool():
        pool = nc.gpsimd
        pool.sem_inc(rows_stored, 16)
        pool.sem_inc(slots_free, 1)
        for u in range(2):
            pool.sem_inc(y_free[u], 1)
        nc.gpsimd.memset(zrow[:], 0.0).then_inc(zeroed, 1)
        pool.wait_ge(zeroed, 1)
        pool.dma_start(xn_rows[B * S:B * S + P, :], zrow[:]).then_inc(rows_set, 16)
        for n in range(B + 1):
            pool.dma_start(acc[n * P:(n + 1) * P, :], zrow[:]).then_inc(acc_set, 16)
        pool.wait_ge(table_set, 16)
        with pool.Fori(0, NCH) as i:
            pool.wait_ge(dve_s.sem, dve_s.at("moe_in", i, "wk1"))
            pool.sem_inc(held, 1)
            for b in range(BC):
                for k in range(TOPK):
                    pool.indirect_dma_start(table[:, :], bass.IndirectOffsetOnAxis(ap=slot[:, b, k:k + 1], axis=0),
                                            rows_w[:, b, k, :], None).then_inc(scattered, 16)
            pool.wait_ge(scattered, i * (16 * BC * TOPK) + 16 * BC * TOPK)
            pool.sem_inc(slots_free, 1)
        others_done(pool, "moe_in")
        pool.wait_ge(table_read, 16)
        pool.wait_ge(rows_stored, 16 * NCH + 16)
        pool.wait_ge(rows_set, 16)
        pool.wait_ge(acc_set, 16 * (B + 1))
        pool.wait_ge(moe_ready, 3)

        def gather(pair):
            pool.sem_inc(held, 1)
            for u in range(2):
                nc.gpsimd.tensor_copy(gidx[:, u:u + 1], idx_all[:, bass.ds(2 * pair + u, 1)]).then_inc(gidx_set, 1)
            pool.wait_ge(gidx_set, 2 * pair + 2)
            pool.sem_inc(held, 1)
            for u in range(2):
                pool.indirect_dma_start(xg[:, u, :], None, xn_rows[:, :],
                                        bass.IndirectOffsetOnAxis(ap=gidx[:, u:u + 1], axis=0)).then_inc(gathered[u], 16)

        gather(0)
        with pool.Fori(0, NE // RING) as o:
            for q in QS:
                pair = o * (RING // 2) + q
                pool.wait_ge(pe_s.sem, pe_s.at("moe_ex", o, f"x{q}1"))
                for u in range(2):
                    pool.wait_ge(gathered[u], 16 * pair + 16)
                gather(pair + 1)
                for u in range(2):
                    if u == 0:
                        pool.sem_inc(held, 1)
                        for n in range(2):
                            nc.gpsimd.tensor_copy(sidx[:, n:n + 1], idx_all[:, bass.ds(2 * pair + n, 1)]).then_inc(sidx_set, 1)
                        pool.wait_ge(sidx_set, 2 * pair + 2)
                    pool.wait_ge(act_s.sem, act_s.at("moe_ex", o, f"y{q}{u}"))
                    pool.sem_inc(held, 1)
                    pool.indirect_dma_start(acc[:, :], bass.IndirectOffsetOnAxis(ap=sidx[:, u:u + 1], axis=0), y[:, u, :], None,
                                            compute_op=ALU.add).then_inc(added[u], 16)
                    pool.wait_ge(added[u], 16 * pair + 16)
                    pool.sem_inc(y_free[u], 1)
        with pool.Fori(0, NCH) as i:
            stats_root("moe", i)

    def moe_dve():
        dve, st = nc.vector, "moe_in"
        others_done(dve, "rec")
        dve.wait_ge(consts_loaded, 16)
        nc.vector.memset(seen[:], 0.0)
        nc.vector.memset(ring[64:P, :, GU + D:], 0.0)
        nc.vector.memset(hsT[64:P, 1, :], 0.0).then_inc(moe_ready, 1)
        nc.vector.memset(ones_b[:], 1.0)
        nc.vector.tensor_copy(tri_b[:], C("tri")).then_inc(moe_ready, 1)
        done = signals(dve_s, st)
        with dve.Fori(0, NCH) as i:
            PE, ACTS, DVE, POOL = after(st, i)
            dve.wait_ge(*PE("xT"))
            nc.vector.tensor_copy(xnT[:].rearrange("p k t -> p (k t)"), bank[7][:]).then_inc(*done("xT"))
            dve.wait_ge(*PE("lg"))
            nc.vector.tensor_copy(lg1[:].rearrange("p b e -> p (b e)"), bank[0][:, 0:BC * NE]).then_inc(*done("lg"))
            dve.wait_ge(*DVE("lg"))
            dve.sem_inc(held, 1)
            for b in range(BC):
                nc.vector.max(mx1[:, b, :], lg1[:, b, :]).then_inc(*done(f"mx{b}"))
            dve.wait_ge(*DVE("mx1"))
            nc.vector.tensor_scalar(nmx1[:], mx1[:, :, 0], -1.0, None, ALU.mult).then_inc(*done("nmx"))
            for b in range(BC):
                nc.vector.match_replace(mr1[:, b, :], mx1[:, b, :], lg1[:, b, :], -3.0e38).then_inc(*done(f"mr{b}"))
            dve.wait_ge(*DVE("mr1"))
            nc.vector.tensor_tensor(pick[:], mr1[:], lg1[:], ALU.not_equal).then_inc(*done("pick"))
            dve.wait_ge(*DVE("pick"))
            nc.vector.tensor_copy(pickb[:], pick[:]).then_inc(*done("pickb"))
            for b in range(BC):
                dve.wait_ge(*ACTS(f"sg{b}"))
                nc.vector.tensor_tensor(hs[:, b, :], sg[:, b, :], bank[1 + b][:, FE:2 * FE], ALU.mult).then_inc(*done(f"hs{b}"))
            dve.wait_ge(*ACTS("ex"))
            nc.vector.tensor_tensor(gates1[:], gates1[:], pick[:], ALU.mult).then_inc(*done("em"))
            dve.wait_ge(*DVE("em"))
            nc.vector.tensor_reduce(den1[:, 0, :], gates1[:], AX.X, ALU.add).then_inc(*done("sum"))
            dve.wait_ge(*DVE("sum"))
            nc.vector.reciprocal(den1[:, 1, :], den1[:, 0, :]).then_inc(*done("rec"))
            dve.wait_ge(*DVE("rec"))
            nc.vector.tensor_tensor(gates1[:], gates1[:], wide(den1[:, 1, :], NE), ALU.mult).then_inc(*done("gates"))
            dve.wait_ge(*PE("pos"))
            pos = bank[3][:, 0:BC * NE].rearrange("p (b e) -> p b e", b=BC)
            nc.vector.tensor_tensor(far[:], over(C("slot_base"), BC), pos, ALU.subtract).then_inc(*done("far"))
            nc.vector.scalar_tensor_tensor(fits[:], pos, float(CAP), pick[:], ALU.is_lt, ALU.mult).then_inc(*done("fits"))
            nc.vector.tensor_tensor(seen[:], seen[:], pickb[:, 0, :], ALU.add).then_inc(*done("seen"))
            dve.wait_ge(*DVE("seen"))
            nc.vector.tensor_tensor(seen[:], seen[:], pickb[:, 1, :], ALU.add).then_inc(*done("seen2"))
            nc.vector.tensor_tensor(key[:], far[:], fits[:], ALU.mult).then_inc(*done("key"))
            dve.wait_ge(*DVE("key"))
            dve.sem_inc(held, 1)
            for b in range(BC):
                nc.vector.max(mk[:, b, :], key[:, b, :]).then_inc(*done(f"mk{b}"))
            dve.wait_ge(*DVE("mk1"))
            nc.vector.scalar_tensor_tensor(back[:].rearrange("p b k -> p (b k)"), mk[:].rearrange("p b k -> p (b k)"), 0.0,
                                           C("spare")[:, bass.ds(i * BC * TOPK, BC * TOPK)], ALU.is_equal, ALU.mult).then_inc(*done("back"))
            dve.wait_ge(*DVE("back"))
            nc.vector.tensor_tensor(back[:], back[:], mk[:], ALU.subtract).then_inc(*done("slot0"))
            dve.wait_ge(*DVE("slot0"))
            dve.wait_ge(slots_free, i + 1)
            nc.vector.tensor_scalar(slot[:], back[:], float(NSLOT), None, ALU.add).then_inc(*done("slot"))
            nc.vector.tensor_copy(rows_w[:, :, :, 0], wide(C("tokens")[:, bass.ds(i * BC, BC)], TOPK)).then_inc(*done("tok"))
            dve.wait_ge(*PE("hsT"))
            nc.vector.tensor_copy(hsT[:, 0, :], bank[4][:, 0:TOK]).then_inc(*done("hsT"))
            nc.vector.tensor_copy(hsT[0:FE - P, 1, :], bank[5][0:FE - P, 0:TOK]).then_inc(*done("hsT1"))
            for b in range(BC):
                if b:
                    dve.wait_ge(*DVE("wk0"))
                nc.vector.tensor_tensor(same[:], over(key[:, b, :], TOPK), wide(mk[:, b, :], NE), ALU.is_equal).then_inc(*done(f"eq{b}"))
                dve.wait_ge(*DVE(f"eq{b}"))
                nc.vector.tensor_tensor(same[:], same[:], over(gates1[:, b, :], TOPK), ALU.mult).then_inc(*done(f"ew{b}"))
                dve.wait_ge(*DVE(f"ew{b}"))
                nc.vector.tensor_reduce(rows_w[:, b, :, 1], same[:], AX.X, ALU.add).then_inc(*done(f"wk{b}"))
            dve.wait_ge(*PE("sout"))
            nc.vector.tensor_tensor(x[:, bass.ds(i * BC, BC), :], bank[6][:].rearrange("p (b d) -> p b d", b=BC),
                                    x[:, bass.ds(i * BC, BC), :], ALU.add).then_inc(*done("sres"))
        dve.wait_ge(table_read, 16)
        nc.vector.tensor_copy(idx_all[:, NE:], C("tokens")[:, 0:2])
        nc.vector.tensor_copy(idx_all[:, 0:NE], slot_tok[:, :, 0]).then_inc(moe_ready, 1)
        done = signals(dve_s, "moe_ex")
        others_done(dve, "moe_in")
        with dve.Fori(0, NE // RING) as o:
            PE, ACTS, DVE, POOL = after("moe_ex", o)
            for q in QS:
                for u in range(2):
                    dve.wait_ge(*ACTS(f"s{q}{u}"))
                    nc.vector.tensor_tensor(hs[:, u, :], sg[:, u, :], bank[2 + u][:, FE:2 * FE], ALU.mult).then_inc(*done(f"h{q}{u}"))
                for u in range(2):
                    dve.wait_ge(*PE(f"h{q}{u}"))
                    nc.vector.tensor_copy(hT[:, 0, u * P:(u + 1) * P], bank[4 + u][:, 0:P])
                    nc.vector.tensor_copy(hT[0:FE - P, 1, u * P:(u + 1) * P], bank[4 + u][0:FE - P, P:2 * P]).then_inc(*done(f"t{q}{u}"))
        done = signals(dve_s, "moe")
        with dve.Fori(0, NCH) as i:
            PE, ACTS, DVE, POOL = after("moe", i)
            dve.wait_ge(acc_read, i * 16 + 16)
            nc.vector.tensor_tensor(x[:, bass.ds(i * BC, BC), :], acc_in[:], x[:, bass.ds(i * BC, BC), :], ALU.add).then_inc(*done("res"))
            dve.wait_ge(*DVE("res"))
            stats("moe", i)

    LW = weights["mlstm"]
    gq = LW("gq").rearrange("p (k g) -> p k g", k=KD)
    BH = BC * HL
    gkv = area("gkv", [P, KD, 2 * HL], 0)
    lnw1 = area("lnw1", [P, D], 16)
    vext = area("vext", [P, BC, HL, DL + 1], 272)
    late_b = area("late_b", [P, HL * P], 800, BF16)
    ident_b = area("ident_b", [P, P], 1056, BF16)
    triI = area("triI", [P, P], 1120)
    gt = area("gt", [P, BC, 2 * HL], 1248)
    mnf, nab, yv, lnu, uu, e1, ru, cr, lf, cs, av, cm, ne, ab, nr, hsum, hsq, hvar, hrs = (
        area(f"s{n}", [P, BC, HL], 1264 + 8 * n) for n in range(19))
    aT = area("aT", [BH, P], 1424)
    cmax = area("cmax", [BH, P], 1552)
    cdiag = area("cdiag", [BH, BH, P], 1680)
    decayT = area("decayT", [P, 2, BC * HL // 2, P], 2704)
    cT = area("cT", [P, 2, BC * HL // 2, P], 3728)
    hst = area("hst", [P, BC, D], 4752)
    hce = area("hce", [P, BC, D], 5264)
    hq = area("hq", [P, BC, D], 5776)
    mhalf8 = area("mhalf8", [P, BH], 6288)
    mlstm_ready = sem("mlstm_constants_ready")
    stage("mlstm", NCH, pe=["xT", "gates", "cs", "aT", "qk", "cb0", "cb1", "cm", "ho0", "ho1"],
          act=["prep0", "prep1", "ey", "ln", "D", "ne"],
          dve=["xT", "gt", "mnf", "nab", "u", "e1", "ru", "cr", "t", "lf", "cs", "a", "aT", "cmax", "cdiag", "cm",
               "cT0", "cT1", "ab0", "ab1", "abs", "nr", "nre", "rn", "h0", "h1", "hsum", "hce", "hq", "hsq", "hvar", "hn", "res"] + LN_DVE,
          pool=["hrs", "w", "rstd"])

    def mlstm_sp():
        sp = nc.sync
        others_done(sp, "moe")
        sp.wait_ge(mlstm_ready, 1)
        with sp.Fori(0, NCH) as i:
            sp.wait_ge(pe_s.sem, pe_s.at("mlstm", i, "qk", back=1))
            sp.dma_start(ctxT[:], ctxT_dram[:, :, bass.ds(i * TOK, TOK)]).then_inc(ctxT3_loaded, 16)
            sp.wait_ge(pe_s.sem, pe_s.at("mlstm", i, "ho1", back=1))
            for b in range(BC):
                sp.dma_start(vext[:, b, :, 0:DL], ctx_dram[:, bass.ds(i * BC + b, 1), :].rearrange("s b (h d) -> s (b h) d", h=HL)).then_inc(
                    ctx_loaded, 16)

    def mlstm_pe():
        pe, st = nc.tensor, "mlstm"
        others_done(pe, "moe")
        pe.wait_ge(w_loaded["mlstm"], 16)
        pe.wait_ge(mlstm_ready, 2)
        done = signals(pe_s, st)
        with pe.Fori(0, NCH) as i:
            PE, ACTS, DVE, POOL = after(st, i)
            turn_x(st, i)
            pe.wait_ge(ctxT3_loaded, i * 16 + 16)
            pe.wait_ge(*DVE("xT"))
            for b in range(BC):
                for n, (src, w) in enumerate(((xnT, gq), (ctxT, gkv))):
                    for k in range(KD):
                        last = nc.tensor.matmul(bank[0][:, b * 2 * HL:(b + 1) * 2 * HL], src[:, k, b * P:(b + 1) * P], w[:, k, :],
                                                start=n == 0 and k == 0, stop=n == 1 and k == KD - 1)
            last.then_inc(*done("gates"))
            pe.wait_ge(*DVE("lf"))
            nc.tensor.matmul(bank[1][:, 0:BH], triI[:], lf[:].rearrange("p b h -> p (b h)"), start=True, stop=True).then_inc(*done("cs"))
            pe.wait_ge(*DVE("a"))
            pe.sem_inc(held, 1)
            nc.tensor.transpose(bank[2][0:BH, 0:P], av[:].rearrange("p b h -> p (b h)"), ident[:]).then_inc(*done("aT"))
            for b in range(BC):
                for h in range(HL):
                    rows = slice(DL * (h % 2), DL * (h % 2) + DL)
                    c = b * HL // 2 + h // 2
                    last = nc.tensor.matmul(bank[5 + h % 2][:, c * P:(c + 1) * P], ctxT[rows, h // 2, b * P:(b + 1) * P],
                                            xnT[rows, h // 2, b * P:(b + 1) * P], start=True, stop=True)
            last.then_inc(*done("qk"))
            pe.wait_ge(*DVE("cdiag"))
            for b in range(BC):
                nc.tensor.matmul(bank[3 + b][:], ones[0:BH, :], cdiag[:, b * HL:(b + 1) * HL, :].rearrange("r h s -> r (h s)"),
                                 start=True, stop=False)
                nc.tensor.matmul(bank[3 + b][:], ident_b[:], late_b[:], start=False, stop=True).then_inc(*done(f"cb{b}"))
            nc.tensor.transpose(bank[2][:, 0:BH], cmax[:], ident[0:BH, 0:BH]).then_inc(*done("cm"))
            pe.wait_ge(ctx_loaded, i * 32 + 32)
            for b in range(BC):
                pe.wait_ge(*DVE(f"cT1"))
                for h in range(HL):
                    last = nc.tensor.matmul(bank[b][:, h * (DL + 1):(h + 1) * (DL + 1)], cT[:, h % 2, b * HL // 2 + h // 2, :],
                                            vext[:, b, h, :], start=True, stop=True)
                last.then_inc(*done(f"ho{b}"))

    def mlstm_act():
        act, st = nc.scalar, "mlstm"
        others_done(act, "moe")
        done = signals(act_s, st)
        with act.Fori(0, NCH) as i:
            PE, ACTS, DVE, POOL = after(st, i)
            prep(st, i)
            act.wait_ge(*DVE("nab"))
            nc.scalar.activation(yv[:], nab[:], ACT.Exp).then_inc(*done("ey"))
            act.wait_ge(*ACTS("ey"))
            nc.scalar.activation(lnu[:], yv[:], ACT.Ln, bias=ones[:, 0:1]).then_inc(*done("ln"))
            for b in range(BC):
                act.wait_ge(*PE(f"cb{b}"))
                for h in range(HL):
                    last = nc.scalar.activation(decayT[:, h % 2, b * HL // 2 + h // 2, :], bank[3 + b][:, h * P:(h + 1) * P], ACT.Exp,
                                                bias=av[:, b, h:h + 1], scale=-1.0)
            last.then_inc(*done("D"))
            act.wait_ge(*DVE("cm"))
            nc.scalar.activation(ne[:], cm[:], ACT.Exp, scale=-1.0).then_inc(*done("ne"))

    def mlstm_pool():
        pool, st = nc.gpsimd, "mlstm"
        others_done(pool, "moe")
        nc.gpsimd.memset(mhalf8[:], -0.5).then_inc(zeroed, 1)
        pool.wait_ge(zeroed, 2)
        done = signals(pool_s, st)
        with pool.Fori(0, NCH) as i:
            PE, ACTS, DVE, POOL = after(st, i)
            pool.wait_ge(*DVE("hvar"))
            nc.gpsimd.tensor_tensor(hrs[:].rearrange("p b h -> p (b h)"), hvar[:].rearrange("p b h -> p (b h)"), mhalf8[:],
                                    ALU.pow).then_inc(*done("hrs"))
            pool.wait_ge(*DVE("hn"))
            nc.gpsimd.tensor_tensor(hce[:], hce[:], over(lnw1[:], BC), ALU.mult).then_inc(*done("w"))
            stats_root(st, i)

    def mlstm_dve():
        dve, st = nc.vector, "mlstm"
        others_done(dve, "moe")
        dve.wait_ge(w_loaded["mlstm"], 16)
        nc.vector.memset(vext[:, :, :, DL:], 1.0).then_inc(mlstm_ready, 1)
        nc.vector.tensor_copy(ident_b[:], ident[:])
        nc.vector.tensor_tensor(triI[:], ident[:], C("tri"), ALU.add)
        nc.vector.tensor_tensor(gkv[:].rearrange("p k g -> p (k g)"), LW("gk"), LW("gv"), ALU.add)
        nc.vector.tensor_scalar(lnw1[:], LW("lnw"), 1.0, None, ALU.add)
        nc.vector.tensor_scalar(late_b[:].rearrange("p (h s) -> p h s", h=HL), over(C("late"), HL), 1e30, None, ALU.mult).then_inc(mlstm_ready, 1)
        done = signals(dve_s, st)
        V = nc.vector
        with dve.Fori(0, NCH) as i:
            PE, ACTS, DVE, POOL = after(st, i)
            dve.wait_ge(*PE("xT"))
            V.tensor_copy(xnT[:].rearrange("p k t -> p (k t)"), bank[7][:]).then_inc(*done("xT"))
            dve.wait_ge(*PE("gates"))
            V.tensor_tensor(gt[:], bank[0][:, 0:BC * 2 * HL].rearrange("p (b g) -> p b g", b=BC), over(LW("gb"), BC), ALU.add).then_inc(*done("gt"))
            dve.wait_ge(*DVE("gt"))
            fg, ig = gt[:, :, HL:], gt[:, :, 0:HL]
            V.tensor_scalar(mnf[:], fg, 0.0, None, ALU.min).then_inc(*done("mnf"))
            dve.wait_ge(*DVE("mnf"))
            V.scalar_tensor_tensor(nab[:], mnf[:], 2.0, fg, ALU.mult, ALU.subtract).then_inc(*done("nab"))
            dve.wait_ge(*ACTS("ey"))
            V.tensor_scalar(uu[:], yv[:], 1.0, None, ALU.add).then_inc(*done("u"))
            dve.wait_ge(*DVE("u"))
            V.scalar_tensor_tensor(e1[:], uu[:], -1.0, yv[:], ALU.add, ALU.subtract).then_inc(*done("e1"))
            V.reciprocal(ru[:], uu[:]).then_inc(*done("ru"))
            dve.wait_ge(*DVE("ru"))
            V.tensor_tensor(cr[:], e1[:], ru[:], ALU.mult).then_inc(*done("cr"))
            dve.wait_ge(*ACTS("ln"))
            V.tensor_tensor(lnu[:], mnf[:], lnu[:], ALU.subtract).then_inc(*done("t"))
            dve.wait_ge(*DVE("t"))
            V.tensor_tensor(lf[:], lnu[:], cr[:], ALU.add).then_inc(*done("lf"))
            dve.wait_ge(*PE("cs"))
            V.tensor_copy(cs[:].rearrange("p b h -> p (b h)"), bank[1][:, 0:BH]).then_inc(*done("cs"))
            V.tensor_tensor(av[:], ig, bank[1][:, 0:BH].rearrange("p (b h) -> p b h", b=BC), ALU.subtract).then_inc(*done("a"))
            dve.wait_ge(*PE("aT"))
            V.tensor_copy(aT[:], bank[2][0:BH, 0:P]).then_inc(*done("aT"))
            dve.wait_ge(*DVE("aT"))
            V.tensor_tensor_scan(cmax[:], aT[:], aT[:], -3.0e38, ALU.max, ALU.max).then_inc(*done("cmax"))
            dve.wait_ge(*DVE("cmax"))
            V.tensor_tensor(cdiag[:], over(cmax[:], BH), wide(ident[0:BH, 0:BH], P), ALU.mult).then_inc(*done("cdiag"))
            dve.wait_ge(*PE("cm"))
            V.tensor_tensor(cm[:].rearrange("p b h -> p (b h)"), bank[2][:, 0:BH], cs[:].rearrange("p b h -> p (b h)"), ALU.add).then_inc(*done("cm"))
            dve.wait_ge(*ACTS("D"))
            for par in range(2):
                V.scalar_tensor_tensor(cT[:, par].rearrange("p c s -> p (c s)"), bank[5 + par][:], DL ** -0.5,
                                       decayT[:, par].rearrange("p c s -> p (c s)"), ALU.mult, ALU.mult).then_inc(*done(f"cT{par}"))
            dve.wait_ge(*PE("ho1"))
            sums = [bank[b][:, 0:HL * (DL + 1)].rearrange("p (h c) -> p h c", h=HL) for b in range(BC)]
            for b in range(BC):
                V.tensor_copy(ab[:, b, :], sums[b][:, :, DL]).then_inc(*done(f"ab{b}"))
            dve.wait_ge(*DVE("ab1"))
            V.scalar_tensor_tensor(nr[:], ab[:], -1.0, ab[:], ALU.mult, ALU.max).then_inc(*done("abs"))
            dve.wait_ge(*DVE("abs"))
            dve.wait_ge(*ACTS("ne"))
            V.tensor_tensor(nr[:], nr[:], ne[:], ALU.max).then_inc(*done("nr"))
            dve.wait_ge(*DVE("nr"))
            V.tensor_scalar(nr[:], nr[:], 1e-6, None, ALU.add).then_inc(*done("nre"))
            dve.wait_ge(*DVE("nre"))
            V.reciprocal(nr[:], nr[:]).then_inc(*done("rn"))
            dve.wait_ge(*DVE("rn"))
            for b in range(BC):
                V.tensor_tensor(hst[:, b, :].rearrange("p (h d) -> p h d", h=HL), sums[b][:, :, 0:DL], wide(nr[:, b, :], DL),
                                ALU.mult).then_inc(*done(f"h{b}"))
            dve.wait_ge(*DVE("h1"))
            h4 = [t[:].rearrange("p b (h d) -> p (b h) d", h=HL) for t in (hst, hce, hq)]
            f8 = [t[:].rearrange("p b h -> p (b h)") for t in (hsum, hsq, hvar, hrs)]
            V.tensor_reduce(f8[0], h4[0], AX.X, ALU.add).then_inc(*done("hsum"))
            dve.wait_ge(*DVE("hsum"))
            V.scalar_tensor_tensor(h4[1], wide(f8[0], DL), -1.0 / DL, h4[0], ALU.mult, ALU.add).then_inc(*done("hce"))
            dve.wait_ge(*DVE("hce"))
            V.tensor_tensor(h4[2], h4[1], h4[1], ALU.mult).then_inc(*done("hq"))
            dve.wait_ge(*DVE("hq"))
            V.tensor_reduce(f8[1], h4[2], AX.X, ALU.add).then_inc(*done("hsq"))
            dve.wait_ge(*DVE("hsq"))
            V.tensor_scalar(f8[2], f8[1], 1.0 / DL, EPS, ALU.mult, ALU.add).then_inc(*done("hvar"))
            dve.wait_ge(*POOL("hrs"))
            V.tensor_tensor(h4[1], h4[1], wide(f8[3], DL), ALU.mult).then_inc(*done("hn"))
            dve.wait_ge(*POOL("w"))
            V.tensor_tensor(x[:, bass.ds(i * BC, BC), :], hce[:], x[:, bass.ds(i * BC, BC), :], ALU.add).then_inc(*done("res"))
            dve.wait_ge(*DVE("res"))
            stats(st, i)

    BW = weights["bit"]
    ROUND = 1.5 * 2.0 ** 23
    KI = INNER // P
    NB_W = ("wg", "wu", "wd")
    wq_b = {n: area(f"q_{n}", [P, KD * INNER], k * 1024, BF16) for k, n in enumerate(NB_W)}
    wgq, wuq = (wq_b[n].rearrange("p (k f) -> p k f", k=KD) for n in ("wg", "wu"))
    wdq = wq_b["wd"].rearrange("p (k d) -> p k d", k=KI)
    wtmp = area("wtmp", [P, KD * INNER], 3072)
    wsum = area("wsum", [P, 3], 5120)
    wsc = area("wsc", [P, 3], 5123)
    winv = area("winv", [P, 3], 5126)
    xr = area("xr", [P, BC, D], 5136)
    xq = area("xq", [P, BC, D], 5648, BF16)
    xqT = area("xqT", [P, KD, TOK], 5904, BF16)
    sil = area("sil", [P, 2, 512], 6160)
    hb = area("hb", [P, BC, INNER], 7184)
    hr = area("hr", [P, BC, INNER], 9232)
    hqb = area("hqb", [P, BC, INNER], 11280, BF16)
    hqT = area("hqT", [P, BC, KI, P], 12304, BF16)
    am, qs, qi, am2, qs2, qi2, sc_g, sc_u, sc_d = (area(f"b{n}", [P, BC], 13328 + 2 * n) for n in range(9))
    id_b = area("id_b", [P, P], 13352, BF16)
    assert 13352 + 64 <= SPACE
    bit_sum, bit_ready = sem("weight_magnitudes_summed"), sem("weights_quantised")
    HU = [(b, hh) for b in range(BC) for hh in range(2)]
    stage("bit", NCH, pe=["xqT", "n0", "n1", "n2", "n3", "hT0", "hT1", "out0", "out1"],
          act=["prep0", "prep1", "n0", "n1", "n2", "n3"],
          dve=["am", "amc", "rq", "qs", "qi", "scg", "scu", "r0", "r1", "q", "xqT", "n0", "n1", "am20", "amc20", "rq20", "qs20", "n2", "n3", "am21", "amc21", "rq21", "qs21",
               "qi20", "r20", "q20", "scd0", "hT0", "qi21", "r21", "q21", "scd1", "hT1", "res0", "res1"] + LN_DVE,
          pool=["rstd"])

    def bit_pe():
        pe, st = nc.tensor, "bit"
        others_done(pe, "mlstm")
        pe.wait_ge(bit_sum, 3)
        nc.tensor.matmul(bank[0][:, 0:3], ones[:], wsum[:], start=True, stop=True).then_inc(bit_sum, 1)
        pe.wait_ge(bit_ready, 1)
        done = signals(pe_s, st)
        hT_bank = bank[7][:].bitcast(BF16)
        with pe.Fori(0, NCH) as i:
            PE, ACTS, DVE, POOL = after(st, i)
            pe.wait_ge(*DVE("q"))
            for k in range(KD):
                for b in range(BC):
                    last = nc.tensor.transpose(hT_bank[:, (k * BC + b) * P:(k * BC + b + 1) * P], xq[:, b, k * P:(k + 1) * P], id_b[:])
            last.then_inc(*done("xqT"))
            pe.wait_ge(*DVE("xqT"))
            for n, (b, hh) in enumerate(HU):
                if n == 3:
                    pe.wait_ge(*DVE("n0"))
                for w, bk in ((wgq, bank[2 * (n % 3)]), (wuq, bank[2 * (n % 3) + 1])):
                    for k in range(KD):
                        last = nc.tensor.matmul(bk[:], xqT[:, k, b * P:(b + 1) * P], w[:, k, hh * 512:(hh + 1) * 512],
                                                start=k == 0, stop=k == KD - 1)
                last.then_inc(*done(f"n{n}"))
            for b in range(BC):
                pe.wait_ge(*DVE(f"q2{b}"))
                if b:
                    pe.wait_ge(*DVE("hT0"))
                for k in range(KI):
                    last = nc.tensor.transpose(hT_bank[:, k * P:(k + 1) * P], hqb[:, b, k * P:(k + 1) * P], id_b[:])
                last.then_inc(*done(f"hT{b}"))
            for b in range(BC):
                pe.wait_ge(*DVE(f"hT{b}"))
                for k in range(KI):
                    last = nc.tensor.matmul(bank[6][:, b * D:(b + 1) * D], hqT[:, b, k, :], wdq[:, k, :], start=k == 0, stop=k == KI - 1)
                last.then_inc(*done(f"out{b}"))

    def bit_act():
        act, st = nc.scalar, "bit"
        others_done(act, "mlstm")
        done = signals(act_s, st)
        with act.Fori(0, NCH) as i:
            PE, ACTS, DVE, POOL = after(st, i)
            prep(st, i)
            for n, (b, hh) in enumerate(HU):
                act.wait_ge(*PE(f"n{n}"))
                act.wait_ge(*DVE("scg"))
                if n >= 2:
                    act.wait_ge(*DVE(f"n{n - 2}"))
                nc.scalar.activation(sil[:, n % 2, :], bank[2 * (n % 3)][:], ACT.Silu, scale=sc_g[:, b:b + 1]).then_inc(*done(f"n{n}"))

    def bit_pool():
        pool, st = nc.gpsimd, "bit"
        others_done(pool, "mlstm")
        done = signals(pool_s, st)
        with pool.Fori(0, NCH) as i:
            PE, ACTS, DVE, POOL = after(st, i)
            stats_root(st, i)

    def bit_dve():
        dve, st = nc.vector, "bit"
        V = nc.vector
        others_done(dve, "mlstm")
        dve.wait_ge(w_loaded["bit"], 16)
        for n, name in enumerate(NB_W):
            V.tensor_reduce(wsum[:, n:n + 1], BW(name), AX.X, ALU.add, apply_absolute_value=True).then_inc(bit_sum, 1)
        V.tensor_copy(id_b[:], ident[:])
        dve.wait_ge(bit_sum, 4)
        V.tensor_scalar(wsum[:], bank[0][:, 0:3], 1.0 / (D * INNER), 1e-5, ALU.mult, ALU.max).then_inc(bit_q, 1)
        dve.wait_ge(bit_q, 1)
        V.reciprocal(wsc[:], wsum[:]).then_inc(bit_q, 1)
        dve.wait_ge(bit_q, 2)
        V.reciprocal(winv[:], wsc[:]).then_inc(bit_q, 1)
        for n, name in enumerate(NB_W):
            dve.wait_ge(bit_q, 3 + 3 * n)
            V.tensor_scalar(wtmp[:], BW(name), wsc[:, n:n + 1], ROUND, ALU.mult, ALU.add).then_inc(bit_q, 1)
            dve.wait_ge(bit_q, 4 + 3 * n)
            V.tensor_scalar(wtmp[:], wtmp[:], ROUND, 1.0, ALU.subtract, ALU.min).then_inc(bit_q, 1)
            dve.wait_ge(bit_q, 5 + 3 * n)
            V.tensor_scalar(wq_b[name], wtmp[:], -1.0, None, ALU.max).then_inc(bit_q, 1)
        dve.wait_ge(bit_q, 12)
        dve.sem_inc(bit_ready, 1)
        done = signals(dve_s, st)
        with dve.Fori(0, NCH) as i:
            PE, ACTS, DVE, POOL = after(st, i)
            dve.wait_ge(act_s.sem, act_s.at(st, i, "prep1"))
            V.tensor_reduce(am[:], xn[:], AX.X, ALU.max, apply_absolute_value=True).then_inc(*done("am"))
            dve.wait_ge(*DVE("am"))
            V.tensor_scalar(am[:], am[:], 1e-5, None, ALU.max).then_inc(*done("amc"))
            dve.wait_ge(*DVE("amc"))
            V.reciprocal(am[:], am[:]).then_inc(*done("rq"))
            dve.wait_ge(*DVE("rq"))
            V.tensor_scalar(qs[:], am[:], 127.0, None, ALU.mult).then_inc(*done("qs"))
            dve.wait_ge(*DVE("qs"))
            V.reciprocal(qi[:], qs[:]).then_inc(*done("qi"))
            dve.wait_ge(*DVE("qi"))
            V.tensor_scalar(sc_g[:], qi[:], winv[:, 0:1], None, ALU.mult).then_inc(*done("scg"))
            V.tensor_scalar(sc_u[:], qi[:], winv[:, 1:2], None, ALU.mult).then_inc(*done("scu"))
            for b in range(BC):
                V.tensor_scalar(xr[:, b, :], xn[:, b, :], qs[:, b:b + 1], ROUND, ALU.mult, ALU.add).then_inc(*done(f"r{b}"))
            dve.wait_ge(*DVE("r1"))
            V.tensor_scalar(xq[:], xr[:], ROUND, 127.0, ALU.subtract, ALU.min).then_inc(*done("q"))
            dve.wait_ge(*PE("xqT"))
            V.tensor_scalar(xqT[:].rearrange("p k t -> p (k t)"), bank[7][:].bitcast(BF16)[:, 0:KD * TOK], -128.0, None,
                            ALU.max).then_inc(*done("xqT"))

            def gated(n):
                b, hh = HU[n]
                dve.wait_ge(*ACTS(f"n{n}"))
                V.scalar_tensor_tensor(hb[:, b, hh * 512:(hh + 1) * 512], bank[2 * (n % 3) + 1][:], sc_u[:, b:b + 1], sil[:, n % 2, :],
                                       ALU.mult, ALU.mult).then_inc(*done(f"n{n}"))

            def largest(b):
                dve.wait_ge(*DVE(f"n{2 * b + 1}"))
                V.tensor_reduce(am2[:, b:b + 1], hb[:, b, :], AX.X, ALU.max, apply_absolute_value=True).then_inc(*done(f"am2{b}"))
                dve.wait_ge(*DVE(f"am2{b}"))
                V.tensor_scalar(am2[:, b:b + 1], am2[:, b:b + 1], 1e-5, None, ALU.max).then_inc(*done(f"amc2{b}"))
                dve.wait_ge(*DVE(f"amc2{b}"))
                V.reciprocal(am2[:, b:b + 1], am2[:, b:b + 1]).then_inc(*done(f"rq2{b}"))
                dve.wait_ge(*DVE(f"rq2{b}"))
                V.tensor_scalar(qs2[:, b:b + 1], am2[:, b:b + 1], 127.0, None, ALU.mult).then_inc(*done(f"qs2{b}"))

            gated(0)
            gated(1)
            largest(0)
            gated(2)
            gated(3)
            largest(1)
            for b in range(BC):
                dve.wait_ge(*DVE(f"qs2{b}"))
                V.reciprocal(qi2[:, b:b + 1], qs2[:, b:b + 1]).then_inc(*done(f"qi2{b}"))
                V.tensor_scalar(hr[:, b, :], hb[:, b, :], qs2[:, b:b + 1], ROUND, ALU.mult, ALU.add).then_inc(*done(f"r2{b}"))
                dve.wait_ge(*DVE(f"r2{b}"))
                V.tensor_scalar(hqb[:, b, :], hr[:, b, :], ROUND, 127.0, ALU.subtract, ALU.min).then_inc(*done(f"q2{b}"))
                V.tensor_scalar(sc_d[:, b:b + 1], qi2[:, b:b + 1], winv[:, 2:3], None, ALU.mult).then_inc(*done(f"scd{b}"))
                dve.wait_ge(*PE(f"hT{b}"))
                V.tensor_scalar(hqT[:, b].rearrange("p k t -> p (k t)"), bank[7][:].bitcast(BF16), -128.0, None,
                                ALU.max).then_inc(*done(f"hT{b}"))
            dve.wait_ge(*PE("out1"))
            for b in range(BC):
                V.scalar_tensor_tensor(x[:, bass.ds(i * BC + b, 1), :], bank[6][:, b * D:(b + 1) * D], sc_d[:, b:b + 1],
                                       x[:, bass.ds(i * BC + b, 1), :], ALU.mult, ALU.add).then_inc(*done(f"res{b}"))
            dve.wait_ge(*DVE("res1"))
            stats(st, i)

    def bit_sp():
        sp = nc.sync
        others_done(sp, "mlstm")
        load_weights(sp, "mqa")

    QW = weights["mqa"]
    q_w = QW("wq").rearrange("p (k m) -> p k m", k=KD)
    k_w, v_w = (QW(n).rearrange("p (k m) -> p k m", k=KD) for n in ("wk", "wv"))
    wout = QW("wout").rearrange("p (k n) -> p k n", k=HM)
    w1 = QW("w1").rearrange("p (k f) -> p k f", k=KD)
    w2 = QW("w2").rearrange("p (k n) -> p k n", k=KI)
    q4 = area("q4", [P, HM, TOK], 0)
    m4 = area("m4", [P, HM, TOK], 2048)
    ff = area("ff", [P, KI, TOK], 4096)
    prob4 = area("prob4", [P, 4, FAN, P], 6144)
    probT4 = area("probT4", [P, 2, FAN, P], 8192)
    masked = area("masked", [P, 2, FAN, P], 9216)
    k4 = area("k4", [P, TOK], 10240)
    v4 = area("v4", [P, BC, HD], 10496)
    mask4 = area("mask4", [P, BC, P], 10624)
    ctx4 = area("ctx4", [P, BC, D], 10880)
    cn4 = area("cn4", [P, BC, D], 11392)
    cnT = area("cnT", [P, KD, TOK], 11904)
    sgb = area("sgb", [P, 2, TOK], 12416)
    sm4 = area("sm4", [P, 3, 4, FAN], 12928)
    cbn = area("cbn", [P, BC, 6], 12976)
    cmv = area("cmv", [P, BC, 2], 12988)
    cveps = area("cveps", [P, BC], 12992)
    crstd = area("crstd", [P, BC], 12994)
    DORDER4 = []
    for t in range(UNITS + 3):
        DORDER4 += [("add", t), ("max", t)] * (t < UNITS) + [("rec", t - 1)] * (0 <= t - 1 < UNITS)
        DORDER4 += [("copy", t - 2)] * (0 <= t - 2 < UNITS) + [("o", t - 3)] * (0 <= t - 3 < UNITS and t % 2 == 0)
    stage("mqa", NCH,
          pe=["xT"] + [f"ff{n}" for n in range(KI)] + ["cT", "k", "v", "q0", "q1", "q2", "q3"] + [f"{a}{t}" for a, t in ORDER] + ["out0", "out1"],
          act=["prep0", "prep1"] + [f"ff{n}" for n in range(KI)] + [f"exp{t}" for t in range(UNITS)],
          dve=["xT", "cbn0", "cbn1", "cag0", "cag1", "cveps", "ff0", "ff1", "cn0", "cn1"] + [f"ff{n}" for n in range(2, KI)]
          + ["cT", "k", "v", "q0", "q1", "q2", "q3"] + [f"{a}{t}" for a, t in DORDER4] + ["res"] + LN_DVE,
          pool=["crstd"] + [f"norm{t}" for t in range(UNITS)] + ["rstd"])

    def mqa_sp():
        sp, st = nc.sync, "mqa"
        others_done(sp, "bit")
        load_weights(sp, "low")
        with sp.Fori(0, NCH) as i:
            sp.wait_ge(dve_s.sem, dve_s.at(st, i, "cn1", back=1))
            sp.dma_start(ctx4[:], ctx_dram[:, bass.ds(i * BC, BC), :]).then_inc(ctx4_loaded, 16)
            sp.wait_ge(dve_s.sem, dve_s.at(st, i, f"add{UNITS - 1}", back=1))
            sp.dma_start(mask4[:], mask_dram[:, bass.ds(i * BC, BC), :]).then_inc(mask_loaded, 16)

    def mqa_pe():
        pe, st = nc.tensor, "mqa"
        others_done(pe, "bit")
        pe.wait_ge(w_loaded[st], 16)
        done = signals(pe_s, st)
        with pe.Fori(0, NCH) as i:
            PE, ACTS, DVE, POOL = after(st, i)
            turn_x(st, i)
            pe.wait_ge(*DVE("xT"))
            for n in range(KI):
                if n >= 4:
                    pe.wait_ge(*DVE(f"ff{n - 4}"))
                for part, first in ((0, INNER + n * P), (1, n * P)):
                    for k in range(KD):
                        last = nc.tensor.matmul(bank[n % 4][:, part * TOK:(part + 1) * TOK], w1[:, k, first:first + P], xnT[:, k, :],
                                                start=k == 0, stop=k == KD - 1)
                last.then_inc(*done(f"ff{n}"))
            pe.wait_ge(*DVE("res", back=1))
            pe.wait_ge(*DVE("cn1"))
            for k in range(KD):
                for b in range(BC):
                    last = nc.tensor.transpose(bank[6][:, (k * BC + b) * P:(k * BC + b + 1) * P], cn4[:, b, k * P:(k + 1) * P], ident[:])
            last.then_inc(*done("cT"))
            pe.wait_ge(*DVE("cT"))
            for k in range(KD):
                last = nc.tensor.matmul(bank[4][:, 0:TOK], k_w[:, k, :], cnT[:, k, :], start=k == 0, stop=k == KD - 1)
            last.then_inc(*done("k"))
            for b in range(BC):
                for k in range(KD):
                    last = nc.tensor.matmul(bank[5][:, b * HD:(b + 1) * HD], cnT[:, k, b * P:(b + 1) * P], v_w[:, k, 0:HD],
                                            start=k == 0, stop=k == KD - 1)
            last.then_inc(*done("v"))
            for g in range(4):
                pe.wait_ge(*DVE(f"ff{g + 4}"))
                for m in range(2):
                    mm = 2 * g + m
                    for k in range(KD):
                        last = nc.tensor.matmul(bank[g][:, m * TOK:(m + 1) * TOK], q_w[:, k, mm * P:(mm + 1) * P], xnT[:, k, :],
                                                start=k == 0, stop=k == KD - 1)
                last.then_inc(*done(f"q{g}"))
            pe.wait_ge(*DVE("q3"))
            for what, t in ORDER:
                b, u, par = unit(t)
                rows = slice(HD * par, HD * par + HD)
                if what == "S":
                    if t >= 2:
                        pe.wait_ge(*DVE(f"add{t - 2}"))
                    for j in range(FAN):
                        last = nc.tensor.matmul(bank[t % 2][:, j * P:(j + 1) * P], q4[rows, FAN * u + j, b * P:(b + 1) * P],
                                                k4[rows, b * P:(b + 1) * P], start=True, stop=True)
                elif what == "T":
                    pe.wait_ge(*POOL(f"norm{t}"))
                    if t >= 2:
                        pe.wait_ge(*DVE(f"copy{t - 2}"))
                    for j in range(FAN):
                        last = nc.tensor.transpose(bank[2 + t % 2][:, j * P:(j + 1) * P], prob4[:, t % 4, j, :], ident[:])
                else:
                    pe.wait_ge(*DVE(f"copy{t}"))
                    if b == 1 and par == 0:
                        pe.wait_ge(*DVE(f"o{t - 3}"))
                    last = nc.tensor.matmul(bank[4 + u][rows, :], v4[:, b, :], probT4[:, t % 2].rearrange("p j s -> p (j s)"),
                                            start=True, stop=True)
                last.then_inc(*done(f"{what}{t}"))
            for b in range(BC):
                pe.wait_ge(*DVE(f"o{4 * b + 3}"))
                for n, (src, w) in enumerate(((ff, w2), (m4, wout))):
                    for k in range(HM):
                        last = nc.tensor.matmul(bank[6][:, b * D:(b + 1) * D], src[:, k, b * P:(b + 1) * P], w[:, k, :],
                                                start=n == 0 and k == 0, stop=n == 1 and k == HM - 1)
                last.then_inc(*done(f"out{b}"))

    def mqa_act():
        act, st = nc.scalar, "mqa"
        others_done(act, "bit")
        done = signals(act_s, st)
        with act.Fori(0, NCH) as i:
            PE, ACTS, DVE, POOL = after(st, i)
            prep(st, i)
            for n in range(KI):
                act.wait_ge(*PE(f"ff{n}"))
                if n >= 2:
                    act.wait_ge(*DVE(f"ff{n - 2}"))
                nc.scalar.activation(sgb[:, n % 2, :], bank[n % 4][:, 0:TOK], ACT.Silu).then_inc(*done(f"ff{n}"))
            for t in range(UNITS):
                act.wait_ge(*DVE(f"max{t}"))
                if t >= 4:
                    act.wait_ge(*PE(f"T{t - 4}"))
                for j in range(FAN):
                    last = nc.scalar.activation(prob4[:, t % 4, j, :], masked[:, t % 2, j, :], ACT.Exp,
                                                bias=sm4[:, 0, t % 4, j:j + 1], accum_out=sm4[:, 1, t % 4, j:j + 1])
                last.then_inc(*done(f"exp{t}"))

    def mqa_pool():
        pool, st = nc.gpsimd, "mqa"
        others_done(pool, "bit")
        done = signals(pool_s, st)
        with pool.Fori(0, NCH) as i:
            PE, ACTS, DVE, POOL = after(st, i)
            pool.wait_ge(*DVE("cveps"))
            nc.gpsimd.tensor_tensor(crstd[:], cveps[:], mhalf[:], ALU.pow).then_inc(*done("crstd"))
            for t in range(UNITS):
                pool.wait_ge(*DVE(f"rec{t}"))
                nc.gpsimd.tensor_tensor(prob4[:, t % 4], prob4[:, t % 4], sm4[:, 2, t % 4, :].unsqueeze(2).to_broadcast([P, FAN, P]),
                                        ALU.mult).then_inc(*done(f"norm{t}"))
            stats_root(st, i)

    def mqa_dve():
        dve, st = nc.vector, "mqa"
        V = nc.vector
        others_done(dve, "bit")
        dve.wait_ge(w_loaded[st], 16)
        done = signals(dve_s, st)
        with dve.Fori(0, NCH) as i:
            PE, ACTS, DVE, POOL = after(st, i)

            def ffn(n):
                dve.wait_ge(*ACTS(f"ff{n}"))
                V.tensor_tensor(ff[:, n, :], bank[n % 4][:, TOK:2 * TOK], sgb[:, n % 2, :], ALU.mult).then_inc(*done(f"ff{n}"))

            dve.wait_ge(*PE("xT"))
            for k in range(KD):
                last = V.tensor_scalar(xnT[:, k, :], bank[7][:, k * TOK:(k + 1) * TOK], QW("ln_g")[:, k:k + 1], QW("ln_b")[:, k:k + 1],
                                       ALU.mult, ALU.add)
            last.then_inc(*done("xT"))
            dve.wait_ge(ctx4_loaded, i * 16 + 16)
            dve.sem_inc(held, 1)
            for b in range(BC):
                V.bn_stats(cbn[:, b, :], ctx4[:, b, :]).then_inc(*done(f"cbn{b}"))
            for b in range(BC):
                dve.wait_ge(*DVE(f"cbn{b}"))
                dve.sem_inc(held, 1)
                V.bn_aggr(cmv[:, b, :], cbn[:, b, :]).then_inc(*done(f"cag{b}"))
            dve.wait_ge(*DVE("cag1"))
            V.tensor_scalar(cveps[:], cmv[:, :, 1], EPS, None, ALU.add).then_inc(*done("cveps"))
            ffn(0)
            ffn(1)
            dve.wait_ge(*POOL("crstd"))
            for b in range(BC):
                V.tensor_scalar(cn4[:, b, :], ctx4[:, b, :], cmv[:, b, 0:1], crstd[:, b:b + 1], ALU.subtract, ALU.mult).then_inc(*done(f"cn{b}"))
            for n in range(2, KI):
                ffn(n)
            dve.wait_ge(*PE("cT"))
            for k in range(KD):
                last = V.tensor_scalar(cnT[:, k, :], bank[6][:, k * TOK:(k + 1) * TOK], QW("cln_g")[:, k:k + 1], QW("cln_b")[:, k:k + 1],
                                       ALU.mult, ALU.add)
            last.then_inc(*done("cT"))
            dve.wait_ge(*PE("k"))
            V.tensor_copy(k4[:], bank[4][:, 0:TOK]).then_inc(*done("k"))
            dve.wait_ge(*PE("v"))
            V.tensor_copy(v4[:].rearrange("p b d -> p (b d)"), bank[5][:, 0:BC * HD]).then_inc(*done("v"))
            for g in range(4):
                dve.wait_ge(*PE(f"q{g}"))
                V.tensor_scalar(q4[:, 2 * g:2 * g + 2, :].rearrange("p m t -> p (m t)"), bank[g][:], HD ** -0.5, None,
                                ALU.mult).then_inc(*done(f"q{g}"))
            for what, t in DORDER4:
                b, u, par = unit(t)
                if what == "add":
                    dve.wait_ge(*PE(f"S{t}"))
                    if t == 0:
                        dve.wait_ge(mask_loaded, i * 16 + 16)
                    if t >= 2:
                        dve.wait_ge(*ACTS(f"exp{t - 2}"))
                    ins = V.tensor_tensor(masked[:, t % 2], bank[t % 2][:].rearrange("p (j s) -> p j s", j=FAN), over(mask4[:, b, :], FAN), ALU.add)
                elif what == "max":
                    dve.wait_ge(*DVE(f"add{t}"))
                    ins = V.tensor_reduce(sm4[:, 0, t % 4, :], masked[:, t % 2], AX.X, ALU.max, negate=True)
                elif what == "rec":
                    dve.wait_ge(*ACTS(f"exp{t}"))
                    ins = V.reciprocal(sm4[:, 2, t % 4, :], sm4[:, 1, t % 4, :])
                elif what == "copy":
                    dve.wait_ge(*PE(f"T{t}"))
                    ins = V.tensor_copy(probT4[:, t % 2].rearrange("p j s -> p (j s)"), bank[2 + t % 2][:])
                else:
                    dve.wait_ge(*PE(f"PV{t}"))
                    ins = V.tensor_copy(m4[:, FAN * u:FAN * u + FAN, b * P:(b + 1) * P], bank[4 + u][:].rearrange("p (j s) -> p j s", j=FAN))
                ins.then_inc(*done(f"{what}{t}"))
            dve.wait_ge(*PE("out1"))
            V.tensor_tensor(x[:, bass.ds(i * BC, BC), :], bank[6][:].rearrange("p (b d) -> p b d", b=BC),
                            x[:, bass.ds(i * BC, BC), :], ALU.add).then_inc(*done("res"))
            dve.wait_ge(*DVE("res"))
            stats(st, i)

    FW = weights["low"]
    RK = 64
    u1 = FW("u1").rearrange("p (k r) -> p k r", k=KD)
    v1 = FW("v1").rearrange("p (j m) -> p j m", m=P)
    u2 = FW("u2").rearrange("p (k r) -> p k r", k=KI)
    pT5 = area("pT5", [P, TOK], 0)
    h5 = area("h5", [P, KI, TOK], 256)
    q5 = area("q5", [RK, TOK], 2304)
    stage("low", NCH, pe=["xT", "p"] + [f"h{g}{half}" for g in range(2) for half in range(2)] + ["q", "out"],
          act=["prep0", "prep1"] + [f"h{g}{half}" for g in range(2) for half in range(2)],
          dve=["xT", "p", "q", "res"], pool=["b2"])

    def low_sp():
        sp = nc.sync
        with sp.Fori(0, NCH) as i:
            sp.wait_ge(dve_s.sem, dve_s.at("low", i, "res"))
            sp.dma_start(out_dram[:, bass.ds(i * BC, BC), :], x[:, bass.ds(i * BC, BC), :]).then_inc(out_stored, 16)

    def low_pe():
        pe, st = nc.tensor, "low"
        others_done(pe, "mqa")
        pe.wait_ge(w_loaded[st], 16)
        done = signals(pe_s, st)
        with pe.Fori(0, NCH) as i:
            PE, ACTS, DVE, POOL = after(st, i)
            turn_x(st, i)
            pe.wait_ge(*DVE("xT"))
            for k in range(KD):
                last = nc.tensor.matmul(bank[0][:, 0:TOK], u1[:, k, :], xnT[:, k, :], start=k == 0, stop=k == KD - 1)
            last.then_inc(*done("p"))
            pe.wait_ge(*DVE("p"))
            for g in range(2):
                for half in range(2):
                    rows = slice(RK * half, RK * half + RK)
                    for j in range(2):
                        last = nc.tensor.matmul(bank[1 + 2 * g + half][:, j * TOK:(j + 1) * TOK], v1[rows, 2 * g + j, :], pT5[rows, :],
                                                start=True, stop=True)
                    last.then_inc(*done(f"h{g}{half}"))
            for m in range(KI):
                pe.wait_ge(*ACTS(f"h{m // 4}{1}"))
                last = nc.tensor.matmul(bank[5][0:RK, 0:TOK], u2[:, m, :], h5[:, m, :], start=m == 0, stop=m == KI - 1)
            last.then_inc(*done("q"))
            pe.wait_ge(*DVE("q"))
            pe.wait_ge(*DVE("res", back=1))
            for b in range(BC):
                last = nc.tensor.matmul(bank[6][:, b * D:(b + 1) * D], q5[:, b * P:(b + 1) * P], FW("v2")[0:RK, :], start=True, stop=True)
            last.then_inc(*done("out"))

    def low_act():
        act, st = nc.scalar, "low"
        others_done(act, "mqa")
        act.wait_ge(w_loaded[st], 16)
        done = signals(act_s, st)
        with act.Fori(0, NCH) as i:
            PE, ACTS, DVE, POOL = after(st, i)
            prep(st, i)
            for g in range(2):
                for half in range(2):
                    act.wait_ge(*PE(f"h{g}{half}"))
                    for j in range(2):
                        m = 2 * (2 * g + j) + half
                        last = nc.scalar.activation(h5[:, m, :], bank[1 + 2 * g + half][:, j * TOK:(j + 1) * TOK], ACT.Gelu_apprx_tanh,
                                                    bias=FW("b1")[:, m:m + 1])
                    last.then_inc(*done(f"h{g}{half}"))

    def low_pool():
        pool = nc.gpsimd
        others_done(pool, "mqa")
        pool.wait_ge(w_loaded["low"], 16)
        done = signals(pool_s, "low")
        with pool.Fori(0, NCH) as i:
            pool.wait_ge(act_s.sem, act_s.at("low", i, "prep1"))
            pool.sem_inc(held, 1)
            nc.gpsimd.tensor_tensor(x[:, bass.ds(i * BC, BC), :], x[:, bass.ds(i * BC, BC), :], over(FW("b2"), BC), ALU.add).then_inc(*done("b2"))

    def low_dve():
        dve, st = nc.vector, "low"
        V = nc.vector
        others_done(dve, "mqa")
        done = signals(dve_s, st)
        with dve.Fori(0, NCH) as i:
            PE, ACTS, DVE, POOL = after(st, i)
            dve.wait_ge(*PE("xT"))
            V.tensor_copy(xnT[:].rearrange("p k t -> p (k t)"), bank[7][:]).then_inc(*done("xT"))
            dve.wait_ge(*PE("p"))
            V.tensor_copy(pT5[:], bank[0][:, 0:TOK]).then_inc(*done("p"))
            dve.wait_ge(*PE("q"))
            V.tensor_copy(q5[:], bank[5][0:RK, 0:TOK]).then_inc(*done("q"))
            dve.wait_ge(*PE("out"))
            dve.wait_ge(*POOL("b2"))
            V.tensor_tensor(x[:, bass.ds(i * BC, BC), :], bank[6][:].rearrange("p (b d) -> p b d", b=BC),
                            x[:, bass.ds(i * BC, BC), :], ALU.add).then_inc(*done("res"))
    sp_prog = [attn_sp, rec_sp, moe_sp, mlstm_sp, bit_sp, mqa_sp, low_sp]
    pe_prog = [attn_pe, spike_pe, rec_pe, moe_pe, mlstm_pe, bit_pe, mqa_pe, low_pe]
    act_prog = [attn_act, spike_act, rec_act, moe_act, mlstm_act, bit_act, mqa_act, low_act]
    dve_prog = [load_dve, attn_dve, spike_dve, rec_dve, moe_dve, mlstm_dve, bit_dve, mqa_dve, low_dve]
    pool_prog = [load_pool, attn_pool, spike_pool, rec_pool, moe_pool, mlstm_pool, bit_pool, mqa_pool, low_pool]
    block = ctx.enter_context(nc.Block())

    @block.sync
    def _(sp):
        sp.dma_start(x[:], x_dram).then_inc(x_loaded, 16)
        load_weights(sp, "attn")
        sp.dma_start(shape_consts[:], ins["consts"]).then_inc(consts_loaded, 16)
        load_weights(sp, "spike")
        for f in sp_prog:
            f()
        sp.wait_ge(out_stored, 16 * NCH)

    @block.tensor
    def _(pe):
        for f in pe_prog:
            f()

    @block.scalar
    def _(act):
        for f in act_prog:
            f()

    @block.vector
    def _(dve):
        for f in dve_prog:
            f()

    @block.gpsimd
    def _(pool):
        for f in pool_prog:
            f()


def pack(inputs):
    import numpy as np

    def a(name):
        return np.asarray(inputs[name])

    def rows(w):
        return w.reshape(-1, P, w.shape[1]).transpose(1, 0, 2).reshape(P, -1)

    def col(v, n=P):
        return v.reshape(-1, n).T

    def all_rows(v):
        return np.broadcast_to(v.reshape(1, -1), (P, v.size))

    def twice(w):
        return np.concatenate([w, w], 0)

    def put(stage, parts):
        cols = []
        for name, n in LAYOUT[stage]:
            v = parts[name]
            assert v.shape[1] == n and v.shape[0] in (P, 64), (stage, name, v.shape, n)
            if v.shape[0] == 64:
                v = twice(v)
            cols.append(v)
        return np.ascontiguousarray(np.concatenate(cols, 1))

    w = {}
    p = "L0_xattn_"
    w["attn"] = put("attn", dict(wk=rows(a(p + "Wk")), wv=rows(a(p + "Wv")), wq=rows(a(p + "Wq")), bk=col(a(p + "bk")),
                                 bq=col(a(p + "bq")), bv=col(a(p + "bv")), wu=rows(a(p + "Wu")), bu=all_rows(a(p + "bu"))))
    p = "L0_ffn_"
    e_w1 = a(p + "e_w1").reshape(NE0, MD, 2, P).transpose(2, 1, 0, 3).reshape(P, NE0 * P)
    w["spike"] = put("spike", dict(
        enc=rows(a(p + "enc_w")), enc_b=col(a(p + "enc_b")),
        s2c=rows(np.concatenate([a(p + "s2c_w")] * 2, 1)), s2c_b=twice(a(p + "s2c_b").reshape(-1, 1)),
        rw1=a(p + "r_w1"), rb1=a(p + "r_b1").reshape(-1, 1), rw2=a(p + "r_w2"), rb2=all_rows(a(p + "r_b2")),
        ew1=e_w1, eb1=a(p + "e_b1").reshape(NE0 * 2, P).T,
        ew2=a(p + "e_w2").reshape(NE0, 2, P, MD).transpose(2, 0, 1, 3).reshape(P, -1), eb2=all_rows(a(p + "e_b2")),
        c2s=a(p + "c2s_w"), c2s_b=col(a(p + "c2s_b")), dec=rows(a(p + "dec_w")), dec_b=all_rows(a(p + "dec_b")),
        ln_g=all_rows(a(p + "ln_g")), ln_b=all_rows(a(p + "ln_b"))))
    p = "L1_xattn_"
    w["rec"] = put("rec", dict(wi=rows(a(p + "Wi").T), bi=col(a(p + "bi")), wg=rows(a(p + "Wg").T), bg=col(a(p + "bg")),
                               a=rows(a(p + "A").T), bm=rows(a(p + "Bm").T), wo=rows(a(p + "Wo").T), bo=all_rows(a(p + "bo")),
                               decay=col(np.repeat(a(p + "decay").reshape(-1), D // 16))))
    p = "L1_ffn_"
    down = a(p + "ws_down")
    pad = np.zeros((P - (FE - P), D), down.dtype)
    w["moe"] = put("moe", dict(router=rows(a(p + "router_w").T), sgu=rows(a(p + "ws_gate_up")), sdown=rows(np.concatenate([down, pad], 0))))
    gu = np.concatenate([a(p + "w_gate").reshape(NE, KD, P, FE), a(p + "w_up").reshape(NE, KD, P, FE)], 3)
    w["gate_up"] = np.ascontiguousarray(gu.transpose(0, 2, 1, 3).reshape(NE, P, KD * 2 * FE))
    wd = a(p + "w_down")
    w["down"] = np.ascontiguousarray(wd)
    p = "L2_xattn_"
    gates = np.concatenate([a(p + "w_igate"), a(p + "w_fgate")], 0).T
    w["mlstm"] = put("mlstm", dict(gq=rows(gates[:D]), gk=rows(gates[D:2 * D]), gv=rows(gates[2 * D:]),
                                   gb=all_rows(np.concatenate([a(p + "b_igate"), a(p + "b_fgate")])), lnw=all_rows(a(p + "ln_weight"))))
    p = "L2_ffn_"
    w["bit"] = put("bit", dict(wg=rows(a(p + "w_gate").T), wu=rows(a(p + "w_up").T), wd=rows(a(p + "w_down").T)))
    p = "L3_xattn_"
    kv = a(p + "Wkv")
    w["mqa"] = put("mqa", dict(wq=rows(a(p + "Wq")), wk=rows(np.concatenate([kv[:, :HD]] * 2, 1)), wv=rows(np.concatenate([kv[:, HD:]] * 2, 1)),
                               wout=rows(a(p + "Wout")), w1=rows(a(p + "W1")), w2=rows(a(p + "W2")), ln_g=col(a(p + "ln_g")),
                               ln_b=col(a(p + "ln_b")), cln_g=col(a(p + "cln_g")), cln_b=col(a(p + "cln_b"))))
    p = "L3_ffn_"
    v1 = a(p + "V1").reshape(64, 4, 2, P).transpose(2, 0, 1, 3).reshape(P, -1)
    w["low"] = put("low", dict(u1=rows(np.concatenate([a(p + "U1")] * 2, 1)), v1=v1, b1=col(a(p + "b1")), u2=rows(a(p + "U2")),
                               v2=a(p + "V2"), b2=all_rows(a(p + "b2"))))
    return w


def kernel(**inputs):
    import numpy as np
    import concourse.bacc as bacc
    from concourse.bass_utils import run_bass_kernel_spmd

    w = pack(inputs)
    arrays = {"w_" + k: v for k, v in w.items()}
    arrays["x"] = np.ascontiguousarray(inputs["x"])
    arrays["ctx"] = np.ascontiguousarray(inputs["ctx_1024"])
    arrays["ctxT"] = np.ascontiguousarray(np.asarray(inputs["ctx_1024"]).reshape(B * S, D).T)
    arrays["mask"] = np.ascontiguousarray(inputs["mask_BxSxS2_ff0"])
    p = np.arange(P, dtype=np.float32)
    arrays["consts"] = np.concatenate([
        (p[:, None] < p[None, :]).astype(np.float32),
        p[:, None] + P * np.arange(B, dtype=np.float32)[None, :],
        np.broadcast_to(NE * CAP - CAP * np.arange(NE, dtype=np.float32), (P, NE)),
        (TOPK * (p[:, None, None] + P * np.arange(B)[None, :, None]) + np.arange(TOPK)[None, None, :]).reshape(P, -1).astype(np.float32),
        (p[:, None] > p[None, :]).astype(np.float32),
    ], 1)
    slots = np.arange(NE * CAP + B * S * TOPK)
    arrays["table0"] = np.stack([B * S + slots % P, 0 * slots], 1).astype(np.float32)
    nc = bacc.Bacc("TRN2", target_bir_lowering=False, num_devices=1)
    ins = {k: nc.dram_tensor(f"in_{k}", v.shape, mybir.dt.from_np(v.dtype), kind="ExternalInput").ap() for k, v in arrays.items()}
    out = nc.dram_tensor("out_x", (B, S, D), F32, kind="ExternalOutput").ap()
    build(nc, ins, out)
    r = run_bass_kernel_spmd(nc, [{f"in_{k}": v for k, v in arrays.items()}], core_ids=[0])
    return r.results[0]["out_x"]
```

```python
from contextlib import ExitStack

import concourse.bass as bass
from concourse import mybir

ALU = mybir.AluOpType
ACT = mybir.ActivationFunctionType
AX = mybir.AxisListType
F32 = mybir.dt.float32
BF16 = mybir.dt.bfloat16
I32 = mybir.dt.int32
U32 = mybir.dt.uint32

P = 128
B, S, D = 16, 128, 256
KD = D // P
BC = 2
TOK = BC * S
NCH = B // BC
H, HD = 16, 64
HM = H * HD // P
FAN = 4
NE0, EH0, MD = 8, 256, 64
HID0 = 512
NE, CAP, FE = 64, 128, 192
TOPK = 8
HL, DL = 4, 64
INNER = 1024
EPS = 1e-5
LEAD = 512

LAYOUT = {
    "attn": [("wk", KD * 1024), ("wv", KD * 1024), ("wq", KD * 1024), ("bk", HM), ("bq", HM), ("bv", HM),
             ("wu", HM * D), ("bu", D)],
    "spike": [("enc", KD * HID0), ("enc_b", 4), ("s2c", 4 * P), ("s2c_b", 1), ("rw1", 64), ("rb1", 1),
              ("rw2", NE0), ("rb2", NE0), ("ew1", NE0 * P), ("eb1", NE0 * 2), ("ew2", NE0 * 2 * MD),
              ("eb2", NE0 * MD), ("c2s", HID0), ("c2s_b", 4), ("dec", 4 * D), ("dec_b", D), ("ln_g", D),
              ("ln_b", D)],
    "rec": [("wi", KD * D), ("bi", KD), ("wg", KD * D), ("bg", KD), ("a", KD * D), ("bm", KD * D),
            ("wo", KD * D), ("bo", D), ("decay", KD)],
    "moe": [("router", KD * NE), ("sgu", KD * 2 * FE), ("sdown", 2 * D)],
    "mlstm": [("gq", KD * 2 * HL), ("gk", KD * 2 * HL), ("gv", KD * 2 * HL), ("gb", 2 * HL), ("lnw", D)],
    "bit": [("wg", KD * INNER), ("wu", KD * INNER), ("wd", INNER // P * D)],
    "mqa": [("wq", KD * 1024), ("wk", KD * P), ("wv", KD * P), ("wout", HM * D), ("w1", KD * 2 * INNER),
            ("w2", INNER // P * D), ("ln_g", KD), ("ln_b", KD), ("cln_g", KD), ("cln_b", KD)],
    "low": [("u1", KD * P), ("v1", INNER // 2), ("b1", INNER // P), ("u2", INNER // P * 64), ("v2", D), ("b2", D)],
}
CONSTS = [("tri", P), ("tokens", B), ("slot_base", NE), ("spare", B * TOPK), ("late", P)]
COLS = {stage: sum(n for _, n in parts) for stage, parts in LAYOUT.items()}


class Steps:

    def __init__(self, sem):
        self.sem, self.end, self.table, self.next = sem, LEAD, {}, 0

    def plan(self, stage, names, iterations):
        self.table[stage] = (self.end, {n: k for k, n in enumerate(names)}, len(names))
        assert len(set(names)) == len(names)
        self.end += len(names) * iterations
        self.table[stage, "end"] = self.end

    def at(self, stage, i, name, back=0):
        start, index, n = self.table[stage]
        return i * n + (start + index[name] + 1 - back * n)

    def one(self, stage, name):
        index = self.table[stage][1]
        assert index[name] == self.next % len(index), (stage, name, self.next % len(index))
        self.next = (self.next + 1) % len(index)
        return 1

    def all(self, stage):
        return self.table[stage, "end"]
SPACE = 22528


def build(nc, ins, out):
    ctx = ExitStack()
    with ctx:
        block_program(nc, ins, out, ctx)


def block_program(nc, ins, out, ctx):
    def sb(name, shape, dt=F32):
        return ctx.enter_context(nc.sbuf_tensor(name, shape, dt))

    def sem(name):
        return ctx.enter_context(nc.semaphore(name))

    ctxT_dram = ins["ctxT"].rearrange("(k p) t -> p k t", p=P)
    mask_dram = ins["mask"].rearrange("b q k -> q b k")
    x_dram = ins["x"].rearrange("b s d -> s b d")
    ctx_dram = ins["ctx"].rearrange("b s d -> s b d")
    out_dram = out.rearrange("b s d -> s b d")

    x = sb("x", [P, B, D])
    nmr = sb("nmr", [P, B])
    rstd = sb("rstd", [P, B])
    xn = [sb(f"xn{n}", [P, BC, D]) for n in range(2)]
    xnT = [sb(f"xnT{n}", [P, KD, TOK]) for n in range(2)]
    ctxT = [sb(f"ctxT{n}", [P, KD, TOK]) for n in range(2)]
    ident = sb("ident", [P, P])
    ones = sb("ones", [P, P])
    mhalf = sb("mhalf", [P, BC])
    iota8 = sb("iota8", [P, NE0])
    zrow = sb("zrow", [P, D])
    bnst = [sb(f"bnst{n}", [P, BC, 6]) for n in range(2)]
    mv = [sb(f"mv{n}", [P, BC, 2]) for n in range(2)]
    veps = [sb(f"veps{n}", [P, BC]) for n in range(2)]
    w_place = {0: sb("w_even", [P, max(COLS[s] for s in ("attn", "rec", "mqa"))]),
               1: sb("w_odd", [P, max(COLS[s] for s in ("spike", "moe", "bit"))])}
    WPLACE = {"attn": (0, 0), "spike": (1, 0), "rec": (0, 0), "moe": (0, COLS["rec"]), "mlstm": (0, COLS["rec"] + COLS["moe"]),
              "bit": (1, 0), "mqa": (0, 0), "low": (1, 0)}
    space = sb("space", [P, SPACE])
    shape_consts = sb("shape_consts", [P, sum(n for _, n in CONSTS)])

    def C(name):
        at = sum(n for k, (m, n) in enumerate(CONSTS) if k < [m for m, _ in CONSTS].index(name))
        return shape_consts[:, at:at + dict(CONSTS)[name]]
    bank = [ctx.enter_context(nc.psum_tensor(f"bank{n}", [P, 512], F32)) for n in range(8)]

    def area(name, shape, at, dt=F32):
        n = 1
        for s in shape[1:]:
            n *= s
        words = n if dt == F32 else (n + 1) // 2
        assert at + words <= SPACE, (name, at + words)
        ap = space[0:shape[0], at:at + words]
        if dt != F32:
            ap = ap.bitcast(dt)
        if len(shape) == 3:
            ap = ap.rearrange("p (a b) -> p a b", a=shape[1])
        if len(shape) == 4:
            ap = ap.rearrange("p (a b c) -> p a b c", a=shape[1], b=shape[2])
        return ap

    def weight_reader(stage_name):
        place, first = WPLACE[stage_name]
        offsets, at = {}, first
        for n, c in LAYOUT[stage_name]:
            offsets[n] = (at, c)
            at += c
        return lambda n: w_place[place][:, offsets[n][0]:offsets[n][0] + offsets[n][1]]

    weights = {s: weight_reader(s) for s in LAYOUT}

    pe_s, act_s, dve_s, pool_s = (Steps(sem(n)) for n in ("tensor_steps", "scalar_steps", "vector_steps", "gpsimd_steps"))
    consts = sem("consts_written")
    x_loaded = sem("x_loaded")
    w_loaded = {s: sem(f"weights_{s}_loaded") for s in LAYOUT}
    ctxT_loaded = sem("ctxT_chunk_loaded")
    ctxT2_loaded = [sem(f"ctxT_chunk_loaded_for_rec_{n}") for n in range(2)]
    ctxT3_loaded = [sem(f"ctxT_chunk_loaded_for_mlstm_{n}") for n in range(2)]
    ctx_loaded = [sem(f"ctx_chunk_loaded_for_mlstm_{n}") for n in range(2)]
    ctx4_loaded, mask_loaded = sem("ctx_chunk_loaded_for_mqa"), sem("mask_chunk_loaded")
    consts_loaded = sem("shape_constants_loaded")
    zeroed = sem("zero_rows_written")
    gidx_set, sidx_set = sem("gather_rows_set"), sem("scatter_rows_set")
    bit_q = sem("weight_quantiser_steps")
    held = sem("waits_held_apart")
    bq8_ready = sem("bq8_ready")
    out_stored = sem("out_stored")

    def stage(name, iterations, pe, act, dve, pool):
        for s, names in ((pe_s, pe), (act_s, act), (dve_s, dve), (pool_s, pool)):
            s.plan(name, names, iterations)

    def others_done(eng, stage_name):
        for s in (pe_s, act_s, dve_s, pool_s):
            eng.wait_ge(s.sem, s.all(stage_name))

    def load_weights(eng, stage_name):
        place, first = WPLACE[stage_name]
        eng.dma_start(w_place[place][:, first:first + COLS[stage_name]], ins["w_" + stage_name]).then_inc(w_loaded[stage_name], 16)

    def after(st, i, lane=""):
        return tuple(lambda name, back=0, s=s: (s.sem, s.at(st, i, f"{name}{lane}", back)) for s in (pe_s, act_s, dve_s, pool_s))

    def signals(steps, st, lane=""):
        return lambda name: (steps.sem, steps.one(st, f"{name}{lane}"))

    def both(names):
        parts = [n if isinstance(n, tuple) else (n,) for n in names]
        return [f"{name}{lane}" for part in parts for lane in "AB" for name in part]

    def in_turns(body):
        lanes = [body(0), body(1)]
        while lanes:
            lanes = [b for b in lanes if next(b, "end") != "end"]

    def wide(ap, n):
        return ap.unsqueeze(2).to_broadcast([ap.shape[0], ap.shape[1], n])

    def over(ap, n):
        return ap.unsqueeze(1).to_broadcast([ap.shape[0], n, ap.shape[1]])

    LN_DVE = ["bn0", "bn1", "ag0", "ag1", "veps", "nmr"]
    stage("load", NCH, pe=[], act=[], dve=LN_DVE, pool=["rstd"])

    def place(i, lane):
        return (i, 0, "") if lane is None else (2 * i + lane, lane, "AB"[lane])

    def stats(st, i, lane=None):
        c, n, end = place(i, lane)
        PE, ACTS, DVE, POOL = after(st, i, end)
        done = signals(dve_s, st, end)
        if st != "load":
            nc.vector.wait_ge(*DVE("res1" if st == "bit" else "res"))
            nc.vector.sem_inc(held, 1)
        for b in range(BC):
            nc.vector.bn_stats(bnst[n][:, b, :], x[:, bass.ds(c * BC + b, 1), :]).then_inc(*done(f"bn{b}"))
            yield
        for b in range(BC):
            nc.vector.wait_ge(*DVE(f"bn{b}"))
            nc.vector.sem_inc(held, 1)
            nc.vector.bn_aggr(mv[n][:, b, :], bnst[n][:, b, :]).then_inc(*done(f"ag{b}"))
            yield
        nc.vector.wait_ge(*DVE("ag1"))
        nc.vector.tensor_scalar(veps[n][:], mv[n][:, :, 1], EPS, None, ALU.add).then_inc(*done("veps"))
        yield
        nc.vector.wait_ge(*POOL("rstd"))
        nc.vector.scalar_tensor_tensor(nmr[:, bass.ds(c * BC, BC)], mv[n][:, :, 0], -1.0, rstd[:, bass.ds(c * BC, BC)],
                                       ALU.mult, ALU.mult).then_inc(*done("nmr"))
        yield

    def stats_root(st, i, lane=None):
        c, n, end = place(i, lane)
        PE, ACTS, DVE, POOL = after(st, i, end)
        nc.gpsimd.wait_ge(*DVE("veps"))
        nc.gpsimd.tensor_tensor(rstd[:, bass.ds(c * BC, BC)], veps[n][:], mhalf[:], ALU.pow).then_inc(*signals(pool_s, st, end)("rstd"))
        yield

    def prep(st, i, lane=None):
        c, n, end = place(i, lane)
        done = signals(act_s, st, end)
        for b in range(BC):
            nc.scalar.activation(xn[n][:, b, :], x[:, bass.ds(c * BC + b, 1), :], ACT.Identity,
                                 bias=nmr[:, bass.ds(c * BC + b, 1)], scale=rstd[:, bass.ds(c * BC + b, 1)]).then_inc(*done(f"prep{b}"))
            yield

    def turn_x(st, i, lane=None, dst=None):
        c, n, end = place(i, lane)
        PE, ACTS, DVE, POOL = after(st, i, end)
        dst = bank[7] if dst is None else dst
        nc.tensor.wait_ge(*ACTS("prep1"))
        for k in range(KD):
            for b in range(BC):
                last = nc.tensor.transpose(dst[:, (k * BC + b) * P:(k * BC + b + 1) * P], xn[n][:, b, k * P:(k + 1) * P], ident[:])
        last.then_inc(*signals(pe_s, st, end)("xT"))
        yield

    def copy_xT(st, i, lane=None, src=None):
        c, n, end = place(i, lane)
        src = bank[7] if src is None else src
        nc.vector.wait_ge(pe_s.sem, pe_s.at(st, i, f"xT{end}"))
        nc.vector.tensor_copy(xnT[n][:].rearrange("p k t -> p (k t)"), src[:]).then_inc(*signals(dve_s, st, end)("xT"))
        yield

    def alone(steps):
        for _ in steps:
            pass

    def load_dve():
        nc.vector.sem_inc(dve_s.sem, LEAD)
        nc.vector.wait_ge(x_loaded, 16)
        with nc.vector.Fori(0, NCH) as i:
            alone(stats("load", i))

    def load_pool():
        nc.gpsimd.sem_inc(pool_s.sem, LEAD)
        nc.gpsimd.memset(ident[:], 0.0).then_inc(consts, 1)
        nc.gpsimd.memset(mhalf[:], -0.5).then_inc(consts, 1)
        nc.gpsimd.memset(ones[:], 1.0).then_inc(consts, 1)
        nc.gpsimd.memset(zrow[:], 0.0).then_inc(zeroed, 1)
        nc.gpsimd.wait_ge(consts, 3)
        nc.gpsimd.affine_select(out=ident[:], in_=ident[:], compare_op=ALU.not_equal, fill=1.0, base=0,
                                pattern=[[-1, P]], channel_multiplier=1).then_inc(consts, 1)
        with nc.gpsimd.Fori(0, NCH) as i:
            alone(stats_root("load", i))

    GROUPS = ["k0", "k1", "v00", "v01", "k2", "k3", "v10", "v11", "q0", "q1", "q2", "q3"]
    UNITS = 2 * HM // FAN * BC
    AW = weights["attn"]
    wk, wv, wq = (AW(n).rearrange("p (k m) -> p k m", k=KD) for n in ("wk", "wv", "wq"))
    wu = AW("wu").rearrange("p (k n) -> p k n", k=HM)
    qT, kT, mT = (area(n, [P, HM, TOK], at) for n, at in (("qT", 0), ("kT", 2048), ("mT", 4096)))
    v = area("v", [P, BC, H * HD], 6144)
    prob = area("prob", [P, 4, FAN, P], 8192)
    probT = area("probT", [P, 2, FAN, P], 10240)
    sm = area("sm", [P, 3, 4, FAN], 11264)
    bq8 = area("bq8", [P, HM], 11328)
    ORDER = []
    for t in range(UNITS + 3):
        ORDER += [("S", t)] * (t < UNITS) + [("T", t - 2)] * (0 <= t - 2 < UNITS) + [("PV", t - 3)] * (0 <= t - 3 < UNITS)

    def unit(t):
        return t // 4, t % 4 // 2, t % 2

    DORDER = []
    for t in range(UNITS + 3):
        DORDER += [("max", t)] * (t < UNITS) + [("rec", t - 1)] * (0 <= t - 1 < UNITS)
        DORDER += [("copy", t - 2)] * (0 <= t - 2 < UNITS) + [("o", t - 3)] * (0 <= t - 3 < UNITS and t % 2 == 0)
    stage("attn", NCH,
          pe=GROUPS[:8] + ["xT"] + GROUPS[8:] + [f"{a}{t}" for a, t in ORDER] + ["out0", "out1"],
          act=["prep0", "prep1", "v00", "v01", "v10", "v11"] + [f"exp{t}" for t in range(UNITS)],
          dve=["k0", "k1", "k2", "k3", "xT", "q0", "q1", "q2", "q3"] + [f"{a}{t}" for a, t in DORDER] + ["res"] + LN_DVE,
          pool=["bu"] + [f"norm{t}" for t in range(UNITS)] + ["rstd"])

    def attn_sp():
        sp = nc.sync
        with sp.Fori(0, NCH) as i:
            sp.wait_ge(pe_s.sem, pe_s.at("attn", i, "v11", back=1))
            sp.dma_start(ctxT[0][:], ctxT_dram[:, :, bass.ds(i * TOK, TOK)]).then_inc(ctxT_loaded, 16)

    def attn_pe():
        pe, st = nc.tensor, "attn"
        pe.sem_inc(pe_s.sem, LEAD)
        pe.wait_ge(consts, 4)
        pe.wait_ge(w_loaded["attn"], 16)
        with pe.Fori(0, NCH) as i:
            pe.wait_ge(ctxT_loaded, i * 16 + 16)
            for n, g in enumerate(GROUPS):
                if g == "q0":
                    alone(turn_x(st, i))
                    pe.wait_ge(dve_s.sem, dve_s.at(st, i, "xT"))
                if n >= 6:
                    user = GROUPS[n - 6]
                    who = act_s if user[0] == "v" else dve_s
                    pe.wait_ge(who.sem, who.at(st, i, user))
                dst = bank[n % 6]
                if g[0] == "v":
                    b, half = int(g[1]), int(g[2])
                    for k in range(KD):
                        last = nc.tensor.matmul(dst[:], ctxT[0][:, k, b * P:(b + 1) * P], wv[:, k, half * 512:(half + 1) * 512],
                                                start=k == 0, stop=k == KD - 1)
                else:
                    w, src = (wk, ctxT[0]) if g[0] == "k" else (wq, xnT[0])
                    for m in range(2):
                        mm = 2 * int(g[1]) + m
                        for k in range(KD):
                            last = nc.tensor.matmul(dst[:, m * TOK:(m + 1) * TOK], w[:, k, mm * P:(mm + 1) * P], src[:, k, :],
                                                    start=k == 0, stop=k == KD - 1)
                last.then_inc(pe_s.sem, pe_s.one(st, g))
            pe.wait_ge(dve_s.sem, dve_s.at(st, i, "q3"))
            pe.wait_ge(act_s.sem, act_s.at(st, i, "v11"))
            for what, t in ORDER:
                b, u, par = unit(t)
                rows = slice(HD * par, HD * par + HD)
                if what == "S":
                    if t >= 2:
                        pe.wait_ge(act_s.sem, act_s.at(st, i, f"exp{t - 2}"))
                    for j in range(FAN):
                        m = FAN * u + j
                        last = nc.tensor.matmul(bank[t % 2][:, j * P:(j + 1) * P], qT[rows, m, b * P:(b + 1) * P],
                                                kT[rows, m, b * P:(b + 1) * P], start=True, stop=True)
                elif what == "T":
                    pe.wait_ge(pool_s.sem, pool_s.at(st, i, f"norm{t}"))
                    if t >= 2:
                        pe.wait_ge(dve_s.sem, dve_s.at(st, i, f"copy{t - 2}"))
                    for j in range(FAN):
                        last = nc.tensor.transpose(bank[2 + t % 2][:, j * P:(j + 1) * P], prob[:, t % 4, j, :], ident[:])
                else:
                    pe.wait_ge(dve_s.sem, dve_s.at(st, i, f"copy{t}"))
                    if b == 1 and par == 0:
                        pe.wait_ge(dve_s.sem, dve_s.at(st, i, f"o{t - 3}"))
                    for j in range(FAN):
                        h = 2 * (FAN * u + j) + par
                        last = nc.tensor.matmul(bank[4 + u][rows, j * P:(j + 1) * P], v[:, b, h * HD:(h + 1) * HD],
                                                probT[:, t % 2, j, :], start=True, stop=True)
                last.then_inc(pe_s.sem, pe_s.one(st, f"{what}{t}"))
            pe.wait_ge(dve_s.sem, dve_s.at(st, i, "res", back=1))
            for b in range(BC):
                pe.wait_ge(dve_s.sem, dve_s.at(st, i, f"o{4 * b + 3}"))
                for k in range(HM):
                    last = nc.tensor.matmul(bank[6][:, b * D:(b + 1) * D], mT[:, k, b * P:(b + 1) * P], wu[:, k, :],
                                            start=k == 0, stop=k == HM - 1)
                last.then_inc(pe_s.sem, pe_s.one(st, f"out{b}"))

    def attn_act():
        act, st = nc.scalar, "attn"
        act.sem_inc(act_s.sem, LEAD)
        act.wait_ge(dve_s.sem, dve_s.all("load"))
        with act.Fori(0, NCH) as i:
            alone(prep(st, i))
            for b in range(BC):
                for half in range(2):
                    act.wait_ge(pe_s.sem, pe_s.at(st, i, f"v{b}{half}"))
                    nc.scalar.copy(v[:, b, half * 512:(half + 1) * 512], bank[GROUPS.index(f"v{b}{half}") % 6][:]).then_inc(
                        act_s.sem, act_s.one(st, f"v{b}{half}"))
            for t in range(UNITS):
                act.wait_ge(dve_s.sem, dve_s.at(st, i, f"max{t}"))
                if t >= 4:
                    act.wait_ge(pe_s.sem, pe_s.at(st, i, f"T{t - 4}"))
                for j in range(FAN):
                    last = nc.scalar.activation(prob[:, t % 4, j, :], bank[t % 2][:, j * P:(j + 1) * P], ACT.Exp,
                                                bias=sm[:, 0, t % 4, j:j + 1], accum_out=sm[:, 1, t % 4, j:j + 1])
                last.then_inc(act_s.sem, act_s.one(st, f"exp{t}"))

    def attn_pool():
        pool, st = nc.gpsimd, "attn"
        pool.wait_ge(w_loaded["attn"], 16)
        with pool.Fori(0, NCH) as i:
            pool.wait_ge(act_s.sem, act_s.at(st, i, "prep1"))
            nc.gpsimd.tensor_tensor(x[:, bass.ds(i * BC, BC), :], x[:, bass.ds(i * BC, BC), :],
                                    AW("bu").unsqueeze(1).to_broadcast([P, BC, D]), ALU.add).then_inc(pool_s.sem, pool_s.one(st, "bu"))
            for t in range(UNITS):
                pool.wait_ge(dve_s.sem, dve_s.at(st, i, f"rec{t}"))
                nc.gpsimd.tensor_tensor(prob[:, t % 4], prob[:, t % 4], sm[:, 2, t % 4, :].unsqueeze(2).to_broadcast([P, FAN, P]),
                                        ALU.mult).then_inc(pool_s.sem, pool_s.one(st, f"norm{t}"))
            alone(stats_root(st, i))

    def attn_dve():
        dve, st = nc.vector, "attn"
        dve.wait_ge(w_loaded["attn"], 16)
        nc.vector.tensor_scalar(bq8[:], AW("bq"), HD ** -0.5, None, ALU.mult).then_inc(bq8_ready, 1)
        dve.wait_ge(bq8_ready, 1)
        with dve.Fori(0, NCH) as i:
            for n in range(4):
                g = f"k{n}"
                dve.wait_ge(pe_s.sem, pe_s.at(st, i, g))
                nc.vector.tensor_tensor(kT[:, 2 * n:2 * n + 2, :], bank[GROUPS.index(g) % 6][:].rearrange("p (m t) -> p m t", m=2),
                                        AW("bk")[:, 2 * n:2 * n + 2].unsqueeze(2).to_broadcast([P, 2, TOK]), ALU.add).then_inc(
                    dve_s.sem, dve_s.one(st, g))
            alone(copy_xT(st, i))
            for n in range(4):
                g = f"q{n}"
                dve.wait_ge(pe_s.sem, pe_s.at(st, i, g))
                nc.vector.scalar_tensor_tensor(qT[:, 2 * n:2 * n + 2, :], bank[GROUPS.index(g) % 6][:].rearrange("p (m t) -> p m t", m=2),
                                               HD ** -0.5, bq8[:, 2 * n:2 * n + 2].unsqueeze(2).to_broadcast([P, 2, TOK]),
                                               ALU.mult, ALU.add).then_inc(dve_s.sem, dve_s.one(st, g))
            for what, t in DORDER:
                b, u, par = unit(t)
                if what == "max":
                    dve.wait_ge(pe_s.sem, pe_s.at(st, i, f"S{t}"))
                    ins = nc.vector.tensor_reduce(sm[:, 0, t % 4, :], bank[t % 2][:].rearrange("p (j s) -> p j s", j=FAN),
                                                  AX.X, ALU.max, negate=True)
                elif what == "rec":
                    dve.wait_ge(act_s.sem, act_s.at(st, i, f"exp{t}"))
                    ins = nc.vector.reciprocal(sm[:, 2, t % 4, :], sm[:, 1, t % 4, :])
                elif what == "copy":
                    dve.wait_ge(pe_s.sem, pe_s.at(st, i, f"T{t}"))
                    ins = nc.vector.tensor_copy(probT[:, t % 2].rearrange("p j s -> p (j s)"), bank[2 + t % 2][:])
                else:
                    dve.wait_ge(pe_s.sem, pe_s.at(st, i, f"PV{t}"))
                    ins = nc.vector.tensor_tensor(mT[:, FAN * u:FAN * u + FAN, b * P:(b + 1) * P],
                                                  bank[4 + u][:].rearrange("p (j s) -> p j s", j=FAN),
                                                  AW("bv")[:, FAN * u:FAN * u + FAN].unsqueeze(2).to_broadcast([P, FAN, P]), ALU.add)
                ins.then_inc(dve_s.sem, dve_s.one(st, f"{what}{t}"))
            dve.wait_ge(pe_s.sem, pe_s.at(st, i, "out1"))
            dve.wait_ge(pool_s.sem, pool_s.at(st, i, "bu"))
            nc.vector.tensor_tensor(x[:, bass.ds(i * BC, BC), :], bank[6][:].rearrange("p (b d) -> p b d", b=BC),
                                    x[:, bass.ds(i * BC, BC), :], ALU.add).then_inc(dve_s.sem, dve_s.one(st, "res"))
            alone(stats(st, i))


    SW = weights["spike"]
    enc = SW("enc").rearrange("p (k m) -> p k m", k=KD)
    s2c = SW("s2c").rearrange("p (k m) -> p k m", k=4)
    ew1 = SW("ew1").rearrange("p (e m) -> p e m", e=NE0)
    ew2 = SW("ew2").rearrange("p (e m) -> p e m", e=NE0 * 2)
    dec_w = SW("dec").rearrange("p (k m) -> p k m", k=4)
    SPIKE_LANE = 9238
    spT = [area(f"spT{n}", [P, 4, TOK], 0 + n * SPIKE_LANE) for n in range(2)]
    contT = [area(f"contT{n}", [P, TOK], 1024 + n * SPIKE_LANE) for n in range(2)]
    rhT = [area(f"rhT{n}", [64, TOK], 1280 + n * SPIKE_LANE) for n in range(2)]
    ehT = [area(f"ehT{n}", [P, NE0 * 2, TOK], 1536 + n * SPIKE_LANE) for n in range(2)]
    lg0 = [area(f"lg0{n}", [P, BC, NE0], 5632 + n * SPIKE_LANE) for n in range(2)]
    mx0 = [area(f"mx0{n}", [P, BC, 8], 5648 + n * SPIKE_LANE) for n in range(2)]
    ix0 = [area(f"ix0{n}", [P, BC, 8], 5664 + n * SPIKE_LANE) for n in range(2)]
    ixf0 = [area(f"ixf0{n}", [P, BC, 8], 5680 + n * SPIKE_LANE) for n in range(2)]
    gap0 = [area(f"gap0{n}", [P, BC], 5696 + n * SPIKE_LANE) for n in range(2)]
    w0 = [area(f"w0{n}", [P, 2, BC], 5698 + n * SPIKE_LANE) for n in range(2)]
    pick0 = [area(f"pick0{n}", [P, 2, BC, NE0], 5704 + n * SPIKE_LANE) for n in range(2)]
    comb0 = [area(f"comb0{n}", [P, BC, NE0], 5736 + n * SPIKE_LANE) for n in range(2)]
    eo = [area(f"eo{n}", [P, BC, NE0 * MD], 5760 + n * SPIKE_LANE) for n in range(2)]
    moe0 = [area(f"moe0{n}", [P, BC, MD], 6784 + n * SPIKE_LANE) for n in range(2)]
    moe0T = [area(f"moe0T{n}", [64, TOK], 6912 + n * SPIKE_LANE) for n in range(2)]
    rT = [area(f"rT{n}", [P, 4, TOK], 7168 + n * SPIKE_LANE) for n in range(2)]
    dec = [area(f"dec{n}", [P, BC, D], 8192 + n * SPIKE_LANE) for n in range(2)]
    decn = [area(f"decn{n}", [P, BC, D], 8704 + n * SPIKE_LANE) for n in range(2)]
    dveps = [area(f"dveps{n}", [P, BC], 9218 + n * SPIKE_LANE) for n in range(2)]
    drstd = [area(f"drstd{n}", [P, BC], 9220 + n * SPIKE_LANE) for n in range(2)]
    dbn = [area(f"dbn{n}", [P, BC, 6], 9222 + n * SPIKE_LANE) for n in range(2)]
    dmv = [area(f"dmv{n}", [P, BC, 2], 9234 + n * SPIKE_LANE) for n in range(2)]
    EP = NE0 // 2
    stage("spike", NCH // 2,
          pe=both(["xT", "e0", "e1", "s2c", "rh", "lg"] + [(f"h{n}0", f"h{n}1") for n in range(EP)]
          + ["eo0", "eo1", "mT", "c0", "c1", "dec"]),
          act=both(["prep0", "prep1", "e0", "e1", "rh", "w"] + [f"h{n}" for n in range(EP)] + ["c0", "c1", "dec"]),
          dve=both(["xT", "s2c", "lg", "mx0", "mx1", "ix0", "ix1", "ixf", "gap", "h0"]
          + ["p00", "p01", "p10", "p11", "comb"] + ["h1", "h2", "h3"]
          + ["a0", "m0", "r0", "a1", "m1", "r1", "mT", "dadd", "dbn0", "dbn1", "dag0", "dag1", "dveps", "dn0", "dn1", "res"] + LN_DVE),
          pool=both(["drstd", "g", "b", "rstd"]))

    def pair_bank(n, half):
        return (1 + half, 3 * (1 - half))[n % 2]

    def spike_pe():
        pe, st = nc.tensor, "spike"
        others_done(pe, "attn")
        pe.wait_ge(w_loaded[st], 16)
        with pe.Fori(0, NCH // 2) as i:
            def chunk(lane):
                bk = bank[4 * lane:4 * lane + 4]
                PE, ACTS, DVE, POOL = after(st, i, "AB"[lane])
                done = signals(pe_s, st, "AB"[lane])
                yield from turn_x(st, i, lane, bk[0])
                pe.wait_ge(*DVE("xT"))
                for n in range(2):
                    for m in range(2):
                        for k in range(KD):
                            last = nc.tensor.matmul(bk[1 + n][:, m * TOK:(m + 1) * TOK], enc[:, k, (2 * n + m) * P:(2 * n + m + 1) * P],
                                                    xnT[lane][:, k, :], start=k == 0, stop=k == KD - 1)
                    last.then_inc(*done(f"e{n}"))
                    yield
                pe.wait_ge(*ACTS("e1"))
                for k in range(4):
                    last = nc.tensor.matmul(bk[3][:, 0:TOK], s2c[:, k, :], spT[lane][:, k, :], start=k == 0, stop=k == 3)
                last.then_inc(*done("s2c"))
                yield
                pe.wait_ge(*DVE("s2c"))
                pe.sem_inc(held, 1)
                nc.tensor.matmul(bk[0][0:64, 0:TOK], SW("rw1")[0:64], contT[lane][0:64], start=True, stop=True).then_inc(*done("rh"))
                yield
                pe.wait_ge(*ACTS("rh"))
                for b in range(BC):
                    last = nc.tensor.matmul(bk[0][:, b * NE0:(b + 1) * NE0], rhT[lane][:, b * P:(b + 1) * P], SW("rw2")[0:64],
                                            start=True, stop=True)
                last.then_inc(*done("lg"))
                yield
                pe.wait_ge(*DVE("lg"))
                for n in range(EP):
                    if n >= 2:
                        pe.wait_ge(*ACTS(f"h{n - 2}"))
                        pe.wait_ge(*DVE(f"h{n - 2}"))
                    for half in range(2):
                        rows = slice(64 * half, 64 * half + 64)
                        for e in range(2):
                            last = nc.tensor.matmul(bk[pair_bank(n, half)][:, e * TOK:(e + 1) * TOK], ew1[rows, 2 * n + e, :],
                                                    contT[lane][rows, :], start=True, stop=True)
                        last.then_inc(*done(f"h{n}{half}"))
                    yield
                pe.wait_ge(*ACTS(f"h{EP - 1}"))
                pe.wait_ge(*DVE(f"h{EP - 1}"))
                for b in range(BC):
                    for e in range(NE0):
                        for half in range(2):
                            last = nc.tensor.matmul(bk[1 + b][:, e * MD:(e + 1) * MD], ehT[lane][:, 2 * e + half, b * P:(b + 1) * P],
                                                    ew2[:, 2 * e + half, :], start=half == 0, stop=half == 1)
                    last.then_inc(*done(f"eo{b}"))
                    yield
                pe.wait_ge(*DVE("r1"))
                pe.sem_inc(held, 1)
                for b in range(BC):
                    last = nc.tensor.transpose(bk[3][0:64, b * P:(b + 1) * P], moe0[lane][:, b, :], ident[:])
                last.then_inc(*done("mT"))
                yield
                pe.wait_ge(*DVE("mT"))
                for n in range(2):
                    for m in range(2):
                        last = nc.tensor.matmul(bk[3 * n][:, m * TOK:(m + 1) * TOK], SW("c2s")[0:64, (2 * n + m) * P:(2 * n + m + 1) * P],
                                                moe0T[lane][:], start=True, stop=True)
                    last.then_inc(*done(f"c{n}"))
                    yield
                pe.wait_ge(*ACTS("c1"))
                for b in range(BC):
                    for k in range(4):
                        last = nc.tensor.matmul(bk[1][:, b * D:(b + 1) * D], rT[lane][:, k, b * P:(b + 1) * P], dec_w[:, k, :],
                                                start=k == 0, stop=k == 3)
                last.then_inc(*done("dec"))
                yield

            in_turns(chunk)

    def spike_act():
        act, st = nc.scalar, "spike"
        others_done(act, "attn")
        act.wait_ge(w_loaded[st], 16)
        with act.Fori(0, NCH // 2) as i:
            def chunk(lane):
                bk = bank[4 * lane:4 * lane + 4]
                PE, ACTS, DVE, POOL = after(st, i, "AB"[lane])
                done = signals(act_s, st, "AB"[lane])
                yield from prep(st, i, lane)
                for n in range(2):
                    act.wait_ge(*PE(f"e{n}"))
                    for m in range(2):
                        last = nc.scalar.activation(spT[lane][:, 2 * n + m, :], bk[1 + n][:, m * TOK:(m + 1) * TOK], ACT.Sigmoid,
                                                    bias=SW("enc_b")[:, 2 * n + m:2 * n + m + 1])
                    last.then_inc(*done(f"e{n}"))
                    yield
                act.wait_ge(*PE("rh"))
                nc.scalar.activation(rhT[lane][:], bk[0][0:64, 0:TOK], ACT.Relu, bias=SW("rb1")[0:64]).then_inc(*done("rh"))
                yield
                act.wait_ge(*DVE("gap"))
                nc.scalar.activation(w0[lane][:, 0, :], gap0[lane][:], ACT.Sigmoid, scale=-1.0)
                nc.scalar.activation(w0[lane][:, 1, :], gap0[lane][:], ACT.Sigmoid).then_inc(*done("w"))
                yield
                for n in range(EP):
                    act.wait_ge(*PE(f"h{n}0"))
                    for e in range(2):
                        last = nc.scalar.activation(ehT[lane][:, 2 * (2 * n + e), :], bk[pair_bank(n, 0)][:, e * TOK:(e + 1) * TOK], ACT.Relu,
                                                    bias=SW("eb1")[:, 2 * (2 * n + e):2 * (2 * n + e) + 1])
                    last.then_inc(*done(f"h{n}"))
                    yield
                for n in range(2):
                    act.wait_ge(*PE(f"c{n}"))
                    for m in range(2):
                        last = nc.scalar.activation(rT[lane][:, 2 * n + m, :], bk[3 * n][:, m * TOK:(m + 1) * TOK], ACT.Sigmoid,
                                                    bias=SW("c2s_b")[:, 2 * n + m:2 * n + m + 1])
                    last.then_inc(*done(f"c{n}"))
                    yield
                act.wait_ge(*DVE("dadd"))
                nc.scalar.activation(dec[lane][:], dec[lane][:], ACT.Sigmoid).then_inc(*done("dec"))
                yield

            in_turns(chunk)

    def spike_pool():
        pool, st = nc.gpsimd, "spike"
        others_done(pool, "attn")
        pool.wait_ge(w_loaded[st], 16)
        for e in range(NE0):
            last = nc.gpsimd.memset(iota8[:, e:e + 1], float(e))
        last.then_inc(consts, 1)
        with pool.Fori(0, NCH // 2) as i:
            def chunk(lane):
                PE, ACTS, DVE, POOL = after(st, i, "AB"[lane])
                done = signals(pool_s, st, "AB"[lane])
                pool.wait_ge(*DVE("dveps"))
                nc.gpsimd.tensor_tensor(drstd[lane][:], dveps[lane][:], mhalf[:], ALU.pow).then_inc(*done("drstd"))
                yield
                pool.wait_ge(*DVE("dn1"))
                nc.gpsimd.tensor_tensor(decn[lane][:], decn[lane][:], over(SW("ln_g"), BC), ALU.mult).then_inc(*done("g"))
                yield
                pool.wait_ge(*POOL("g"))
                nc.gpsimd.tensor_tensor(decn[lane][:], decn[lane][:], over(SW("ln_b"), BC), ALU.add).then_inc(*done("b"))
                yield
                yield from stats_root(st, i, lane)

            in_turns(chunk)

    def spike_dve():
        dve, st = nc.vector, "spike"
        others_done(dve, "attn")
        dve.wait_ge(w_loaded[st], 16)
        dve.wait_ge(consts, 5)
        with dve.Fori(0, NCH // 2) as i:
            def chunk(lane):
                c = 2 * i + lane
                bk = bank[4 * lane:4 * lane + 4]
                PE, ACTS, DVE, POOL = after(st, i, "AB"[lane])
                done = signals(dve_s, st, "AB"[lane])

                def relu(n):
                    dve.wait_ge(*PE(f"h{n}1"))
                    for e in range(2):
                        c = 2 * (2 * n + e) + 1
                        last = nc.vector.tensor_scalar(ehT[lane][:, c, :], bk[pair_bank(n, 1)][:, e * TOK:(e + 1) * TOK],
                                                       SW("eb1")[:, c:c + 1], 0.0, ALU.add, ALU.max)
                    last.then_inc(*done(f"h{n}"))
                    yield

                dve.wait_ge(*PE("xT"))
                nc.vector.tensor_copy(xnT[lane][:].rearrange("p k t -> p (k t)"), bk[0][:]).then_inc(*done("xT"))
                yield
                dve.wait_ge(*PE("s2c"))
                nc.vector.tensor_scalar(contT[lane][:], bk[3][:, 0:TOK], SW("s2c_b"), None, ALU.add).then_inc(*done("s2c"))
                yield
                dve.wait_ge(*PE("lg"))
                nc.vector.tensor_tensor(lg0[lane][:], bk[0][:, 0:BC * NE0].rearrange("p (b e) -> p b e", b=BC), over(SW("rb2"), BC),
                                        ALU.add).then_inc(*done("lg"))
                yield
                dve.wait_ge(*DVE("lg"))
                dve.sem_inc(held, 1)
                for b in range(BC):
                    nc.vector.max(mx0[lane][:, b, :], lg0[lane][:, b, :]).then_inc(*done(f"mx{b}"))
                    yield
                dve.wait_ge(*DVE("mx1"))
                dve.sem_inc(held, 1)
                for b in range(BC):
                    nc.vector.max_index(ix0[lane][:, b, :].bitcast(U32), mx0[lane][:, b, :], lg0[lane][:, b, :]).then_inc(*done(f"ix{b}"))
                    yield
                dve.wait_ge(*DVE("ix1"))
                nc.vector.tensor_copy(ixf0[lane][:], ix0[lane][:].bitcast(U32)).then_inc(*done("ixf"))
                yield
                nc.vector.tensor_tensor(gap0[lane][:], mx0[lane][:, :, 1], mx0[lane][:, :, 0], ALU.subtract).then_inc(*done("gap"))
                yield
                yield from relu(0)
                dve.wait_ge(*ACTS("w"))
                for b in range(BC):
                    for k in range(2):
                        nc.vector.tensor_scalar(pick0[lane][:, k, b, :], iota8[:], ixf0[lane][:, b, k:k + 1], w0[lane][:, k, b:b + 1], ALU.is_equal,
                                                ALU.mult).then_inc(*done(f"p{b}{k}"))
                        yield
                dve.wait_ge(*DVE("p11"))
                nc.vector.tensor_tensor(comb0[lane][:], pick0[lane][:, 0], pick0[lane][:, 1], ALU.add).then_inc(*done("comb"))
                yield
                for n in range(1, EP):
                    yield from relu(n)
                for b in range(BC):
                    dve.wait_ge(*PE(f"eo{b}"))
                    nc.vector.tensor_tensor(eo[lane][:, b, :], bk[1 + b][:], SW("eb2"), ALU.add).then_inc(*done(f"a{b}"))
                    yield
                    dve.wait_ge(*DVE(f"a{b}"))
                    nc.vector.tensor_tensor(eo[lane][:, b, :].rearrange("p (e d) -> p e d", e=NE0), eo[lane][:, b, :].rearrange("p (e d) -> p e d", e=NE0),
                                            wide(comb0[lane][:, b, :], MD), ALU.mult).then_inc(*done(f"m{b}"))
                    yield
                    dve.wait_ge(*DVE(f"m{b}"))
                    nc.vector.tensor_reduce(moe0[lane][:, b, :], eo[lane][:, b, :].rearrange("p (e d) -> p d e", e=NE0), AX.X,
                                            ALU.add).then_inc(*done(f"r{b}"))
                    yield
                dve.wait_ge(*PE("mT"))
                nc.vector.tensor_copy(moe0T[lane][:], bk[3][0:64, 0:TOK]).then_inc(*done("mT"))
                yield
                dve.wait_ge(*PE("dec"))
                nc.vector.tensor_tensor(dec[lane][:], bk[1][:].rearrange("p (b d) -> p b d", b=BC), over(SW("dec_b"), BC),
                                        ALU.add).then_inc(*done("dadd"))
                yield
                dve.wait_ge(*ACTS("dec"))
                for b in range(BC):
                    nc.vector.bn_stats(dbn[lane][:, b, :], dec[lane][:, b, :]).then_inc(*done(f"dbn{b}"))
                    yield
                for b in range(BC):
                    dve.wait_ge(*DVE(f"dbn{b}"))
                    nc.vector.sem_inc(held, 1)
                    nc.vector.bn_aggr(dmv[lane][:, b, :], dbn[lane][:, b, :]).then_inc(*done(f"dag{b}"))
                    yield
                dve.wait_ge(*DVE("dag1"))
                nc.vector.tensor_scalar(dveps[lane][:], dmv[lane][:, :, 1], EPS, None, ALU.add).then_inc(*done("dveps"))
                yield
                dve.wait_ge(*POOL("drstd"))
                for b in range(BC):
                    nc.vector.tensor_scalar(decn[lane][:, b, :], dec[lane][:, b, :], dmv[lane][:, b, 0:1], drstd[lane][:, b:b + 1], ALU.subtract,
                                            ALU.mult).then_inc(*done(f"dn{b}"))
                    yield
                dve.wait_ge(*POOL("b"))
                nc.vector.tensor_tensor(x[:, bass.ds(c * BC, BC), :], decn[lane][:], x[:, bass.ds(c * BC, BC), :], ALU.add).then_inc(*done("res"))
                yield
                yield from stats(st, i, lane)

            in_turns(chunk)

    RW = weights["rec"]
    wi, wg1, wa, wbm, wo1 = (RW(n).rearrange("p (k m) -> p k m", k=KD) for n in ("wi", "wg", "a", "bm", "wo"))
    gate = area("gate", [P, KD, S, B], 0)
    drive = area("drive", [P, KD, S, B], 4096)
    state = area("state", [P, KD, S, B], 8192)
    REC_LANE = 5120
    c2 = [area(f"c2{n}", [P, KD, TOK], 8192 + n * REC_LANE) for n in range(2)]
    rT1 = [area(f"rT1{n}", [P, KD, TOK], 8704 + n * REC_LANE) for n in range(2)]
    ret = [area(f"ret{n}", [P, KD, TOK], 9216 + n * REC_LANE) for n in range(2)]
    inp = [area(f"inp{n}", [P, KD, TOK], 9728 + n * REC_LANE) for n in range(2)]
    gc = [area(f"gc{n}", [P, KD, TOK], 10240 + n * REC_LANE) for n in range(2)]
    cin = [area(f"cin{n}", [P, KD, TOK], 10752 + n * REC_LANE) for n in range(2)]
    z = area("z", [P, KD, B], 12288)
    sT = area("sT", [P, KD, TOK], 12352)
    CH = [f"{k}{b}" for k in range(KD) for b in range(BC)]
    stage("rec_in", NCH // 2, pe=both(["xT", "inp", "gate", "drive"]),
          act=both(["prep0", "prep1", "inp", "gate", "drive"]),
          dve=both(["c2"] + [f"r{c}" for c in CH] + ["xT", "ret", "gc", "cin"]), pool=[])
    stage("rec_0", 1, pe=["t0"], act=["t0"], dve=["z0"], pool=[])
    stage("rec_loop", (S - 2) // 2, pe=["t0", "t1"], act=["t0", "t1"], dve=["z0", "z1"], pool=[])
    stage("rec_9", 1, pe=["t0"], act=["t0"], dve=["z0"], pool=[])
    stage("rec", NCH, pe=["out"], act=["sT"], dve=["res"] + LN_DVE, pool=["bo", "rstd"])

    def rec_sp():
        sp = nc.sync
        others_done(sp, "attn")
        for name in ("rec", "moe", "mlstm"):
            load_weights(sp, name)
        others_done(sp, "spike")
        st = "rec_in"
        with sp.Fori(0, NCH // 2) as i:
            def chunk(lane):
                c = 2 * i + lane
                PE, ACTS, DVE, POOL = after(st, i, "AB"[lane])
                sp.wait_ge(*DVE("c2", back=1))
                sp.dma_start(ctxT[lane][:], ctxT_dram[:, :, bass.ds(c * TOK, TOK)]).then_inc(ctxT2_loaded[lane], 16)
                yield

            in_turns(chunk)

    def rec_pe():
        pe, st = nc.tensor, "rec_in"
        others_done(pe, "spike")
        pe.wait_ge(w_loaded["rec"], 16)
        with pe.Fori(0, NCH // 2) as i:
            def chunk(lane):
                bk = bank[4 * lane:4 * lane + 4]
                PE, ACTS, DVE, POOL = after(st, i, "AB"[lane])
                done = signals(pe_s, st, "AB"[lane])
                yield from turn_x(st, i, lane, bk[0])
                for n, (w, src, what) in enumerate(((wi, ret[lane], "inp"), (wg1, inp[lane], "gate"))):
                    pe.wait_ge(*(DVE("ret") if n == 0 else ACTS("inp")))
                    for m in range(KD):
                        for k in range(KD):
                            last = nc.tensor.matmul(bk[1 + n][:, m * TOK:(m + 1) * TOK], w[:, k, m * P:(m + 1) * P], src[:, k, :],
                                                    start=k == 0, stop=k == KD - 1)
                    last.then_inc(*done(what))
                    yield
                pe.wait_ge(*DVE("cin"))
                for m in range(KD):
                    for k in range(KD):
                        nc.tensor.matmul(bk[3][:, m * TOK:(m + 1) * TOK], wbm[:, k, m * P:(m + 1) * P], inp[lane][:, k, :],
                                         start=k == 0, stop=False)
                    for k in range(KD):
                        last = nc.tensor.matmul(bk[3][:, m * TOK:(m + 1) * TOK], wa[:, k, m * P:(m + 1) * P], cin[lane][:, k, :],
                                                start=False, stop=k == KD - 1)
                last.then_inc(*done("drive"))
                yield

            in_turns(chunk)

        def drive_part(t, bk):
            nc.tensor.matmul(bk[:, 0:KD * B], ident[:], drive[:, :, t, :], start=True, stop=False, skip_group_check=True)

        def state_part(bk, signal):
            for m in range(KD):
                for k in range(KD):
                    last = nc.tensor.matmul(bk[:, m * B:(m + 1) * B], wa[:, k, m * P:(m + 1) * P], z[:, k, :],
                                            start=False, stop=m == KD - 1 and k == KD - 1, skip_group_check=True)
            last.then_inc(*signal)

        pe.wait_ge(act_s.sem, act_s.all("rec_in"))
        drive_part(0, bank[0])
        pe.wait_ge(dve_s.sem, dve_s.at("rec_0", 0, "z0"))
        state_part(bank[0], signals(pe_s, "rec_0")("t0"))
        done = signals(pe_s, "rec_loop")
        with pe.Fori(0, (S - 2) // 2) as i:
            PE, ACTS, DVE, POOL = after("rec_loop", i)
            for u in range(2):
                drive_part(bass.ds(2 * i + 1 + u, 1), bank[(1 + u) % 2])
                pe.wait_ge(*DVE(f"z{u}"))
                state_part(bank[(1 + u) % 2], done(f"t{u}"))
        drive_part(S - 1, bank[1])
        pe.wait_ge(dve_s.sem, dve_s.at("rec_9", 0, "z0"))
        state_part(bank[1], signals(pe_s, "rec_9")("t0"))

        done = signals(pe_s, "rec")
        with pe.Fori(0, NCH) as i:
            PE, ACTS, DVE, POOL = after("rec", i)
            pe.wait_ge(*ACTS("sT"))
            pe.wait_ge(*DVE("res", back=1))
            for b in range(BC):
                for k in range(KD):
                    last = nc.tensor.matmul(bank[3][:, b * D:(b + 1) * D], sT[:, k, b * P:(b + 1) * P], wo1[:, k, :],
                                            start=k == 0, stop=k == KD - 1)
            last.then_inc(*done("out"))

    def rec_act():
        act, st = nc.scalar, "rec_in"
        others_done(act, "spike")
        act.wait_ge(w_loaded["rec"], 16)
        with act.Fori(0, NCH // 2) as i:
            def chunk(lane):
                c = 2 * i + lane
                bk = bank[4 * lane:4 * lane + 4]
                PE, ACTS, DVE, POOL = after(st, i, "AB"[lane])
                done = signals(act_s, st, "AB"[lane])
                yield from prep(st, i, lane)
                act.wait_ge(*PE("inp"))
                for m in range(KD):
                    last = nc.scalar.activation(inp[lane][:, m, :], bk[1][:, m * TOK:(m + 1) * TOK], ACT.Identity, bias=RW("bi")[:, m:m + 1])
                last.then_inc(*done("inp"))
                yield
                act.wait_ge(*PE("gate"))
                act.sem_inc(held, 1)
                for m in range(KD):
                    last = nc.scalar.activation(gate[:, m, :, bass.ds(c * BC, BC)].rearrange("p t b -> p b t"),
                                                bk[2][:, m * TOK:(m + 1) * TOK].rearrange("p (b t) -> p b t", b=BC), ACT.Sigmoid,
                                                bias=RW("bg")[:, m:m + 1])
                last.then_inc(*done("gate"))
                yield
                act.wait_ge(*PE("drive"))
                act.sem_inc(held, 1)
                for m in range(KD):
                    last = nc.scalar.activation(drive[:, m, :, bass.ds(c * BC, BC)].rearrange("p t b -> p b t"),
                                                bk[3][:, m * TOK:(m + 1) * TOK].rearrange("p (b t) -> p b t", b=BC), ACT.Identity)
                last.then_inc(*done("drive"))
                yield

            in_turns(chunk)

        def step(t, bk, signal):
            act.sem_inc(held, 1)
            nc.scalar.activation(state[:, :, t, :], bk[:, 0:KD * B].rearrange("p (k b) -> p k b", k=KD), ACT.Tanh).then_inc(*signal)

        act.wait_ge(pe_s.sem, pe_s.at("rec_0", 0, "t0"))
        step(0, bank[0], signals(act_s, "rec_0")("t0"))
        done = signals(act_s, "rec_loop")
        with act.Fori(0, (S - 2) // 2) as i:
            PE, ACTS, DVE, POOL = after("rec_loop", i)
            for u in range(2):
                act.wait_ge(*PE(f"t{u}"))
                step(bass.ds(2 * i + 1 + u, 1), bank[(1 + u) % 2], done(f"t{u}"))
        act.wait_ge(pe_s.sem, pe_s.at("rec_9", 0, "t0"))
        step(S - 1, bank[1], signals(act_s, "rec_9")("t0"))

        done = signals(act_s, "rec")
        act.wait_ge(act_s.sem, act_s.all("rec_9"))
        with act.Fori(0, NCH) as i:
            PE, ACTS, DVE, POOL = after("rec", i)
            act.wait_ge(*PE("out", back=1))
            act.sem_inc(held, 1)
            for k in range(KD):
                last = nc.scalar.activation(sT[:, k, :].rearrange("p (b t) -> p b t", b=BC),
                                            state[:, k, :, bass.ds(i * BC, BC)].rearrange("p t b -> p b t"), ACT.Identity)
            last.then_inc(*done("sT"))

    def rec_dve():
        dve, st = nc.vector, "rec_in"
        others_done(dve, "spike")
        dve.wait_ge(w_loaded["rec"], 16)
        with dve.Fori(0, NCH // 2) as i:
            def chunk(lane):
                c = 2 * i + lane
                bk = bank[4 * lane:4 * lane + 4]
                PE, ACTS, DVE, POOL = after(st, i, "AB"[lane])
                done = signals(dve_s, st, "AB"[lane])
                dve.wait_ge(ctxT2_loaded[lane], i * 16 + 16)
                nc.vector.tensor_tensor(c2[lane][:], ctxT[lane][:], ctxT[lane][:], ALU.mult).then_inc(*done("c2"))
                yield
                dve.wait_ge(*DVE("c2"))
                for k in range(KD):
                    for b in range(BC):
                        nc.vector.tensor_tensor_scan(rT1[lane][:, k, b * P:(b + 1) * P], RW("decay")[:, k:k + 1].to_broadcast([P, P]),
                                                     c2[lane][:, k, b * P:(b + 1) * P], 0.0, ALU.mult, ALU.add).then_inc(*done(f"r{k}{b}"))
                        yield
                dve.wait_ge(*PE("xT"))
                nc.vector.tensor_copy(xnT[lane][:].rearrange("p k t -> p (k t)"), bk[0][:]).then_inc(*done("xT"))
                yield
                dve.wait_ge(*DVE("xT"))
                nc.vector.tensor_tensor(ret[lane][:], xnT[lane][:], rT1[lane][:], ALU.mult).then_inc(*done("ret"))
                yield
                dve.wait_ge(*ACTS("gate"))
                nc.vector.tensor_tensor(gc[lane][:].rearrange("p k (b t) -> p k b t", b=BC),
                                        gate[:, :, :, bass.ds(c * BC, BC)].rearrange("p k t b -> p k b t"),
                                        inp[lane][:].rearrange("p k (b t) -> p k b t", b=BC), ALU.mult).then_inc(*done("gc"))
                yield
                dve.wait_ge(*DVE("gc"))
                nc.vector.tensor_tensor(cin[lane][:], inp[lane][:], gc[lane][:], ALU.subtract).then_inc(*done("cin"))
                yield

            in_turns(chunk)

        nc.vector.memset(z[:], 0.0).then_inc(*signals(dve_s, "rec_0")("z0"))

        def gated(t_gate, t_state, signal):
            nc.vector.tensor_tensor(z[:], gate[:, :, t_gate, :], state[:, :, t_state, :], ALU.mult).then_inc(*signal)

        done = signals(dve_s, "rec_loop")
        with dve.Fori(0, (S - 2) // 2) as i:
            PE, ACTS, DVE, POOL = after("rec_loop", i)
            dve.wait_ge(act_s.sem, act_s.at("rec_loop", i, "t1", back=1))
            gated(bass.ds(2 * i + 1, 1), bass.ds(2 * i, 1), done("z0"))
            dve.wait_ge(*ACTS("t0"))
            gated(bass.ds(2 * i + 2, 1), bass.ds(2 * i + 1, 1), done("z1"))
        dve.wait_ge(act_s.sem, act_s.all("rec_loop"))
        gated(S - 1, S - 2, signals(dve_s, "rec_9")("z0"))
        done = signals(dve_s, "rec")
        with dve.Fori(0, NCH) as i:
            PE, ACTS, DVE, POOL = after("rec", i)
            dve.wait_ge(*PE("out"))
            dve.wait_ge(*POOL("bo"))
            nc.vector.tensor_tensor(x[:, bass.ds(i * BC, BC), :], bank[3][:].rearrange("p (b d) -> p b d", b=BC),
                                    x[:, bass.ds(i * BC, BC), :], ALU.add).then_inc(*done("res"))
            alone(stats("rec", i))

    def rec_pool():
        pool = nc.gpsimd
        others_done(pool, "spike")
        pool.wait_ge(w_loaded["rec"], 16)
        pool.wait_ge(act_s.sem, act_s.all("rec_in"))
        done = signals(pool_s, "rec")
        with pool.Fori(0, NCH) as i:
            nc.gpsimd.tensor_tensor(x[:, bass.ds(i * BC, BC), :], x[:, bass.ds(i * BC, BC), :], over(RW("bo"), BC),
                                    ALU.add).then_inc(*done("bo"))
            alone(stats_root("rec", i))

    MW = weights["moe"]
    router = MW("router").rearrange("p (k e) -> p k e", k=KD)
    sgu = MW("sgu").rearrange("p (k f) -> p k f", k=KD)
    sdown = MW("sdown").rearrange("p (k d) -> p k d", k=2)
    RING = 8
    GU = KD * 2 * FE
    ring = area("ring", [P, RING, GU + 2 * D], 0)
    M0 = RING * (GU + 2 * D)
    MOE_LANE = 3014
    EX0 = M0 + 2 * MOE_LANE
    lg1 = [area(f"lg1{n}", [P, BC, NE], M0 + n * MOE_LANE) for n in range(2)]
    mr1 = [area(f"mr1{n}", [P, BC, NE], M0 + 128 + n * MOE_LANE) for n in range(2)]
    pick = [area(f"pick{n}", [P, BC, NE], M0 + 256 + n * MOE_LANE) for n in range(2)]
    gates1 = [area(f"gates1{n}", [P, BC, NE], M0 + 384 + n * MOE_LANE) for n in range(2)]
    far = [area(f"far{n}", [P, BC, NE], M0 + 512 + n * MOE_LANE) for n in range(2)]
    fits = [area(f"fits{n}", [P, BC, NE], M0 + 640 + n * MOE_LANE) for n in range(2)]
    key = [area(f"key{n}", [P, BC, NE], M0 + 768 + n * MOE_LANE) for n in range(2)]
    same = [area(f"same{n}", [P, TOPK, NE], M0 + 896 + n * MOE_LANE) for n in range(2)]
    pickb = [area(f"pickb{n}", [P, BC, NE], M0 + 1408 + n * MOE_LANE, BF16) for n in range(2)]
    seen = area("seen", [P, NE], M0 + 1472, BF16)
    mx1 = [area(f"mx1{n}", [P, BC, TOPK], M0 + 1504 + n * MOE_LANE) for n in range(2)]
    nmx1 = [area(f"nmx1{n}", [P, BC], M0 + 1520 + n * MOE_LANE) for n in range(2)]
    den1 = [area(f"den1{n}", [P, 2, BC], M0 + 1522 + n * MOE_LANE) for n in range(2)]
    mk = [area(f"mk{n}", [P, BC, TOPK], M0 + 1526 + n * MOE_LANE) for n in range(2)]
    spill = [area(f"spill{n}", [P, BC, TOPK], M0 + 1542 + n * MOE_LANE) for n in range(2)]
    slot = [area(f"slot{n}", [P, BC, TOPK], M0 + 1558 + n * MOE_LANE).bitcast(I32) for n in range(2)]
    rows_w = [area(f"rows_w{n}", [P, BC, TOPK, 2], M0 + 1574 + n * MOE_LANE) for n in range(2)]
    tri_b = area("tri_b", [P, P], M0 + 1606, BF16)
    ones_b = area("ones_b", [P, P], M0 + 1670, BF16)
    sg = [area(f"sg{n}", [P, BC, FE], M0 + 1734 + n * MOE_LANE) for n in range(2)]
    hs = [area(f"hs{n}", [P, BC, FE], M0 + 2118 + n * MOE_LANE) for n in range(2)]
    hsT = [area(f"hsT{n}", [P, 2, TOK], M0 + 2502 + n * MOE_LANE) for n in range(2)]
    xg = [area(f"xg{n}", [P, 2, D], EX0 + 512 * n) for n in range(2)]
    xgT = [area(f"xgT{n}", [P, 2, D], EX0 + 1024 + 512 * n) for n in range(2)]
    y = [area(f"y{n}", [P, 2, D], EX0 + 2048 + 512 * n) for n in range(2)]
    slot_tok = area("slot_tok", [P, NE, 2], EX0 + 3072)
    acc_in = [area(f"acc_in{n}", [P, 2, BC, D], 1024 * n) for n in range(2)]
    gidx = sb("gather_rows", [P, 4], I32)
    sidx = sb("scatter_rows", [P, 2], I32)
    idx_all = sb("idx_all", [P, NE + 4], I32)
    NSLOT = NE * CAP
    table = nc.dram_tensor("slot_table", (NSLOT + B * S * TOPK, 2), F32, kind="Internal").ap()
    xn_rows = nc.dram_tensor("normalised_rows", (B * S + P, D), F32, kind="Internal").ap()
    acc = [nc.dram_tensor(f"routed_sum_{u}", (B * S + P, D), F32, kind="Internal").ap() for u in range(2)]
    table_set, rows_set, acc_set = sem("table_initialised"), sem("spare_row_zeroed"), sem("routed_sum_zeroed")
    rows_stored = [sem(f"rows_stored_{n}") for n in range(2)]
    scattered, table_read = sem("slots_scattered"), sem("table_read")
    gu_in = [sem(f"expert_weights_loaded_{q}") for q in range(RING // 2)]
    gathered = [[sem(f"rows_gathered_{par}{u}") for u in range(2)] for par in range(2)]
    added, acc_read = ([sem(f"{n}_{u}") for u in range(2)] for n in ("routed_rows_added", "routed_sum_read"))
    slots_free = sem("chunk_scattered")
    y_free = [[sem(f"expert_rows_added_{par}{u}") for u in range(2)] for par in range(2)]
    moe_ready = sem("moe_constants_ready")
    stage("moe_in", NCH // 2, pe=both(["xT", "lg", "sgu0", "sgu1", "pos", "hsT", "sout"]),
          act=both(["prep0", "prep1", "ex", "sg0", "sg1"]),
          dve=both(["xT", "lg", "mx0", "mx1", "nmx", "mr0", "mr1", "pick", "pickb", "hs0", "hs1", "em", "sum", "rec", "gates",
                    ("seen", "seen2"), "far", "fits", "key", "mk0", "mk1", "back", "slot0", "slot", "tok", "hsT", "hsT1"]
                   + [f"{a}{b}" for b in range(BC) for a in ("eq", "ew", "wk")] + ["sres"]), pool=[])
    QS = range(RING // 2)
    stage("moe_x", 1, pe=["x0", "x1"], act=["x0", "x1"], dve=[], pool=[])
    stage("moe_ex", NE // RING, pe=[f"{a}{q}{u}" for q in QS for a in "gxhd" for u in range(2)],
          act=[f"{a}{q}{u}" for q in QS for a in "sxy" for u in range(2)],
          dve=[f"{a}{q}{u}" for q in QS for a in "ht" for u in range(2)], pool=[])

    def pair_before(q):
        return (q - 1) % (RING // 2), int(q == 0)
    stage("moe", NCH // 2, pe=[], act=[], dve=both(["res0", "res"] + LN_DVE), pool=both(["rstd"]))
    hT = hsT[0]
    sg_ex, hs_ex = sg[0], hs[0]

    def moe_sp():
        sp = nc.sync
        sp.dma_start(table, ins["table0"]).then_inc(table_set, 16)
        sp.wait_ge(zeroed, 1)
        sp.dma_start(xn_rows[B * S:B * S + P, :], zrow[:]).then_inc(rows_set, 16)
        for u in range(2):
            sp.dma_start(acc[u].rearrange("(b p) d -> p b d", p=P), over(zrow[:], B + 1)).then_inc(acc_set, 16)
        others_done(sp, "rec")
        load_weights(sp, "bit")
        st = "moe_in"
        with sp.Fori(0, NCH // 2) as i:
            def chunk(lane):
                c = 2 * i + lane
                PE, ACTS, DVE, POOL = after(st, i, "AB"[lane])
                sp.wait_ge(*ACTS("prep1"))
                sp.dma_start(xn_rows[bass.ds(c * TOK, TOK), :].rearrange("(b p) d -> p b d", p=P), xn[lane][:]).then_inc(rows_stored[lane], 16)
                yield

            in_turns(chunk)

        sp.wait_ge(slots_free, NCH + 2)
        sp.dma_start(slot_tok[:], table[0:NSLOT, :].rearrange("(e p) c -> p e c", p=P)).then_inc(table_read, 16)
        sp.wait_ge(moe_ready, 1)
        with sp.Fori(0, NE // RING) as o:
            for q in QS:
                sp.wait_ge(pe_s.sem, pe_s.at("moe_ex", o, f"d{q}1", back=1))
                e = o * RING + 2 * q
                sp.dma_start(ring[:, 2 * q:2 * q + 2, 0:GU], ins["w_gate_up"][bass.ds(e, 2)].rearrange("e p c -> p e c")).then_inc(gu_in[q], 16)
                sp.dma_start(ring[:, 2 * q:2 * q + 2, GU:GU + D], ins["w_down"][bass.ds(e, 2), 0:P].rearrange("e p c -> p e c")).then_inc(gu_in[q], 16)
                sp.dma_start(ring[0:FE - P, 2 * q:2 * q + 2, GU + D:], ins["w_down"][bass.ds(e, 2), P:FE].rearrange("e p c -> p e c")).then_inc(gu_in[q], 16)
        others_done(sp, "moe_ex")
        for u in range(2):
            sp.wait_ge(added[u], 8 * NE + 16)
            for par in range(2):
                sp.wait_ge(gathered[par][u], 4 * NE + 16)
        with sp.Fori(0, NCH // 2) as i:
            for lane in range(2):
                sp.wait_ge(dve_s.sem, dve_s.at("moe", i, f"res{"AB"[lane]}", back=1))
                for u in range(2):
                    sp.dma_start(acc_in[lane][:, u], acc[u][bass.ds((2 * i + lane) * TOK, TOK), :].rearrange("(b p) d -> p b d", p=P)).then_inc(
                        acc_read[lane], 16)

    def moe_pe():
        pe, st = nc.tensor, "moe_in"
        others_done(pe, "rec")
        pe.wait_ge(w_loaded["moe"], 16)
        pe.wait_ge(moe_ready, 2)
        with pe.Fori(0, NCH // 2) as i:
            def chunk(lane):
                bk = bank[4 * lane:4 * lane + 4]
                PE, ACTS, DVE, POOL = after(st, i, "AB"[lane])
                done = signals(pe_s, st, "AB"[lane])
                yield from turn_x(st, i, lane, bk[0])
                pe.wait_ge(*DVE("xT"))
                for b in range(BC):
                    for k in range(KD):
                        last = nc.tensor.matmul(bk[1][:, b * NE:(b + 1) * NE], xnT[lane][:, k, b * P:(b + 1) * P], router[:, k, :],
                                                start=k == 0, stop=k == KD - 1)
                last.then_inc(*done("lg"))
                yield
                for b in range(BC):
                    for k in range(KD):
                        last = nc.tensor.matmul(bk[2 + b][:, 0:2 * FE], xnT[lane][:, k, b * P:(b + 1) * P], sgu[:, k, :],
                                                start=k == 0, stop=k == KD - 1)
                    last.then_inc(*done(f"sgu{b}"))
                    yield
                pe.wait_ge(*DVE("pickb"))
                pe.wait_ge(dve_s.sem, dve_s.at(st, i, "seen2A") if lane else dve_s.at(st, i, "seen2B", back=1))
                for b in range(BC):
                    parts = [(tri_b, pickb[lane][:, b, :]), (ones_b, seen[:])] + [(ones_b, pickb[lane][:, 0, :])] * b
                    for n, (w, m) in enumerate(parts):
                        last = nc.tensor.matmul(bk[0][:, b * NE:(b + 1) * NE], w[:], m, start=n == 0, stop=n == len(parts) - 1)
                last.then_inc(*done("pos"))
                yield
                pe.wait_ge(*DVE("hs1"))
                for b in range(BC):
                    nc.tensor.transpose(bk[1][:, b * P:(b + 1) * P], hs[lane][:, b, 0:P], ident[:])
                for b in range(BC):
                    last = nc.tensor.transpose(bk[1][0:FE - P, TOK + b * P:TOK + (b + 1) * P], hs[lane][:, b, P:FE], ident[:])
                last.then_inc(*done("hsT"))
                yield
                pe.wait_ge(*DVE("hsT1"))
                for b in range(BC):
                    for k in range(2):
                        last = nc.tensor.matmul(bk[2][:, b * D:(b + 1) * D], hsT[lane][:, k, b * P:(b + 1) * P], sdown[:, k, :],
                                                start=k == 0, stop=k == 1)
                last.then_inc(*done("sout"))
                yield

            in_turns(chunk)

        others_done(pe, "moe_in")

        def turn_rows(par, u, value, signal):
            pe.wait_ge(gathered[par][u], value)
            for k in range(KD):
                last = nc.tensor.transpose(bank[u][:, k * P:(k + 1) * P], xg[par][:, u, k * P:(k + 1) * P], ident[:])
            last.then_inc(*signal)

        for u in range(2):
            turn_rows(0, u, 16, signals(pe_s, "moe_x")(f"x{u}"))
        pe.wait_ge(act_s.sem, act_s.all("moe_x"))
        done = signals(pe_s, "moe_ex")
        with pe.Fori(0, NE // RING) as o:
            PE, ACTS, DVE, POOL = after("moe_ex", o)
            for q in QS:
                before, back = pair_before(q)
                pe.wait_ge(gu_in[q], o * 48 + 48)
                for u in range(2):
                    pe.wait_ge(*ACTS(f"x{before}{u}", back=back))
                    for k in range(KD):
                        last = nc.tensor.matmul(bank[2 + u][:, 0:2 * FE], xgT[q % 2][:, u, k * P:(k + 1) * P],
                                                ring[:, 2 * q + u, k * 2 * FE:(k + 1) * 2 * FE], start=k == 0, stop=k == KD - 1)
                    last.then_inc(*done(f"g{q}{u}"))
                for u in range(2):
                    turn_rows((q + 1) % 2, u, o * (8 * (RING // 2)) + 16 * ((q + 1) // 2 + 1), done(f"x{q}{u}"))
                for u in range(2):
                    pe.wait_ge(*DVE(f"h{q}{u}"))
                    pe.sem_inc(held, 1)
                    nc.tensor.transpose(bank[4 + u][:, 0:P], hs_ex[:, u, 0:P], ident[:])
                    nc.tensor.transpose(bank[4 + u][0:FE - P, P:2 * P], hs_ex[:, u, P:FE], ident[:]).then_inc(*done(f"h{q}{u}"))
                for u in range(2):
                    pe.wait_ge(*DVE(f"t{q}{u}"))
                    pe.wait_ge(*ACTS(f"y{before}{u}", back=back))
                    for k in range(2):
                        last = nc.tensor.matmul(bank[6 + u][:, 0:D], hT[:, k, u * P:(u + 1) * P],
                                                ring[:, 2 * q + u, GU + k * D:GU + (k + 1) * D], start=k == 0, stop=k == 1)
                    last.then_inc(*done(f"d{q}{u}"))

    def moe_act():
        act, st = nc.scalar, "moe_in"
        others_done(act, "rec")
        with act.Fori(0, NCH // 2) as i:
            def chunk(lane):
                bk = bank[4 * lane:4 * lane + 4]
                PE, ACTS, DVE, POOL = after(st, i, "AB"[lane])
                done = signals(act_s, st, "AB"[lane])
                act.wait_ge(rows_stored[lane], i * 16 + 16)
                act.sem_inc(held, 1)
                yield from prep(st, i, lane)
                act.wait_ge(*DVE("nmx"))
                for b in range(BC):
                    last = nc.scalar.activation(gates1[lane][:, b, :], lg1[lane][:, b, :], ACT.Exp, bias=nmx1[lane][:, b:b + 1])
                last.then_inc(*done("ex"))
                yield
                for b in range(BC):
                    act.wait_ge(*PE(f"sgu{b}"))
                    nc.scalar.activation(sg[lane][:, b, :], bk[2 + b][:, 0:FE], ACT.Silu).then_inc(*done(f"sg{b}"))
                    yield

            in_turns(chunk)

        others_done(act, "moe_in")
        for u in range(2):
            act.wait_ge(pe_s.sem, pe_s.at("moe_x", 0, f"x{u}"))
            nc.scalar.activation(xgT[0][:, u, :], bank[u][:, 0:D], ACT.Identity).then_inc(*signals(act_s, "moe_x")(f"x{u}"))
        act.wait_ge(table_read, 16)
        done = signals(act_s, "moe_ex")
        with act.Fori(0, NE // RING) as o:
            PE, ACTS, DVE, POOL = after("moe_ex", o)
            for q in QS:
                for u in range(2):
                    act.wait_ge(*PE(f"g{q}{u}"))
                    nc.scalar.activation(sg_ex[:, u, :], bank[2 + u][:, 0:FE], ACT.Silu).then_inc(*done(f"s{q}{u}"))
                for u in range(2):
                    act.wait_ge(*PE(f"x{q}{u}"))
                    nc.scalar.activation(xgT[(q + 1) % 2][:, u, :], bank[u][:, 0:D], ACT.Identity).then_inc(*done(f"x{q}{u}"))
                for u in range(2):
                    act.wait_ge(*PE(f"d{q}{u}"))
                    act.wait_ge(y_free[q % 2][u], o * (RING // 4) + q // 2 + 1)
                    act.sem_inc(held, 1)
                    nc.scalar.activation(y[q % 2][:, u, :], bank[6 + u][:, 0:D], ACT.Identity,
                                         scale=slot_tok[:, bass.ds(o * RING + 2 * q + u, 1), 1]).then_inc(*done(f"y{q}{u}"))

    def moe_pool():
        pool = nc.gpsimd
        pool.sem_inc(slots_free, 2)
        for u in range(2):
            pool.sem_inc(rows_stored[u], 16)
            pool.sem_inc(y_free[0][u], 1)
        pool.wait_ge(table_set, 16)
        with pool.Fori(0, NCH // 2) as i:
            for lane in range(2):
                pool.wait_ge(dve_s.sem, dve_s.at("moe_in", i, f"wk1{"AB"[lane]}"))
                pool.sem_inc(held, 1)
                for b in range(BC):
                    for k in range(TOPK):
                        pool.indirect_dma_start(table[:, :], bass.IndirectOffsetOnAxis(ap=slot[lane][:, b, k:k + 1], axis=0),
                                                rows_w[lane][:, b, k, :], None).then_inc(scattered, 16)
                pool.wait_ge(scattered, (2 * i + lane + 1) * (16 * BC * TOPK))
                pool.sem_inc(slots_free, 1)
        others_done(pool, "moe_in")
        pool.wait_ge(table_read, 16)
        for lane in range(2):
            pool.wait_ge(rows_stored[lane], 16 * (NCH // 2) + 16)
        pool.wait_ge(rows_set, 16)
        pool.wait_ge(acc_set, 32)
        pool.wait_ge(moe_ready, 3)

        def gather(pair, par):
            pool.sem_inc(held, 1)
            for u in range(2):
                nc.gpsimd.tensor_copy(gidx[:, 2 * par + u:2 * par + u + 1], idx_all[:, bass.ds(2 * pair + u, 1)]).then_inc(gidx_set, 1)
            pool.wait_ge(gidx_set, 2 * pair + 2)
            pool.sem_inc(held, 1)
            for u in range(2):
                pool.indirect_dma_start(xg[par][:, u, :], None, xn_rows[:, :],
                                        bass.IndirectOffsetOnAxis(ap=gidx[:, 2 * par + u:2 * par + u + 1], axis=0)).then_inc(gathered[par][u], 16)

        gather(0, 0)
        gather(1, 1)
        for u in range(2):
            nc.gpsimd.tensor_copy(sidx[:, u:u + 1], idx_all[:, NE:NE + 1]).then_inc(sidx_set, 1)
        pool.wait_ge(sidx_set, 2)
        pool.sem_inc(held, 1)
        for u in range(2):
            pool.indirect_dma_start(acc[u][:, :], bass.IndirectOffsetOnAxis(ap=sidx[:, u:u + 1], axis=0), zrow[:], None,
                                    compute_op=ALU.add).then_inc(added[u], 16)
        pool.wait_ge(pe_s.sem, pe_s.all("moe_x"))
        with pool.Fori(0, NE // RING) as o:
            for q in QS:
                pair = o * (RING // 2) + q
                before, back = pair_before(q)
                pool.wait_ge(pe_s.sem, pe_s.at("moe_ex", o, f"x{before}1", back=back))
                gather(pair + 2, q % 2)
                for u in range(2):
                    pool.wait_ge(added[u], 16 * pair + 16)
                    pool.sem_inc(y_free[(q + 1) % 2][u], 1)
                for u in range(2):
                    nc.gpsimd.tensor_copy(sidx[:, u:u + 1], idx_all[:, bass.ds(2 * pair + u, 1)]).then_inc(sidx_set, 1)
                pool.wait_ge(sidx_set, 2 * pair + 4)
                for u in range(2):
                    pool.wait_ge(act_s.sem, act_s.at("moe_ex", o, f"y{q}{u}"))
                    pool.sem_inc(held, 1)
                    pool.indirect_dma_start(acc[u][:, :], bass.IndirectOffsetOnAxis(ap=sidx[:, u:u + 1], axis=0), y[q % 2][:, u, :], None,
                                            compute_op=ALU.add).then_inc(added[u], 16)
        with pool.Fori(0, NCH // 2) as i:
            in_turns(lambda lane: stats_root("moe", i, lane))

    def moe_dve():
        dve, st = nc.vector, "moe_in"
        others_done(dve, "rec")
        dve.wait_ge(consts_loaded, 16)
        nc.vector.memset(seen[:], 0.0)
        nc.vector.memset(ring[64:P, :, GU + D:], 0.0)
        nc.vector.memset(hsT[0][64:P, 1, :], 0.0)
        nc.vector.memset(hsT[1][64:P, 1, :], 0.0).then_inc(moe_ready, 1)
        nc.vector.memset(ones_b[:], 1.0)
        nc.vector.tensor_copy(tri_b[:], C("tri")).then_inc(moe_ready, 1)
        with dve.Fori(0, NCH // 2) as i:
            def chunk(lane):
                c = 2 * i + lane
                bk = bank[4 * lane:4 * lane + 4]
                PE, ACTS, DVE, POOL = after(st, i, "AB"[lane])
                done = signals(dve_s, st, "AB"[lane])
                dve.wait_ge(*PE("xT"))
                nc.vector.tensor_copy(xnT[lane][:].rearrange("p k t -> p (k t)"), bk[0][:]).then_inc(*done("xT"))
                yield
                dve.wait_ge(*PE("lg"))
                nc.vector.tensor_copy(lg1[lane][:].rearrange("p b e -> p (b e)"), bk[1][:, 0:BC * NE]).then_inc(*done("lg"))
                yield
                dve.wait_ge(*DVE("lg"))
                dve.sem_inc(held, 1)
                for b in range(BC):
                    nc.vector.max(mx1[lane][:, b, :], lg1[lane][:, b, :]).then_inc(*done(f"mx{b}"))
                    yield
                dve.wait_ge(*DVE("mx1"))
                nc.vector.tensor_scalar(nmx1[lane][:], mx1[lane][:, :, 0], -1.0, None, ALU.mult).then_inc(*done("nmx"))
                yield
                for b in range(BC):
                    nc.vector.match_replace(mr1[lane][:, b, :], mx1[lane][:, b, :], lg1[lane][:, b, :], -3.0e38).then_inc(*done(f"mr{b}"))
                    yield
                dve.wait_ge(*DVE("mr1"))
                nc.vector.tensor_tensor(pick[lane][:], mr1[lane][:], lg1[lane][:], ALU.not_equal).then_inc(*done("pick"))
                yield
                dve.wait_ge(*DVE("pick"))
                nc.vector.tensor_copy(pickb[lane][:], pick[lane][:]).then_inc(*done("pickb"))
                yield
                for b in range(BC):
                    dve.wait_ge(*ACTS(f"sg{b}"))
                    nc.vector.tensor_tensor(hs[lane][:, b, :], sg[lane][:, b, :], bk[2 + b][:, FE:2 * FE], ALU.mult).then_inc(*done(f"hs{b}"))
                    yield
                dve.wait_ge(*ACTS("ex"))
                nc.vector.tensor_tensor(gates1[lane][:], gates1[lane][:], pick[lane][:], ALU.mult).then_inc(*done("em"))
                yield
                dve.wait_ge(*DVE("em"))
                nc.vector.tensor_reduce(den1[lane][:, 0, :], gates1[lane][:], AX.X, ALU.add).then_inc(*done("sum"))
                yield
                dve.wait_ge(*DVE("sum"))
                nc.vector.reciprocal(den1[lane][:, 1, :], den1[lane][:, 0, :]).then_inc(*done("rec"))
                yield
                dve.wait_ge(*DVE("rec"))
                nc.vector.tensor_tensor(gates1[lane][:], gates1[lane][:], wide(den1[lane][:, 1, :], NE), ALU.mult).then_inc(*done("gates"))
                yield
                dve.wait_ge(*PE("pos"))
                nc.vector.tensor_tensor(seen[:], seen[:], pickb[lane][:, 0, :], ALU.add).then_inc(*done("seen"))
                dve.wait_ge(*DVE("seen"))
                nc.vector.tensor_tensor(seen[:], seen[:], pickb[lane][:, 1, :], ALU.add).then_inc(*done("seen2"))
                yield
                pos = bk[0][:, 0:BC * NE].rearrange("p (b e) -> p b e", b=BC)
                nc.vector.tensor_tensor(far[lane][:], over(C("slot_base"), BC), pos, ALU.subtract).then_inc(*done("far"))
                yield
                nc.vector.scalar_tensor_tensor(fits[lane][:], pos, float(CAP), pick[lane][:], ALU.is_lt, ALU.mult).then_inc(*done("fits"))
                yield
                dve.wait_ge(*DVE("fits"))
                nc.vector.tensor_tensor(key[lane][:], far[lane][:], fits[lane][:], ALU.mult).then_inc(*done("key"))
                yield
                dve.wait_ge(*DVE("key"))
                dve.sem_inc(held, 1)
                for b in range(BC):
                    nc.vector.max(mk[lane][:, b, :], key[lane][:, b, :]).then_inc(*done(f"mk{b}"))
                    yield
                dve.wait_ge(*DVE("mk1"))
                nc.vector.scalar_tensor_tensor(spill[lane][:].rearrange("p b k -> p (b k)"), mk[lane][:].rearrange("p b k -> p (b k)"), 0.0,
                                               C("spare")[:, bass.ds(c * BC * TOPK, BC * TOPK)], ALU.is_equal, ALU.mult).then_inc(*done("back"))
                yield
                dve.wait_ge(*DVE("back"))
                nc.vector.tensor_tensor(spill[lane][:], spill[lane][:], mk[lane][:], ALU.subtract).then_inc(*done("slot0"))
                yield
                dve.wait_ge(*DVE("slot0"))
                dve.wait_ge(slots_free, c + 1)
                nc.vector.tensor_scalar(slot[lane][:], spill[lane][:], float(NSLOT), None, ALU.add).then_inc(*done("slot"))
                yield
                nc.vector.tensor_copy(rows_w[lane][:, :, :, 0], wide(C("tokens")[:, bass.ds(c * BC, BC)], TOPK)).then_inc(*done("tok"))
                yield
                dve.wait_ge(*PE("hsT"))
                nc.vector.tensor_copy(hsT[lane][:, 0, :], bk[1][:, 0:TOK]).then_inc(*done("hsT"))
                yield
                nc.vector.tensor_copy(hsT[lane][0:FE - P, 1, :], bk[1][0:FE - P, TOK:2 * TOK]).then_inc(*done("hsT1"))
                yield
                for b in range(BC):
                    if b:
                        dve.wait_ge(*DVE("wk0"))
                    nc.vector.tensor_tensor(same[lane][:], over(key[lane][:, b, :], TOPK), wide(mk[lane][:, b, :], NE), ALU.is_equal).then_inc(*done(f"eq{b}"))
                    yield
                    dve.wait_ge(*DVE(f"eq{b}"))
                    nc.vector.tensor_tensor(same[lane][:], same[lane][:], over(gates1[lane][:, b, :], TOPK), ALU.mult).then_inc(*done(f"ew{b}"))
                    yield
                    dve.wait_ge(*DVE(f"ew{b}"))
                    nc.vector.tensor_reduce(rows_w[lane][:, b, :, 1], same[lane][:], AX.X, ALU.add).then_inc(*done(f"wk{b}"))
                    yield
                dve.wait_ge(*PE("sout"))
                nc.vector.tensor_tensor(x[:, bass.ds(c * BC, BC), :], bk[2][:].rearrange("p (b d) -> p b d", b=BC),
                                        x[:, bass.ds(c * BC, BC), :], ALU.add).then_inc(*done("sres"))
                yield

            in_turns(chunk)

        dve.wait_ge(table_read, 16)
        nc.vector.tensor_copy(idx_all[:, NE:], C("tokens")[:, 0:4])
        nc.vector.tensor_copy(idx_all[:, 0:NE], slot_tok[:, :, 0]).then_inc(moe_ready, 1)
        done = signals(dve_s, "moe_ex")
        others_done(dve, "moe_in")
        with dve.Fori(0, NE // RING) as o:
            PE, ACTS, DVE, POOL = after("moe_ex", o)
            for q in QS:
                for u in range(2):
                    dve.wait_ge(*ACTS(f"s{q}{u}"))
                    nc.vector.tensor_tensor(hs_ex[:, u, :], sg_ex[:, u, :], bank[2 + u][:, FE:2 * FE], ALU.mult).then_inc(*done(f"h{q}{u}"))
                for u in range(2):
                    dve.wait_ge(*PE(f"h{q}{u}"))
                    nc.vector.tensor_copy(hT[:, 0, u * P:(u + 1) * P], bank[4 + u][:, 0:P])
                    nc.vector.tensor_copy(hT[0:FE - P, 1, u * P:(u + 1) * P], bank[4 + u][0:FE - P, P:2 * P]).then_inc(*done(f"t{q}{u}"))
        with dve.Fori(0, NCH // 2) as i:
            def chunk(lane):
                c = 2 * i + lane
                done = signals(dve_s, "moe", "AB"[lane])
                PE, ACTS, DVE, POOL = after("moe", i, "AB"[lane])
                dve.wait_ge(acc_read[lane], i * 32 + 32)
                nc.vector.tensor_tensor(x[:, bass.ds(c * BC, BC), :], acc_in[lane][:, 0], x[:, bass.ds(c * BC, BC), :], ALU.add).then_inc(*done("res0"))
                yield
                dve.wait_ge(*DVE("res0"))
                nc.vector.tensor_tensor(x[:, bass.ds(c * BC, BC), :], acc_in[lane][:, 1], x[:, bass.ds(c * BC, BC), :], ALU.add).then_inc(*done("res"))
                yield
                yield from stats("moe", i, lane)

            in_turns(chunk)

    LW = weights["mlstm"]
    gq = LW("gq").rearrange("p (k g) -> p k g", k=KD)
    BH = BC * HL
    gkv = area("gkv", [P, KD, 2 * HL], 0)
    MLSTM_LANE = 5600
    lnw1 = area("lnw1", [P, D], 16)
    vext = [area(f"vext{n}", [P, BC, HL, DL + 1], 1264 + n * MLSTM_LANE) for n in range(2)]
    late_b = area("late_b", [P, HL * P], 272, BF16)
    ident_b = area("ident_b", [P, P], 528, BF16)
    triI = area("triI", [P, P], 592)
    mhalf8 = area("mhalf8", [P, BH], 720)
    gt = [area(f"gt{n}", [P, BC, 2 * HL], 1784 + n * MLSTM_LANE) for n in range(2)]
    mnf, nab, yv, lnu, uu, e1, ru, cr, lf, cs, av, cm, ne, ab, nr, hsum, hsq, hvar, hrs = (
        [area(f"s{k}_{n}", [P, BC, HL], 1800 + 8 * k + n * MLSTM_LANE) for n in range(2)] for k in range(19))
    aT = [area(f"aT{n}", [BH, P], 1952 + n * MLSTM_LANE) for n in range(2)]
    cmax = [area(f"cmax{n}", [BH, P], 2080 + n * MLSTM_LANE) for n in range(2)]
    cdiag = [area(f"cdiag{n}", [BH, BH, P], 2208 + n * MLSTM_LANE) for n in range(2)]
    decayT = [area(f"decayT{n}", [P, 2, BC * HL // 2, P], 3232 + n * MLSTM_LANE) for n in range(2)]
    cT = [area(f"cT{n}", [P, 2, BC * HL // 2, P], 4256 + n * MLSTM_LANE) for n in range(2)]
    hst = [area(f"hst{n}", [P, BC, D], 5280 + n * MLSTM_LANE) for n in range(2)]
    hce = [area(f"hce{n}", [P, BC, D], 5792 + n * MLSTM_LANE) for n in range(2)]
    hq = [area(f"hq{n}", [P, BC, D], 6304 + n * MLSTM_LANE) for n in range(2)]
    mlstm_ready = sem("mlstm_constants_ready")
    stage("mlstm", NCH // 2, pe=both(["xT", "gates", "cs", "aT", "qk", "cm", "cb0", "cb1", "ho0", "ho1"]),
          act=both(["prep0", "prep1", "ey", "ln", "D", "ne"]),
          dve=both(["xT", "gt", "mnf", "nab", "u", "e1", "ru", "cr", "t", "lf", "cs", "a", "aT", "cmax", "cdiag", "cm",
                    "cT0", "cT1", "ab0", "ab1", "abs", "nr", "nre", "rn", "h0", "h1", "hsum", "hce", "hq", "hsq", "hvar", "hn", "res"] + LN_DVE),
          pool=both(["hrs", "w", "rstd"]))

    def mlstm_sp():
        sp, st = nc.sync, "mlstm"
        others_done(sp, "moe")
        sp.wait_ge(mlstm_ready, 1)
        with sp.Fori(0, NCH // 2) as i:
            def chunk(lane):
                c = 2 * i + lane
                PE, ACTS, DVE, POOL = after(st, i, "AB"[lane])
                sp.wait_ge(*PE("qk", back=1))
                sp.dma_start(ctxT[lane][:], ctxT_dram[:, :, bass.ds(c * TOK, TOK)]).then_inc(ctxT3_loaded[lane], 16)
                sp.wait_ge(*PE("ho1", back=1))
                for b in range(BC):
                    sp.dma_start(vext[lane][:, b, :, 0:DL], ctx_dram[:, bass.ds(c * BC + b, 1), :].rearrange("s b (h d) -> s (b h) d", h=HL)).then_inc(
                        ctx_loaded[lane], 16)
                yield

            in_turns(chunk)

    def mlstm_pe():
        pe, st = nc.tensor, "mlstm"
        others_done(pe, "moe")
        pe.wait_ge(w_loaded["mlstm"], 16)
        pe.wait_ge(mlstm_ready, 2)
        with pe.Fori(0, NCH // 2) as i:
            def chunk(lane):
                bk = bank[4 * lane:4 * lane + 4]
                PE, ACTS, DVE, POOL = after(st, i, "AB"[lane])
                done = signals(pe_s, st, "AB"[lane])
                pe.wait_ge(*DVE("h1", back=1))
                yield from turn_x(st, i, lane, bk[0])
                pe.wait_ge(ctxT3_loaded[lane], i * 16 + 16)
                pe.wait_ge(*DVE("xT"))
                for b in range(BC):
                    for n, (src, w) in enumerate(((xnT[lane], gq), (ctxT[lane], gkv))):
                        for k in range(KD):
                            last = nc.tensor.matmul(bk[1][:, b * 2 * HL:(b + 1) * 2 * HL], src[:, k, b * P:(b + 1) * P], w[:, k, :],
                                                    start=n == 0 and k == 0, stop=n == 1 and k == KD - 1)
                last.then_inc(*done("gates"))
                yield
                pe.wait_ge(*DVE("lf"))
                nc.tensor.matmul(bk[0][:, 0:BH], triI[:], lf[lane][:].rearrange("p b h -> p (b h)"), start=True, stop=True).then_inc(*done("cs"))
                yield
                pe.wait_ge(*DVE("a"))
                pe.sem_inc(held, 1)
                nc.tensor.transpose(bk[1][0:BH, 0:P], av[lane][:].rearrange("p b h -> p (b h)"), ident[:]).then_inc(*done("aT"))
                yield
                for b in range(BC):
                    for h in range(HL):
                        rows = slice(DL * (h % 2), DL * (h % 2) + DL)
                        c = b * HL // 2 + h // 2
                        last = nc.tensor.matmul(bk[2 + h % 2][:, c * P:(c + 1) * P], ctxT[lane][rows, h // 2, b * P:(b + 1) * P],
                                                xnT[lane][rows, h // 2, b * P:(b + 1) * P], start=True, stop=True)
                last.then_inc(*done("qk"))
                yield
                pe.wait_ge(*DVE("cmax"))
                pe.sem_inc(held, 1)
                nc.tensor.transpose(bk[0][:, 0:BH], cmax[lane][:], ident[0:BH, 0:BH]).then_inc(*done("cm"))
                yield
                pe.wait_ge(*DVE("cdiag"))
                for b in range(BC):
                    if b:
                        pe.wait_ge(*DVE("cm"))
                    nc.tensor.matmul(bk[1 - b][:], ones[0:BH, :], cdiag[lane][:, b * HL:(b + 1) * HL, :].rearrange("r h s -> r (h s)"),
                                     start=True, stop=False)
                    nc.tensor.matmul(bk[1 - b][:], ident_b[:], late_b[:], start=False, stop=True).then_inc(*done(f"cb{b}"))
                    yield
                pe.wait_ge(ctx_loaded[lane], i * 32 + 32)
                for b in range(BC):
                    pe.wait_ge(*DVE(f"cT1"))
                    for h in range(HL):
                        last = nc.tensor.matmul(bk[b][:, h * (DL + 1):(h + 1) * (DL + 1)], cT[lane][:, h % 2, b * HL // 2 + h // 2, :],
                                                vext[lane][:, b, h, :], start=True, stop=True)
                    last.then_inc(*done(f"ho{b}"))
                    yield

            in_turns(chunk)

    def mlstm_act():
        act, st = nc.scalar, "mlstm"
        others_done(act, "moe")
        with act.Fori(0, NCH // 2) as i:
            def chunk(lane):
                bk = bank[4 * lane:4 * lane + 4]
                PE, ACTS, DVE, POOL = after(st, i, "AB"[lane])
                done = signals(act_s, st, "AB"[lane])
                yield from prep(st, i, lane)
                act.wait_ge(*DVE("nab"))
                nc.scalar.activation(yv[lane][:], nab[lane][:], ACT.Exp).then_inc(*done("ey"))
                yield
                act.wait_ge(*ACTS("ey"))
                nc.scalar.activation(lnu[lane][:], yv[lane][:], ACT.Ln, bias=ones[:, 0:1]).then_inc(*done("ln"))
                yield
                for b in range(BC):
                    act.wait_ge(*PE(f"cb{b}"))
                    for h in range(HL):
                        last = nc.scalar.activation(decayT[lane][:, h % 2, b * HL // 2 + h // 2, :], bk[1 - b][:, h * P:(h + 1) * P], ACT.Exp,
                                                    bias=av[lane][:, b, h:h + 1], scale=-1.0)
                last.then_inc(*done("D"))
                yield
                act.wait_ge(*DVE("cm"))
                nc.scalar.activation(ne[lane][:], cm[lane][:], ACT.Exp, scale=-1.0).then_inc(*done("ne"))
                yield

            in_turns(chunk)

    def mlstm_pool():
        pool, st = nc.gpsimd, "mlstm"
        others_done(pool, "moe")
        nc.gpsimd.memset(mhalf8[:], -0.5).then_inc(zeroed, 1)
        pool.wait_ge(zeroed, 2)
        with pool.Fori(0, NCH // 2) as i:
            def chunk(lane):
                PE, ACTS, DVE, POOL = after(st, i, "AB"[lane])
                done = signals(pool_s, st, "AB"[lane])
                pool.wait_ge(*DVE("hvar"))
                nc.gpsimd.tensor_tensor(hrs[lane][:].rearrange("p b h -> p (b h)"), hvar[lane][:].rearrange("p b h -> p (b h)"), mhalf8[:],
                                        ALU.pow).then_inc(*done("hrs"))
                yield
                pool.wait_ge(*DVE("hn"))
                nc.gpsimd.tensor_tensor(hce[lane][:], hce[lane][:], over(lnw1[:], BC), ALU.mult).then_inc(*done("w"))
                yield
                yield from stats_root(st, i, lane)

            in_turns(chunk)

    def mlstm_dve():
        dve, st = nc.vector, "mlstm"
        others_done(dve, "moe")
        dve.wait_ge(w_loaded["mlstm"], 16)
        for v in vext:
            last = nc.vector.memset(v[:, :, :, DL:], 1.0)
        last.then_inc(mlstm_ready, 1)
        nc.vector.tensor_copy(ident_b[:], ident[:])
        nc.vector.tensor_tensor(triI[:], ident[:], C("tri"), ALU.add)
        nc.vector.tensor_tensor(gkv[:].rearrange("p k g -> p (k g)"), LW("gk"), LW("gv"), ALU.add)
        nc.vector.tensor_scalar(lnw1[:], LW("lnw"), 1.0, None, ALU.add)
        nc.vector.tensor_scalar(late_b[:].rearrange("p (h s) -> p h s", h=HL), over(C("late"), HL), 1e30, None, ALU.mult).then_inc(mlstm_ready, 1)
        V = nc.vector
        with dve.Fori(0, NCH // 2) as i:
            def chunk(lane):
                c = 2 * i + lane
                bk = bank[4 * lane:4 * lane + 4]
                PE, ACTS, DVE, POOL = after(st, i, "AB"[lane])
                done = signals(dve_s, st, "AB"[lane])
                dve.wait_ge(*PE("xT"))
                V.tensor_copy(xnT[lane][:].rearrange("p k t -> p (k t)"), bk[0][:]).then_inc(*done("xT"))
                yield
                dve.wait_ge(*PE("gates"))
                V.tensor_tensor(gt[lane][:], bk[1][:, 0:BC * 2 * HL].rearrange("p (b g) -> p b g", b=BC), over(LW("gb"), BC), ALU.add).then_inc(*done("gt"))
                yield
                dve.wait_ge(*DVE("gt"))
                fg, ig = gt[lane][:, :, HL:], gt[lane][:, :, 0:HL]
                V.tensor_scalar(mnf[lane][:], fg, 0.0, None, ALU.min).then_inc(*done("mnf"))
                yield
                dve.wait_ge(*DVE("mnf"))
                V.scalar_tensor_tensor(nab[lane][:], mnf[lane][:], 2.0, fg, ALU.mult, ALU.subtract).then_inc(*done("nab"))
                yield
                dve.wait_ge(*ACTS("ey"))
                V.tensor_scalar(uu[lane][:], yv[lane][:], 1.0, None, ALU.add).then_inc(*done("u"))
                yield
                dve.wait_ge(*DVE("u"))
                V.scalar_tensor_tensor(e1[lane][:], uu[lane][:], -1.0, yv[lane][:], ALU.add, ALU.subtract).then_inc(*done("e1"))
                yield
                V.reciprocal(ru[lane][:], uu[lane][:]).then_inc(*done("ru"))
                yield
                dve.wait_ge(*DVE("ru"))
                V.tensor_tensor(cr[lane][:], e1[lane][:], ru[lane][:], ALU.mult).then_inc(*done("cr"))
                yield
                dve.wait_ge(*ACTS("ln"))
                V.tensor_tensor(lnu[lane][:], mnf[lane][:], lnu[lane][:], ALU.subtract).then_inc(*done("t"))
                yield
                dve.wait_ge(*DVE("t"))
                V.tensor_tensor(lf[lane][:], lnu[lane][:], cr[lane][:], ALU.add).then_inc(*done("lf"))
                yield
                dve.wait_ge(*PE("cs"))
                V.tensor_copy(cs[lane][:].rearrange("p b h -> p (b h)"), bk[0][:, 0:BH]).then_inc(*done("cs"))
                yield
                V.tensor_tensor(av[lane][:], ig, bk[0][:, 0:BH].rearrange("p (b h) -> p b h", b=BC), ALU.subtract).then_inc(*done("a"))
                yield
                dve.wait_ge(*PE("aT"))
                V.tensor_copy(aT[lane][:], bk[1][0:BH, 0:P]).then_inc(*done("aT"))
                yield
                dve.wait_ge(*DVE("aT"))
                V.tensor_tensor_scan(cmax[lane][:], aT[lane][:], aT[lane][:], -3.0e38, ALU.max, ALU.max).then_inc(*done("cmax"))
                yield
                dve.wait_ge(*DVE("cmax"))
                V.tensor_tensor(cdiag[lane][:], over(cmax[lane][:], BH), wide(ident[0:BH, 0:BH], P), ALU.mult).then_inc(*done("cdiag"))
                yield
                dve.wait_ge(*PE("cm"))
                V.tensor_tensor(cm[lane][:].rearrange("p b h -> p (b h)"), bk[0][:, 0:BH], cs[lane][:].rearrange("p b h -> p (b h)"), ALU.add).then_inc(*done("cm"))
                yield
                dve.wait_ge(*ACTS("D"))
                for par in range(2):
                    V.scalar_tensor_tensor(cT[lane][:, par].rearrange("p c s -> p (c s)"), bk[2 + par][:], DL ** -0.5,
                                           decayT[lane][:, par].rearrange("p c s -> p (c s)"), ALU.mult, ALU.mult).then_inc(*done(f"cT{par}"))
                    yield
                dve.wait_ge(*PE("ho1"))
                sums = [bk[b][:, 0:HL * (DL + 1)].rearrange("p (h c) -> p h c", h=HL) for b in range(BC)]
                for b in range(BC):
                    V.tensor_copy(ab[lane][:, b, :], sums[b][:, :, DL]).then_inc(*done(f"ab{b}"))
                    yield
                dve.wait_ge(*DVE("ab1"))
                V.scalar_tensor_tensor(nr[lane][:], ab[lane][:], -1.0, ab[lane][:], ALU.mult, ALU.max).then_inc(*done("abs"))
                yield
                dve.wait_ge(*DVE("abs"))
                dve.wait_ge(*ACTS("ne"))
                V.tensor_tensor(nr[lane][:], nr[lane][:], ne[lane][:], ALU.max).then_inc(*done("nr"))
                yield
                dve.wait_ge(*DVE("nr"))
                V.tensor_scalar(nr[lane][:], nr[lane][:], 1e-6, None, ALU.add).then_inc(*done("nre"))
                yield
                dve.wait_ge(*DVE("nre"))
                V.reciprocal(nr[lane][:], nr[lane][:]).then_inc(*done("rn"))
                yield
                dve.wait_ge(*DVE("rn"))
                for b in range(BC):
                    V.tensor_tensor(hst[lane][:, b, :].rearrange("p (h d) -> p h d", h=HL), sums[b][:, :, 0:DL], wide(nr[lane][:, b, :], DL),
                                    ALU.mult).then_inc(*done(f"h{b}"))
                    yield
                dve.wait_ge(*DVE("h1"))
                h4 = [t[:].rearrange("p b (h d) -> p (b h) d", h=HL) for t in (hst[lane], hce[lane], hq[lane])]
                f8 = [t[:].rearrange("p b h -> p (b h)") for t in (hsum[lane], hsq[lane], hvar[lane], hrs[lane])]
                V.tensor_reduce(f8[0], h4[0], AX.X, ALU.add).then_inc(*done("hsum"))
                yield
                dve.wait_ge(*DVE("hsum"))
                V.scalar_tensor_tensor(h4[1], wide(f8[0], DL), -1.0 / DL, h4[0], ALU.mult, ALU.add).then_inc(*done("hce"))
                yield
                dve.wait_ge(*DVE("hce"))
                V.tensor_tensor(h4[2], h4[1], h4[1], ALU.mult).then_inc(*done("hq"))
                yield
                dve.wait_ge(*DVE("hq"))
                V.tensor_reduce(f8[1], h4[2], AX.X, ALU.add).then_inc(*done("hsq"))
                yield
                dve.wait_ge(*DVE("hsq"))
                V.tensor_scalar(f8[2], f8[1], 1.0 / DL, EPS, ALU.mult, ALU.add).then_inc(*done("hvar"))
                yield
                dve.wait_ge(*POOL("hrs"))
                V.tensor_tensor(h4[1], h4[1], wide(f8[3], DL), ALU.mult).then_inc(*done("hn"))
                yield
                dve.wait_ge(*POOL("w"))
                V.tensor_tensor(x[:, bass.ds(c * BC, BC), :], hce[lane][:], x[:, bass.ds(c * BC, BC), :], ALU.add).then_inc(*done("res"))
                yield
                yield from stats(st, i, lane)

            in_turns(chunk)

    BW = weights["bit"]
    ROUND = 1.5 * 2.0 ** 23
    KI = INNER // P
    NB_W = ("wg", "wu", "wd")
    wq_b = {n: area(f"q_{n}", [P, KD * INNER], k * 1024, BF16) for k, n in enumerate(NB_W)}
    wgq, wuq = (wq_b[n].rearrange("p (k f) -> p k f", k=KD) for n in ("wg", "wu"))
    wdq = wq_b["wd"].rearrange("p (k d) -> p k d", k=KI)
    wtmp = area("wtmp", [P, KD * INNER], 3072)
    wsum = area("wsum", [P, 3], 5120)
    wsc = area("wsc", [P, 3], 5123)
    winv = area("winv", [P, 3], 5126)
    id_b = area("id_b", [P, P], 5136, BF16)
    BIT_LANE = 8280
    xr = [area(f"xr{n}", [P, BC, D], 5200 + n * BIT_LANE) for n in range(2)]
    xq = [area(f"xq{n}", [P, BC, D], 5712 + n * BIT_LANE, BF16) for n in range(2)]
    xqT = [area(f"xqT{n}", [P, KD, TOK], 5968 + n * BIT_LANE, BF16) for n in range(2)]
    sil = [area(f"sil{n}", [P, 2, 512], 6224 + n * BIT_LANE) for n in range(2)]
    hb = [area(f"hb{n}", [P, BC, INNER], 7248 + n * BIT_LANE) for n in range(2)]
    hr = [area(f"hr{n}", [P, BC, INNER], 9296 + n * BIT_LANE) for n in range(2)]
    hqb = [area(f"hqb{n}", [P, BC, INNER], 11344 + n * BIT_LANE, BF16) for n in range(2)]
    hqT = [area(f"hqT{n}", [P, BC, KI, P], 12368 + n * BIT_LANE, BF16) for n in range(2)]
    am, qs, qi, am2, qs2, qi2, sc_g, sc_u, sc_d = (
        [area(f"b{k}_{n}", [P, BC], 13392 + 2 * k + n * BIT_LANE) for n in range(2)] for k in range(9))
    bit_sum, bit_ready = sem("weight_magnitudes_summed"), sem("weights_quantised")
    HU = [(b, hh) for b in range(BC) for hh in range(2)]
    stage("bit", NCH // 2, pe=both(["xqT", "n0", "n1", "n2", "n3", "hT0", "hT1", "out0", "out1"]),
          act=both(["prep0", "prep1", "n0", "n1", "n2", "n3"]),
          dve=both(["am", "amc", "rq", "qs", "qi", "scg", "scu", "r0", "r1", "q", "xqT", "n0", "n1", "am20", "amc20", "rq20", "qs20",
                    "n2", "n3", "am21", "amc21", "rq21", "qs21", "qi20", "r20", "q20", "scd0", "hT0", "qi21", "r21", "q21", "scd1",
                    "hT1", "res0", "res1"] + LN_DVE),
          pool=both(["rstd"]))

    def up_banks(n):
        return ((1, 2), (3, 0))[n % 2]

    def bit_pe():
        pe, st = nc.tensor, "bit"
        others_done(pe, "mlstm")
        pe.wait_ge(bit_sum, 3)
        nc.tensor.matmul(bank[0][:, 0:3], ones[:], wsum[:], start=True, stop=True).then_inc(bit_sum, 1)
        pe.wait_ge(bit_ready, 1)
        with pe.Fori(0, NCH // 2) as i:
            def chunk(lane):
                bk = bank[4 * lane:4 * lane + 4]
                PE, ACTS, DVE, POOL = after(st, i, "AB"[lane])
                done = signals(pe_s, st, "AB"[lane])
                pe.wait_ge(*DVE("q"))
                for k in range(KD):
                    for b in range(BC):
                        last = nc.tensor.transpose(bk[0][:].bitcast(BF16)[:, (k * BC + b) * P:(k * BC + b + 1) * P], xq[lane][:, b, k * P:(k + 1) * P], id_b[:])
                last.then_inc(*done("xqT"))
                yield
                pe.wait_ge(*DVE("xqT"))
                for n, (b, hh) in enumerate(HU):
                    if n >= 2:
                        pe.wait_ge(*DVE(f"n{n - 2}"))
                    for w, dst in ((wgq, up_banks(n)[0]), (wuq, up_banks(n)[1])):
                        for k in range(KD):
                            last = nc.tensor.matmul(bk[dst][:], xqT[lane][:, k, b * P:(b + 1) * P], w[:, k, hh * 512:(hh + 1) * 512],
                                                    start=k == 0, stop=k == KD - 1)
                    last.then_inc(*done(f"n{n}"))
                    yield
                for b in range(BC):
                    pe.wait_ge(*DVE(f"q2{b}"))
                    for k in range(KI):
                        last = nc.tensor.transpose(bk[1 + b][:].bitcast(BF16)[:, k * P:(k + 1) * P], hqb[lane][:, b, k * P:(k + 1) * P], id_b[:])
                    last.then_inc(*done(f"hT{b}"))
                    yield
                for b in range(BC):
                    pe.wait_ge(*DVE(f"hT{b}"))
                    for k in range(KI):
                        last = nc.tensor.matmul(bk[3][:, b * D:(b + 1) * D], hqT[lane][:, b, k, :], wdq[:, k, :], start=k == 0, stop=k == KI - 1)
                    last.then_inc(*done(f"out{b}"))
                    yield

            in_turns(chunk)

    def bit_act():
        act, st = nc.scalar, "bit"
        others_done(act, "mlstm")
        with act.Fori(0, NCH // 2) as i:
            def chunk(lane):
                bk = bank[4 * lane:4 * lane + 4]
                PE, ACTS, DVE, POOL = after(st, i, "AB"[lane])
                done = signals(act_s, st, "AB"[lane])
                yield from prep(st, i, lane)
                for n, (b, hh) in enumerate(HU):
                    act.wait_ge(*PE(f"n{n}"))
                    act.wait_ge(*DVE("scg"))
                    if n >= 2:
                        act.wait_ge(*DVE(f"n{n - 2}"))
                    nc.scalar.activation(sil[lane][:, n % 2, :], bk[up_banks(n)[0]][:], ACT.Silu, scale=sc_g[lane][:, b:b + 1]).then_inc(*done(f"n{n}"))
                    yield

            in_turns(chunk)

    def bit_pool():
        pool, st = nc.gpsimd, "bit"
        others_done(pool, "mlstm")
        with pool.Fori(0, NCH // 2) as i:
            def chunk(lane):
                PE, ACTS, DVE, POOL = after(st, i, "AB"[lane])
                done = signals(pool_s, st, "AB"[lane])
                yield from stats_root(st, i, lane)

            in_turns(chunk)

    def bit_dve():
        dve, st = nc.vector, "bit"
        V = nc.vector
        others_done(dve, "mlstm")
        dve.wait_ge(w_loaded["bit"], 16)
        for n, name in enumerate(NB_W):
            V.tensor_reduce(wsum[:, n:n + 1], BW(name), AX.X, ALU.add, apply_absolute_value=True).then_inc(bit_sum, 1)
        V.tensor_copy(id_b[:], ident[:])
        dve.wait_ge(bit_sum, 4)
        V.tensor_scalar(wsum[:], bank[0][:, 0:3], 1.0 / (D * INNER), 1e-5, ALU.mult, ALU.max).then_inc(bit_q, 1)
        dve.wait_ge(bit_q, 1)
        V.reciprocal(wsc[:], wsum[:]).then_inc(bit_q, 1)
        dve.wait_ge(bit_q, 2)
        V.reciprocal(winv[:], wsc[:]).then_inc(bit_q, 1)
        for n, name in enumerate(NB_W):
            dve.wait_ge(bit_q, 3 + 3 * n)
            V.tensor_scalar(wtmp[:], BW(name), wsc[:, n:n + 1], ROUND, ALU.mult, ALU.add).then_inc(bit_q, 1)
            dve.wait_ge(bit_q, 4 + 3 * n)
            V.tensor_scalar(wtmp[:], wtmp[:], ROUND, 1.0, ALU.subtract, ALU.min).then_inc(bit_q, 1)
            dve.wait_ge(bit_q, 5 + 3 * n)
            V.tensor_scalar(wq_b[name], wtmp[:], -1.0, None, ALU.max).then_inc(bit_q, 1)
        dve.wait_ge(bit_q, 12)
        dve.sem_inc(bit_ready, 1)
        with dve.Fori(0, NCH // 2) as i:
            def chunk(lane):
                c = 2 * i + lane
                bk = bank[4 * lane:4 * lane + 4]
                PE, ACTS, DVE, POOL = after(st, i, "AB"[lane])
                done = signals(dve_s, st, "AB"[lane])
                dve.wait_ge(*ACTS("prep1"))
                V.tensor_reduce(am[lane][:], xn[lane][:], AX.X, ALU.max, apply_absolute_value=True).then_inc(*done("am"))
                yield
                dve.wait_ge(*DVE("am"))
                V.tensor_scalar(am[lane][:], am[lane][:], 1e-5, None, ALU.max).then_inc(*done("amc"))
                yield
                dve.wait_ge(*DVE("amc"))
                V.reciprocal(am[lane][:], am[lane][:]).then_inc(*done("rq"))
                yield
                dve.wait_ge(*DVE("rq"))
                V.tensor_scalar(qs[lane][:], am[lane][:], 127.0, None, ALU.mult).then_inc(*done("qs"))
                yield
                dve.wait_ge(*DVE("qs"))
                V.reciprocal(qi[lane][:], qs[lane][:]).then_inc(*done("qi"))
                yield
                dve.wait_ge(*DVE("qi"))
                V.tensor_scalar(sc_g[lane][:], qi[lane][:], winv[:, 0:1], None, ALU.mult).then_inc(*done("scg"))
                yield
                V.tensor_scalar(sc_u[lane][:], qi[lane][:], winv[:, 1:2], None, ALU.mult).then_inc(*done("scu"))
                yield
                for b in range(BC):
                    V.tensor_scalar(xr[lane][:, b, :], xn[lane][:, b, :], qs[lane][:, b:b + 1], ROUND, ALU.mult, ALU.add).then_inc(*done(f"r{b}"))
                    yield
                dve.wait_ge(*DVE("r1"))
                V.tensor_scalar(xq[lane][:], xr[lane][:], ROUND, 127.0, ALU.subtract, ALU.min).then_inc(*done("q"))
                yield
                dve.wait_ge(*PE("xqT"))
                V.tensor_scalar(xqT[lane][:].rearrange("p k t -> p (k t)"), bk[0][:].bitcast(BF16)[:, 0:KD * TOK], -128.0, None,
                                ALU.max).then_inc(*done("xqT"))
                yield

                def gated(n):
                    b, hh = HU[n]
                    dve.wait_ge(*ACTS(f"n{n}"))
                    V.scalar_tensor_tensor(hb[lane][:, b, hh * 512:(hh + 1) * 512], bk[up_banks(n)[1]][:], sc_u[lane][:, b:b + 1], sil[lane][:, n % 2, :],
                                           ALU.mult, ALU.mult).then_inc(*done(f"n{n}"))
                    yield

                def largest(b):
                    dve.wait_ge(*DVE(f"n{2 * b + 1}"))
                    V.tensor_reduce(am2[lane][:, b:b + 1], hb[lane][:, b, :], AX.X, ALU.max, apply_absolute_value=True).then_inc(*done(f"am2{b}"))
                    yield
                    dve.wait_ge(*DVE(f"am2{b}"))
                    V.tensor_scalar(am2[lane][:, b:b + 1], am2[lane][:, b:b + 1], 1e-5, None, ALU.max).then_inc(*done(f"amc2{b}"))
                    yield
                    dve.wait_ge(*DVE(f"amc2{b}"))
                    V.reciprocal(am2[lane][:, b:b + 1], am2[lane][:, b:b + 1]).then_inc(*done(f"rq2{b}"))
                    yield
                    dve.wait_ge(*DVE(f"rq2{b}"))
                    V.tensor_scalar(qs2[lane][:, b:b + 1], am2[lane][:, b:b + 1], 127.0, None, ALU.mult).then_inc(*done(f"qs2{b}"))
                    yield

                yield from gated(0)
                yield from gated(1)
                yield from largest(0)
                yield from gated(2)
                yield from gated(3)
                yield from largest(1)
                for b in range(BC):
                    dve.wait_ge(*DVE(f"qs2{b}"))
                    V.reciprocal(qi2[lane][:, b:b + 1], qs2[lane][:, b:b + 1]).then_inc(*done(f"qi2{b}"))
                    yield
                    V.tensor_scalar(hr[lane][:, b, :], hb[lane][:, b, :], qs2[lane][:, b:b + 1], ROUND, ALU.mult, ALU.add).then_inc(*done(f"r2{b}"))
                    yield
                    dve.wait_ge(*DVE(f"r2{b}"))
                    V.tensor_scalar(hqb[lane][:, b, :], hr[lane][:, b, :], ROUND, 127.0, ALU.subtract, ALU.min).then_inc(*done(f"q2{b}"))
                    yield
                    V.tensor_scalar(sc_d[lane][:, b:b + 1], qi2[lane][:, b:b + 1], winv[:, 2:3], None, ALU.mult).then_inc(*done(f"scd{b}"))
                    yield
                    dve.wait_ge(*PE(f"hT{b}"))
                    V.tensor_scalar(hqT[lane][:, b].rearrange("p k t -> p (k t)"), bk[1 + b][:].bitcast(BF16), -128.0, None,
                                    ALU.max).then_inc(*done(f"hT{b}"))
                    yield
                dve.wait_ge(*PE("out1"))
                for b in range(BC):
                    V.scalar_tensor_tensor(x[:, bass.ds(c * BC + b, 1), :], bk[3][:, b * D:(b + 1) * D], sc_d[lane][:, b:b + 1],
                                           x[:, bass.ds(c * BC + b, 1), :], ALU.mult, ALU.add).then_inc(*done(f"res{b}"))
                    yield
                yield from stats(st, i, lane)

            in_turns(chunk)

    def bit_sp():
        sp = nc.sync
        others_done(sp, "mlstm")
        load_weights(sp, "mqa")


    QW = weights["mqa"]
    q_w = QW("wq").rearrange("p (k m) -> p k m", k=KD)
    k_w, v_w = (QW(n).rearrange("p (k m) -> p k m", k=KD) for n in ("wk", "wv"))
    wout = QW("wout").rearrange("p (k n) -> p k n", k=HM)
    w1 = QW("w1").rearrange("p (k f) -> p k f", k=KD)
    w2 = QW("w2").rearrange("p (k n) -> p k n", k=KI)
    q4 = area("q4", [P, HM, TOK], 0)
    m4 = area("m4", [P, HM, TOK], 2048)
    ff = area("ff", [P, KI, TOK], 4096)
    prob4 = area("prob4", [P, 4, FAN, P], 6144)
    probT4 = area("probT4", [P, 2, FAN, P], 8192)
    masked = area("masked", [P, 2, FAN, P], 9216)
    k4 = area("k4", [P, TOK], 10240)
    v4 = area("v4", [P, BC, HD], 10496)
    mask4 = area("mask4", [P, BC, P], 10624)
    ctx4 = area("ctx4", [P, BC, D], 10880)
    cn4 = area("cn4", [P, BC, D], 11392)
    cnT = area("cnT", [P, KD, TOK], 11904)
    sgb = area("sgb", [P, 2, TOK], 12416)
    sm4 = area("sm4", [P, 3, 4, FAN], 12928)
    cbn = area("cbn", [P, BC, 6], 12976)
    cmv = area("cmv", [P, BC, 2], 12988)
    cveps = area("cveps", [P, BC], 12992)
    crstd = area("crstd", [P, BC], 12994)
    DORDER4 = []
    for t in range(UNITS + 3):
        DORDER4 += [("add", t), ("max", t)] * (t < UNITS) + [("rec", t - 1)] * (0 <= t - 1 < UNITS)
        DORDER4 += [("copy", t - 2)] * (0 <= t - 2 < UNITS) + [("o", t - 3)] * (0 <= t - 3 < UNITS and t % 2 == 0)
    stage("mqa", NCH,
          pe=["xT"] + [f"ff{n}" for n in range(KI)] + ["cT", "k", "v", "q0", "q1", "q2", "q3"] + [f"{a}{t}" for a, t in ORDER] + ["out0", "out1"],
          act=["prep0", "prep1"] + [f"ff{n}" for n in range(KI)] + [f"exp{t}" for t in range(UNITS)],
          dve=["xT", "cbn0", "cbn1", "cag0", "cag1", "cveps", "ff0", "ff1", "cn0", "cn1"] + [f"ff{n}" for n in range(2, KI)]
          + ["cT", "k", "v", "q0", "q1", "q2", "q3"] + [f"{a}{t}" for a, t in DORDER4] + ["res"] + LN_DVE,
          pool=["crstd"] + [f"norm{t}" for t in range(UNITS)] + ["rstd"])

    def mqa_sp():
        sp, st = nc.sync, "mqa"
        others_done(sp, "bit")
        load_weights(sp, "low")
        with sp.Fori(0, NCH) as i:
            sp.wait_ge(dve_s.sem, dve_s.at(st, i, "cn1", back=1))
            sp.dma_start(ctx4[:], ctx_dram[:, bass.ds(i * BC, BC), :]).then_inc(ctx4_loaded, 16)
            sp.wait_ge(dve_s.sem, dve_s.at(st, i, f"add{UNITS - 1}", back=1))
            sp.dma_start(mask4[:], mask_dram[:, bass.ds(i * BC, BC), :]).then_inc(mask_loaded, 16)

    def mqa_pe():
        pe, st = nc.tensor, "mqa"
        others_done(pe, "bit")
        pe.wait_ge(w_loaded[st], 16)
        done = signals(pe_s, st)
        with pe.Fori(0, NCH) as i:
            PE, ACTS, DVE, POOL = after(st, i)
            alone(turn_x(st, i))
            pe.wait_ge(*DVE("xT"))
            for n in range(KI):
                if n >= 4:
                    pe.wait_ge(*DVE(f"ff{n - 4}"))
                for part, first in ((0, INNER + n * P), (1, n * P)):
                    for k in range(KD):
                        last = nc.tensor.matmul(bank[n % 4][:, part * TOK:(part + 1) * TOK], w1[:, k, first:first + P], xnT[0][:, k, :],
                                                start=k == 0, stop=k == KD - 1)
                last.then_inc(*done(f"ff{n}"))
            pe.wait_ge(*DVE("res", back=1))
            pe.wait_ge(*DVE("cn1"))
            for k in range(KD):
                for b in range(BC):
                    last = nc.tensor.transpose(bank[6][:, (k * BC + b) * P:(k * BC + b + 1) * P], cn4[:, b, k * P:(k + 1) * P], ident[:])
            last.then_inc(*done("cT"))
            pe.wait_ge(*DVE("cT"))
            for k in range(KD):
                last = nc.tensor.matmul(bank[4][:, 0:TOK], k_w[:, k, :], cnT[:, k, :], start=k == 0, stop=k == KD - 1)
            last.then_inc(*done("k"))
            for b in range(BC):
                for k in range(KD):
                    last = nc.tensor.matmul(bank[5][:, b * HD:(b + 1) * HD], cnT[:, k, b * P:(b + 1) * P], v_w[:, k, 0:HD],
                                            start=k == 0, stop=k == KD - 1)
            last.then_inc(*done("v"))
            for g in range(4):
                pe.wait_ge(*DVE(f"ff{g + 4}"))
                for m in range(2):
                    mm = 2 * g + m
                    for k in range(KD):
                        last = nc.tensor.matmul(bank[g][:, m * TOK:(m + 1) * TOK], q_w[:, k, mm * P:(mm + 1) * P], xnT[0][:, k, :],
                                                start=k == 0, stop=k == KD - 1)
                last.then_inc(*done(f"q{g}"))
            pe.wait_ge(*DVE("q3"))
            for what, t in ORDER:
                b, u, par = unit(t)
                rows = slice(HD * par, HD * par + HD)
                if what == "S":
                    if t >= 2:
                        pe.wait_ge(*DVE(f"add{t - 2}"))
                    for j in range(FAN):
                        last = nc.tensor.matmul(bank[t % 2][:, j * P:(j + 1) * P], q4[rows, FAN * u + j, b * P:(b + 1) * P],
                                                k4[rows, b * P:(b + 1) * P], start=True, stop=True)
                elif what == "T":
                    pe.wait_ge(*POOL(f"norm{t}"))
                    if t >= 2:
                        pe.wait_ge(*DVE(f"copy{t - 2}"))
                    for j in range(FAN):
                        last = nc.tensor.transpose(bank[2 + t % 2][:, j * P:(j + 1) * P], prob4[:, t % 4, j, :], ident[:])
                else:
                    pe.wait_ge(*DVE(f"copy{t}"))
                    if b == 1 and par == 0:
                        pe.wait_ge(*DVE(f"o{t - 3}"))
                    last = nc.tensor.matmul(bank[4 + u][rows, :], v4[:, b, :], probT4[:, t % 2].rearrange("p j s -> p (j s)"),
                                            start=True, stop=True)
                last.then_inc(*done(f"{what}{t}"))
            for b in range(BC):
                pe.wait_ge(*DVE(f"o{4 * b + 3}"))
                for n, (src, w) in enumerate(((ff, w2), (m4, wout))):
                    for k in range(HM):
                        last = nc.tensor.matmul(bank[6][:, b * D:(b + 1) * D], src[:, k, b * P:(b + 1) * P], w[:, k, :],
                                                start=n == 0 and k == 0, stop=n == 1 and k == HM - 1)
                last.then_inc(*done(f"out{b}"))

    def mqa_act():
        act, st = nc.scalar, "mqa"
        others_done(act, "bit")
        done = signals(act_s, st)
        with act.Fori(0, NCH) as i:
            PE, ACTS, DVE, POOL = after(st, i)
            alone(prep(st, i))
            for n in range(KI):
                act.wait_ge(*PE(f"ff{n}"))
                if n >= 2:
                    act.wait_ge(*DVE(f"ff{n - 2}"))
                nc.scalar.activation(sgb[:, n % 2, :], bank[n % 4][:, 0:TOK], ACT.Silu).then_inc(*done(f"ff{n}"))
            for t in range(UNITS):
                act.wait_ge(*DVE(f"max{t}"))
                if t >= 4:
                    act.wait_ge(*PE(f"T{t - 4}"))
                for j in range(FAN):
                    last = nc.scalar.activation(prob4[:, t % 4, j, :], masked[:, t % 2, j, :], ACT.Exp,
                                                bias=sm4[:, 0, t % 4, j:j + 1], accum_out=sm4[:, 1, t % 4, j:j + 1])
                last.then_inc(*done(f"exp{t}"))

    def mqa_pool():
        pool, st = nc.gpsimd, "mqa"
        others_done(pool, "bit")
        done = signals(pool_s, st)
        with pool.Fori(0, NCH) as i:
            PE, ACTS, DVE, POOL = after(st, i)
            pool.wait_ge(*DVE("cveps"))
            nc.gpsimd.tensor_tensor(crstd[:], cveps[:], mhalf[:], ALU.pow).then_inc(*done("crstd"))
            for t in range(UNITS):
                pool.wait_ge(*DVE(f"rec{t}"))
                nc.gpsimd.tensor_tensor(prob4[:, t % 4], prob4[:, t % 4], sm4[:, 2, t % 4, :].unsqueeze(2).to_broadcast([P, FAN, P]),
                                        ALU.mult).then_inc(*done(f"norm{t}"))
            alone(stats_root(st, i))

    def mqa_dve():
        dve, st = nc.vector, "mqa"
        V = nc.vector
        others_done(dve, "bit")
        dve.wait_ge(w_loaded[st], 16)
        done = signals(dve_s, st)
        with dve.Fori(0, NCH) as i:
            PE, ACTS, DVE, POOL = after(st, i)

            def ffn(n):
                dve.wait_ge(*ACTS(f"ff{n}"))
                V.tensor_tensor(ff[:, n, :], bank[n % 4][:, TOK:2 * TOK], sgb[:, n % 2, :], ALU.mult).then_inc(*done(f"ff{n}"))

            dve.wait_ge(*PE("xT"))
            for k in range(KD):
                last = V.tensor_scalar(xnT[0][:, k, :], bank[7][:, k * TOK:(k + 1) * TOK], QW("ln_g")[:, k:k + 1], QW("ln_b")[:, k:k + 1],
                                       ALU.mult, ALU.add)
            last.then_inc(*done("xT"))
            dve.wait_ge(ctx4_loaded, i * 16 + 16)
            dve.sem_inc(held, 1)
            for b in range(BC):
                V.bn_stats(cbn[:, b, :], ctx4[:, b, :]).then_inc(*done(f"cbn{b}"))
            for b in range(BC):
                dve.wait_ge(*DVE(f"cbn{b}"))
                dve.sem_inc(held, 1)
                V.bn_aggr(cmv[:, b, :], cbn[:, b, :]).then_inc(*done(f"cag{b}"))
            dve.wait_ge(*DVE("cag1"))
            V.tensor_scalar(cveps[:], cmv[:, :, 1], EPS, None, ALU.add).then_inc(*done("cveps"))
            ffn(0)
            ffn(1)
            dve.wait_ge(*POOL("crstd"))
            for b in range(BC):
                V.tensor_scalar(cn4[:, b, :], ctx4[:, b, :], cmv[:, b, 0:1], crstd[:, b:b + 1], ALU.subtract, ALU.mult).then_inc(*done(f"cn{b}"))
            for n in range(2, KI):
                ffn(n)
            dve.wait_ge(*PE("cT"))
            for k in range(KD):
                last = V.tensor_scalar(cnT[:, k, :], bank[6][:, k * TOK:(k + 1) * TOK], QW("cln_g")[:, k:k + 1], QW("cln_b")[:, k:k + 1],
                                       ALU.mult, ALU.add)
            last.then_inc(*done("cT"))
            dve.wait_ge(*PE("k"))
            V.tensor_copy(k4[:], bank[4][:, 0:TOK]).then_inc(*done("k"))
            dve.wait_ge(*PE("v"))
            V.tensor_copy(v4[:].rearrange("p b d -> p (b d)"), bank[5][:, 0:BC * HD]).then_inc(*done("v"))
            for g in range(4):
                dve.wait_ge(*PE(f"q{g}"))
                V.tensor_scalar(q4[:, 2 * g:2 * g + 2, :].rearrange("p m t -> p (m t)"), bank[g][:], HD ** -0.5, None,
                                ALU.mult).then_inc(*done(f"q{g}"))
            for what, t in DORDER4:
                b, u, par = unit(t)
                if what == "add":
                    dve.wait_ge(*PE(f"S{t}"))
                    if t == 0:
                        dve.wait_ge(mask_loaded, i * 16 + 16)
                    if t >= 2:
                        dve.wait_ge(*ACTS(f"exp{t - 2}"))
                    ins = V.tensor_tensor(masked[:, t % 2], bank[t % 2][:].rearrange("p (j s) -> p j s", j=FAN), over(mask4[:, b, :], FAN), ALU.add)
                elif what == "max":
                    dve.wait_ge(*DVE(f"add{t}"))
                    ins = V.tensor_reduce(sm4[:, 0, t % 4, :], masked[:, t % 2], AX.X, ALU.max, negate=True)
                elif what == "rec":
                    dve.wait_ge(*ACTS(f"exp{t}"))
                    ins = V.reciprocal(sm4[:, 2, t % 4, :], sm4[:, 1, t % 4, :])
                elif what == "copy":
                    dve.wait_ge(*PE(f"T{t}"))
                    ins = V.tensor_copy(probT4[:, t % 2].rearrange("p j s -> p (j s)"), bank[2 + t % 2][:])
                else:
                    dve.wait_ge(*PE(f"PV{t}"))
                    ins = V.tensor_copy(m4[:, FAN * u:FAN * u + FAN, b * P:(b + 1) * P], bank[4 + u][:].rearrange("p (j s) -> p j s", j=FAN))
                ins.then_inc(*done(f"{what}{t}"))
            dve.wait_ge(*PE("out1"))
            V.tensor_tensor(x[:, bass.ds(i * BC, BC), :], bank[6][:].rearrange("p (b d) -> p b d", b=BC),
                            x[:, bass.ds(i * BC, BC), :], ALU.add).then_inc(*done("res"))
            alone(stats(st, i))

    FW = weights["low"]
    RK = 64
    u1 = FW("u1").rearrange("p (k r) -> p k r", k=KD)
    v1 = FW("v1").rearrange("p (j m) -> p j m", m=P)
    u2 = FW("u2").rearrange("p (k r) -> p k r", k=KI)
    pT5 = area("pT5", [P, TOK], 0)
    h5 = area("h5", [P, KI, TOK], 256)
    q5 = area("q5", [RK, TOK], 2304)
    stage("low", NCH, pe=["xT", "p"] + [f"h{g}{half}" for g in range(2) for half in range(2)] + ["q", "out"],
          act=["prep0", "prep1"] + [f"h{g}{half}" for g in range(2) for half in range(2)],
          dve=["xT", "p", "q", "res"], pool=["b2"])

    def low_sp():
        sp = nc.sync
        with sp.Fori(0, NCH) as i:
            sp.wait_ge(dve_s.sem, dve_s.at("low", i, "res"))
            sp.dma_start(out_dram[:, bass.ds(i * BC, BC), :], x[:, bass.ds(i * BC, BC), :]).then_inc(out_stored, 16)

    def low_pe():
        pe, st = nc.tensor, "low"
        others_done(pe, "mqa")
        pe.wait_ge(w_loaded[st], 16)
        done = signals(pe_s, st)
        with pe.Fori(0, NCH) as i:
            PE, ACTS, DVE, POOL = after(st, i)
            alone(turn_x(st, i))
            pe.wait_ge(*DVE("xT"))
            for k in range(KD):
                last = nc.tensor.matmul(bank[0][:, 0:TOK], u1[:, k, :], xnT[0][:, k, :], start=k == 0, stop=k == KD - 1)
            last.then_inc(*done("p"))
            pe.wait_ge(*DVE("p"))
            for g in range(2):
                for half in range(2):
                    rows = slice(RK * half, RK * half + RK)
                    for j in range(2):
                        last = nc.tensor.matmul(bank[1 + 2 * g + half][:, j * TOK:(j + 1) * TOK], v1[rows, 2 * g + j, :], pT5[rows, :],
                                                start=True, stop=True)
                    last.then_inc(*done(f"h{g}{half}"))
            for m in range(KI):
                pe.wait_ge(*ACTS(f"h{m // 4}{1}"))
                last = nc.tensor.matmul(bank[5][0:RK, 0:TOK], u2[:, m, :], h5[:, m, :], start=m == 0, stop=m == KI - 1)
            last.then_inc(*done("q"))
            pe.wait_ge(*DVE("q"))
            pe.wait_ge(*DVE("res", back=1))
            for b in range(BC):
                last = nc.tensor.matmul(bank[6][:, b * D:(b + 1) * D], q5[:, b * P:(b + 1) * P], FW("v2")[0:RK, :], start=True, stop=True)
            last.then_inc(*done("out"))

    def low_act():
        act, st = nc.scalar, "low"
        others_done(act, "mqa")
        act.wait_ge(w_loaded[st], 16)
        done = signals(act_s, st)
        with act.Fori(0, NCH) as i:
            PE, ACTS, DVE, POOL = after(st, i)
            alone(prep(st, i))
            for g in range(2):
                for half in range(2):
                    act.wait_ge(*PE(f"h{g}{half}"))
                    for j in range(2):
                        m = 2 * (2 * g + j) + half
                        last = nc.scalar.activation(h5[:, m, :], bank[1 + 2 * g + half][:, j * TOK:(j + 1) * TOK], ACT.Gelu_apprx_tanh,
                                                    bias=FW("b1")[:, m:m + 1])
                    last.then_inc(*done(f"h{g}{half}"))

    def low_pool():
        pool = nc.gpsimd
        others_done(pool, "mqa")
        pool.wait_ge(w_loaded["low"], 16)
        done = signals(pool_s, "low")
        with pool.Fori(0, NCH) as i:
            pool.wait_ge(act_s.sem, act_s.at("low", i, "prep1"))
            pool.sem_inc(held, 1)
            nc.gpsimd.tensor_tensor(x[:, bass.ds(i * BC, BC), :], x[:, bass.ds(i * BC, BC), :], over(FW("b2"), BC), ALU.add).then_inc(*done("b2"))

    def low_dve():
        dve, st = nc.vector, "low"
        V = nc.vector
        others_done(dve, "mqa")
        done = signals(dve_s, st)
        with dve.Fori(0, NCH) as i:
            PE, ACTS, DVE, POOL = after(st, i)
            dve.wait_ge(*PE("xT"))
            V.tensor_copy(xnT[0][:].rearrange("p k t -> p (k t)"), bank[7][:]).then_inc(*done("xT"))
            dve.wait_ge(*PE("p"))
            V.tensor_copy(pT5[:], bank[0][:, 0:TOK]).then_inc(*done("p"))
            dve.wait_ge(*PE("q"))
            V.tensor_copy(q5[:], bank[5][0:RK, 0:TOK]).then_inc(*done("q"))
            dve.wait_ge(*PE("out"))
            dve.wait_ge(*POOL("b2"))
            V.tensor_tensor(x[:, bass.ds(i * BC, BC), :], bank[6][:].rearrange("p (b d) -> p b d", b=BC),
                            x[:, bass.ds(i * BC, BC), :], ALU.add).then_inc(*done("res"))
    sp_prog = [attn_sp, rec_sp, moe_sp, mlstm_sp, bit_sp, mqa_sp, low_sp]
    pe_prog = [attn_pe, spike_pe, rec_pe, moe_pe, mlstm_pe, bit_pe, mqa_pe, low_pe]
    act_prog = [attn_act, spike_act, rec_act, moe_act, mlstm_act, bit_act, mqa_act, low_act]
    dve_prog = [load_dve, attn_dve, spike_dve, rec_dve, moe_dve, mlstm_dve, bit_dve, mqa_dve, low_dve]
    pool_prog = [load_pool, attn_pool, spike_pool, rec_pool, moe_pool, mlstm_pool, bit_pool, mqa_pool, low_pool]
    block = ctx.enter_context(nc.Block())

    @block.sync
    def _(sp):
        sp.dma_start(x[:], x_dram).then_inc(x_loaded, 16)
        load_weights(sp, "attn")
        sp.dma_start(shape_consts[:], ins["consts"]).then_inc(consts_loaded, 16)
        load_weights(sp, "spike")
        for f in sp_prog:
            f()
        sp.wait_ge(out_stored, 16 * NCH)

    @block.tensor
    def _(pe):
        for f in pe_prog:
            f()

    @block.scalar
    def _(act):
        for f in act_prog:
            f()

    @block.vector
    def _(dve):
        for f in dve_prog:
            f()

    @block.gpsimd
    def _(pool):
        for f in pool_prog:
            f()


def pack(inputs):
    import numpy as np

    def a(name):
        return np.asarray(inputs[name])

    def rows(w):
        return w.reshape(-1, P, w.shape[1]).transpose(1, 0, 2).reshape(P, -1)

    def col(v, n=P):
        return v.reshape(-1, n).T

    def all_rows(v):
        return np.broadcast_to(v.reshape(1, -1), (P, v.size))

    def twice(w):
        return np.concatenate([w, w], 0)

    def put(stage, parts):
        cols = []
        for name, n in LAYOUT[stage]:
            v = parts[name]
            assert v.shape[1] == n and v.shape[0] in (P, 64), (stage, name, v.shape, n)
            if v.shape[0] == 64:
                v = twice(v)
            cols.append(v)
        return np.ascontiguousarray(np.concatenate(cols, 1))

    w = {}
    p = "L0_xattn_"
    w["attn"] = put("attn", dict(wk=rows(a(p + "Wk")), wv=rows(a(p + "Wv")), wq=rows(a(p + "Wq")), bk=col(a(p + "bk")),
                                 bq=col(a(p + "bq")), bv=col(a(p + "bv")), wu=rows(a(p + "Wu")), bu=all_rows(a(p + "bu"))))
    p = "L0_ffn_"
    e_w1 = a(p + "e_w1").reshape(NE0, MD, 2, P).transpose(2, 1, 0, 3).reshape(P, NE0 * P)
    w["spike"] = put("spike", dict(
        enc=rows(a(p + "enc_w")), enc_b=col(a(p + "enc_b")),
        s2c=rows(np.concatenate([a(p + "s2c_w")] * 2, 1)), s2c_b=twice(a(p + "s2c_b").reshape(-1, 1)),
        rw1=a(p + "r_w1"), rb1=a(p + "r_b1").reshape(-1, 1), rw2=a(p + "r_w2"), rb2=all_rows(a(p + "r_b2")),
        ew1=e_w1, eb1=a(p + "e_b1").reshape(NE0 * 2, P).T,
        ew2=a(p + "e_w2").reshape(NE0, 2, P, MD).transpose(2, 0, 1, 3).reshape(P, -1), eb2=all_rows(a(p + "e_b2")),
        c2s=a(p + "c2s_w"), c2s_b=col(a(p + "c2s_b")), dec=rows(a(p + "dec_w")), dec_b=all_rows(a(p + "dec_b")),
        ln_g=all_rows(a(p + "ln_g")), ln_b=all_rows(a(p + "ln_b"))))
    p = "L1_xattn_"
    w["rec"] = put("rec", dict(wi=rows(a(p + "Wi").T), bi=col(a(p + "bi")), wg=rows(a(p + "Wg").T), bg=col(a(p + "bg")),
                               a=rows(a(p + "A").T), bm=rows(a(p + "Bm").T), wo=rows(a(p + "Wo").T), bo=all_rows(a(p + "bo")),
                               decay=col(np.repeat(a(p + "decay").reshape(-1), D // 16))))
    p = "L1_ffn_"
    down = a(p + "ws_down")
    pad = np.zeros((P - (FE - P), D), down.dtype)
    w["moe"] = put("moe", dict(router=rows(a(p + "router_w").T), sgu=rows(a(p + "ws_gate_up")), sdown=rows(np.concatenate([down, pad], 0))))
    gu = np.concatenate([a(p + "w_gate").reshape(NE, KD, P, FE), a(p + "w_up").reshape(NE, KD, P, FE)], 3)
    w["gate_up"] = np.ascontiguousarray(gu.transpose(0, 2, 1, 3).reshape(NE, P, KD * 2 * FE))
    wd = a(p + "w_down")
    w["down"] = np.ascontiguousarray(wd)
    p = "L2_xattn_"
    gates = np.concatenate([a(p + "w_igate"), a(p + "w_fgate")], 0).T
    w["mlstm"] = put("mlstm", dict(gq=rows(gates[:D]), gk=rows(gates[D:2 * D]), gv=rows(gates[2 * D:]),
                                   gb=all_rows(np.concatenate([a(p + "b_igate"), a(p + "b_fgate")])), lnw=all_rows(a(p + "ln_weight"))))
    p = "L2_ffn_"
    w["bit"] = put("bit", dict(wg=rows(a(p + "w_gate").T), wu=rows(a(p + "w_up").T), wd=rows(a(p + "w_down").T)))
    p = "L3_xattn_"
    kv = a(p + "Wkv")
    w["mqa"] = put("mqa", dict(wq=rows(a(p + "Wq")), wk=rows(np.concatenate([kv[:, :HD]] * 2, 1)), wv=rows(np.concatenate([kv[:, HD:]] * 2, 1)),
                               wout=rows(a(p + "Wout")), w1=rows(a(p + "W1")), w2=rows(a(p + "W2")), ln_g=col(a(p + "ln_g")),
                               ln_b=col(a(p + "ln_b")), cln_g=col(a(p + "cln_g")), cln_b=col(a(p + "cln_b"))))
    p = "L3_ffn_"
    v1 = a(p + "V1").reshape(64, 4, 2, P).transpose(2, 0, 1, 3).reshape(P, -1)
    w["low"] = put("low", dict(u1=rows(np.concatenate([a(p + "U1")] * 2, 1)), v1=v1, b1=col(a(p + "b1")), u2=rows(a(p + "U2")),
                               v2=a(p + "V2"), b2=all_rows(a(p + "b2"))))
    return w


def kernel(**inputs):
    import numpy as np
    import concourse.bacc as bacc
    from concourse.bass_utils import run_bass_kernel_spmd

    w = pack(inputs)
    arrays = {"w_" + k: v for k, v in w.items()}
    arrays["x"] = np.ascontiguousarray(inputs["x"])
    arrays["ctx"] = np.ascontiguousarray(inputs["ctx_1024"])
    arrays["ctxT"] = np.ascontiguousarray(np.asarray(inputs["ctx_1024"]).reshape(B * S, D).T)
    arrays["mask"] = np.ascontiguousarray(inputs["mask_BxSxS2_ff0"])
    p = np.arange(P, dtype=np.float32)
    arrays["consts"] = np.concatenate([
        (p[:, None] < p[None, :]).astype(np.float32),
        p[:, None] + P * np.arange(B, dtype=np.float32)[None, :],
        np.broadcast_to(NE * CAP - CAP * np.arange(NE, dtype=np.float32), (P, NE)),
        (TOPK * (p[:, None, None] + P * np.arange(B)[None, :, None]) + np.arange(TOPK)[None, None, :]).reshape(P, -1).astype(np.float32),
        (p[:, None] > p[None, :]).astype(np.float32),
    ], 1)
    slots = np.arange(NE * CAP + B * S * TOPK)
    arrays["table0"] = np.stack([B * S + slots % P, 0 * slots], 1).astype(np.float32)
    nc = bacc.Bacc("TRN2", target_bir_lowering=False, num_devices=1)
    ins = {k: nc.dram_tensor(f"in_{k}", v.shape, mybir.dt.from_np(v.dtype), kind="ExternalInput").ap() for k, v in arrays.items()}
    out = nc.dram_tensor("out_x", (B, S, D), F32, kind="ExternalOutput").ap()
    build(nc, ins, out)
    r = run_bass_kernel_spmd(nc, [{f"in_{k}": v for k, v in arrays.items()}], core_ids=[0])
    return r.results[0]["out_x"]
```

```python
from contextlib import ExitStack

import concourse.bass as bass
from concourse import mybir

ALU = mybir.AluOpType
ACT = mybir.ActivationFunctionType
AX = mybir.AxisListType
F32 = mybir.dt.float32
BF16 = mybir.dt.bfloat16
I32 = mybir.dt.int32
U32 = mybir.dt.uint32

P = 128
B, S, D = 16, 128, 256
KD = D // P
BC = 2
TOK = BC * S
NCH = B // BC
H, HD = 16, 64
HM = H * HD // P
FAN = 4
NE0, EH0, MD = 8, 256, 64
HID0 = 512
NE, CAP, FE = 64, 128, 192
TOPK = 8
HL, DL = 4, 64
INNER = 1024
EPS = 1e-5
LEAD = 512

LAYOUT = {
    "attn": [("wk", KD * 1024), ("wv", KD * 1024), ("bk", HM), ("bq", HM), ("bv", HM), ("wq", KD * 1024),
             ("wu", HM * D), ("bu", D)],
    "spike": [("enc", KD * HID0), ("enc_b", 4), ("s2c", 4 * P), ("s2c_b", 1), ("rw1", 64), ("rb1", 1),
              ("rw2", NE0), ("rb2", NE0), ("ew1", NE0 * P), ("eb1", NE0 * 2), ("ew2", NE0 * 2 * MD),
              ("eb2", NE0 * MD), ("c2s", HID0), ("c2s_b", 4), ("dec", 4 * D), ("dec_b", D), ("ln_g", D),
              ("ln_b", D)],
    "rec": [("wi", KD * D), ("bi", KD), ("wg", KD * D), ("bg", KD), ("a", KD * D), ("bm", KD * D),
            ("wo", KD * D), ("bo", D), ("decay", KD)],
    "moe": [("router", KD * NE), ("sgu", KD * 2 * FE), ("sdown", 2 * D)],
    "mlstm": [("gq", KD * 2 * HL), ("gk", KD * 2 * HL), ("gv", KD * 2 * HL), ("gb", 2 * HL), ("lnw", D)],
    "bit": [("wg", KD * INNER), ("wu", KD * INNER), ("wd", INNER // P * D)],
    "mqa": [("wq", KD * 1024), ("wk", KD * P), ("wv", KD * P), ("wout", HM * D), ("w1", KD * 2 * INNER),
            ("w2", INNER // P * D), ("ln_g", KD), ("ln_b", KD), ("cln_g", KD), ("cln_b", KD)],
    "low": [("u1", KD * P), ("v1", INNER // 2), ("b1", INNER // P), ("u2", INNER // P * 64), ("v2", D), ("b2", D)],
}
CONSTS = [("tri", P), ("tokens", B), ("slot_base", NE), ("spare", B * TOPK), ("late", P)]
COLS = {stage: sum(n for _, n in parts) for stage, parts in LAYOUT.items()}


class Steps:

    def __init__(self, sem):
        self.sem, self.end, self.table, self.next = sem, LEAD, {}, 0

    def plan(self, stage, names, iterations):
        self.table[stage] = (self.end, {n: k for k, n in enumerate(names)}, len(names))
        assert len(set(names)) == len(names)
        self.end += len(names) * iterations
        self.table[stage, "end"] = self.end

    def at(self, stage, i, name, back=0):
        start, index, n = self.table[stage]
        return i * n + (start + index[name] + 1 - back * n)

    def one(self, stage, name):
        index = self.table[stage][1]
        assert index[name] == self.next % len(index), (stage, name, self.next % len(index))
        self.next = (self.next + 1) % len(index)
        return 1

    def all(self, stage):
        return self.table[stage, "end"]
SPACE = 24832


def build(nc, ins, out):
    ctx = ExitStack()
    with ctx:
        block_program(nc, ins, out, ctx)


def block_program(nc, ins, out, ctx):
    def sb(name, shape, dt=F32):
        return ctx.enter_context(nc.sbuf_tensor(name, shape, dt))

    def sem(name):
        return ctx.enter_context(nc.semaphore(name))

    ctxT_dram = ins["ctxT"].rearrange("(k p) t -> p k t", p=P)
    mask_dram = ins["mask"].rearrange("b q k -> q b k")
    x_dram = ins["x"].rearrange("b s d -> s b d")
    ctx_dram = ins["ctx"].rearrange("b s d -> s b d")
    out_dram = out.rearrange("b s d -> s b d")

    x = sb("x", [P, B + BC, D])
    nmr = sb("nmr", [P, B + BC])
    rstd = sb("rstd", [P, B + BC])
    xn = [sb(f"xn{n}", [P, BC, D]) for n in range(2)]
    xnT = [sb(f"xnT{n}", [P, KD, TOK]) for n in range(2)]
    ctxT = [sb(f"ctxT{n}", [P, KD, TOK]) for n in range(2)]
    ident = sb("ident", [P, P])
    ones = sb("ones", [P, P])
    mhalf = sb("mhalf", [P, BC])
    iota8 = sb("iota8", [P, NE0])
    zrow = sb("zrow", [P, D])
    bnst = [sb(f"bnst{n}", [P, BC, 6]) for n in range(2)]
    mv = [sb(f"mv{n}", [P, BC, 2]) for n in range(2)]
    veps = [sb(f"veps{n}", [P, BC]) for n in range(2)]
    w_place = {0: sb("w_even", [P, max(COLS[s] for s in ("attn", "rec", "mqa"))]),
               1: sb("w_odd", [P, max(COLS[s] for s in ("spike", "moe", "bit"))])}
    WPLACE = {"attn": (0, 0), "spike": (1, 0), "rec": (0, 0), "moe": (0, COLS["rec"]), "mlstm": (0, COLS["rec"] + COLS["moe"]),
              "bit": (1, 0), "mqa": (0, 0), "low": (1, 0)}
    space = sb("space", [P, SPACE])
    shape_consts = sb("shape_consts", [P, sum(n for _, n in CONSTS)])

    def C(name):
        at = sum(n for k, (m, n) in enumerate(CONSTS) if k < [m for m, _ in CONSTS].index(name))
        return shape_consts[:, at:at + dict(CONSTS)[name]]
    bank = [ctx.enter_context(nc.psum_tensor(f"bank{n}", [P, 512], F32)) for n in range(8)]

    def area(name, shape, at, dt=F32):
        n = 1
        for s in shape[1:]:
            n *= s
        words = n if dt == F32 else (n + 1) // 2
        assert at + words <= SPACE, (name, at + words)
        ap = space[0:shape[0], at:at + words]
        if dt != F32:
            ap = ap.bitcast(dt)
        if len(shape) == 3:
            ap = ap.rearrange("p (a b) -> p a b", a=shape[1])
        if len(shape) == 4:
            ap = ap.rearrange("p (a b c) -> p a b c", a=shape[1], b=shape[2])
        return ap

    def weight_reader(stage_name):
        place, first = WPLACE[stage_name]
        offsets, at = {}, first
        for n, c in LAYOUT[stage_name]:
            offsets[n] = (at, c)
            at += c
        return lambda n: w_place[place][:, offsets[n][0]:offsets[n][0] + offsets[n][1]]

    weights = {s: weight_reader(s) for s in LAYOUT}

    pe_s, act_s, dve_s, pool_s = (Steps(sem(n)) for n in ("tensor_steps", "scalar_steps", "vector_steps", "gpsimd_steps"))
    consts = sem("consts_written")
    x_loaded, spare_ready = sem("x_loaded"), sem("spare_chunk_written")
    attn_rest_loaded = sem("attention_query_and_output_weights_loaded")
    w_loaded = {s: sem(f"weights_{s}_loaded") for s in LAYOUT}
    ctxT_loaded = sem("ctxT_chunk_loaded")
    ctxT2_loaded = [sem(f"ctxT_chunk_loaded_for_rec_{n}") for n in range(2)]
    ctxT3_loaded = [sem(f"ctxT_chunk_loaded_for_mlstm_{n}") for n in range(2)]
    ctx_loaded = [sem(f"ctx_chunk_loaded_for_mlstm_{n}") for n in range(2)]
    ctx4_loaded, mask_loaded = sem("ctx_chunk_loaded_for_mqa"), sem("mask_chunk_loaded")
    consts_loaded = sem("shape_constants_loaded")
    zeroed = sem("zero_rows_written")
    gidx_set, sidx_set = sem("gather_rows_set"), sem("scatter_rows_set")
    bit_q = sem("weight_quantiser_steps")
    held = sem("waits_held_apart")
    bq8_ready = sem("bq8_ready")
    out_stored = sem("out_stored")

    def stage(name, iterations, pe, act, dve, pool):
        for s, names in ((pe_s, pe), (act_s, act), (dve_s, dve), (pool_s, pool)):
            s.plan(name, names, iterations)

    def others_done(eng, stage_name):
        for s in (pe_s, act_s, dve_s, pool_s):
            eng.wait_ge(s.sem, s.all(stage_name))

    def load_weights(eng, stage_name):
        place, first = WPLACE[stage_name]
        eng.dma_start(w_place[place][:, first:first + COLS[stage_name]], ins["w_" + stage_name]).then_inc(w_loaded[stage_name], 16)

    def after(st, i, lane=""):
        return tuple(lambda name, back=0, s=s: (s.sem, s.at(st, i, f"{name}{lane}", back)) for s in (pe_s, act_s, dve_s, pool_s))

    def signals(steps, st, lane=""):
        return lambda name: (steps.sem, steps.one(st, f"{name}{lane}"))

    def both(names):
        parts = [n if isinstance(n, tuple) else (n,) for n in names]
        return [f"{name}{lane}" for part in parts for lane in "AB" for name in part]

    def in_turns(body):
        lanes = [body(0), body(1)]
        while lanes:
            lanes = [b for b in lanes if next(b, "end") != "end"]

    def wide(ap, n):
        return ap.unsqueeze(2).to_broadcast([ap.shape[0], ap.shape[1], n])

    def over(ap, n):
        return ap.unsqueeze(1).to_broadcast([ap.shape[0], n, ap.shape[1]])

    LN_DVE = ["bn0", "bn1", "ag0", "ag1", "veps", "nmr"]

    def place(i, lane, chunk=None):
        if lane is None:
            return (i if chunk is None else chunk), 0, ""
        return 2 * i + lane, lane, "AB"[lane]

    def stats(st, i, lane=None, chunk=None, ahead=None):
        c, n, end = (i + ahead, 1, "X") if ahead is not None else place(i, lane, chunk)
        PE, ACTS, DVE, POOL = after(st, i, end)
        done = signals(dve_s, st, end)
        if ahead is None:
            nc.vector.wait_ge(*DVE("res1" if st == "bit" else "res"))
            nc.vector.sem_inc(held, 1)
        for b in range(BC):
            nc.vector.bn_stats(bnst[n][:, b, :], x[:, bass.ds(c * BC + b, 1), :]).then_inc(*done(f"bn{b}"))
            yield
        for b in range(BC):
            nc.vector.wait_ge(*DVE(f"bn{b}"))
            nc.vector.sem_inc(held, 1)
            nc.vector.bn_aggr(mv[n][:, b, :], bnst[n][:, b, :]).then_inc(*done(f"ag{b}"))
            yield
        nc.vector.wait_ge(*DVE("ag1"))
        nc.vector.tensor_scalar(veps[n][:], mv[n][:, :, 1], EPS, None, ALU.add).then_inc(*done("veps"))
        yield
        nc.vector.wait_ge(*POOL("rstd"))
        nc.vector.scalar_tensor_tensor(nmr[:, bass.ds(c * BC, BC)], mv[n][:, :, 0], -1.0, rstd[:, bass.ds(c * BC, BC)],
                                       ALU.mult, ALU.mult).then_inc(*done("nmr"))
        yield

    def stats_root(st, i, lane=None, chunk=None, ahead=None):
        c, n, end = (i + ahead, 1, "X") if ahead is not None else place(i, lane, chunk)
        PE, ACTS, DVE, POOL = after(st, i, end)
        nc.gpsimd.wait_ge(*DVE("veps"))
        nc.gpsimd.sem_inc(held, 1)
        nc.gpsimd.tensor_tensor(rstd[:, bass.ds(c * BC, BC)], veps[n][:], mhalf[:], ALU.pow).then_inc(*signals(pool_s, st, end)("rstd"))
        yield

    def prep(st, i, lane=None, chunk=None):
        c, n, end = place(i, lane, chunk)
        done = signals(act_s, st, end)
        for b in range(BC):
            nc.scalar.activation(xn[n][:, b, :], x[:, bass.ds(c * BC + b, 1), :], ACT.Identity,
                                 bias=nmr[:, bass.ds(c * BC + b, 1)], scale=rstd[:, bass.ds(c * BC + b, 1)]).then_inc(*done(f"prep{b}"))
            yield

    def turn_x(st, i, lane=None, dst=None):
        c, n, end = place(i, lane)
        PE, ACTS, DVE, POOL = after(st, i, end)
        dst = bank[7] if dst is None else dst
        nc.tensor.wait_ge(*ACTS("prep1"))
        for k in range(KD):
            for b in range(BC):
                last = nc.tensor.transpose(dst[:, (k * BC + b) * P:(k * BC + b + 1) * P], xn[n][:, b, k * P:(k + 1) * P], ident[:])
        last.then_inc(*signals(pe_s, st, end)("xT"))
        yield

    def copy_xT(st, i, lane=None, src=None):
        c, n, end = place(i, lane)
        src = bank[7] if src is None else src
        nc.vector.wait_ge(pe_s.sem, pe_s.at(st, i, f"xT{end}"))
        nc.vector.tensor_copy(xnT[n][:].rearrange("p k t -> p (k t)"), src[:]).then_inc(*signals(dve_s, st, end)("xT"))
        yield

    def alone(steps):
        for _ in steps:
            pass

    def consts_pool():
        nc.gpsimd.sem_inc(pool_s.sem, LEAD)
        nc.gpsimd.memset(ident[:], 0.0).then_inc(consts, 1)
        nc.gpsimd.memset(mhalf[:], -0.5).then_inc(consts, 1)
        nc.gpsimd.memset(ones[:], 1.0).then_inc(consts, 1)
        nc.gpsimd.memset(zrow[:], 0.0).then_inc(zeroed, 1)
        nc.gpsimd.memset(x[:, B:, :], 0.0).then_inc(spare_ready, 1)
        nc.gpsimd.wait_ge(consts, 3)
        nc.gpsimd.affine_select(out=ident[:], in_=ident[:], compare_op=ALU.not_equal, fill=1.0, base=0,
                                pattern=[[-1, P]], channel_multiplier=1).then_inc(consts, 1)

    UNITS = 2 * HM // FAN * BC
    AW = weights["attn"]
    wk, wv, wq = (AW(n).rearrange("p (k m) -> p k m", k=KD) for n in ("wk", "wv", "wq"))
    wu = AW("wu").rearrange("p (k n) -> p k n", k=HM)
    qT, kT, mT = (area(n, [P, HM, TOK], at) for n, at in (("qT", 0), ("kT", 2048), ("mT", 4096)))
    v = area("v", [P, BC, H * HD], 6144)
    prob = area("prob", [P, 4, FAN, P], 8192)
    probT = area("probT", [P, 2, FAN, P], 10240)
    sm = area("sm", [P, 3, 4, FAN], 11264)
    bq8 = area("bq8", [P, HM], 11328)
    GROUP_BANK = dict(k0=0, k1=1, v00=2, v01=3, q0=4, q1=5, k2=6, q2=7, k3=5, q3=4, v10=6, v11=7)
    FILL_FIRST = {0: ["k2"], 2: ["v10"]}
    FILL = {0: ["q2"], 1: ["k3", "q3"], 5: ["v11"], 8: ["out0a"], 9: ["out0"]}
    SLOTS = range(UNITS + 3)

    def at_slot(t, *parts):
        return [(what, t - late) for what, late in parts if 0 <= t - late < UNITS]

    PORDER = [[(g, None) for g in FILL_FIRST.get(t, [])] + at_slot(t, ("S", 0)) + [(g, None) for g in FILL.get(t, []) if t < 8] + at_slot(t, ("T", 2), ("PV", 3))
              + [(g, None) for g in FILL.get(t, []) if t >= 8] for t in SLOTS]

    def unit(t):
        return t // 4, t % 4 // 2, t % 2

    DORDER = [[(g, None) for g in FILL_FIRST.get(t, []) if g[0] in "kq"] + at_slot(t, ("max", 0)) + [(g, None) for g in FILL.get(t, []) if g[0] in "kq"] + at_slot(t, ("rec", 1), ("copy", 2))
              + [("o", t - 3)] * (t >= 3 and t % 2 == 0) for t in SLOTS]
    XSLOT = 5

    def names_of(order):
        return [a if t is None else f"{a}{t}" for slot_steps in order for a, t in slot_steps]

    LN_X = [f"{n}X" for n in LN_DVE]
    stage("attn_first", 1, pe=[], act=[], dve=LN_X, pool=["rstdX"])
    stage("attn", NCH,
          pe=["k0", "k1", "v00", "v01", "xT", "q0", "q1"] + names_of(PORDER) + ["out1"],
          act=["prep0", "prep1", "v00", "v01", "exp0", "exp1", "v10", "exp2", "exp3", "exp4", "exp5", "v11", "exp6", "exp7"],
          dve=["k0", "k1", "xT", "q0", "q1"] + names_of(DORDER[:XSLOT]) + LN_X[:-1] + names_of(DORDER[XSLOT:XSLOT + 1]) + LN_X[-1:] + names_of(DORDER[XSLOT + 1:]) + ["res"] + LN_DVE,
          pool=["bu"] + [f"norm{t}" for t in range(XSLOT - 1)] + ["rstdX"] + [f"norm{t}" for t in range(XSLOT - 1, UNITS)] + ["rstd"])

    def attn_sp():
        sp = nc.sync

        def load_ctx(c):
            sp.dma_start(ctxT[0][:], ctxT_dram[:, :, bass.ds(c * TOK, TOK)]).then_inc(ctxT_loaded, 16)

        KV = 2 * KD * 1024 + 3 * HM
        sp.dma_start(w_place[0][:, 0:KV], ins["w_attn"][:, 0:KV]).then_inc(w_loaded["attn"], 16)
        load_ctx(0)
        sp.dma_start(x[:, 0:B, :], x_dram).then_inc(x_loaded, 16)
        sp.dma_start(w_place[0][:, KV:COLS["attn"]], ins["w_attn"][:, KV:]).then_inc(attn_rest_loaded, 16)
        with sp.Fori(0, NCH - 1) as i:
            sp.wait_ge(pe_s.sem, pe_s.at("attn", i, "v11"))
            load_ctx(i + 1)
        sp.dma_start(shape_consts[:], ins["consts"]).then_inc(consts_loaded, 16)
        load_weights(sp, "spike")

    def attn_pe():
        pe, st = nc.tensor, "attn"
        pe.sem_inc(pe_s.sem, LEAD)
        pe.wait_ge(consts, 4)
        pe.wait_ge(w_loaded["attn"], 16)
        with pe.Fori(0, NCH) as i:
            PE, ACTS, DVE, POOL = after(st, i)
            done = signals(pe_s, st)

            def project(g):
                dst = bank[GROUP_BANK[g]]
                if g[0] == "v":
                    b, half = int(g[1]), int(g[2])
                    for k in range(KD):
                        last = nc.tensor.matmul(dst[:], ctxT[0][:, k, b * P:(b + 1) * P], wv[:, k, half * 512:(half + 1) * 512],
                                                start=k == 0, stop=k == KD - 1)
                else:
                    w, src = (wk, ctxT[0]) if g[0] == "k" else (wq, xnT[0])
                    for m in range(2):
                        mm = 2 * int(g[1]) + m
                        for k in range(KD):
                            last = nc.tensor.matmul(dst[:, m * TOK:(m + 1) * TOK], w[:, k, mm * P:(mm + 1) * P], src[:, k, :],
                                                    start=k == 0, stop=k == KD - 1)
                last.then_inc(*done(g))

            def project_out(b, ks, name):
                for k in ks:
                    last = nc.tensor.matmul(bank[6][:, b * D:(b + 1) * D], mT[:, k, b * P:(b + 1) * P], wu[:, k, :],
                                            start=k == 0, stop=k == HM - 1)
                last.then_inc(*done(name))

            pe.wait_ge(ctxT_loaded, i * 16 + 16)
            for g in ("k0", "k1", "v00", "v01"):
                project(g)
            pe.wait_ge(attn_rest_loaded, 16)
            pe.wait_ge(*ACTS("v11", back=1))
            alone(turn_x(st, i))
            pe.wait_ge(*DVE("xT"))
            project("q0")
            project("q1")
            for slot_steps in PORDER:
                for what, t in slot_steps:
                    if t is None:
                        if what == "k2":
                            pe.wait_ge(*DVE("res", back=1))
                        if what == "v10":
                            pe.wait_ge(*DVE("k2"))
                        if what == "out0a":
                            pe.wait_ge(*ACTS("v10"))
                            pe.wait_ge(*DVE("o3"))
                        if what == "out0a":
                            project_out(0, range(HM // 2), what)
                        elif what == "out0":
                            project_out(0, range(HM // 2, HM), what)
                        else:
                            project(what)
                        continue
                    b, u, par = unit(t)
                    rows = slice(HD * par, HD * par + HD)
                    if what == "S":
                        if t == 0:
                            pe.wait_ge(*DVE("q1"))
                        if t == 2:
                            pe.wait_ge(*DVE("q3"))
                        if t >= 2:
                            pe.wait_ge(*ACTS(f"exp{t - 2}"))
                        for j in range(FAN):
                            m = FAN * u + j
                            last = nc.tensor.matmul(bank[t % 2][:, j * P:(j + 1) * P], qT[rows, m, b * P:(b + 1) * P],
                                                    kT[rows, m, b * P:(b + 1) * P], start=True, stop=True)
                    elif what == "T":
                        pe.wait_ge(*POOL(f"norm{t}"))
                        if t >= 2:
                            pe.wait_ge(*DVE(f"copy{t - 2}"))
                        for j in range(FAN):
                            last = nc.tensor.transpose(bank[2 + t % 2][:, j * P:(j + 1) * P], prob[:, t % 4, j, :], ident[:])
                    else:
                        pe.wait_ge(*DVE(f"copy{t}"))
                        if t in (0, 4):
                            pe.wait_ge(*ACTS(f"v{b}1"))
                        if b == 1 and par == 0:
                            pe.wait_ge(*DVE(f"o{t - 3}"))
                        for j in range(FAN):
                            h = 2 * (FAN * u + j) + par
                            last = nc.tensor.matmul(bank[4 + u][rows, j * P:(j + 1) * P], v[:, b, h * HD:(h + 1) * HD],
                                                    probT[:, t % 2, j, :], start=True, stop=True)
                    last.then_inc(*done(f"{what}{t}"))
            pe.wait_ge(*DVE("o7"))
            project_out(1, range(HM), "out1")

    def attn_act():
        act, st = nc.scalar, "attn"
        act.sem_inc(act_s.sem, LEAD)
        act.wait_ge(dve_s.sem, dve_s.all("attn_first"))
        with act.Fori(0, NCH) as i:
            PE, ACTS, DVE, POOL = after(st, i)
            done = signals(act_s, st)

            def values(g):
                act.wait_ge(*PE(g))
                b, half = int(g[1]), int(g[2])
                nc.scalar.copy(v[:, b, half * 512:(half + 1) * 512], bank[GROUP_BANK[g]][:]).then_inc(*done(g))

            act.wait_ge(*DVE("nmrX", back=1))
            act.sem_inc(held, 1)
            alone(prep(st, i))
            values("v00")
            values("v01")
            for t in range(UNITS):
                if t == 2:
                    values("v10")
                if t == 6:
                    values("v11")
                act.wait_ge(*DVE(f"max{t}"))
                if t >= 4:
                    act.wait_ge(*PE(f"T{t - 4}"))
                for j in range(FAN):
                    last = nc.scalar.activation(prob[:, t % 4, j, :], bank[t % 2][:, j * P:(j + 1) * P], ACT.Exp,
                                                bias=sm[:, 0, t % 4, j:j + 1], accum_out=sm[:, 1, t % 4, j:j + 1])
                last.then_inc(*done(f"exp{t}"))

    def attn_pool():
        pool, st = nc.gpsimd, "attn"
        pool.wait_ge(attn_rest_loaded, 16)
        alone(stats_root("attn_first", 0, ahead=0))
        with pool.Fori(0, NCH) as i:
            PE, ACTS, DVE, POOL = after(st, i)
            done = signals(pool_s, st)
            pool.wait_ge(*ACTS("prep1"))
            pool.sem_inc(held, 1)
            nc.gpsimd.tensor_tensor(x[:, bass.ds(i * BC, BC), :], x[:, bass.ds(i * BC, BC), :],
                                    AW("bu").unsqueeze(1).to_broadcast([P, BC, D]), ALU.add).then_inc(*done("bu"))
            for t in range(UNITS):
                if t == XSLOT - 1:
                    alone(stats_root(st, i, ahead=1))
                pool.wait_ge(*DVE(f"rec{t}"))
                nc.gpsimd.tensor_tensor(prob[:, t % 4], prob[:, t % 4], sm[:, 2, t % 4, :].unsqueeze(2).to_broadcast([P, FAN, P]),
                                        ALU.mult).then_inc(*done(f"norm{t}"))
            alone(stats_root(st, i))

    def attn_dve():
        dve, st = nc.vector, "attn"
        nc.vector.sem_inc(dve_s.sem, LEAD)
        dve.wait_ge(w_loaded["attn"], 16)
        nc.vector.tensor_scalar(bq8[:], AW("bq"), HD ** -0.5, None, ALU.mult).then_inc(bq8_ready, 1)
        dve.wait_ge(bq8_ready, 1)
        dve.wait_ge(x_loaded, 16)
        dve.wait_ge(spare_ready, 1)
        alone(stats("attn_first", 0, ahead=0))
        with dve.Fori(0, NCH) as i:
            PE, ACTS, DVE, POOL = after(st, i)
            done = signals(dve_s, st)

            def keys(g):
                n = int(g[1])
                dve.wait_ge(*PE(g))
                nc.vector.tensor_tensor(kT[:, 2 * n:2 * n + 2, :], bank[GROUP_BANK[g]][:].rearrange("p (m t) -> p m t", m=2),
                                        AW("bk")[:, 2 * n:2 * n + 2].unsqueeze(2).to_broadcast([P, 2, TOK]), ALU.add).then_inc(*done(g))

            def queries(g):
                n = int(g[1])
                dve.wait_ge(*PE(g))
                nc.vector.scalar_tensor_tensor(qT[:, 2 * n:2 * n + 2, :], bank[GROUP_BANK[g]][:].rearrange("p (m t) -> p m t", m=2),
                                               HD ** -0.5, bq8[:, 2 * n:2 * n + 2].unsqueeze(2).to_broadcast([P, 2, TOK]),
                                               ALU.mult, ALU.add).then_inc(*done(g))

            keys("k0")
            keys("k1")
            alone(copy_xT(st, i))
            queries("q0")
            queries("q1")
            for n, slot_steps in enumerate(DORDER):
                if n == XSLOT:
                    next_stats = stats(st, i, ahead=1)
                    for _ in LN_X[:-1]:
                        next(next_stats)
                if n == XSLOT + 1:
                    alone(next_stats)
                for what, t in slot_steps:
                    if t is None:
                        (keys if what[0] == "k" else queries)(what)
                        continue
                    b, u, par = unit(t)
                    if what == "max":
                        dve.wait_ge(*PE(f"S{t}"))
                        ins = nc.vector.tensor_reduce(sm[:, 0, t % 4, :], bank[t % 2][:].rearrange("p (j s) -> p j s", j=FAN),
                                                      AX.X, ALU.max, negate=True)
                    elif what == "rec":
                        dve.wait_ge(*ACTS(f"exp{t}"))
                        ins = nc.vector.reciprocal(sm[:, 2, t % 4, :], sm[:, 1, t % 4, :])
                    elif what == "copy":
                        dve.wait_ge(*PE(f"T{t}"))
                        ins = nc.vector.tensor_copy(probT[:, t % 2].rearrange("p j s -> p (j s)"), bank[2 + t % 2][:])
                    else:
                        dve.wait_ge(*PE(f"PV{t}"))
                        ins = nc.vector.tensor_tensor(mT[:, FAN * u:FAN * u + FAN, b * P:(b + 1) * P],
                                                      bank[4 + u][:].rearrange("p (j s) -> p j s", j=FAN),
                                                      AW("bv")[:, FAN * u:FAN * u + FAN].unsqueeze(2).to_broadcast([P, FAN, P]), ALU.add)
                    ins.then_inc(*done(f"{what}{t}"))
            dve.wait_ge(*PE("out1"))
            dve.wait_ge(*POOL("bu"))
            nc.vector.tensor_tensor(x[:, bass.ds(i * BC, BC), :], bank[6][:].rearrange("p (b d) -> p b d", b=BC),
                                    x[:, bass.ds(i * BC, BC), :], ALU.add).then_inc(*done("res"))
            alone(stats(st, i))

    SW = weights["spike"]
    enc = SW("enc").rearrange("p (k m) -> p k m", k=KD)
    s2c = SW("s2c").rearrange("p (k m) -> p k m", k=4)
    ew1 = SW("ew1").rearrange("p (e m) -> p e m", e=NE0)
    ew2 = SW("ew2").rearrange("p (e m) -> p e m", e=NE0 * 2)
    dec_w = SW("dec").rearrange("p (k m) -> p k m", k=4)
    SPIKE_LANE = 9238
    spT = [area(f"spT{n}", [P, 4, TOK], 0 + n * SPIKE_LANE) for n in range(2)]
    contT = [area(f"contT{n}", [P, TOK], 1024 + n * SPIKE_LANE) for n in range(2)]
    rhT = [area(f"rhT{n}", [64, TOK], 1280 + n * SPIKE_LANE) for n in range(2)]
    ehT = [area(f"ehT{n}", [P, NE0 * 2, TOK], 1536 + n * SPIKE_LANE) for n in range(2)]
    lg0 = [area(f"lg0{n}", [P, BC, NE0], 5632 + n * SPIKE_LANE) for n in range(2)]
    mx0 = [area(f"mx0{n}", [P, BC, 8], 5648 + n * SPIKE_LANE) for n in range(2)]
    ix0 = [area(f"ix0{n}", [P, BC, 8], 5664 + n * SPIKE_LANE) for n in range(2)]
    ixf0 = [area(f"ixf0{n}", [P, BC, 8], 5680 + n * SPIKE_LANE) for n in range(2)]
    gap0 = [area(f"gap0{n}", [P, BC], 5696 + n * SPIKE_LANE) for n in range(2)]
    w0 = [area(f"w0{n}", [P, 2, BC], 5698 + n * SPIKE_LANE) for n in range(2)]
    pick0 = [area(f"pick0{n}", [P, 2, BC, NE0], 5704 + n * SPIKE_LANE) for n in range(2)]
    comb0 = [area(f"comb0{n}", [P, BC, NE0], 5736 + n * SPIKE_LANE) for n in range(2)]
    eo = [area(f"eo{n}", [P, BC, NE0 * MD], 5760 + n * SPIKE_LANE) for n in range(2)]
    moe0 = [area(f"moe0{n}", [P, BC, MD], 6784 + n * SPIKE_LANE) for n in range(2)]
    moe0T = [area(f"moe0T{n}", [64, TOK], 6912 + n * SPIKE_LANE) for n in range(2)]
    rT = [area(f"rT{n}", [P, 4, TOK], 7168 + n * SPIKE_LANE) for n in range(2)]
    dec = [area(f"dec{n}", [P, BC, D], 8192 + n * SPIKE_LANE) for n in range(2)]
    decn = [area(f"decn{n}", [P, BC, D], 8704 + n * SPIKE_LANE) for n in range(2)]
    dveps = [area(f"dveps{n}", [P, BC], 9218 + n * SPIKE_LANE) for n in range(2)]
    drstd = [area(f"drstd{n}", [P, BC], 9220 + n * SPIKE_LANE) for n in range(2)]
    dbn = [area(f"dbn{n}", [P, BC, 6], 9222 + n * SPIKE_LANE) for n in range(2)]
    dmv = [area(f"dmv{n}", [P, BC, 2], 9234 + n * SPIKE_LANE) for n in range(2)]
    EP = NE0 // 2
    stage("spike", NCH // 2,
          pe=both(["xT", "e0", "e1", "s2c", "rh", "lg"] + [(f"h{n}0", f"h{n}1") for n in range(EP)]
          + ["eo0", "eo1", "mT", "c0", "c1", "dec"]),
          act=both(["prep0", "prep1", "e0", "e1", "rh", "w"] + [f"h{n}" for n in range(EP)] + ["c0", "c1", "dec"]),
          dve=both(["xT", "s2c", "lg", "mx0", "mx1", "ix0", "ix1", "ixf", "gap", "h0"]
          + ["p00", "p01", "p10", "p11", "comb"] + ["h1", "h2", "h3"]
          + ["a0", "m0", "r0", "a1", "m1", "r1", "mT", "dadd", "dbn0", "dbn1", "dag0", "dag1", "dveps", "dn0", "dn1", "g", "res"] + LN_DVE),
          pool=both(["b", "drstd", "rstd"]))

    def pair_bank(n, half):
        return (1 + half, 3 * (1 - half))[n % 2]

    def spike_pe():
        pe, st = nc.tensor, "spike"
        others_done(pe, "attn")
        pe.wait_ge(w_loaded[st], 16)
        with pe.Fori(0, NCH // 2) as i:
            def chunk(lane):
                bk = bank[4 * lane:4 * lane + 4]
                PE, ACTS, DVE, POOL = after(st, i, "AB"[lane])
                done = signals(pe_s, st, "AB"[lane])
                yield from turn_x(st, i, lane, bk[0])
                pe.wait_ge(*DVE("xT"))
                for n in range(2):
                    for m in range(2):
                        for k in range(KD):
                            last = nc.tensor.matmul(bk[1 + n][:, m * TOK:(m + 1) * TOK], enc[:, k, (2 * n + m) * P:(2 * n + m + 1) * P],
                                                    xnT[lane][:, k, :], start=k == 0, stop=k == KD - 1)
                    last.then_inc(*done(f"e{n}"))
                    yield
                pe.wait_ge(*ACTS("e1"))
                for k in range(4):
                    last = nc.tensor.matmul(bk[3][:, 0:TOK], s2c[:, k, :], spT[lane][:, k, :], start=k == 0, stop=k == 3)
                last.then_inc(*done("s2c"))
                yield
                pe.wait_ge(*DVE("s2c"))
                pe.sem_inc(held, 1)
                nc.tensor.matmul(bk[0][0:64, 0:TOK], SW("rw1")[0:64], contT[lane][0:64], start=True, stop=True).then_inc(*done("rh"))
                yield
                pe.wait_ge(*ACTS("rh"))
                for b in range(BC):
                    last = nc.tensor.matmul(bk[0][:, b * NE0:(b + 1) * NE0], rhT[lane][:, b * P:(b + 1) * P], SW("rw2")[0:64],
                                            start=True, stop=True)
                last.then_inc(*done("lg"))
                yield
                pe.wait_ge(*DVE("lg"))
                for n in range(EP):
                    if n >= 2:
                        pe.wait_ge(*ACTS(f"h{n - 2}"))
                        pe.wait_ge(*DVE(f"h{n - 2}"))
                    for half in range(2):
                        rows = slice(64 * half, 64 * half + 64)
                        for e in range(2):
                            last = nc.tensor.matmul(bk[pair_bank(n, half)][:, e * TOK:(e + 1) * TOK], ew1[rows, 2 * n + e, :],
                                                    contT[lane][rows, :], start=True, stop=True)
                        last.then_inc(*done(f"h{n}{half}"))
                    yield
                pe.wait_ge(*ACTS(f"h{EP - 1}"))
                pe.wait_ge(*DVE(f"h{EP - 1}"))
                for b in range(BC):
                    for e in range(NE0):
                        for half in range(2):
                            last = nc.tensor.matmul(bk[1 + b][:, e * MD:(e + 1) * MD], ehT[lane][:, 2 * e + half, b * P:(b + 1) * P],
                                                    ew2[:, 2 * e + half, :], start=half == 0, stop=half == 1)
                    last.then_inc(*done(f"eo{b}"))
                    yield
                pe.wait_ge(*DVE("r1"))
                pe.sem_inc(held, 1)
                for b in range(BC):
                    last = nc.tensor.transpose(bk[3][0:64, b * P:(b + 1) * P], moe0[lane][:, b, :], ident[:])
                last.then_inc(*done("mT"))
                yield
                pe.wait_ge(*DVE("mT"))
                for n in range(2):
                    for m in range(2):
                        last = nc.tensor.matmul(bk[3 * n][:, m * TOK:(m + 1) * TOK], SW("c2s")[0:64, (2 * n + m) * P:(2 * n + m + 1) * P],
                                                moe0T[lane][:], start=True, stop=True)
                    last.then_inc(*done(f"c{n}"))
                    yield
                pe.wait_ge(*ACTS("c1"))
                for b in range(BC):
                    for k in range(4):
                        last = nc.tensor.matmul(bk[1][:, b * D:(b + 1) * D], rT[lane][:, k, b * P:(b + 1) * P], dec_w[:, k, :],
                                                start=k == 0, stop=k == 3)
                last.then_inc(*done("dec"))
                yield

            in_turns(chunk)

    def spike_act():
        act, st = nc.scalar, "spike"
        others_done(act, "attn")
        act.wait_ge(w_loaded[st], 16)
        with act.Fori(0, NCH // 2) as i:
            def chunk(lane):
                bk = bank[4 * lane:4 * lane + 4]
                PE, ACTS, DVE, POOL = after(st, i, "AB"[lane])
                done = signals(act_s, st, "AB"[lane])
                yield from prep(st, i, lane)
                for n in range(2):
                    act.wait_ge(*PE(f"e{n}"))
                    for m in range(2):
                        last = nc.scalar.activation(spT[lane][:, 2 * n + m, :], bk[1 + n][:, m * TOK:(m + 1) * TOK], ACT.Sigmoid,
                                                    bias=SW("enc_b")[:, 2 * n + m:2 * n + m + 1])
                    last.then_inc(*done(f"e{n}"))
                    yield
                act.wait_ge(*PE("rh"))
                nc.scalar.activation(rhT[lane][:], bk[0][0:64, 0:TOK], ACT.Relu, bias=SW("rb1")[0:64]).then_inc(*done("rh"))
                yield
                act.wait_ge(*DVE("gap"))
                nc.scalar.activation(w0[lane][:, 0, :], gap0[lane][:], ACT.Sigmoid, scale=-1.0)
                nc.scalar.activation(w0[lane][:, 1, :], gap0[lane][:], ACT.Sigmoid).then_inc(*done("w"))
                yield
                for n in range(EP):
                    act.wait_ge(*PE(f"h{n}0"))
                    for e in range(2):
                        last = nc.scalar.activation(ehT[lane][:, 2 * (2 * n + e), :], bk[pair_bank(n, 0)][:, e * TOK:(e + 1) * TOK], ACT.Relu,
                                                    bias=SW("eb1")[:, 2 * (2 * n + e):2 * (2 * n + e) + 1])
                    last.then_inc(*done(f"h{n}"))
                    yield
                for n in range(2):
                    act.wait_ge(*PE(f"c{n}"))
                    for m in range(2):
                        last = nc.scalar.activation(rT[lane][:, 2 * n + m, :], bk[3 * n][:, m * TOK:(m + 1) * TOK], ACT.Sigmoid,
                                                    bias=SW("c2s_b")[:, 2 * n + m:2 * n + m + 1])
                    last.then_inc(*done(f"c{n}"))
                    yield
                act.wait_ge(*DVE("dadd"))
                nc.scalar.activation(dec[lane][:], dec[lane][:], ACT.Sigmoid).then_inc(*done("dec"))
                yield

            in_turns(chunk)

    def spike_pool():
        pool, st = nc.gpsimd, "spike"
        others_done(pool, "attn")
        pool.wait_ge(w_loaded[st], 16)
        for e in range(NE0):
            last = nc.gpsimd.memset(iota8[:, e:e + 1], float(e))
        last.then_inc(consts, 1)
        with pool.Fori(0, NCH // 2) as i:
            def chunk(lane):
                c = 2 * i + lane
                PE, ACTS, DVE, POOL = after(st, i, "AB"[lane])
                done = signals(pool_s, st, "AB"[lane])
                pool.wait_ge(*ACTS("prep1"))
                pool.sem_inc(held, 1)
                nc.gpsimd.tensor_tensor(x[:, bass.ds(c * BC, BC), :], x[:, bass.ds(c * BC, BC), :], over(SW("ln_b"), BC), ALU.add).then_inc(*done("b"))
                yield
                pool.wait_ge(*DVE("dveps"))
                nc.gpsimd.tensor_tensor(drstd[lane][:], dveps[lane][:], mhalf[:], ALU.pow).then_inc(*done("drstd"))
                yield
                yield from stats_root(st, i, lane)

            in_turns(chunk)

    def spike_dve():
        dve, st = nc.vector, "spike"
        others_done(dve, "attn")
        dve.wait_ge(w_loaded[st], 16)
        dve.wait_ge(consts, 5)
        with dve.Fori(0, NCH // 2) as i:
            def chunk(lane):
                c = 2 * i + lane
                bk = bank[4 * lane:4 * lane + 4]
                PE, ACTS, DVE, POOL = after(st, i, "AB"[lane])
                done = signals(dve_s, st, "AB"[lane])

                def relu(n):
                    dve.wait_ge(*PE(f"h{n}1"))
                    for e in range(2):
                        c = 2 * (2 * n + e) + 1
                        last = nc.vector.tensor_scalar(ehT[lane][:, c, :], bk[pair_bank(n, 1)][:, e * TOK:(e + 1) * TOK],
                                                       SW("eb1")[:, c:c + 1], 0.0, ALU.add, ALU.max)
                    last.then_inc(*done(f"h{n}"))
                    yield

                dve.wait_ge(*PE("xT"))
                nc.vector.tensor_copy(xnT[lane][:].rearrange("p k t -> p (k t)"), bk[0][:]).then_inc(*done("xT"))
                yield
                dve.wait_ge(*PE("s2c"))
                nc.vector.tensor_scalar(contT[lane][:], bk[3][:, 0:TOK], SW("s2c_b"), None, ALU.add).then_inc(*done("s2c"))
                yield
                dve.wait_ge(*PE("lg"))
                nc.vector.tensor_tensor(lg0[lane][:], bk[0][:, 0:BC * NE0].rearrange("p (b e) -> p b e", b=BC), over(SW("rb2"), BC),
                                        ALU.add).then_inc(*done("lg"))
                yield
                dve.wait_ge(*DVE("lg"))
                dve.sem_inc(held, 1)
                for b in range(BC):
                    nc.vector.max(mx0[lane][:, b, :], lg0[lane][:, b, :]).then_inc(*done(f"mx{b}"))
                    yield
                dve.wait_ge(*DVE("mx1"))
                dve.sem_inc(held, 1)
                for b in range(BC):
                    nc.vector.max_index(ix0[lane][:, b, :].bitcast(U32), mx0[lane][:, b, :], lg0[lane][:, b, :]).then_inc(*done(f"ix{b}"))
                    yield
                dve.wait_ge(*DVE("ix1"))
                nc.vector.tensor_copy(ixf0[lane][:], ix0[lane][:].bitcast(U32)).then_inc(*done("ixf"))
                yield
                nc.vector.tensor_tensor(gap0[lane][:], mx0[lane][:, :, 1], mx0[lane][:, :, 0], ALU.subtract).then_inc(*done("gap"))
                yield
                yield from relu(0)
                dve.wait_ge(*ACTS("w"))
                for b in range(BC):
                    for k in range(2):
                        nc.vector.tensor_scalar(pick0[lane][:, k, b, :], iota8[:], ixf0[lane][:, b, k:k + 1], w0[lane][:, k, b:b + 1], ALU.is_equal,
                                                ALU.mult).then_inc(*done(f"p{b}{k}"))
                        yield
                dve.wait_ge(*DVE("p11"))
                nc.vector.tensor_tensor(comb0[lane][:], pick0[lane][:, 0], pick0[lane][:, 1], ALU.add).then_inc(*done("comb"))
                yield
                for n in range(1, EP):
                    yield from relu(n)
                for b in range(BC):
                    dve.wait_ge(*PE(f"eo{b}"))
                    nc.vector.tensor_tensor(eo[lane][:, b, :], bk[1 + b][:], SW("eb2"), ALU.add).then_inc(*done(f"a{b}"))
                    yield
                    dve.wait_ge(*DVE(f"a{b}"))
                    nc.vector.tensor_tensor(eo[lane][:, b, :].rearrange("p (e d) -> p e d", e=NE0), eo[lane][:, b, :].rearrange("p (e d) -> p e d", e=NE0),
                                            wide(comb0[lane][:, b, :], MD), ALU.mult).then_inc(*done(f"m{b}"))
                    yield
                    dve.wait_ge(*DVE(f"m{b}"))
                    nc.vector.tensor_reduce(moe0[lane][:, b, :], eo[lane][:, b, :].rearrange("p (e d) -> p d e", e=NE0), AX.X,
                                            ALU.add).then_inc(*done(f"r{b}"))
                    yield
                dve.wait_ge(*PE("mT"))
                nc.vector.tensor_copy(moe0T[lane][:], bk[3][0:64, 0:TOK]).then_inc(*done("mT"))
                yield
                dve.wait_ge(*PE("dec"))
                nc.vector.tensor_tensor(dec[lane][:], bk[1][:].rearrange("p (b d) -> p b d", b=BC), over(SW("dec_b"), BC),
                                        ALU.add).then_inc(*done("dadd"))
                yield
                dve.wait_ge(*ACTS("dec"))
                for b in range(BC):
                    nc.vector.bn_stats(dbn[lane][:, b, :], dec[lane][:, b, :]).then_inc(*done(f"dbn{b}"))
                    yield
                for b in range(BC):
                    dve.wait_ge(*DVE(f"dbn{b}"))
                    nc.vector.sem_inc(held, 1)
                    nc.vector.bn_aggr(dmv[lane][:, b, :], dbn[lane][:, b, :]).then_inc(*done(f"dag{b}"))
                    yield
                dve.wait_ge(*DVE("dag1"))
                nc.vector.tensor_scalar(dveps[lane][:], dmv[lane][:, :, 1], EPS, None, ALU.add).then_inc(*done("dveps"))
                yield
                dve.wait_ge(*POOL("drstd"))
                for b in range(BC):
                    nc.vector.tensor_scalar(decn[lane][:, b, :], dec[lane][:, b, :], dmv[lane][:, b, 0:1], drstd[lane][:, b:b + 1], ALU.subtract,
                                            ALU.mult).then_inc(*done(f"dn{b}"))
                    yield
                dve.wait_ge(*DVE("dn1"))
                nc.vector.tensor_tensor(decn[lane][:], decn[lane][:], over(SW("ln_g"), BC), ALU.mult).then_inc(*done("g"))
                yield
                dve.wait_ge(*DVE("g"))
                dve.wait_ge(*POOL("b"))
                nc.vector.tensor_tensor(x[:, bass.ds(c * BC, BC), :], decn[lane][:], x[:, bass.ds(c * BC, BC), :], ALU.add).then_inc(*done("res"))
                yield
                yield from stats(st, i, lane)

            in_turns(chunk)

    RW = weights["rec"]
    wi, wg1, wa, wbm, wo1 = (RW(n).rearrange("p (k m) -> p k m", k=KD) for n in ("wi", "wg", "a", "bm", "wo"))
    gate = area("gate", [P, KD, S, B], 0)
    drive = area("drive", [P, KD, S, B], 4096)
    state = area("state", [P, KD, S, B], 8192)
    REC_LANE = 5120
    c2 = [area(f"c2{n}", [P, KD, TOK], 8192 + n * REC_LANE) for n in range(2)]
    rT1 = [area(f"rT1{n}", [P, KD, TOK], 8704 + n * REC_LANE) for n in range(2)]
    ret = [area(f"ret{n}", [P, KD, TOK], 9216 + n * REC_LANE) for n in range(2)]
    inp = [area(f"inp{n}", [P, KD, TOK], 9728 + n * REC_LANE) for n in range(2)]
    gc = [area(f"gc{n}", [P, KD, TOK], 10240 + n * REC_LANE) for n in range(2)]
    cin = [area(f"cin{n}", [P, KD, TOK], 10752 + n * REC_LANE) for n in range(2)]
    zrow_b = zrow[:].bitcast(BF16)
    BUSY = 4
    z = area("z", [P, KD, B], 12288)
    sT = area("sT", [P, KD, TOK], 12352)
    CH = [f"{k}{b}" for k in range(KD) for b in range(BC)]
    stage("rec_in", NCH // 2, pe=both(["xT", "inp", "gate", "drive"]),
          act=both(["prep0", "prep1", "inp", "gate", "drive"]),
          dve=both(["c2"] + [f"r{c}" for c in CH] + ["xT", "ret", "gc", "cin"]), pool=[])
    stage("rec_0", 1, pe=["t0"], act=["t0"], dve=["z0"], pool=[])
    stage("rec_loop", (S - 2) // 2, pe=["t0", "t1"], act=["t0", "t1"], dve=["z0", "z1"], pool=[])
    stage("rec_9", 1, pe=["t0"], act=["t0"], dve=["z0"], pool=[])
    stage("rec", NCH, pe=["out"], act=["sT"], dve=["res"] + LN_DVE, pool=["bo", "rstd"])

    def rec_sp():
        sp = nc.sync
        others_done(sp, "attn")
        for name in ("rec", "moe", "mlstm"):
            load_weights(sp, name)
        others_done(sp, "spike")
        st = "rec_in"
        with sp.Fori(0, NCH // 2) as i:
            def chunk(lane):
                c = 2 * i + lane
                PE, ACTS, DVE, POOL = after(st, i, "AB"[lane])
                sp.wait_ge(*DVE("c2", back=1))
                sp.dma_start(ctxT[lane][:], ctxT_dram[:, :, bass.ds(c * TOK, TOK)]).then_inc(ctxT2_loaded[lane], 16)
                yield

            in_turns(chunk)

    def rec_pe():
        pe, st = nc.tensor, "rec_in"
        others_done(pe, "spike")
        pe.wait_ge(w_loaded["rec"], 16)
        with pe.Fori(0, NCH // 2) as i:
            def chunk(lane):
                bk = bank[4 * lane:4 * lane + 4]
                PE, ACTS, DVE, POOL = after(st, i, "AB"[lane])
                done = signals(pe_s, st, "AB"[lane])
                yield from turn_x(st, i, lane, bk[0])
                for n, (w, src, what) in enumerate(((wi, ret[lane], "inp"), (wg1, inp[lane], "gate"))):
                    pe.wait_ge(*(DVE("ret") if n == 0 else ACTS("inp")))
                    for m in range(KD):
                        for k in range(KD):
                            last = nc.tensor.matmul(bk[1 + n][:, m * TOK:(m + 1) * TOK], w[:, k, m * P:(m + 1) * P], src[:, k, :],
                                                    start=k == 0, stop=k == KD - 1)
                    last.then_inc(*done(what))
                    yield
                pe.wait_ge(*DVE("cin"))
                for m in range(KD):
                    for k in range(KD):
                        nc.tensor.matmul(bk[3][:, m * TOK:(m + 1) * TOK], wbm[:, k, m * P:(m + 1) * P], inp[lane][:, k, :],
                                         start=k == 0, stop=False)
                    for k in range(KD):
                        last = nc.tensor.matmul(bk[3][:, m * TOK:(m + 1) * TOK], wa[:, k, m * P:(m + 1) * P], cin[lane][:, k, :],
                                                start=False, stop=k == KD - 1)
                last.then_inc(*done("drive"))
                yield

            in_turns(chunk)

        def drive_part(t, bk):
            nc.tensor.matmul(bk[:, 0:KD * B], ident[:], drive[:, :, t, :], start=True, stop=False, skip_group_check=True)

        def state_part(bk, signal):
            for m in range(KD):
                for k in range(KD):
                    last = nc.tensor.matmul(bk[:, m * B:(m + 1) * B], wa[:, k, m * P:(m + 1) * P], z[:, k, :],
                                            start=False, stop=m == KD - 1 and k == KD - 1, skip_group_check=True)
            last.then_inc(*signal)

        def keep_busy():
            for _ in range(BUSY):
                nc.tensor.matmul(bank[7][:, 0:512], zrow_b[:, 0:P], zrow_b[:, 0:512], start=True, stop=True)

        pe.wait_ge(act_s.sem, act_s.all("rec_in"))
        drive_part(0, bank[0])
        pe.wait_ge(dve_s.sem, dve_s.at("rec_0", 0, "z0"))
        state_part(bank[0], signals(pe_s, "rec_0")("t0"))
        done = signals(pe_s, "rec_loop")
        with pe.Fori(0, (S - 2) // 2) as i:
            PE, ACTS, DVE, POOL = after("rec_loop", i)
            for u in range(2):
                drive_part(bass.ds(2 * i + 1 + u, 1), bank[(1 + u) % 2])
                keep_busy()
                pe.wait_ge(*DVE(f"z{u}"))
                state_part(bank[(1 + u) % 2], done(f"t{u}"))
        drive_part(S - 1, bank[1])
        pe.wait_ge(dve_s.sem, dve_s.at("rec_9", 0, "z0"))
        state_part(bank[1], signals(pe_s, "rec_9")("t0"))

        done = signals(pe_s, "rec")
        with pe.Fori(0, NCH) as i:
            PE, ACTS, DVE, POOL = after("rec", i)
            pe.wait_ge(*ACTS("sT"))
            pe.wait_ge(*DVE("res", back=1))
            for b in range(BC):
                for k in range(KD):
                    last = nc.tensor.matmul(bank[3][:, b * D:(b + 1) * D], sT[:, k, b * P:(b + 1) * P], wo1[:, k, :],
                                            start=k == 0, stop=k == KD - 1)
            last.then_inc(*done("out"))

    def rec_act():
        act, st = nc.scalar, "rec_in"
        others_done(act, "spike")
        act.wait_ge(w_loaded["rec"], 16)
        with act.Fori(0, NCH // 2) as i:
            def chunk(lane):
                c = 2 * i + lane
                bk = bank[4 * lane:4 * lane + 4]
                PE, ACTS, DVE, POOL = after(st, i, "AB"[lane])
                done = signals(act_s, st, "AB"[lane])
                yield from prep(st, i, lane)
                act.wait_ge(*PE("inp"))
                for m in range(KD):
                    last = nc.scalar.activation(inp[lane][:, m, :], bk[1][:, m * TOK:(m + 1) * TOK], ACT.Identity, bias=RW("bi")[:, m:m + 1])
                last.then_inc(*done("inp"))
                yield
                act.wait_ge(*PE("gate"))
                act.sem_inc(held, 1)
                for m in range(KD):
                    last = nc.scalar.activation(gate[:, m, :, bass.ds(c * BC, BC)].rearrange("p t b -> p b t"),
                                                bk[2][:, m * TOK:(m + 1) * TOK].rearrange("p (b t) -> p b t", b=BC), ACT.Sigmoid,
                                                bias=RW("bg")[:, m:m + 1])
                last.then_inc(*done("gate"))
                yield
                act.wait_ge(*PE("drive"))
                act.sem_inc(held, 1)
                for m in range(KD):
                    last = nc.scalar.activation(drive[:, m, :, bass.ds(c * BC, BC)].rearrange("p t b -> p b t"),
                                                bk[3][:, m * TOK:(m + 1) * TOK].rearrange("p (b t) -> p b t", b=BC), ACT.Identity)
                last.then_inc(*done("drive"))
                yield

            in_turns(chunk)

        def step(t, bk, signal):
            act.sem_inc(held, 1)
            nc.scalar.activation(state[:, :, t, :], bk[:, 0:KD * B].rearrange("p (k b) -> p k b", k=KD), ACT.Tanh).then_inc(*signal)

        act.wait_ge(pe_s.sem, pe_s.at("rec_0", 0, "t0"))
        step(0, bank[0], signals(act_s, "rec_0")("t0"))
        done = signals(act_s, "rec_loop")
        with act.Fori(0, (S - 2) // 2) as i:
            PE, ACTS, DVE, POOL = after("rec_loop", i)
            for u in range(2):
                act.wait_ge(*PE(f"t{u}"))
                step(bass.ds(2 * i + 1 + u, 1), bank[(1 + u) % 2], done(f"t{u}"))
        act.wait_ge(pe_s.sem, pe_s.at("rec_9", 0, "t0"))
        step(S - 1, bank[1], signals(act_s, "rec_9")("t0"))

        done = signals(act_s, "rec")
        act.wait_ge(act_s.sem, act_s.all("rec_9"))
        with act.Fori(0, NCH) as i:
            PE, ACTS, DVE, POOL = after("rec", i)
            act.wait_ge(*PE("out", back=1))
            act.sem_inc(held, 1)
            for k in range(KD):
                last = nc.scalar.activation(sT[:, k, :].rearrange("p (b t) -> p b t", b=BC),
                                            state[:, k, :, bass.ds(i * BC, BC)].rearrange("p t b -> p b t"), ACT.Identity)
            last.then_inc(*done("sT"))

    def rec_dve():
        dve, st = nc.vector, "rec_in"
        others_done(dve, "spike")
        dve.wait_ge(w_loaded["rec"], 16)
        with dve.Fori(0, NCH // 2) as i:
            def chunk(lane):
                c = 2 * i + lane
                bk = bank[4 * lane:4 * lane + 4]
                PE, ACTS, DVE, POOL = after(st, i, "AB"[lane])
                done = signals(dve_s, st, "AB"[lane])
                dve.wait_ge(ctxT2_loaded[lane], i * 16 + 16)
                nc.vector.tensor_tensor(c2[lane][:], ctxT[lane][:], ctxT[lane][:], ALU.mult).then_inc(*done("c2"))
                yield
                dve.wait_ge(*DVE("c2"))
                for k in range(KD):
                    for b in range(BC):
                        nc.vector.tensor_tensor_scan(rT1[lane][:, k, b * P:(b + 1) * P], RW("decay")[:, k:k + 1].to_broadcast([P, P]),
                                                     c2[lane][:, k, b * P:(b + 1) * P], 0.0, ALU.mult, ALU.add).then_inc(*done(f"r{k}{b}"))
                        yield
                dve.wait_ge(*PE("xT"))
                nc.vector.tensor_copy(xnT[lane][:].rearrange("p k t -> p (k t)"), bk[0][:]).then_inc(*done("xT"))
                yield
                dve.wait_ge(*DVE("xT"))
                nc.vector.tensor_tensor(ret[lane][:], xnT[lane][:], rT1[lane][:], ALU.mult).then_inc(*done("ret"))
                yield
                dve.wait_ge(*ACTS("gate"))
                nc.vector.tensor_tensor(gc[lane][:].rearrange("p k (b t) -> p k b t", b=BC),
                                        gate[:, :, :, bass.ds(c * BC, BC)].rearrange("p k t b -> p k b t"),
                                        inp[lane][:].rearrange("p k (b t) -> p k b t", b=BC), ALU.mult).then_inc(*done("gc"))
                yield
                dve.wait_ge(*DVE("gc"))
                nc.vector.tensor_tensor(cin[lane][:], inp[lane][:], gc[lane][:], ALU.subtract).then_inc(*done("cin"))
                yield

            in_turns(chunk)

        nc.vector.memset(z[:], 0.0).then_inc(*signals(dve_s, "rec_0")("z0"))

        def gated(t_gate, t_state, signal):
            nc.vector.tensor_tensor(z[:], gate[:, :, t_gate, :], state[:, :, t_state, :], ALU.mult).then_inc(*signal)

        done = signals(dve_s, "rec_loop")
        with dve.Fori(0, (S - 2) // 2) as i:
            PE, ACTS, DVE, POOL = after("rec_loop", i)
            dve.wait_ge(act_s.sem, act_s.at("rec_loop", i, "t1", back=1))
            gated(bass.ds(2 * i + 1, 1), bass.ds(2 * i, 1), done("z0"))
            dve.wait_ge(*ACTS("t0"))
            gated(bass.ds(2 * i + 2, 1), bass.ds(2 * i + 1, 1), done("z1"))
        dve.wait_ge(act_s.sem, act_s.all("rec_loop"))
        gated(S - 1, S - 2, signals(dve_s, "rec_9")("z0"))
        done = signals(dve_s, "rec")
        with dve.Fori(0, NCH) as i:
            PE, ACTS, DVE, POOL = after("rec", i)
            dve.wait_ge(*PE("out"))
            dve.wait_ge(*POOL("bo"))
            nc.vector.tensor_tensor(x[:, bass.ds(i * BC, BC), :], bank[3][:].rearrange("p (b d) -> p b d", b=BC),
                                    x[:, bass.ds(i * BC, BC), :], ALU.add).then_inc(*done("res"))
            alone(stats("rec", i))

    def rec_pool():
        pool = nc.gpsimd
        others_done(pool, "spike")
        pool.wait_ge(w_loaded["rec"], 16)
        pool.wait_ge(act_s.sem, act_s.all("rec_in"))
        done = signals(pool_s, "rec")
        with pool.Fori(0, NCH) as i:
            nc.gpsimd.tensor_tensor(x[:, bass.ds(i * BC, BC), :], x[:, bass.ds(i * BC, BC), :], over(RW("bo"), BC),
                                    ALU.add).then_inc(*done("bo"))
            alone(stats_root("rec", i))

    MW = weights["moe"]
    router = MW("router").rearrange("p (k e) -> p k e", k=KD)
    sgu = MW("sgu").rearrange("p (k f) -> p k f", k=KD)
    sdown = MW("sdown").rearrange("p (k d) -> p k d", k=2)
    RING = 8
    GU = KD * 2 * FE
    ring = area("ring", [P, RING, GU + 2 * D], 0)
    M0 = RING * (GU + 2 * D)
    MOE_LANE = 3014
    EX0 = M0 + 2 * MOE_LANE
    lg1 = [area(f"lg1{n}", [P, BC, NE], M0 + n * MOE_LANE) for n in range(2)]
    mr1 = [area(f"mr1{n}", [P, BC, NE], M0 + 128 + n * MOE_LANE) for n in range(2)]
    pick = [area(f"pick{n}", [P, BC, NE], M0 + 256 + n * MOE_LANE) for n in range(2)]
    gates1 = [area(f"gates1{n}", [P, BC, NE], M0 + 384 + n * MOE_LANE) for n in range(2)]
    far = [area(f"far{n}", [P, BC, NE], M0 + 512 + n * MOE_LANE) for n in range(2)]
    fits = [area(f"fits{n}", [P, BC, NE], M0 + 640 + n * MOE_LANE) for n in range(2)]
    key = [area(f"key{n}", [P, BC, NE], M0 + 768 + n * MOE_LANE) for n in range(2)]
    same = [area(f"same{n}", [P, TOPK, NE], M0 + 896 + n * MOE_LANE) for n in range(2)]
    pickb = [area(f"pickb{n}", [P, BC, NE], M0 + 1408 + n * MOE_LANE, BF16) for n in range(2)]
    weight = [area(f"weight{n}", [P, BC, TOPK], EX0 + 3200 + 16 * n) for n in range(2)]
    seen = area("seen", [P, NE], M0 + 1472, BF16)
    mx1 = [area(f"mx1{n}", [P, BC, TOPK], M0 + 1504 + n * MOE_LANE) for n in range(2)]
    nmx1 = [area(f"nmx1{n}", [P, BC], M0 + 1520 + n * MOE_LANE) for n in range(2)]
    den1 = [area(f"den1{n}", [P, 2, BC], M0 + 1522 + n * MOE_LANE) for n in range(2)]
    mk = [area(f"mk{n}", [P, BC, TOPK], M0 + 1526 + n * MOE_LANE) for n in range(2)]
    spill = [area(f"spill{n}", [P, BC, TOPK], M0 + 1542 + n * MOE_LANE) for n in range(2)]
    slot = [area(f"slot{n}", [P, BC, TOPK], M0 + 1558 + n * MOE_LANE).bitcast(I32) for n in range(2)]
    rows_w = [area(f"rows_w{n}", [P, BC, TOPK, 2], M0 + 1574 + n * MOE_LANE) for n in range(2)]
    tri_b = area("tri_b", [P, P], M0 + 1606, BF16)
    ones_b = area("ones_b", [P, P], M0 + 1670, BF16)
    sg = [area(f"sg{n}", [P, BC, FE], M0 + 1734 + n * MOE_LANE) for n in range(2)]
    hs = [area(f"hs{n}", [P, BC, FE], M0 + 2118 + n * MOE_LANE) for n in range(2)]
    hsT = [area(f"hsT{n}", [P, 2, TOK], M0 + 2502 + n * MOE_LANE) for n in range(2)]
    xg = [area(f"xg{n}", [P, 2, D], EX0 + 512 * n) for n in range(2)]
    xgT = [area(f"xgT{n}", [P, 2, D], EX0 + 1024 + 512 * n) for n in range(2)]
    y = [area(f"y{n}", [P, 2, D], EX0 + 2048 + 512 * n) for n in range(2)]
    slot_tok = area("slot_tok", [P, NE, 2], EX0 + 3072)
    acc_in = [area(f"acc_in{n}", [P, 2, BC, D], 1024 * n) for n in range(2)]
    gidx = sb("gather_rows", [P, 4], I32)
    sidx = sb("scatter_rows", [P, 2], I32)
    idx_all = sb("idx_all", [P, NE + 4], I32)
    NSLOT = NE * CAP
    table = nc.dram_tensor("slot_table", (NSLOT + B * S * TOPK, 2), F32, kind="Internal").ap()
    xn_rows = nc.dram_tensor("normalised_rows", (B * S + P, D), F32, kind="Internal").ap()
    acc = [nc.dram_tensor(f"routed_sum_{u}", (B * S + P, D), F32, kind="Internal").ap() for u in range(2)]
    table_set, rows_set, acc_set = sem("table_initialised"), sem("spare_row_zeroed"), sem("routed_sum_zeroed")
    rows_stored = [sem(f"rows_stored_{n}") for n in range(2)]
    scattered, table_read = sem("slots_scattered"), sem("table_read")
    gu_in = [sem(f"expert_weights_loaded_{q}") for q in range(RING // 2)]
    gathered = [[sem(f"rows_gathered_{par}{u}") for u in range(2)] for par in range(2)]
    added, acc_read = ([sem(f"{n}_{u}") for u in range(2)] for n in ("routed_rows_added", "routed_sum_read"))
    slots_free = sem("chunk_scattered")
    y_free = [[sem(f"expert_rows_added_{par}{u}") for u in range(2)] for par in range(2)]
    moe_ready = sem("moe_constants_ready")
    stage("moe_in", NCH // 2, pe=both(["xT", "lg", "sgu0", "sgu1", "pos", "hsT", "sout"]),
          act=both(["prep0", "prep1", "ex", "sg0", "sg1"]),
          dve=both(["xT", "lg", "mx0", "mx1", "nmx", "mr0", "mr1", "pick", "pickb", "em", "sum", "rec", "gates",
                    ("seen", "seen2"), "far", "fits", "key", "mk0", "mk1", "back", "slot0"]
                   + [f"{a}{b}" for b in range(BC) for a in ("eq", "ew", "wk")]
                   + ["hs0", "hs1", ("slot", "tok", "weight"), "hsT", "hsT1", "sres"]), pool=[])
    QS = range(RING // 2)
    stage("moe_x", 1, pe=["x0", "x1"], act=["x0", "x1"], dve=[], pool=[])
    stage("moe_ex", NE // RING, pe=[f"{a}{q}{u}" for q in QS for a in "gxhd" for u in range(2)],
          act=[f"{a}{q}{u}" for q in QS for a in "sxy" for u in range(2)],
          dve=[f"{a}{q}{u}" for q in QS for a in "ht" for u in range(2)], pool=[])

    def pair_before(q):
        return (q - 1) % (RING // 2), int(q == 0)
    stage("moe", NCH // 2, pe=[], act=[], dve=both(["res0", "res"] + LN_DVE), pool=both(["rstd"]))
    hT = hsT[0]
    sg_ex, hs_ex = sg[0], hs[0]

    def moe_sp():
        sp = nc.sync
        sp.dma_start(table, ins["table0"]).then_inc(table_set, 16)
        sp.wait_ge(zeroed, 1)
        sp.dma_start(xn_rows[B * S:B * S + P, :], zrow[:]).then_inc(rows_set, 16)
        for u in range(2):
            sp.dma_start(acc[u].rearrange("(b p) d -> p b d", p=P), over(zrow[:], B + 1)).then_inc(acc_set, 16)
        others_done(sp, "rec")
        load_weights(sp, "bit")
        st = "moe_in"
        with sp.Fori(0, NCH // 2) as i:
            def chunk(lane):
                c = 2 * i + lane
                PE, ACTS, DVE, POOL = after(st, i, "AB"[lane])
                sp.wait_ge(*ACTS("prep1"))
                sp.dma_start(xn_rows[bass.ds(c * TOK, TOK), :].rearrange("(b p) d -> p b d", p=P), xn[lane][:]).then_inc(rows_stored[lane], 16)
                yield

            in_turns(chunk)


        def load_pair(q, e):
            sp.dma_start(ring[:, 2 * q:2 * q + 2, 0:GU], ins["w_gate_up"][bass.ds(e, 2)].rearrange("e p c -> p e c")).then_inc(gu_in[q], 16)
            sp.dma_start(ring[:, 2 * q:2 * q + 2, GU:GU + D], ins["w_down"][bass.ds(e, 2), 0:P].rearrange("e p c -> p e c")).then_inc(gu_in[q], 16)
            sp.dma_start(ring[0:FE - P, 2 * q:2 * q + 2, GU + D:], ins["w_down"][bass.ds(e, 2), P:FE].rearrange("e p c -> p e c")).then_inc(gu_in[q], 16)

        sp.wait_ge(moe_ready, 1)
        for q in QS:
            load_pair(q, 2 * q)
        sp.wait_ge(slots_free, NCH + 2)
        sp.dma_start(slot_tok[:], table[0:NSLOT, :].rearrange("(e p) c -> p e c", p=P)).then_inc(table_read, 16)
        with sp.Fori(0, NE // RING - 1) as o:
            for q in QS:
                sp.wait_ge(pe_s.sem, pe_s.at("moe_ex", o, f"d{q}1"))
                load_pair(q, (o + 1) * RING + 2 * q)
        others_done(sp, "moe_ex")
        for u in range(2):
            sp.wait_ge(added[u], 8 * NE + 16)
            for par in range(2):
                sp.wait_ge(gathered[par][u], 4 * NE + 16)
        with sp.Fori(0, NCH // 2) as i:
            for lane in range(2):
                sp.wait_ge(dve_s.sem, dve_s.at("moe", i, f"res{"AB"[lane]}", back=1))
                for u in range(2):
                    sp.dma_start(acc_in[lane][:, u], acc[u][bass.ds((2 * i + lane) * TOK, TOK), :].rearrange("(b p) d -> p b d", p=P)).then_inc(
                        acc_read[lane], 16)

    def moe_pe():
        pe, st = nc.tensor, "moe_in"
        others_done(pe, "rec")
        pe.wait_ge(w_loaded["moe"], 16)
        pe.wait_ge(moe_ready, 2)
        with pe.Fori(0, NCH // 2) as i:
            def chunk(lane):
                bk = bank[4 * lane:4 * lane + 4]
                PE, ACTS, DVE, POOL = after(st, i, "AB"[lane])
                done = signals(pe_s, st, "AB"[lane])
                yield from turn_x(st, i, lane, bk[0])
                pe.wait_ge(*DVE("xT"))
                for b in range(BC):
                    for k in range(KD):
                        last = nc.tensor.matmul(bk[1][:, b * NE:(b + 1) * NE], xnT[lane][:, k, b * P:(b + 1) * P], router[:, k, :],
                                                start=k == 0, stop=k == KD - 1)
                last.then_inc(*done("lg"))
                yield
                for b in range(BC):
                    for k in range(KD):
                        last = nc.tensor.matmul(bk[2 + b][:, 0:2 * FE], xnT[lane][:, k, b * P:(b + 1) * P], sgu[:, k, :],
                                                start=k == 0, stop=k == KD - 1)
                    last.then_inc(*done(f"sgu{b}"))
                    yield
                pe.wait_ge(*DVE("pickb"))
                pe.wait_ge(dve_s.sem, dve_s.at(st, i, "seen2A") if lane else dve_s.at(st, i, "seen2B", back=1))
                for b in range(BC):
                    parts = [(tri_b, pickb[lane][:, b, :]), (ones_b, seen[:])] + [(ones_b, pickb[lane][:, 0, :])] * b
                    for n, (w, m) in enumerate(parts):
                        last = nc.tensor.matmul(bk[0][:, b * NE:(b + 1) * NE], w[:], m, start=n == 0, stop=n == len(parts) - 1)
                last.then_inc(*done("pos"))
                yield
                pe.wait_ge(*DVE("hs1"))
                for b in range(BC):
                    nc.tensor.transpose(bk[1][:, b * P:(b + 1) * P], hs[lane][:, b, 0:P], ident[:])
                for b in range(BC):
                    last = nc.tensor.transpose(bk[1][0:FE - P, TOK + b * P:TOK + (b + 1) * P], hs[lane][:, b, P:FE], ident[:])
                last.then_inc(*done("hsT"))
                yield
                pe.wait_ge(*DVE("hsT1"))
                for b in range(BC):
                    for k in range(2):
                        last = nc.tensor.matmul(bk[2][:, b * D:(b + 1) * D], hsT[lane][:, k, b * P:(b + 1) * P], sdown[:, k, :],
                                                start=k == 0, stop=k == 1)
                last.then_inc(*done("sout"))
                yield

            in_turns(chunk)

        quantise_pe()
        others_done(pe, "moe_in")

        def turn_rows(par, u, value, signal):
            pe.wait_ge(gathered[par][u], value)
            for k in range(KD):
                last = nc.tensor.transpose(bank[u][:, k * P:(k + 1) * P], xg[par][:, u, k * P:(k + 1) * P], ident[:])
            last.then_inc(*signal)

        for u in range(2):
            turn_rows(0, u, 16, signals(pe_s, "moe_x")(f"x{u}"))
        pe.wait_ge(act_s.sem, act_s.all("moe_x"))
        done = signals(pe_s, "moe_ex")
        with pe.Fori(0, NE // RING) as o:
            PE, ACTS, DVE, POOL = after("moe_ex", o)
            for q in QS:
                before, back = pair_before(q)
                pe.wait_ge(gu_in[q], o * 48 + 48)
                for u in range(2):
                    pe.wait_ge(*ACTS(f"x{before}{u}", back=back))
                    for k in range(KD):
                        last = nc.tensor.matmul(bank[2 + u][:, 0:2 * FE], xgT[q % 2][:, u, k * P:(k + 1) * P],
                                                ring[:, 2 * q + u, k * 2 * FE:(k + 1) * 2 * FE], start=k == 0, stop=k == KD - 1)
                    last.then_inc(*done(f"g{q}{u}"))
                for u in range(2):
                    turn_rows((q + 1) % 2, u, o * (8 * (RING // 2)) + 16 * ((q + 1) // 2 + 1), done(f"x{q}{u}"))
                for u in range(2):
                    pe.wait_ge(*DVE(f"h{q}{u}"))
                    pe.sem_inc(held, 1)
                    nc.tensor.transpose(bank[4 + u][:, 0:P], hs_ex[:, u, 0:P], ident[:])
                    nc.tensor.transpose(bank[4 + u][0:FE - P, P:2 * P], hs_ex[:, u, P:FE], ident[:]).then_inc(*done(f"h{q}{u}"))
                for u in range(2):
                    pe.wait_ge(*DVE(f"t{q}{u}"))
                    pe.wait_ge(*ACTS(f"y{before}{u}", back=back))
                    for k in range(2):
                        last = nc.tensor.matmul(bank[6 + u][:, 0:D], hT[:, k, u * P:(u + 1) * P],
                                                ring[:, 2 * q + u, GU + k * D:GU + (k + 1) * D], start=k == 0, stop=k == 1)
                    last.then_inc(*done(f"d{q}{u}"))

    def moe_act():
        act, st = nc.scalar, "moe_in"
        others_done(act, "rec")
        with act.Fori(0, NCH // 2) as i:
            def chunk(lane):
                bk = bank[4 * lane:4 * lane + 4]
                PE, ACTS, DVE, POOL = after(st, i, "AB"[lane])
                done = signals(act_s, st, "AB"[lane])
                act.wait_ge(rows_stored[lane], i * 16 + 16)
                act.sem_inc(held, 1)
                yield from prep(st, i, lane)
                act.wait_ge(*DVE("nmx"))
                for b in range(BC):
                    last = nc.scalar.activation(gates1[lane][:, b, :], lg1[lane][:, b, :], ACT.Exp, bias=nmx1[lane][:, b:b + 1])
                last.then_inc(*done("ex"))
                yield
                for b in range(BC):
                    act.wait_ge(*PE(f"sgu{b}"))
                    nc.scalar.activation(sg[lane][:, b, :], bk[2 + b][:, 0:FE], ACT.Silu).then_inc(*done(f"sg{b}"))
                    yield

            in_turns(chunk)

        others_done(act, "moe_in")
        for u in range(2):
            act.wait_ge(pe_s.sem, pe_s.at("moe_x", 0, f"x{u}"))
            nc.scalar.activation(xgT[0][:, u, :], bank[u][:, 0:D], ACT.Identity).then_inc(*signals(act_s, "moe_x")(f"x{u}"))
        act.wait_ge(table_read, 16)
        done = signals(act_s, "moe_ex")
        with act.Fori(0, NE // RING) as o:
            PE, ACTS, DVE, POOL = after("moe_ex", o)
            for q in QS:
                for u in range(2):
                    act.wait_ge(*PE(f"g{q}{u}"))
                    nc.scalar.activation(sg_ex[:, u, :], bank[2 + u][:, 0:FE], ACT.Silu).then_inc(*done(f"s{q}{u}"))
                for u in range(2):
                    act.wait_ge(*PE(f"x{q}{u}"))
                    nc.scalar.activation(xgT[(q + 1) % 2][:, u, :], bank[u][:, 0:D], ACT.Identity).then_inc(*done(f"x{q}{u}"))
                for u in range(2):
                    act.wait_ge(*PE(f"d{q}{u}"))
                    act.wait_ge(y_free[q % 2][u], o * (RING // 4) + q // 2 + 1)
                    act.sem_inc(held, 1)
                    nc.scalar.activation(y[q % 2][:, u, :], bank[6 + u][:, 0:D], ACT.Identity,
                                         scale=slot_tok[:, bass.ds(o * RING + 2 * q + u, 1), 1]).then_inc(*done(f"y{q}{u}"))

    def moe_pool():
        pool = nc.gpsimd
        pool.sem_inc(slots_free, 2)
        for u in range(2):
            pool.sem_inc(rows_stored[u], 16)
            pool.sem_inc(y_free[0][u], 1)
        pool.wait_ge(table_set, 16)
        with pool.Fori(0, NCH // 2) as i:
            for lane in range(2):
                pool.wait_ge(dve_s.sem, dve_s.at("moe_in", i, f"weight{"AB"[lane]}"))
                pool.sem_inc(held, 1)
                for b in range(BC):
                    for k in range(TOPK):
                        pool.indirect_dma_start(table[:, :], bass.IndirectOffsetOnAxis(ap=slot[lane][:, b, k:k + 1], axis=0),
                                                rows_w[lane][:, b, k, :], None).then_inc(scattered, 16)
                pool.wait_ge(scattered, (2 * i + lane + 1) * (16 * BC * TOPK))
                pool.sem_inc(slots_free, 1)
        others_done(pool, "moe_in")
        pool.wait_ge(table_read, 16)
        for lane in range(2):
            pool.wait_ge(rows_stored[lane], 16 * (NCH // 2) + 16)
        pool.wait_ge(rows_set, 16)
        pool.wait_ge(acc_set, 32)
        pool.wait_ge(moe_ready, 3)

        def gather(pair, par):
            pool.sem_inc(held, 1)
            for u in range(2):
                nc.gpsimd.tensor_copy(gidx[:, 2 * par + u:2 * par + u + 1], idx_all[:, bass.ds(2 * pair + u, 1)]).then_inc(gidx_set, 1)
            pool.wait_ge(gidx_set, 2 * pair + 2)
            pool.sem_inc(held, 1)
            for u in range(2):
                pool.indirect_dma_start(xg[par][:, u, :], None, xn_rows[:, :],
                                        bass.IndirectOffsetOnAxis(ap=gidx[:, 2 * par + u:2 * par + u + 1], axis=0)).then_inc(gathered[par][u], 16)

        gather(0, 0)
        gather(1, 1)
        for u in range(2):
            nc.gpsimd.tensor_copy(sidx[:, u:u + 1], idx_all[:, NE:NE + 1]).then_inc(sidx_set, 1)
        pool.wait_ge(sidx_set, 2)
        pool.sem_inc(held, 1)
        for u in range(2):
            pool.indirect_dma_start(acc[u][:, :], bass.IndirectOffsetOnAxis(ap=sidx[:, u:u + 1], axis=0), zrow[:], None,
                                    compute_op=ALU.add).then_inc(added[u], 16)
        pool.wait_ge(pe_s.sem, pe_s.all("moe_x"))
        with pool.Fori(0, NE // RING) as o:
            for q in QS:
                pair = o * (RING // 2) + q
                before, back = pair_before(q)
                pool.wait_ge(pe_s.sem, pe_s.at("moe_ex", o, f"x{before}1", back=back))
                gather(pair + 2, q % 2)
                for u in range(2):
                    pool.wait_ge(added[u], 16 * pair + 16)
                    pool.sem_inc(y_free[(q + 1) % 2][u], 1)
                for u in range(2):
                    nc.gpsimd.tensor_copy(sidx[:, u:u + 1], idx_all[:, bass.ds(2 * pair + u, 1)]).then_inc(sidx_set, 1)
                pool.wait_ge(sidx_set, 2 * pair + 4)
                for u in range(2):
                    pool.wait_ge(act_s.sem, act_s.at("moe_ex", o, f"y{q}{u}"))
                    pool.sem_inc(held, 1)
                    pool.indirect_dma_start(acc[u][:, :], bass.IndirectOffsetOnAxis(ap=sidx[:, u:u + 1], axis=0), y[q % 2][:, u, :], None,
                                            compute_op=ALU.add).then_inc(added[u], 16)
        with pool.Fori(0, NCH // 2) as i:
            in_turns(lambda lane: stats_root("moe", i, lane))

    def moe_dve():
        dve, st = nc.vector, "moe_in"
        others_done(dve, "rec")
        dve.wait_ge(consts_loaded, 16)
        nc.vector.memset(seen[:], 0.0)
        nc.vector.memset(ring[64:P, :, GU + D:], 0.0)
        nc.vector.memset(hsT[0][64:P, 1, :], 0.0)
        nc.vector.memset(hsT[1][64:P, 1, :], 0.0).then_inc(moe_ready, 1)
        nc.vector.memset(ones_b[:], 1.0)
        nc.vector.tensor_copy(tri_b[:], C("tri")).then_inc(moe_ready, 1)
        with dve.Fori(0, NCH // 2) as i:
            def chunk(lane):
                c = 2 * i + lane
                bk = bank[4 * lane:4 * lane + 4]
                PE, ACTS, DVE, POOL = after(st, i, "AB"[lane])
                done = signals(dve_s, st, "AB"[lane])
                dve.wait_ge(*PE("xT"))
                nc.vector.tensor_copy(xnT[lane][:].rearrange("p k t -> p (k t)"), bk[0][:]).then_inc(*done("xT"))
                yield
                dve.wait_ge(*PE("lg"))
                nc.vector.tensor_copy(lg1[lane][:].rearrange("p b e -> p (b e)"), bk[1][:, 0:BC * NE]).then_inc(*done("lg"))
                yield
                dve.wait_ge(*DVE("lg"))
                dve.sem_inc(held, 1)
                for b in range(BC):
                    nc.vector.max(mx1[lane][:, b, :], lg1[lane][:, b, :]).then_inc(*done(f"mx{b}"))
                    yield
                dve.wait_ge(*DVE("mx1"))
                nc.vector.tensor_scalar(nmx1[lane][:], mx1[lane][:, :, 0], -1.0, None, ALU.mult).then_inc(*done("nmx"))
                yield
                for b in range(BC):
                    nc.vector.match_replace(mr1[lane][:, b, :], mx1[lane][:, b, :], lg1[lane][:, b, :], -3.0e38).then_inc(*done(f"mr{b}"))
                    yield
                dve.wait_ge(*DVE("mr1"))
                nc.vector.tensor_tensor(pick[lane][:], mr1[lane][:], lg1[lane][:], ALU.not_equal).then_inc(*done("pick"))
                yield
                dve.wait_ge(*DVE("pick"))
                nc.vector.tensor_copy(pickb[lane][:], pick[lane][:]).then_inc(*done("pickb"))
                yield
                dve.wait_ge(*ACTS("ex"))
                nc.vector.tensor_tensor(gates1[lane][:], gates1[lane][:], pick[lane][:], ALU.mult).then_inc(*done("em"))
                yield
                dve.wait_ge(*DVE("em"))
                nc.vector.tensor_reduce(den1[lane][:, 0, :], gates1[lane][:], AX.X, ALU.add).then_inc(*done("sum"))
                yield
                dve.wait_ge(*DVE("sum"))
                nc.vector.reciprocal(den1[lane][:, 1, :], den1[lane][:, 0, :]).then_inc(*done("rec"))
                yield
                dve.wait_ge(*DVE("rec"))
                nc.vector.tensor_tensor(gates1[lane][:], gates1[lane][:], wide(den1[lane][:, 1, :], NE), ALU.mult).then_inc(*done("gates"))
                yield
                dve.wait_ge(*PE("pos"))
                nc.vector.tensor_tensor(seen[:], seen[:], pickb[lane][:, 0, :], ALU.add).then_inc(*done("seen"))
                dve.wait_ge(*DVE("seen"))
                nc.vector.tensor_tensor(seen[:], seen[:], pickb[lane][:, 1, :], ALU.add).then_inc(*done("seen2"))
                yield
                pos = bk[0][:, 0:BC * NE].rearrange("p (b e) -> p b e", b=BC)
                nc.vector.tensor_tensor(far[lane][:], over(C("slot_base"), BC), pos, ALU.subtract).then_inc(*done("far"))
                yield
                nc.vector.scalar_tensor_tensor(fits[lane][:], pos, float(CAP), pick[lane][:], ALU.is_lt, ALU.mult).then_inc(*done("fits"))
                yield
                dve.wait_ge(*DVE("fits"))
                nc.vector.tensor_tensor(key[lane][:], far[lane][:], fits[lane][:], ALU.mult).then_inc(*done("key"))
                yield
                dve.wait_ge(*DVE("key"))
                dve.sem_inc(held, 1)
                for b in range(BC):
                    nc.vector.max(mk[lane][:, b, :], key[lane][:, b, :]).then_inc(*done(f"mk{b}"))
                    yield
                dve.wait_ge(*DVE("mk1"))
                nc.vector.scalar_tensor_tensor(spill[lane][:].rearrange("p b k -> p (b k)"), mk[lane][:].rearrange("p b k -> p (b k)"), 0.0,
                                               C("spare")[:, bass.ds(c * BC * TOPK, BC * TOPK)], ALU.is_equal, ALU.mult).then_inc(*done("back"))
                yield
                dve.wait_ge(*DVE("back"))
                nc.vector.tensor_tensor(spill[lane][:], spill[lane][:], mk[lane][:], ALU.subtract).then_inc(*done("slot0"))
                yield
                for b in range(BC):
                    if b:
                        dve.wait_ge(*DVE("wk0"))
                    nc.vector.tensor_tensor(same[lane][:], over(key[lane][:, b, :], TOPK), wide(mk[lane][:, b, :], NE), ALU.is_equal).then_inc(*done(f"eq{b}"))
                    yield
                    dve.wait_ge(*DVE(f"eq{b}"))
                    nc.vector.tensor_tensor(same[lane][:], same[lane][:], over(gates1[lane][:, b, :], TOPK), ALU.mult).then_inc(*done(f"ew{b}"))
                    yield
                    dve.wait_ge(*DVE(f"ew{b}"))
                    nc.vector.tensor_reduce(weight[lane][:, b, :], same[lane][:], AX.X, ALU.add).then_inc(*done(f"wk{b}"))
                    yield
                for b in range(BC):
                    dve.wait_ge(*ACTS(f"sg{b}"))
                    nc.vector.tensor_tensor(hs[lane][:, b, :], sg[lane][:, b, :], bk[2 + b][:, FE:2 * FE], ALU.mult).then_inc(*done(f"hs{b}"))
                    yield
                dve.wait_ge(slots_free, c + 1)
                nc.vector.tensor_scalar(slot[lane][:], spill[lane][:], float(NSLOT), None, ALU.add).then_inc(*done("slot"))
                nc.vector.tensor_copy(rows_w[lane][:, :, :, 0], wide(C("tokens")[:, bass.ds(c * BC, BC)], TOPK)).then_inc(*done("tok"))
                dve.wait_ge(*DVE("wk1"))
                nc.vector.tensor_copy(rows_w[lane][:, :, :, 1], weight[lane][:]).then_inc(*done("weight"))
                yield
                dve.wait_ge(*PE("hsT"))
                nc.vector.tensor_copy(hsT[lane][:, 0, :], bk[1][:, 0:TOK]).then_inc(*done("hsT"))
                yield
                nc.vector.tensor_copy(hsT[lane][0:FE - P, 1, :], bk[1][0:FE - P, TOK:2 * TOK]).then_inc(*done("hsT1"))
                yield
                dve.wait_ge(*PE("sout"))
                nc.vector.tensor_tensor(x[:, bass.ds(c * BC, BC), :], bk[2][:].rearrange("p (b d) -> p b d", b=BC),
                                        x[:, bass.ds(c * BC, BC), :], ALU.add).then_inc(*done("sres"))
                yield

            in_turns(chunk)

        quantise_dve()
        dve.wait_ge(table_read, 16)
        nc.vector.tensor_copy(idx_all[:, NE:], C("tokens")[:, 0:4])
        nc.vector.tensor_copy(idx_all[:, 0:NE], slot_tok[:, :, 0]).then_inc(moe_ready, 1)
        done = signals(dve_s, "moe_ex")
        others_done(dve, "moe_in")
        with dve.Fori(0, NE // RING) as o:
            PE, ACTS, DVE, POOL = after("moe_ex", o)
            for q in QS:
                for u in range(2):
                    dve.wait_ge(*ACTS(f"s{q}{u}"))
                    nc.vector.tensor_tensor(hs_ex[:, u, :], sg_ex[:, u, :], bank[2 + u][:, FE:2 * FE], ALU.mult).then_inc(*done(f"h{q}{u}"))
                for u in range(2):
                    dve.wait_ge(*PE(f"h{q}{u}"))
                    nc.vector.tensor_copy(hT[:, 0, u * P:(u + 1) * P], bank[4 + u][:, 0:P])
                    nc.vector.tensor_copy(hT[0:FE - P, 1, u * P:(u + 1) * P], bank[4 + u][0:FE - P, P:2 * P]).then_inc(*done(f"t{q}{u}"))
        with dve.Fori(0, NCH // 2) as i:
            def chunk(lane):
                c = 2 * i + lane
                done = signals(dve_s, "moe", "AB"[lane])
                PE, ACTS, DVE, POOL = after("moe", i, "AB"[lane])
                dve.wait_ge(acc_read[lane], i * 32 + 32)
                nc.vector.tensor_tensor(x[:, bass.ds(c * BC, BC), :], acc_in[lane][:, 0], x[:, bass.ds(c * BC, BC), :], ALU.add).then_inc(*done("res0"))
                yield
                dve.wait_ge(*DVE("res0"))
                nc.vector.tensor_tensor(x[:, bass.ds(c * BC, BC), :], acc_in[lane][:, 1], x[:, bass.ds(c * BC, BC), :], ALU.add).then_inc(*done("res"))
                yield
                yield from stats("moe", i, lane)

            in_turns(chunk)

    LW = weights["mlstm"]
    gq = LW("gq").rearrange("p (k g) -> p k g", k=KD)
    BH = BC * HL
    gkv = area("gkv", [P, KD, 2 * HL], 0)
    MLSTM_LANE = 5600
    lnw1 = area("lnw1", [P, D], 16)
    vext = [area(f"vext{n}", [P, BC, HL, DL + 1], 1264 + n * MLSTM_LANE) for n in range(2)]
    late_b = area("late_b", [P, HL * P], 272, BF16)
    ident_b = area("ident_b", [P, P], 528, BF16)
    triI = area("triI", [P, P], 592)
    mhalf8 = area("mhalf8", [P, BH], 720)
    gt = [area(f"gt{n}", [P, BC, 2 * HL], 1784 + n * MLSTM_LANE) for n in range(2)]
    mnf, nab, yv, lnu, uu, e1, ru, cr, lf, cs, av, cm, ne, ab, nr, hsum, hsq, hvar, hrs = (
        [area(f"s{k}_{n}", [P, BC, HL], 1800 + 8 * k + n * MLSTM_LANE) for n in range(2)] for k in range(19))
    aT = [area(f"aT{n}", [BH, P], 1952 + n * MLSTM_LANE) for n in range(2)]
    cmax = [area(f"cmax{n}", [BH, P], 2080 + n * MLSTM_LANE) for n in range(2)]
    cdiag = [area(f"cdiag{n}", [BH, BH, P], 2208 + n * MLSTM_LANE) for n in range(2)]
    decayT = [area(f"decayT{n}", [P, 2, BC * HL // 2, P], 3232 + n * MLSTM_LANE) for n in range(2)]
    cT = [area(f"cT{n}", [P, 2, BC * HL // 2, P], 4256 + n * MLSTM_LANE) for n in range(2)]
    hst = [area(f"hst{n}", [P, BC, D], 5280 + n * MLSTM_LANE) for n in range(2)]
    hce = [area(f"hce{n}", [P, BC, D], 5792 + n * MLSTM_LANE) for n in range(2)]
    hq = [area(f"hq{n}", [P, BC, D], 6304 + n * MLSTM_LANE) for n in range(2)]
    mlstm_ready = sem("mlstm_constants_ready")
    stage("mlstm", NCH // 2, pe=both(["xT", "gates", "cs", "aT", "qk", "cm", "cb0", "cb1", "ho0", "ho1"]),
          act=both(["prep0", "prep1", "ey", "ln", "D", "ne"]),
          dve=both(["xT", "gt", "mnf", "nab", "u", "e1", "ru", "cr", "t", "lf", "cs", "a", "aT", "cmax", "cdiag", "cm",
                    "cT0", "cT1", "ab0", "ab1", "abs", "nr", "nre", "rn", "h0", "h1", "hsum", "hce", "hq", "hsq", "hvar", "hn", "w", "res"] + LN_DVE),
          pool=both(["hrs", "rstd"]))

    def mlstm_sp():
        sp, st = nc.sync, "mlstm"
        others_done(sp, "moe")
        sp.wait_ge(mlstm_ready, 1)
        with sp.Fori(0, NCH // 2) as i:
            def chunk(lane):
                c = 2 * i + lane
                PE, ACTS, DVE, POOL = after(st, i, "AB"[lane])
                sp.wait_ge(*PE("qk", back=1))
                sp.dma_start(ctxT[lane][:], ctxT_dram[:, :, bass.ds(c * TOK, TOK)]).then_inc(ctxT3_loaded[lane], 16)
                sp.wait_ge(*PE("ho1", back=1))
                for b in range(BC):
                    sp.dma_start(vext[lane][:, b, :, 0:DL], ctx_dram[:, bass.ds(c * BC + b, 1), :].rearrange("s b (h d) -> s (b h) d", h=HL)).then_inc(
                        ctx_loaded[lane], 16)
                yield

            in_turns(chunk)

    def mlstm_pe():
        pe, st = nc.tensor, "mlstm"
        others_done(pe, "moe")
        pe.wait_ge(w_loaded["mlstm"], 16)
        pe.wait_ge(mlstm_ready, 2)
        with pe.Fori(0, NCH // 2) as i:
            def chunk(lane):
                bk = bank[4 * lane:4 * lane + 4]
                PE, ACTS, DVE, POOL = after(st, i, "AB"[lane])
                done = signals(pe_s, st, "AB"[lane])
                pe.wait_ge(*DVE("h1", back=1))
                yield from turn_x(st, i, lane, bk[0])
                pe.wait_ge(ctxT3_loaded[lane], i * 16 + 16)
                pe.wait_ge(*DVE("xT"))
                for b in range(BC):
                    for n, (src, w) in enumerate(((xnT[lane], gq), (ctxT[lane], gkv))):
                        for k in range(KD):
                            last = nc.tensor.matmul(bk[1][:, b * 2 * HL:(b + 1) * 2 * HL], src[:, k, b * P:(b + 1) * P], w[:, k, :],
                                                    start=n == 0 and k == 0, stop=n == 1 and k == KD - 1)
                last.then_inc(*done("gates"))
                yield
                pe.wait_ge(*DVE("lf"))
                nc.tensor.matmul(bk[0][:, 0:BH], triI[:], lf[lane][:].rearrange("p b h -> p (b h)"), start=True, stop=True).then_inc(*done("cs"))
                yield
                pe.wait_ge(*DVE("a"))
                pe.sem_inc(held, 1)
                nc.tensor.transpose(bk[1][0:BH, 0:P], av[lane][:].rearrange("p b h -> p (b h)"), ident[:]).then_inc(*done("aT"))
                yield
                for b in range(BC):
                    for h in range(HL):
                        rows = slice(DL * (h % 2), DL * (h % 2) + DL)
                        c = b * HL // 2 + h // 2
                        last = nc.tensor.matmul(bk[2 + h % 2][:, c * P:(c + 1) * P], ctxT[lane][rows, h // 2, b * P:(b + 1) * P],
                                                xnT[lane][rows, h // 2, b * P:(b + 1) * P], start=True, stop=True)
                last.then_inc(*done("qk"))
                yield
                pe.wait_ge(*DVE("cmax"))
                pe.sem_inc(held, 1)
                nc.tensor.transpose(bk[0][:, 0:BH], cmax[lane][:], ident[0:BH, 0:BH]).then_inc(*done("cm"))
                yield
                pe.wait_ge(*DVE("cdiag"))
                for b in range(BC):
                    if b:
                        pe.wait_ge(*DVE("cm"))
                    nc.tensor.matmul(bk[1 - b][:], ones[0:BH, :], cdiag[lane][:, b * HL:(b + 1) * HL, :].rearrange("r h s -> r (h s)"),
                                     start=True, stop=False)
                    nc.tensor.matmul(bk[1 - b][:], ident_b[:], late_b[:], start=False, stop=True).then_inc(*done(f"cb{b}"))
                    yield
                pe.wait_ge(ctx_loaded[lane], i * 32 + 32)
                for b in range(BC):
                    pe.wait_ge(*DVE(f"cT1"))
                    for h in range(HL):
                        last = nc.tensor.matmul(bk[b][:, h * (DL + 1):(h + 1) * (DL + 1)], cT[lane][:, h % 2, b * HL // 2 + h // 2, :],
                                                vext[lane][:, b, h, :], start=True, stop=True)
                    last.then_inc(*done(f"ho{b}"))
                    yield

            in_turns(chunk)

    def mlstm_act():
        act, st = nc.scalar, "mlstm"
        others_done(act, "moe")
        with act.Fori(0, NCH // 2) as i:
            def chunk(lane):
                bk = bank[4 * lane:4 * lane + 4]
                PE, ACTS, DVE, POOL = after(st, i, "AB"[lane])
                done = signals(act_s, st, "AB"[lane])
                yield from prep(st, i, lane)
                act.wait_ge(*DVE("nab"))
                nc.scalar.activation(yv[lane][:], nab[lane][:], ACT.Exp).then_inc(*done("ey"))
                yield
                act.wait_ge(*ACTS("ey"))
                nc.scalar.activation(lnu[lane][:], yv[lane][:], ACT.Ln, bias=ones[:, 0:1]).then_inc(*done("ln"))
                yield
                for b in range(BC):
                    act.wait_ge(*PE(f"cb{b}"))
                    for h in range(HL):
                        last = nc.scalar.activation(decayT[lane][:, h % 2, b * HL // 2 + h // 2, :], bk[1 - b][:, h * P:(h + 1) * P], ACT.Exp,
                                                    bias=av[lane][:, b, h:h + 1], scale=-1.0)
                last.then_inc(*done("D"))
                yield
                act.wait_ge(*DVE("cm"))
                nc.scalar.activation(ne[lane][:], cm[lane][:], ACT.Exp, scale=-1.0).then_inc(*done("ne"))
                yield

            in_turns(chunk)

    def mlstm_pool():
        pool, st = nc.gpsimd, "mlstm"
        others_done(pool, "moe")
        nc.gpsimd.memset(mhalf8[:], -0.5).then_inc(zeroed, 1)
        pool.wait_ge(zeroed, 2)
        with pool.Fori(0, NCH // 2) as i:
            def chunk(lane):
                PE, ACTS, DVE, POOL = after(st, i, "AB"[lane])
                done = signals(pool_s, st, "AB"[lane])
                pool.wait_ge(*DVE("hvar"))
                nc.gpsimd.tensor_tensor(hrs[lane][:].rearrange("p b h -> p (b h)"), hvar[lane][:].rearrange("p b h -> p (b h)"), mhalf8[:],
                                        ALU.pow).then_inc(*done("hrs"))
                yield
                yield from stats_root(st, i, lane)

            in_turns(chunk)

    def mlstm_dve():
        dve, st = nc.vector, "mlstm"
        others_done(dve, "moe")
        dve.wait_ge(w_loaded["mlstm"], 16)
        for v in vext:
            last = nc.vector.memset(v[:, :, :, DL:], 1.0)
        last.then_inc(mlstm_ready, 1)
        nc.vector.tensor_copy(ident_b[:], ident[:])
        nc.vector.tensor_tensor(triI[:], ident[:], C("tri"), ALU.add)
        nc.vector.tensor_tensor(gkv[:].rearrange("p k g -> p (k g)"), LW("gk"), LW("gv"), ALU.add)
        nc.vector.tensor_scalar(lnw1[:], LW("lnw"), 1.0, None, ALU.add)
        nc.vector.tensor_scalar(late_b[:].rearrange("p (h s) -> p h s", h=HL), over(C("late"), HL), 1e30, None, ALU.mult).then_inc(mlstm_ready, 1)
        V = nc.vector
        with dve.Fori(0, NCH // 2) as i:
            def chunk(lane):
                c = 2 * i + lane
                bk = bank[4 * lane:4 * lane + 4]
                PE, ACTS, DVE, POOL = after(st, i, "AB"[lane])
                done = signals(dve_s, st, "AB"[lane])
                dve.wait_ge(*PE("xT"))
                V.tensor_copy(xnT[lane][:].rearrange("p k t -> p (k t)"), bk[0][:]).then_inc(*done("xT"))
                yield
                dve.wait_ge(*PE("gates"))
                V.tensor_tensor(gt[lane][:], bk[1][:, 0:BC * 2 * HL].rearrange("p (b g) -> p b g", b=BC), over(LW("gb"), BC), ALU.add).then_inc(*done("gt"))
                yield
                dve.wait_ge(*DVE("gt"))
                fg, ig = gt[lane][:, :, HL:], gt[lane][:, :, 0:HL]
                V.tensor_scalar(mnf[lane][:], fg, 0.0, None, ALU.min).then_inc(*done("mnf"))
                yield
                dve.wait_ge(*DVE("mnf"))
                V.scalar_tensor_tensor(nab[lane][:], mnf[lane][:], 2.0, fg, ALU.mult, ALU.subtract).then_inc(*done("nab"))
                yield
                dve.wait_ge(*ACTS("ey"))
                V.tensor_scalar(uu[lane][:], yv[lane][:], 1.0, None, ALU.add).then_inc(*done("u"))
                yield
                dve.wait_ge(*DVE("u"))
                V.scalar_tensor_tensor(e1[lane][:], uu[lane][:], -1.0, yv[lane][:], ALU.add, ALU.subtract).then_inc(*done("e1"))
                yield
                V.reciprocal(ru[lane][:], uu[lane][:]).then_inc(*done("ru"))
                yield
                dve.wait_ge(*DVE("ru"))
                V.tensor_tensor(cr[lane][:], e1[lane][:], ru[lane][:], ALU.mult).then_inc(*done("cr"))
                yield
                dve.wait_ge(*ACTS("ln"))
                V.tensor_tensor(lnu[lane][:], mnf[lane][:], lnu[lane][:], ALU.subtract).then_inc(*done("t"))
                yield
                dve.wait_ge(*DVE("t"))
                V.tensor_tensor(lf[lane][:], lnu[lane][:], cr[lane][:], ALU.add).then_inc(*done("lf"))
                yield
                dve.wait_ge(*PE("cs"))
                V.tensor_copy(cs[lane][:].rearrange("p b h -> p (b h)"), bk[0][:, 0:BH]).then_inc(*done("cs"))
                yield
                V.tensor_tensor(av[lane][:], ig, bk[0][:, 0:BH].rearrange("p (b h) -> p b h", b=BC), ALU.subtract).then_inc(*done("a"))
                yield
                dve.wait_ge(*PE("aT"))
                V.tensor_copy(aT[lane][:], bk[1][0:BH, 0:P]).then_inc(*done("aT"))
                yield
                dve.wait_ge(*DVE("aT"))
                V.tensor_tensor_scan(cmax[lane][:], aT[lane][:], aT[lane][:], -3.0e38, ALU.max, ALU.max).then_inc(*done("cmax"))
                yield
                dve.wait_ge(*DVE("cmax"))
                V.tensor_tensor(cdiag[lane][:], over(cmax[lane][:], BH), wide(ident[0:BH, 0:BH], P), ALU.mult).then_inc(*done("cdiag"))
                yield
                dve.wait_ge(*PE("cm"))
                V.tensor_tensor(cm[lane][:].rearrange("p b h -> p (b h)"), bk[0][:, 0:BH], cs[lane][:].rearrange("p b h -> p (b h)"), ALU.add).then_inc(*done("cm"))
                yield
                dve.wait_ge(*ACTS("D"))
                for par in range(2):
                    V.scalar_tensor_tensor(cT[lane][:, par].rearrange("p c s -> p (c s)"), bk[2 + par][:], DL ** -0.5,
                                           decayT[lane][:, par].rearrange("p c s -> p (c s)"), ALU.mult, ALU.mult).then_inc(*done(f"cT{par}"))
                    yield
                dve.wait_ge(*PE("ho1"))
                sums = [bk[b][:, 0:HL * (DL + 1)].rearrange("p (h c) -> p h c", h=HL) for b in range(BC)]
                for b in range(BC):
                    V.tensor_copy(ab[lane][:, b, :], sums[b][:, :, DL]).then_inc(*done(f"ab{b}"))
                    yield
                dve.wait_ge(*DVE("ab1"))
                V.scalar_tensor_tensor(nr[lane][:], ab[lane][:], -1.0, ab[lane][:], ALU.mult, ALU.max).then_inc(*done("abs"))
                yield
                dve.wait_ge(*DVE("abs"))
                dve.wait_ge(*ACTS("ne"))
                V.tensor_tensor(nr[lane][:], nr[lane][:], ne[lane][:], ALU.max).then_inc(*done("nr"))
                yield
                dve.wait_ge(*DVE("nr"))
                V.tensor_scalar(nr[lane][:], nr[lane][:], 1e-6, None, ALU.add).then_inc(*done("nre"))
                yield
                dve.wait_ge(*DVE("nre"))
                V.reciprocal(nr[lane][:], nr[lane][:]).then_inc(*done("rn"))
                yield
                dve.wait_ge(*DVE("rn"))
                for b in range(BC):
                    V.tensor_tensor(hst[lane][:, b, :].rearrange("p (h d) -> p h d", h=HL), sums[b][:, :, 0:DL], wide(nr[lane][:, b, :], DL),
                                    ALU.mult).then_inc(*done(f"h{b}"))
                    yield
                dve.wait_ge(*DVE("h1"))
                h4 = [t[:].rearrange("p b (h d) -> p (b h) d", h=HL) for t in (hst[lane], hce[lane], hq[lane])]
                f8 = [t[:].rearrange("p b h -> p (b h)") for t in (hsum[lane], hsq[lane], hvar[lane], hrs[lane])]
                V.tensor_reduce(f8[0], h4[0], AX.X, ALU.add).then_inc(*done("hsum"))
                yield
                dve.wait_ge(*DVE("hsum"))
                V.scalar_tensor_tensor(h4[1], wide(f8[0], DL), -1.0 / DL, h4[0], ALU.mult, ALU.add).then_inc(*done("hce"))
                yield
                dve.wait_ge(*DVE("hce"))
                V.tensor_tensor(h4[2], h4[1], h4[1], ALU.mult).then_inc(*done("hq"))
                yield
                dve.wait_ge(*DVE("hq"))
                V.tensor_reduce(f8[1], h4[2], AX.X, ALU.add).then_inc(*done("hsq"))
                yield
                dve.wait_ge(*DVE("hsq"))
                V.tensor_scalar(f8[2], f8[1], 1.0 / DL, EPS, ALU.mult, ALU.add).then_inc(*done("hvar"))
                yield
                dve.wait_ge(*POOL("hrs"))
                V.tensor_tensor(h4[1], h4[1], wide(f8[3], DL), ALU.mult).then_inc(*done("hn"))
                yield
                dve.wait_ge(*DVE("hn"))
                V.tensor_tensor(hce[lane][:], hce[lane][:], over(lnw1[:], BC), ALU.mult).then_inc(*done("w"))
                yield
                dve.wait_ge(*DVE("w"))
                V.tensor_tensor(x[:, bass.ds(c * BC, BC), :], hce[lane][:], x[:, bass.ds(c * BC, BC), :], ALU.add).then_inc(*done("res"))
                yield
                yield from stats(st, i, lane)

            in_turns(chunk)

    BW = weights["bit"]
    ROUND = 1.5 * 2.0 ** 23
    KI = INNER // P
    NB_W = ("wg", "wu", "wd")
    QAT = EX0 + 3232
    wq_b = {n: area(f"q_{n}", [P, KD * INNER], QAT + k * 1024, BF16) for k, n in enumerate(NB_W)}
    wgq, wuq = (wq_b[n].rearrange("p (k f) -> p k f", k=KD) for n in ("wg", "wu"))
    wdq = wq_b["wd"].rearrange("p (k d) -> p k d", k=KI)
    wtmp = area("wtmp", [P, KD * INNER], QAT + 3072)
    wsum = area("wsum", [P, 3], QAT + 5120)
    wsc = area("wsc", [P, 3], QAT + 5123)
    winv = area("winv", [P, 3], QAT + 5126)
    id_b = area("id_b", [P, P], QAT + 5136, BF16)
    BIT_LANE = 8280
    xr = [area(f"xr{n}", [P, BC, D], 0 + n * BIT_LANE) for n in range(2)]
    xq = [area(f"xq{n}", [P, BC, D], 512 + n * BIT_LANE, BF16) for n in range(2)]
    xqT = [area(f"xqT{n}", [P, KD, TOK], 768 + n * BIT_LANE, BF16) for n in range(2)]
    sil = [area(f"sil{n}", [P, 2, 512], 1024 + n * BIT_LANE) for n in range(2)]
    hb = [area(f"hb{n}", [P, BC, INNER], 2048 + n * BIT_LANE) for n in range(2)]
    hr = [area(f"hr{n}", [P, BC, INNER], 4096 + n * BIT_LANE) for n in range(2)]
    hqb = [area(f"hqb{n}", [P, BC, INNER], 6144 + n * BIT_LANE, BF16) for n in range(2)]
    hqT = [area(f"hqT{n}", [P, BC, KI, P], 7168 + n * BIT_LANE, BF16) for n in range(2)]
    am, qs, qi, am2, qs2, qi2, sc_g, sc_u, sc_d = (
        [area(f"b{k}_{n}", [P, BC], 8192 + 2 * k + n * BIT_LANE) for n in range(2)] for k in range(9))
    bit_sum, bit_ready = sem("weight_magnitudes_summed"), sem("weights_quantised")
    HU = [(b, hh) for b in range(BC) for hh in range(2)]
    stage("bit", NCH // 2, pe=both(["xqT", "n0", "n1", "n2", "n3", "hT0", "hT1", "out0", "out1"]),
          act=both(["prep0", "prep1", "n0", "n1", "n2", "n3"]),
          dve=both(["am", "amc", "rq", "qs", "qi", "scg", "scu", "r0", "r1", "q", "xqT", "n0", "n1", "am20", "amc20", "rq20", "qs20",
                    "n2", "n3", "am21", "amc21", "rq21", "qs21", "qi20", "r20", "q20", "scd0", "hT0", "qi21", "r21", "q21", "scd1",
                    "hT1", "res0", "res1"] + LN_DVE),
          pool=both(["rstd"]))

    def up_banks(n):
        return ((1, 2), (3, 0))[n % 2]

    def quantise_pe():
        pe = nc.tensor
        pe.wait_ge(bit_sum, 3)
        nc.tensor.matmul(bank[0][:, 0:3], ones[:], wsum[:], start=True, stop=True).then_inc(bit_sum, 1)

    def bit_pe():
        pe, st = nc.tensor, "bit"
        others_done(pe, "mlstm")
        pe.wait_ge(bit_ready, 1)
        with pe.Fori(0, NCH // 2) as i:
            def chunk(lane):
                bk = bank[4 * lane:4 * lane + 4]
                PE, ACTS, DVE, POOL = after(st, i, "AB"[lane])
                done = signals(pe_s, st, "AB"[lane])
                pe.wait_ge(*DVE("q"))
                for k in range(KD):
                    for b in range(BC):
                        last = nc.tensor.transpose(bk[0][:].bitcast(BF16)[:, (k * BC + b) * P:(k * BC + b + 1) * P], xq[lane][:, b, k * P:(k + 1) * P], id_b[:])
                last.then_inc(*done("xqT"))
                yield
                pe.wait_ge(*DVE("xqT"))
                for n, (b, hh) in enumerate(HU):
                    if n >= 2:
                        pe.wait_ge(*DVE(f"n{n - 2}"))
                    for w, dst in ((wgq, up_banks(n)[0]), (wuq, up_banks(n)[1])):
                        for k in range(KD):
                            last = nc.tensor.matmul(bk[dst][:], xqT[lane][:, k, b * P:(b + 1) * P], w[:, k, hh * 512:(hh + 1) * 512],
                                                    start=k == 0, stop=k == KD - 1)
                    last.then_inc(*done(f"n{n}"))
                    yield
                for b in range(BC):
                    pe.wait_ge(*DVE(f"q2{b}"))
                    for k in range(KI):
                        last = nc.tensor.transpose(bk[1 + b][:].bitcast(BF16)[:, k * P:(k + 1) * P], hqb[lane][:, b, k * P:(k + 1) * P], id_b[:])
                    last.then_inc(*done(f"hT{b}"))
                    yield
                for b in range(BC):
                    pe.wait_ge(*DVE(f"hT{b}"))
                    for k in range(KI):
                        last = nc.tensor.matmul(bk[3][:, b * D:(b + 1) * D], hqT[lane][:, b, k, :], wdq[:, k, :], start=k == 0, stop=k == KI - 1)
                    last.then_inc(*done(f"out{b}"))
                    yield

            in_turns(chunk)

    def bit_act():
        act, st = nc.scalar, "bit"
        others_done(act, "mlstm")
        with act.Fori(0, NCH // 2) as i:
            def chunk(lane):
                bk = bank[4 * lane:4 * lane + 4]
                PE, ACTS, DVE, POOL = after(st, i, "AB"[lane])
                done = signals(act_s, st, "AB"[lane])
                yield from prep(st, i, lane)
                for n, (b, hh) in enumerate(HU):
                    act.wait_ge(*PE(f"n{n}"))
                    act.wait_ge(*DVE("scg"))
                    if n >= 2:
                        act.wait_ge(*DVE(f"n{n - 2}"))
                    nc.scalar.activation(sil[lane][:, n % 2, :], bk[up_banks(n)[0]][:], ACT.Silu, scale=sc_g[lane][:, b:b + 1]).then_inc(*done(f"n{n}"))
                    yield

            in_turns(chunk)

    def bit_pool():
        pool, st = nc.gpsimd, "bit"
        others_done(pool, "mlstm")
        with pool.Fori(0, NCH // 2) as i:
            def chunk(lane):
                PE, ACTS, DVE, POOL = after(st, i, "AB"[lane])
                done = signals(pool_s, st, "AB"[lane])
                yield from stats_root(st, i, lane)

            in_turns(chunk)

    def quantise_dve():
        dve, V = nc.vector, nc.vector
        dve.wait_ge(w_loaded["bit"], 16)
        for n, name in enumerate(NB_W):
            V.tensor_reduce(wsum[:, n:n + 1], BW(name), AX.X, ALU.add, apply_absolute_value=True).then_inc(bit_sum, 1)
        V.tensor_copy(id_b[:], ident[:])
        dve.wait_ge(bit_sum, 4)
        V.tensor_scalar(wsum[:], bank[0][:, 0:3], 1.0 / (D * INNER), 1e-5, ALU.mult, ALU.max).then_inc(bit_q, 1)
        dve.wait_ge(bit_q, 1)
        V.reciprocal(wsc[:], wsum[:]).then_inc(bit_q, 1)
        dve.wait_ge(bit_q, 2)
        V.reciprocal(winv[:], wsc[:]).then_inc(bit_q, 1)
        for n, name in enumerate(NB_W):
            dve.wait_ge(bit_q, 3 + 3 * n)
            V.tensor_scalar(wtmp[:], BW(name), wsc[:, n:n + 1], ROUND, ALU.mult, ALU.add).then_inc(bit_q, 1)
            dve.wait_ge(bit_q, 4 + 3 * n)
            V.tensor_scalar(wtmp[:], wtmp[:], ROUND, 1.0, ALU.subtract, ALU.min).then_inc(bit_q, 1)
            dve.wait_ge(bit_q, 5 + 3 * n)
            V.tensor_scalar(wq_b[name], wtmp[:], -1.0, None, ALU.max).then_inc(bit_q, 1)
        dve.wait_ge(bit_q, 12)
        dve.sem_inc(bit_ready, 1)

    def bit_dve():
        dve, st = nc.vector, "bit"
        V = nc.vector
        others_done(dve, "mlstm")
        with dve.Fori(0, NCH // 2) as i:
            def chunk(lane):
                c = 2 * i + lane
                bk = bank[4 * lane:4 * lane + 4]
                PE, ACTS, DVE, POOL = after(st, i, "AB"[lane])
                done = signals(dve_s, st, "AB"[lane])
                dve.wait_ge(*ACTS("prep1"))
                V.tensor_reduce(am[lane][:], xn[lane][:], AX.X, ALU.max, apply_absolute_value=True).then_inc(*done("am"))
                yield
                dve.wait_ge(*DVE("am"))
                V.tensor_scalar(am[lane][:], am[lane][:], 1e-5, None, ALU.max).then_inc(*done("amc"))
                yield
                dve.wait_ge(*DVE("amc"))
                V.reciprocal(am[lane][:], am[lane][:]).then_inc(*done("rq"))
                yield
                dve.wait_ge(*DVE("rq"))
                V.tensor_scalar(qs[lane][:], am[lane][:], 127.0, None, ALU.mult).then_inc(*done("qs"))
                yield
                dve.wait_ge(*DVE("qs"))
                V.reciprocal(qi[lane][:], qs[lane][:]).then_inc(*done("qi"))
                yield
                dve.wait_ge(*DVE("qi"))
                V.tensor_scalar(sc_g[lane][:], qi[lane][:], winv[:, 0:1], None, ALU.mult).then_inc(*done("scg"))
                yield
                V.tensor_scalar(sc_u[lane][:], qi[lane][:], winv[:, 1:2], None, ALU.mult).then_inc(*done("scu"))
                yield
                for b in range(BC):
                    V.tensor_scalar(xr[lane][:, b, :], xn[lane][:, b, :], qs[lane][:, b:b + 1], ROUND, ALU.mult, ALU.add).then_inc(*done(f"r{b}"))
                    yield
                dve.wait_ge(*DVE("r1"))
                V.tensor_scalar(xq[lane][:], xr[lane][:], ROUND, 127.0, ALU.subtract, ALU.min).then_inc(*done("q"))
                yield
                dve.wait_ge(*PE("xqT"))
                V.tensor_scalar(xqT[lane][:].rearrange("p k t -> p (k t)"), bk[0][:].bitcast(BF16)[:, 0:KD * TOK], -128.0, None,
                                ALU.max).then_inc(*done("xqT"))
                yield

                def gated(n):
                    b, hh = HU[n]
                    dve.wait_ge(*ACTS(f"n{n}"))
                    V.scalar_tensor_tensor(hb[lane][:, b, hh * 512:(hh + 1) * 512], bk[up_banks(n)[1]][:], sc_u[lane][:, b:b + 1], sil[lane][:, n % 2, :],
                                           ALU.mult, ALU.mult).then_inc(*done(f"n{n}"))
                    yield

                def largest(b):
                    dve.wait_ge(*DVE(f"n{2 * b + 1}"))
                    V.tensor_reduce(am2[lane][:, b:b + 1], hb[lane][:, b, :], AX.X, ALU.max, apply_absolute_value=True).then_inc(*done(f"am2{b}"))
                    yield
                    dve.wait_ge(*DVE(f"am2{b}"))
                    V.tensor_scalar(am2[lane][:, b:b + 1], am2[lane][:, b:b + 1], 1e-5, None, ALU.max).then_inc(*done(f"amc2{b}"))
                    yield
                    dve.wait_ge(*DVE(f"amc2{b}"))
                    V.reciprocal(am2[lane][:, b:b + 1], am2[lane][:, b:b + 1]).then_inc(*done(f"rq2{b}"))
                    yield
                    dve.wait_ge(*DVE(f"rq2{b}"))
                    V.tensor_scalar(qs2[lane][:, b:b + 1], am2[lane][:, b:b + 1], 127.0, None, ALU.mult).then_inc(*done(f"qs2{b}"))
                    yield

                yield from gated(0)
                yield from gated(1)
                yield from largest(0)
                yield from gated(2)
                yield from gated(3)
                yield from largest(1)
                for b in range(BC):
                    dve.wait_ge(*DVE(f"qs2{b}"))
                    V.reciprocal(qi2[lane][:, b:b + 1], qs2[lane][:, b:b + 1]).then_inc(*done(f"qi2{b}"))
                    yield
                    V.tensor_scalar(hr[lane][:, b, :], hb[lane][:, b, :], qs2[lane][:, b:b + 1], ROUND, ALU.mult, ALU.add).then_inc(*done(f"r2{b}"))
                    yield
                    dve.wait_ge(*DVE(f"r2{b}"))
                    V.tensor_scalar(hqb[lane][:, b, :], hr[lane][:, b, :], ROUND, 127.0, ALU.subtract, ALU.min).then_inc(*done(f"q2{b}"))
                    yield
                    V.tensor_scalar(sc_d[lane][:, b:b + 1], qi2[lane][:, b:b + 1], winv[:, 2:3], None, ALU.mult).then_inc(*done(f"scd{b}"))
                    yield
                    dve.wait_ge(*PE(f"hT{b}"))
                    V.tensor_scalar(hqT[lane][:, b].rearrange("p k t -> p (k t)"), bk[1 + b][:].bitcast(BF16), -128.0, None,
                                    ALU.max).then_inc(*done(f"hT{b}"))
                    yield
                dve.wait_ge(*PE("out1"))
                for b in range(BC):
                    V.scalar_tensor_tensor(x[:, bass.ds(c * BC + b, 1), :], bk[3][:, b * D:(b + 1) * D], sc_d[lane][:, b:b + 1],
                                           x[:, bass.ds(c * BC + b, 1), :], ALU.mult, ALU.add).then_inc(*done(f"res{b}"))
                    yield
                yield from stats(st, i, lane)

            in_turns(chunk)

    def bit_sp():
        sp = nc.sync
        others_done(sp, "mlstm")
        load_weights(sp, "mqa")


    QW = weights["mqa"]
    q_w = QW("wq").rearrange("p (k m) -> p k m", k=KD)
    k_w, v_w = (QW(n).rearrange("p (k m) -> p k m", k=KD) for n in ("wk", "wv"))
    wout = QW("wout").rearrange("p (k n) -> p k n", k=HM)
    w1 = QW("w1").rearrange("p (k f) -> p k f", k=KD)
    w2 = QW("w2").rearrange("p (k n) -> p k n", k=KI)
    q4 = area("q4", [P, HM, TOK], 0)
    m4 = area("m4", [P, HM, TOK], 2048)
    ff = area("ff", [P, KI, TOK], 4096)
    prob4 = area("prob4", [P, 4, FAN, P], 6144)
    probT4 = area("probT4", [P, 2, FAN, P], 8192)
    masked = area("masked", [P, 2, FAN, P], 9216)
    k4 = area("k4", [P, TOK], 10240)
    v4 = area("v4", [P, BC, HD], 10496)
    mask4 = area("mask4", [P, BC, P], 10624)
    ctx4 = area("ctx4", [P, BC, D], 10880)
    cn4 = area("cn4", [P, BC, D], 11392)
    cnT = area("cnT", [P, KD, TOK], 11904)
    th = area("th", [P, 2, TOK], 12416)
    gated4 = area("gated4", [P, 2, TOK], 12996)
    sm4 = area("sm4", [P, 3, 4, FAN], 12928)
    cbn = area("cbn", [P, BC, 6], 12976)
    cmv = area("cmv", [P, BC, 2], 12988)
    cveps = area("cveps", [P, BC], 12992)
    crstd = area("crstd", [P, BC], 12994)
    PORDER4 = [at_slot(t, ("S", 0), ("T", 2), ("PV", 3), ("F", 0)) for t in SLOTS]
    DORDER4 = [at_slot(t, ("add", 0), ("max", 0), ("rec", 1), ("copy", 2)) + [("o", t - 3)] * (t >= 3 and t % 2 == 0)
               + at_slot(t, ("g", 1), ("f", 1)) for t in SLOTS]
    CTX_DVE = ["cbn0", "cbn1", "cag0", "cag1", "cveps"]

    def names4(order):
        return [f"{a}{t}" for slot in order for a, t in slot]

    for name, count, ahead in (("mqa_first", 1, None), ("mqa", NCH - 1, True), ("mqa_last", 1, False)):
        lead = name == "mqa_first"
        dve_slots = []
        for t, steps4 in enumerate(DORDER4):
            dve_slots += [f"{a}{n}" for a, n in steps4] + CTX_DVE * (t == 1 and bool(ahead)) + ["cn0", "cn1"] * (t == 4 and bool(ahead))
        act_slots = [f"{a}{t}" for t in range(UNITS) for a in ("exp", "th")]
        if ahead:
            act_slots[10:10] = ["prep0", "prep1"]
        if lead:
            stage(name, count, pe=["xT", "cT"], act=["prep0", "prep1"], dve=CTX_DVE + ["cn0", "cn1", "xT", "cT"], pool=["crstd"])
        else:
            stage(name, count, pe=["k", "v", "q0", "q1", "q2", "q3"] + names4(PORDER4) + ["xT", "cT"] * ahead + ["out0", "out1"],
                  act=act_slots, dve=["k", "v", "q0", "q1", "q2", "q3"] + dve_slots + ["xT", "cT"] * ahead + ["res"] + LN_DVE,
                  pool=["norm0"] + ["crstd"] * ahead + [f"norm{t}" for t in range(1, UNITS)] + ["rstd"])

    def mqa_chunks(eng, chunk):
        with eng.Fori(0, NCH - 1) as i:
            chunk("mqa", i, i, True)
        chunk("mqa_last", 0, NCH - 1, False)

    def chunk_before(steps, c, name):
        return steps.sem, steps.at("mqa", c, name, back=1)

    def mqa_sp():
        sp = nc.sync
        others_done(sp, "bit")
        load_weights(sp, "low")

        def load_ctx(c):
            sp.dma_start(ctx4[:], ctx_dram[:, bass.ds(c * BC, BC), :]).then_inc(ctx4_loaded, 16)

        def load_mask(c):
            sp.dma_start(mask4[:], mask_dram[:, bass.ds(c * BC, BC), :]).then_inc(mask_loaded, 16)

        load_ctx(0)
        load_mask(0)
        sp.wait_ge(dve_s.sem, dve_s.at("mqa_first", 0, "cn1"))
        load_ctx(1)
        with sp.Fori(0, NCH - 2) as i:
            sp.wait_ge(dve_s.sem, dve_s.at("mqa", i, "cn1"))
            load_ctx(i + 2)
            sp.wait_ge(dve_s.sem, dve_s.at("mqa", i, f"add{UNITS - 1}"))
            load_mask(i + 1)
        sp.wait_ge(dve_s.sem, dve_s.at("mqa", NCH - 2, f"add{UNITS - 1}"))
        load_mask(NCH - 1)

    def mqa_pe():
        pe = nc.tensor
        others_done(pe, "bit")
        pe.wait_ge(w_loaded["mqa"], 16)

        def turn_ctx(st, i):
            PE, ACTS, DVE, POOL = after(st, i)
            pe.wait_ge(*DVE("cn1"))
            for k in range(KD):
                for b in range(BC):
                    last = nc.tensor.transpose(bank[4][:, (k * BC + b) * P:(k * BC + b + 1) * P], cn4[:, b, k * P:(k + 1) * P], ident[:])
            last.then_inc(*signals(pe_s, st)("cT"))

        def chunk(st, i, c, more):
            PE, ACTS, DVE, POOL = after(st, i)
            done = signals(pe_s, st)
            pe.wait_ge(*chunk_before(dve_s, c, "cT"))
            for k in range(KD):
                last = nc.tensor.matmul(bank[4][:, 0:TOK], k_w[:, k, :], cnT[:, k, :], start=k == 0, stop=k == KD - 1)
            last.then_inc(*done("k"))
            for b in range(BC):
                for k in range(KD):
                    last = nc.tensor.matmul(bank[5][:, b * HD:(b + 1) * HD], cnT[:, k, b * P:(b + 1) * P], v_w[:, k, 0:HD],
                                            start=k == 0, stop=k == KD - 1)
            last.then_inc(*done("v"))
            for g in range(4):
                for m in range(2):
                    mm = 2 * g + m
                    for k in range(KD):
                        last = nc.tensor.matmul(bank[g][:, m * TOK:(m + 1) * TOK], q_w[:, k, mm * P:(mm + 1) * P], xnT[0][:, k, :],
                                                start=k == 0, stop=k == KD - 1)
                last.then_inc(*done(f"q{g}"))
            pe.wait_ge(*DVE("q3"))
            for slot in PORDER4:
                for what, t in slot:
                    b, u, par = unit(t)
                    rows = slice(HD * par, HD * par + HD)
                    if what == "S":
                        if t >= 2:
                            pe.wait_ge(*DVE(f"add{t - 2}"))
                        for j in range(FAN):
                            last = nc.tensor.matmul(bank[t % 2][:, j * P:(j + 1) * P], q4[rows, FAN * u + j, b * P:(b + 1) * P],
                                                    k4[rows, b * P:(b + 1) * P], start=True, stop=True)
                    elif what == "F":
                        if t == 1:
                            pe.wait_ge(*chunk_before(dve_s, c, "res"))
                        if t >= 2:
                            pe.wait_ge(*DVE(f"f{t - 2}"))
                        for part, first in ((0, INNER + t * P), (1, t * P)):
                            for k in range(KD):
                                last = nc.tensor.matmul(bank[7 - t % 2][:, part * TOK:(part + 1) * TOK], w1[:, k, first:first + P], xnT[0][:, k, :],
                                                        start=k == 0, stop=k == KD - 1)
                    elif what == "T":
                        pe.wait_ge(*POOL(f"norm{t}"))
                        if t >= 2:
                            pe.wait_ge(*DVE(f"copy{t - 2}"))
                        for j in range(FAN):
                            last = nc.tensor.transpose(bank[2 + t % 2][:, j * P:(j + 1) * P], prob4[:, t % 4, j, :], ident[:])
                    else:
                        pe.wait_ge(*DVE(f"copy{t}"))
                        if b == 1 and par == 0:
                            pe.wait_ge(*DVE(f"o{t - 3}"))
                        last = nc.tensor.matmul(bank[4 + u][rows, :], v4[:, b, :], probT4[:, t % 2].rearrange("p j s -> p (j s)"),
                                                start=True, stop=True)
                    last.then_inc(*done(f"{what}{t}"))
            if more:
                pe.wait_ge(*DVE(f"f{KI - 2}"))
                alone(turn_x(st, i))
                pe.wait_ge(*DVE("o5"))
                turn_ctx(st, i)
            pe.wait_ge(*DVE(f"f{KI - 1}"))
            for b in range(BC):
                pe.wait_ge(*DVE(f"o{4 * b + 3}"))
                for n, (src, w) in enumerate(((ff, w2), (m4, wout))):
                    for k in range(HM):
                        last = nc.tensor.matmul(bank[6][:, b * D:(b + 1) * D], src[:, k, b * P:(b + 1) * P], w[:, k, :],
                                                start=n == 0 and k == 0, stop=n == 1 and k == HM - 1)
                last.then_inc(*done(f"out{b}"))

        alone(turn_x("mqa_first", 0))
        turn_ctx("mqa_first", 0)
        pe.wait_ge(dve_s.sem, dve_s.all("mqa_first"))
        mqa_chunks(pe, chunk)

    def mqa_act():
        act = nc.scalar
        others_done(act, "bit")

        def chunk(st, i, c, more):
            PE, ACTS, DVE, POOL = after(st, i)
            done = signals(act_s, st)
            for t in range(UNITS):
                if t == 5 and more:
                    alone(prep(st, i, chunk=c + 1))
                act.wait_ge(*DVE(f"max{t}"))
                if t >= 4:
                    act.wait_ge(*PE(f"T{t - 4}"))
                for j in range(FAN):
                    last = nc.scalar.activation(prob4[:, t % 4, j, :], masked[:, t % 2, j, :], ACT.Exp,
                                                bias=sm4[:, 0, t % 4, j:j + 1], accum_out=sm4[:, 1, t % 4, j:j + 1])
                last.then_inc(*done(f"exp{t}"))
                act.wait_ge(*PE(f"F{t}"))
                nc.scalar.activation(th[:, t % 2, :], bank[7 - t % 2][:, 0:TOK], ACT.Tanh, scale=0.5).then_inc(*done(f"th{t}"))

        alone(prep("mqa_first", 0))
        mqa_chunks(act, chunk)

    def mqa_pool():
        pool = nc.gpsimd
        others_done(pool, "bit")

        def ctx_root(st, i):
            pool.wait_ge(dve_s.sem, dve_s.at(st, i, "cveps"))
            nc.gpsimd.tensor_tensor(crstd[:], cveps[:], mhalf[:], ALU.pow).then_inc(*signals(pool_s, st)("crstd"))

        def chunk(st, i, c, more):
            done = signals(pool_s, st)
            for t in range(UNITS):
                pool.wait_ge(dve_s.sem, dve_s.at(st, i, f"rec{t}"))
                nc.gpsimd.tensor_tensor(prob4[:, t % 4], prob4[:, t % 4], sm4[:, 2, t % 4, :].unsqueeze(2).to_broadcast([P, FAN, P]),
                                        ALU.mult).then_inc(*done(f"norm{t}"))
                if t == 0 and more:
                    ctx_root(st, i)
            alone(stats_root(st, i, chunk=c))

        ctx_root("mqa_first", 0)
        mqa_chunks(pool, chunk)

    def mqa_dve():
        dve = nc.vector
        V = nc.vector
        others_done(dve, "bit")
        dve.wait_ge(w_loaded["mqa"], 16)

        def ctx_stats(st, i, c):
            PE, ACTS, DVE, POOL = after(st, i)
            done = signals(dve_s, st)
            dve.wait_ge(ctx4_loaded, c * 16 + 16)
            dve.sem_inc(held, 1)
            for b in range(BC):
                V.bn_stats(cbn[:, b, :], ctx4[:, b, :]).then_inc(*done(f"cbn{b}"))
            for b in range(BC):
                dve.wait_ge(*DVE(f"cbn{b}"))
                dve.sem_inc(held, 1)
                V.bn_aggr(cmv[:, b, :], cbn[:, b, :]).then_inc(*done(f"cag{b}"))
            dve.wait_ge(*DVE("cag1"))
            V.tensor_scalar(cveps[:], cmv[:, :, 1], EPS, None, ALU.add).then_inc(*done("cveps"))

        def ctx_norm(st, i):
            dve.wait_ge(pool_s.sem, pool_s.at(st, i, "crstd"))
            for b in range(BC):
                V.tensor_scalar(cn4[:, b, :], ctx4[:, b, :], cmv[:, b, 0:1], crstd[:, b:b + 1], ALU.subtract, ALU.mult).then_inc(
                    *signals(dve_s, st)(f"cn{b}"))

        def turned(st, i):
            for what, src, dst, gain, shift in (("xT", bank[7], xnT[0], "ln_g", "ln_b"), ("cT", bank[4], cnT, "cln_g", "cln_b")):
                dve.wait_ge(pe_s.sem, pe_s.at(st, i, what))
                for k in range(KD):
                    last = V.tensor_scalar(dst[:, k, :], src[:, k * TOK:(k + 1) * TOK], QW(gain)[:, k:k + 1], QW(shift)[:, k:k + 1],
                                           ALU.mult, ALU.add)
                last.then_inc(*signals(dve_s, st)(what))

        def chunk(st, i, c, more):
            PE, ACTS, DVE, POOL = after(st, i)
            done = signals(dve_s, st)
            dve.wait_ge(*PE("k"))
            V.tensor_copy(k4[:], bank[4][:, 0:TOK]).then_inc(*done("k"))
            dve.wait_ge(*PE("v"))
            V.tensor_copy(v4[:].rearrange("p b d -> p (b d)"), bank[5][:, 0:BC * HD]).then_inc(*done("v"))
            for g in range(4):
                dve.wait_ge(*PE(f"q{g}"))
                V.tensor_scalar(q4[:, 2 * g:2 * g + 2, :].rearrange("p m t -> p (m t)"), bank[g][:], HD ** -0.5, None,
                                ALU.mult).then_inc(*done(f"q{g}"))
            for n, slot in enumerate(DORDER4):
                for what, t in slot:
                    b, u, par = unit(t)
                    if what == "add":
                        dve.wait_ge(*PE(f"S{t}"))
                        if t == 0:
                            dve.wait_ge(mask_loaded, c * 16 + 16)
                        if t >= 2:
                            dve.wait_ge(*ACTS(f"exp{t - 2}"))
                        ins = V.tensor_tensor(masked[:, t % 2], bank[t % 2][:].rearrange("p (j s) -> p j s", j=FAN), over(mask4[:, b, :], FAN), ALU.add)
                    elif what == "max":
                        dve.wait_ge(*DVE(f"add{t}"))
                        ins = V.tensor_reduce(sm4[:, 0, t % 4, :], masked[:, t % 2], AX.X, ALU.max, negate=True)
                    elif what == "rec":
                        dve.wait_ge(*ACTS(f"exp{t}"))
                        ins = V.reciprocal(sm4[:, 2, t % 4, :], sm4[:, 1, t % 4, :])
                    elif what == "copy":
                        dve.wait_ge(*PE(f"T{t}"))
                        ins = V.tensor_copy(probT4[:, t % 2].rearrange("p j s -> p (j s)"), bank[2 + t % 2][:])
                    elif what == "o":
                        dve.wait_ge(*PE(f"PV{t}"))
                        ins = V.tensor_copy(m4[:, FAN * u:FAN * u + FAN, b * P:(b + 1) * P], bank[4 + u][:].rearrange("p (j s) -> p j s", j=FAN))
                    elif what == "g":
                        dve.wait_ge(*ACTS(f"th{t}"))
                        ins = V.scalar_tensor_tensor(gated4[:, t % 2, :], th[:, t % 2, :], 1.0, bank[7 - t % 2][:, 0:TOK], ALU.add, ALU.mult)
                    else:
                        dve.wait_ge(*DVE(f"g{t}"))
                        ins = V.scalar_tensor_tensor(ff[:, t, :], gated4[:, t % 2, :], 0.5, bank[7 - t % 2][:, TOK:2 * TOK], ALU.mult, ALU.mult)
                    ins.then_inc(*done(f"{what}{t}"))
                if n == 1 and more:
                    ctx_stats(st, i, c + 1)
                if n == 4 and more:
                    ctx_norm(st, i)
            if more:
                turned(st, i)
            dve.wait_ge(*PE("out1"))
            V.tensor_tensor(x[:, bass.ds(c * BC, BC), :], bank[6][:].rearrange("p (b d) -> p b d", b=BC),
                            x[:, bass.ds(c * BC, BC), :], ALU.add).then_inc(*done("res"))
            alone(stats(st, i, chunk=c))

        ctx_stats("mqa_first", 0, 0)
        ctx_norm("mqa_first", 0)
        turned("mqa_first", 0)
        mqa_chunks(dve, chunk)

    FW = weights["low"]
    RK = 64
    u1 = FW("u1").rearrange("p (k r) -> p k r", k=KD)
    v1 = FW("v1").rearrange("p (j m) -> p j m", m=P)
    u2 = FW("u2").rearrange("p (k r) -> p k r", k=KI)
    LOW_LANE = 2560
    pT5 = [area(f"pT5_{n}", [P, TOK], n * LOW_LANE) for n in range(2)]
    h5 = [area(f"h5_{n}", [P, KI, TOK], 256 + n * LOW_LANE) for n in range(2)]
    q5 = [area(f"q5_{n}", [RK, TOK], 2304 + n * LOW_LANE) for n in range(2)]
    stage("low", NCH // 2, pe=both(["xT", "p"] + [(f"h{g}0", f"h{g}1") for g in range(2)] + ["q", "out"]),
          act=both(["prep0", "prep1"] + [f"h{g}{half}" for g in range(2) for half in range(2)]),
          dve=both(["xT", "p", "q", "res"]), pool=both(["b2"]))

    def low_sp():
        sp, st = nc.sync, "low"
        with sp.Fori(0, NCH // 2) as i:
            def chunk(lane):
                c = 2 * i + lane
                PE, ACTS, DVE, POOL = after(st, i, "AB"[lane])
                sp.wait_ge(*DVE("res"))
                sp.dma_start(out_dram[:, bass.ds(c * BC, BC), :], x[:, bass.ds(c * BC, BC), :]).then_inc(out_stored, 16)
                yield

            in_turns(chunk)

    def low_pe():
        pe, st = nc.tensor, "low"
        others_done(pe, "mqa_last")
        pe.wait_ge(w_loaded[st], 16)
        with pe.Fori(0, NCH // 2) as i:
            def chunk(lane):
                bk = bank[4 * lane:4 * lane + 4]
                PE, ACTS, DVE, POOL = after(st, i, "AB"[lane])
                done = signals(pe_s, st, "AB"[lane])
                yield from turn_x(st, i, lane, bk[0])
                pe.wait_ge(*DVE("xT"))
                for k in range(KD):
                    last = nc.tensor.matmul(bk[1][:, 0:TOK], u1[:, k, :], xnT[lane][:, k, :], start=k == 0, stop=k == KD - 1)
                last.then_inc(*done("p"))
                yield
                pe.wait_ge(*DVE("p"))
                for g in range(2):
                    for half in range(2):
                        rows = slice(RK * half, RK * half + RK)
                        for j in range(2):
                            last = nc.tensor.matmul(bk[2 + half - 2 * g][:, j * TOK:(j + 1) * TOK], v1[rows, 2 * g + j, :], pT5[lane][rows, :],
                                                    start=True, stop=True)
                        last.then_inc(*done(f"h{g}{half}"))
                    yield
                for m in range(KI):
                    pe.wait_ge(*ACTS(f"h{m // 4}{1}"))
                    last = nc.tensor.matmul(bk[2][0:RK, 0:TOK], u2[:, m, :], h5[lane][:, m, :], start=m == 0, stop=m == KI - 1)
                last.then_inc(*done("q"))
                yield
                pe.wait_ge(*DVE("q"))
                for b in range(BC):
                    last = nc.tensor.matmul(bk[3][:, b * D:(b + 1) * D], q5[lane][:, b * P:(b + 1) * P], FW("v2")[0:RK, :], start=True, stop=True)
                last.then_inc(*done("out"))
                yield

            in_turns(chunk)

    def low_act():
        act, st = nc.scalar, "low"
        others_done(act, "mqa_last")
        act.wait_ge(w_loaded[st], 16)
        with act.Fori(0, NCH // 2) as i:
            def chunk(lane):
                bk = bank[4 * lane:4 * lane + 4]
                PE, ACTS, DVE, POOL = after(st, i, "AB"[lane])
                done = signals(act_s, st, "AB"[lane])
                yield from prep(st, i, lane)
                for g in range(2):
                    for half in range(2):
                        act.wait_ge(*PE(f"h{g}{half}"))
                        for j in range(2):
                            m = 2 * (2 * g + j) + half
                            last = nc.scalar.activation(h5[lane][:, m, :], bk[2 + half - 2 * g][:, j * TOK:(j + 1) * TOK], ACT.Gelu_apprx_tanh,
                                                        bias=FW("b1")[:, m:m + 1])
                        last.then_inc(*done(f"h{g}{half}"))
                        yield

            in_turns(chunk)

    def low_pool():
        pool = nc.gpsimd
        others_done(pool, "mqa_last")
        pool.wait_ge(w_loaded["low"], 16)
        st = "low"
        with pool.Fori(0, NCH // 2) as i:
            def chunk(lane):
                c = 2 * i + lane
                PE, ACTS, DVE, POOL = after(st, i, "AB"[lane])
                done = signals(pool_s, st, "AB"[lane])
                pool.wait_ge(*ACTS("prep1"))
                pool.sem_inc(held, 1)
                nc.gpsimd.tensor_tensor(x[:, bass.ds(c * BC, BC), :], x[:, bass.ds(c * BC, BC), :], over(FW("b2"), BC), ALU.add).then_inc(*done("b2"))
                yield

            in_turns(chunk)

    def low_dve():
        dve, st = nc.vector, "low"
        V = nc.vector
        others_done(dve, "mqa_last")
        with dve.Fori(0, NCH // 2) as i:
            def chunk(lane):
                c = 2 * i + lane
                bk = bank[4 * lane:4 * lane + 4]
                PE, ACTS, DVE, POOL = after(st, i, "AB"[lane])
                done = signals(dve_s, st, "AB"[lane])
                dve.wait_ge(*PE("xT"))
                V.tensor_copy(xnT[lane][:].rearrange("p k t -> p (k t)"), bk[0][:]).then_inc(*done("xT"))
                yield
                dve.wait_ge(*PE("p"))
                V.tensor_copy(pT5[lane][:], bk[1][:, 0:TOK]).then_inc(*done("p"))
                yield
                dve.wait_ge(*PE("q"))
                V.tensor_copy(q5[lane][:], bk[2][0:RK, 0:TOK]).then_inc(*done("q"))
                yield
                dve.wait_ge(*PE("out"))
                dve.wait_ge(*POOL("b2"))
                V.tensor_tensor(x[:, bass.ds(c * BC, BC), :], bk[3][:].rearrange("p (b d) -> p b d", b=BC),
                                x[:, bass.ds(c * BC, BC), :], ALU.add).then_inc(*done("res"))
                yield

            in_turns(chunk)
    sp_prog = [attn_sp, rec_sp, moe_sp, mlstm_sp, bit_sp, mqa_sp, low_sp]
    pe_prog = [attn_pe, spike_pe, rec_pe, moe_pe, mlstm_pe, bit_pe, mqa_pe, low_pe]
    act_prog = [attn_act, spike_act, rec_act, moe_act, mlstm_act, bit_act, mqa_act, low_act]
    dve_prog = [attn_dve, spike_dve, rec_dve, moe_dve, mlstm_dve, bit_dve, mqa_dve, low_dve]
    pool_prog = [consts_pool, attn_pool, spike_pool, rec_pool, moe_pool, mlstm_pool, bit_pool, mqa_pool, low_pool]
    block = ctx.enter_context(nc.Block())

    @block.sync
    def _(sp):
        for f in sp_prog:
            f()
        sp.wait_ge(out_stored, 16 * NCH)

    @block.tensor
    def _(pe):
        for f in pe_prog:
            f()

    @block.scalar
    def _(act):
        for f in act_prog:
            f()

    @block.vector
    def _(dve):
        for f in dve_prog:
            f()

    @block.gpsimd
    def _(pool):
        for f in pool_prog:
            f()


def pack(inputs):
    import numpy as np

    def a(name):
        return np.asarray(inputs[name])

    def rows(w):
        return w.reshape(-1, P, w.shape[1]).transpose(1, 0, 2).reshape(P, -1)

    def col(v, n=P):
        return v.reshape(-1, n).T

    def all_rows(v):
        return np.broadcast_to(v.reshape(1, -1), (P, v.size))

    def twice(w):
        return np.concatenate([w, w], 0)

    def put(stage, parts):
        cols = []
        for name, n in LAYOUT[stage]:
            v = parts[name]
            assert v.shape[1] == n and v.shape[0] in (P, 64), (stage, name, v.shape, n)
            if v.shape[0] == 64:
                v = twice(v)
            cols.append(v)
        return np.ascontiguousarray(np.concatenate(cols, 1))

    w = {}
    p = "L0_xattn_"
    w["attn"] = put("attn", dict(wk=rows(a(p + "Wk")), wv=rows(a(p + "Wv")), wq=rows(a(p + "Wq")), bk=col(a(p + "bk")),
                                 bq=col(a(p + "bq")), bv=col(a(p + "bv")), wu=rows(a(p + "Wu")), bu=all_rows(a(p + "bu"))))
    p = "L0_ffn_"
    e_w1 = a(p + "e_w1").reshape(NE0, MD, 2, P).transpose(2, 1, 0, 3).reshape(P, NE0 * P)
    w["spike"] = put("spike", dict(
        enc=rows(a(p + "enc_w")), enc_b=col(a(p + "enc_b")),
        s2c=rows(np.concatenate([a(p + "s2c_w")] * 2, 1)), s2c_b=twice(a(p + "s2c_b").reshape(-1, 1)),
        rw1=a(p + "r_w1"), rb1=a(p + "r_b1").reshape(-1, 1), rw2=a(p + "r_w2"), rb2=all_rows(a(p + "r_b2")),
        ew1=e_w1, eb1=a(p + "e_b1").reshape(NE0 * 2, P).T,
        ew2=a(p + "e_w2").reshape(NE0, 2, P, MD).transpose(2, 0, 1, 3).reshape(P, -1), eb2=all_rows(a(p + "e_b2")),
        c2s=a(p + "c2s_w"), c2s_b=col(a(p + "c2s_b")), dec=rows(a(p + "dec_w")), dec_b=all_rows(a(p + "dec_b")),
        ln_g=all_rows(a(p + "ln_g")), ln_b=all_rows(a(p + "ln_b"))))
    p = "L1_xattn_"
    w["rec"] = put("rec", dict(wi=rows(a(p + "Wi").T), bi=col(a(p + "bi")), wg=rows(a(p + "Wg").T), bg=col(a(p + "bg")),
                               a=rows(a(p + "A").T), bm=rows(a(p + "Bm").T), wo=rows(a(p + "Wo").T), bo=all_rows(a(p + "bo")),
                               decay=col(np.repeat(a(p + "decay").reshape(-1), D // 16))))
    p = "L1_ffn_"
    down = a(p + "ws_down")
    pad = np.zeros((P - (FE - P), D), down.dtype)
    w["moe"] = put("moe", dict(router=rows(a(p + "router_w").T), sgu=rows(a(p + "ws_gate_up")), sdown=rows(np.concatenate([down, pad], 0))))
    gu = np.concatenate([a(p + "w_gate").reshape(NE, KD, P, FE), a(p + "w_up").reshape(NE, KD, P, FE)], 3)
    w["gate_up"] = np.ascontiguousarray(gu.transpose(0, 2, 1, 3).reshape(NE, P, KD * 2 * FE))
    wd = a(p + "w_down")
    w["down"] = np.ascontiguousarray(wd)
    p = "L2_xattn_"
    gates = np.concatenate([a(p + "w_igate"), a(p + "w_fgate")], 0).T
    w["mlstm"] = put("mlstm", dict(gq=rows(gates[:D]), gk=rows(gates[D:2 * D]), gv=rows(gates[2 * D:]),
                                   gb=all_rows(np.concatenate([a(p + "b_igate"), a(p + "b_fgate")])), lnw=all_rows(a(p + "ln_weight"))))
    p = "L2_ffn_"
    w["bit"] = put("bit", dict(wg=rows(a(p + "w_gate").T), wu=rows(a(p + "w_up").T), wd=rows(a(p + "w_down").T)))
    p = "L3_xattn_"
    kv = a(p + "Wkv")
    w["mqa"] = put("mqa", dict(wq=rows(a(p + "Wq")), wk=rows(np.concatenate([kv[:, :HD]] * 2, 1)), wv=rows(np.concatenate([kv[:, HD:]] * 2, 1)),
                               wout=rows(a(p + "Wout")), w1=rows(a(p + "W1")), w2=rows(a(p + "W2")), ln_g=col(a(p + "ln_g")),
                               ln_b=col(a(p + "ln_b")), cln_g=col(a(p + "cln_g")), cln_b=col(a(p + "cln_b"))))
    p = "L3_ffn_"
    v1 = a(p + "V1").reshape(64, 4, 2, P).transpose(2, 0, 1, 3).reshape(P, -1)
    w["low"] = put("low", dict(u1=rows(np.concatenate([a(p + "U1")] * 2, 1)), v1=v1, b1=col(a(p + "b1")), u2=rows(a(p + "U2")),
                               v2=a(p + "V2"), b2=all_rows(a(p + "b2"))))
    return w


def kernel(**inputs):
    import numpy as np
    import concourse.bacc as bacc
    from concourse.bass_utils import run_bass_kernel_spmd

    w = pack(inputs)
    arrays = {"w_" + k: v for k, v in w.items()}
    arrays["x"] = np.ascontiguousarray(inputs["x"])
    arrays["ctx"] = np.ascontiguousarray(inputs["ctx_1024"])
    arrays["ctxT"] = np.ascontiguousarray(np.asarray(inputs["ctx_1024"]).reshape(B * S, D).T)
    arrays["mask"] = np.ascontiguousarray(inputs["mask_BxSxS2_ff0"])
    p = np.arange(P, dtype=np.float32)
    arrays["consts"] = np.concatenate([
        (p[:, None] < p[None, :]).astype(np.float32),
        p[:, None] + P * np.arange(B, dtype=np.float32)[None, :],
        np.broadcast_to(NE * CAP - CAP * np.arange(NE, dtype=np.float32), (P, NE)),
        (TOPK * (p[:, None, None] + P * np.arange(B)[None, :, None]) + np.arange(TOPK)[None, None, :]).reshape(P, -1).astype(np.float32),
        (p[:, None] > p[None, :]).astype(np.float32),
    ], 1)
    slots = np.arange(NE * CAP + B * S * TOPK)
    arrays["table0"] = np.stack([B * S + slots % P, 0 * slots], 1).astype(np.float32)
    nc = bacc.Bacc("TRN2", target_bir_lowering=False, num_devices=1)
    ins = {k: nc.dram_tensor(f"in_{k}", v.shape, mybir.dt.from_np(v.dtype), kind="ExternalInput").ap() for k, v in arrays.items()}
    out = nc.dram_tensor("out_x", (B, S, D), F32, kind="ExternalOutput").ap()
    build(nc, ins, out)
    r = run_bass_kernel_spmd(nc, [{f"in_{k}": v for k, v in arrays.items()}], core_ids=[0])
    return r.results[0]["out_x"]
```
